# Optimizing a Trainium2 kernel written in Bass

```python
import numpy as np
import jax
import jax.numpy as jnp

def _softmax(x, axis=-1):
    return jax.nn.softmax(x, axis=axis)

def _gelu(x):
    return jax.nn.gelu(x, approximate=True)

def _silu(x):
    return jax.nn.silu(x)

def _sigmoid(x):
    return jax.nn.sigmoid(x)

def _layernorm(x, axis=-1, eps=1e-05):
    m = jnp.mean(x, axis=axis, keepdims=True)
    v = jnp.var(x, axis=axis, keepdims=True)
    return (x - m) / jnp.sqrt(v + eps)

def _scatter_add(tgt, idx, src, axis=0):
    return tgt.at[idx].add(src)

def _segment_sum(src, seg, n):
    return jax.ops.segment_sum(src, seg, n)
kernel_name = 'mk_audio_tower_d4_tok_aud1d256_r4_574c9d'

def setup_inputs(seed: int=0):
    np.random.seed(seed)
    _w = jnp.asarray

    def _rec_inputs():
        import jax
        import jax.numpy as jnp
        _rk = jax.random.key(seed)
        x = 0.000296351 + 0.99907 * jax.random.normal(jax.random.fold_in(_rk, 1), (64, 4000), jnp.float32)
        return x
    x = _rec_inputs()

    def _L0_tok_setup():
        import jax, jax.numpy as jnp
        import numpy as np
        B, L = (64, 4096)
        INTERP_FACTOR = 0.25
        WINDOW, STEP = (64, 64)
        ALPHA, BETA, TEMP = (0.12, 0.9, 1.0)
        A = -0.75

        def _cubic_w(t):
            at = jnp.abs(t)
            w_near = ((A + 2.0) * at - (A + 3.0)) * at * at + 1.0
            w_far = ((A * at - 5.0 * A) * at + 8.0 * A) * at - 4.0 * A
            return jnp.where(at <= 1.0, w_near, jnp.where(at < 2.0, w_far, 0.0))

        def cubic_interpolate_1d(signal, interp_factor):
            b, n = signal.shape
            num_points = int((n - 1) / interp_factor) + 1
            x = jnp.linspace(0.0, 1.0, num_points) * (n - 1)
            i0 = jnp.floor(x).astype(jnp.int32)
            frac = x - i0.astype(x.dtype)
            offs = jnp.arange(-1, 3)
            idx = jnp.clip(i0[:, None] + offs[None, :], 0, n - 1)
            w = _cubic_w(frac[:, None] - offs[None, :].astype(x.dtype))
            taps = signal[:, idx]
            return jnp.einsum('bpk,pk->bp', taps, w)

        def _apply_kernels(x):
            poly = (x + 1.3) ** 2
            gauss = jnp.exp(-0.5 * ((x - 0.7) / 1.0) ** 2)
            return 0.5 * poly + 0.5 * gauss

        def soft_minimum(a, b, temperature):
            b = jnp.broadcast_to(b, a.shape)
            stacked = jnp.stack([-a * temperature, -b * temperature], axis=0)
            return -jax.nn.logsumexp(stacked, axis=0) / temperature

        def _forward(signal):
            interp = cubic_interpolate_1d(signal, INTERP_FACTOR)
            n = interp.shape[1]
            n_windows = (n - WINDOW) // STEP + 1
            starts = jnp.arange(n_windows) * STEP
            idx = starts[:, None] + jnp.arange(WINDOW)[None, :]
            windows = interp[:, idx]
            kw = _apply_kernels(windows)
            M = jnp.abs(jnp.fft.fft(kw, axis=-1))
            Mmax = jnp.max(M, axis=-1, keepdims=True)
            thr = ALPHA * Mmax
            mask = jax.nn.sigmoid((M - thr) * TEMP)
            Mt = M * mask
            return soft_minimum(Mt, BETA * Mmax, TEMP)
        key = jax.random.key(seed)
        return {'signal': jax.random.normal(key, (B, L), dtype=jnp.float32)}
    _L0_tok_all = _L0_tok_setup()
    _L0_tok_in = {k: v for k, v in _L0_tok_all.items() if k in ()}
    del _L0_tok_all

    def _L0_attn_setup():
        import jax, jax.numpy as jnp
        import numpy as np
        DIM = 64
        HEADS = 4
        HEAD_DIM = DIM // HEADS
        SCALE = HEAD_DIM ** (-0.5)
        key = jax.random.key(seed)
        ks = jax.random.split(key, 9)
        B, N, C = (2, 1024, DIM)
        x = jax.random.normal(ks[0], (B, N, C), dtype=jnp.float32)
        lim = np.sqrt(6.0 / (C + C)).astype(np.float32)

        def w(k):
            return jax.random.uniform(k, (C, C), dtype=jnp.float32, minval=-lim, maxval=lim)
        return {'x': x, 'Wq': w(ks[1]), 'bq': jnp.zeros((C,), jnp.float32), 'Wk': w(ks[2]), 'bk': jnp.zeros((C,), jnp.float32), 'Wv': w(ks[3]), 'bv': jnp.zeros((C,), jnp.float32), 'Wo': w(ks[4]), 'bo': jnp.zeros((C,), jnp.float32)}
    _L0_attn_all = _L0_attn_setup()
    _L0_attn_in = {k: v for k, v in _L0_attn_all.items() if k in ('Wq', 'bq', 'Wk', 'bk', 'Wv', 'bv', 'Wo', 'bo')}
    del _L0_attn_all

    def _L0_ffn_setup():
        import math
        import jax, jax.numpy as jnp
        import numpy as np
        CAPACITY_FACTOR = 1.25
        TOP_K = 2
        LN_EPS = 1e-05

        def _layer_norm(x, gamma, beta):
            mu = jnp.mean(x, axis=-1, keepdims=True)
            var = jnp.var(x, axis=-1, keepdims=True)
            return (x - mu) * jax.lax.rsqrt(var + LN_EPS) * gamma + beta
        key = jax.random.key(seed)
        ks = jax.random.split(key, 4)
        B, S, D, F, E = (8, 1024, 64, 128, 8)
        x = jax.random.normal(ks[0], (B, S, D), dtype=jnp.float32)
        Wr = jax.random.normal(ks[1], (D, E), dtype=jnp.float32) / np.sqrt(D)
        br = jnp.zeros((E,), jnp.float32)
        W1 = jax.random.normal(ks[2], (E, D, F), dtype=jnp.float32) / np.sqrt(D)
        b1 = jnp.zeros((E, F), jnp.float32)
        W2 = jax.random.normal(ks[3], (E, F, D), dtype=jnp.float32) / np.sqrt(F)
        b2 = jnp.zeros((E, D), jnp.float32)
        gamma = jnp.ones((D,), jnp.float32)
        beta = jnp.zeros((D,), jnp.float32)
        return {'x': x, 'Wr': Wr, 'br': br, 'W1': W1, 'b1': b1, 'W2': W2, 'b2': b2, 'gamma': gamma, 'beta': beta}
    _L0_ffn_all = _L0_ffn_setup()
    _L0_ffn_in = {k: v for k, v in _L0_ffn_all.items() if k in ('Wr', 'br', 'W1', 'b1', 'W2', 'b2', 'gamma', 'beta')}
    del _L0_ffn_all

    def _L1_attn_setup():
        import jax, jax.numpy as jnp
        import numpy as np
        GAMMA = 0.96875
        ROPE_THETA = 10000.0

        def _rope(x):
            B, S, d = x.shape
            inv_freq = 1.0 / ROPE_THETA ** (jnp.arange(0, d, 2, dtype=jnp.float32) / d)
            angles = jnp.arange(S, dtype=jnp.float32)[:, None] * inv_freq[None, :]
            cos = jnp.cos(angles).astype(x.dtype)
            sin = jnp.sin(angles).astype(x.dtype)
            xs = x.reshape(B, S, d // 2, 2)
            x0, x1 = (xs[..., 0], xs[..., 1])
            out = jnp.stack([x0 * cos - x1 * sin, x1 * cos + x0 * sin], axis=-1)
            return out.reshape(B, S, d)

        def _decay_mask(S, dtype):
            n = jnp.arange(S)[:, None]
            m = jnp.arange(S)[None, :]
            diff = n - m
            D = jnp.exp(jnp.maximum(diff, 0).astype(jnp.float32) * np.log(GAMMA))
            return jnp.where(diff >= 0, D, 0.0).astype(dtype)
        key = jax.random.key(seed)
        k1, k2, k3, k4 = jax.random.split(key, 4)
        H = 64
        X = jax.random.normal(k1, (4, 2048, H), dtype=jnp.float32)
        W_Q = jax.random.normal(k2, (H, H), dtype=jnp.float32) / H
        W_K = jax.random.normal(k3, (H, H), dtype=jnp.float32) / H
        W_V = jax.random.normal(k4, (H, H), dtype=jnp.float32) / H
        return {'X': X, 'W_Q': W_Q, 'W_K': W_K, 'W_V': W_V}
    _L1_attn_all = _L1_attn_setup()
    _L1_attn_in = {k: v for k, v in _L1_attn_all.items() if k in ('W_Q', 'W_K', 'W_V')}
    del _L1_attn_all

    def _L1_ffn_setup():
        import jax, jax.numpy as jnp
        import numpy as np
        B, T, C = (64, 96, 64)
        NH, NKV = (4, 2)
        HD = C // NH
        NREP = NH // NKV
        NE, TOPK = (8, 2)
        HID = int(8 / 3 * C)
        EPS_RMS = 1e-06

        def _rope_tables(t_len):
            inv_freq = 1.0 / 10000.0 ** (np.arange(0, HD, 2, dtype=np.float32) / HD)
            t = np.arange(t_len, dtype=np.float32)
            freqs = np.outer(t, inv_freq)
            emb = np.concatenate([freqs, freqs], axis=-1)
            return (jnp.asarray(np.cos(emb)), jnp.asarray(np.sin(emb)))

        def _rotate_half(x):
            h = x.shape[-1] // 2
            return jnp.concatenate([-x[..., h:], x[..., :h]], axis=-1)

        def _rmsnorm(v, w):
            return v * jax.lax.rsqrt(jnp.mean(v * v, axis=-1, keepdims=True) + EPS_RMS) * w
        key = jax.random.key(seed)
        ks = jax.random.split(key, 10)
        s = lambda k, shape: jax.random.normal(k, shape, jnp.float32) * 0.02
        return {'x': jax.random.normal(ks[0], (B, T, C), jnp.float32), 'ln1_w': jnp.ones((C,), jnp.float32), 'ln2_w': jnp.ones((C,), jnp.float32), 'wq': s(ks[1], (NH * HD, C)), 'wk': s(ks[2], (NKV * HD, C)), 'wv': s(ks[3], (NKV * HD, C)), 'wo': s(ks[4], (C, C)), 'router_w': s(ks[5], (NE, C)), 'w1': s(ks[6], (NE, HID, C)), 'w2': s(ks[7], (NE, C, HID)), 'w3': s(ks[8], (NE, HID, C))}
    _L1_ffn_all = _L1_ffn_setup()
    _L1_ffn_in = {k: v for k, v in _L1_ffn_all.items() if k in ('ln1_w', 'ln2_w', 'wq', 'wk', 'wv', 'wo', 'router_w', 'w1', 'w2', 'w3')}
    del _L1_ffn_all

    def _L2_attn_setup():
        import jax, jax.numpy as jnp
        import numpy as np
        IN_CHANNELS = 64
        SCALE = IN_CHANNELS ** (-0.5)
        key = jax.random.key(seed)
        k_x, k_we, k_wo = jax.random.split(key, 3)
        B, M, C, H3, NH = (4, 3072, 64, 192, 3)
        x = jax.random.normal(k_x, (B, M, C), dtype=jnp.float32)
        W_embed = jax.random.normal(k_we, (NH, H3, C), dtype=jnp.float32) * 0.01
        b_embed = jnp.zeros((NH, H3), dtype=jnp.float32)
        W_out = jax.random.normal(k_wo, (C, H3), dtype=jnp.float32) * 0.01
        b_out = jnp.zeros((C,), dtype=jnp.float32)
        return {'x': x, 'W_embed': W_embed, 'b_embed': b_embed, 'W_out': W_out, 'b_out': b_out}
    _L2_attn_all = _L2_attn_setup()
    _L2_attn_in = {k: v for k, v in _L2_attn_all.items() if k in ('W_embed', 'b_embed', 'W_out', 'b_out')}
    del _L2_attn_all

    def _L2_ffn_setup():
        import jax, jax.numpy as jnp
        import numpy as np
        B, S, D = (8, 1024, 64)
        H = 4 * D
        CAPACITY = 0.5
        key = jax.random.key(seed)
        ks = jax.random.split(key, 6)
        x = jax.random.normal(ks[0], (B, S, D), dtype=jnp.float32)
        attention_mask = jnp.zeros((B, 1, 1, S), dtype=jnp.float32)
        wr = jax.random.normal(ks[1], (D, 1), dtype=jnp.float32) * 0.02
        br = jnp.zeros((1,), dtype=jnp.float32)
        w1 = jax.random.normal(ks[2], (D, H), dtype=jnp.float32) * 0.02
        b1 = jnp.zeros((H,), dtype=jnp.float32)
        w2 = jax.random.normal(ks[3], (H, D), dtype=jnp.float32) * 0.02
        b2 = jnp.zeros((D,), dtype=jnp.float32)
        return {'x': x, 'attention_mask': attention_mask, 'wr': wr, 'br': br, 'w1': w1, 'b1': b1, 'w2': w2, 'b2': b2}
    _L2_ffn_all = _L2_ffn_setup()
    _L2_ffn_in = {k: v for k, v in _L2_ffn_all.items() if k in ('attention_mask', 'wr', 'br', 'w1', 'b1', 'w2', 'b2')}
    del _L2_ffn_all

    def _L3_attn_setup():
        import jax, jax.numpy as jnp
        import numpy as np
        HEADS = 8
        DIM_HEAD = 64
        KNN = 32
        SCALE = DIM_HEAD ** (-0.5)

        def _knn_adjacency(x, k):
            B, N, _ = x.shape
            x2 = jnp.sum(x * x, axis=-1)
            d2 = x2[:, :, None] + x2[:, None, :] - 2.0 * jnp.einsum('bnc,bmc->bnm', x, x)
            big = jnp.finfo(d2.dtype).max
            d2 = d2 + big * jnp.eye(N, dtype=d2.dtype)
            _, idx = jax.lax.top_k(-d2, k)
            rows = jnp.arange(N)[:, None]

            def scatter_one(idx_b):
                return jnp.zeros((N, N), dtype=bool).at[rows, idx_b].set(True)
            return jax.vmap(scatter_one)(idx)
        key = jax.random.key(seed)
        k1, k2, k3 = jax.random.split(key, 3)
        B, N, C = (2, 512, 64)
        inner = HEADS * DIM_HEAD
        x = jax.random.normal(k1, (B, N, C), dtype=jnp.float32)
        Wqkv = jax.random.normal(k2, (C, 3 * inner), dtype=jnp.float32) * C ** (-0.5)
        Wout = jax.random.normal(k3, (inner, C), dtype=jnp.float32) * inner ** (-0.5)
        bout = jnp.zeros((C,), dtype=jnp.float32)
        return {'x': x, 'Wqkv': Wqkv, 'Wout': Wout, 'bout': bout}
    _L3_attn_all = _L3_attn_setup()
    _L3_attn_in = {k: v for k, v in _L3_attn_all.items() if k in ('Wqkv', 'Wout', 'bout')}
    del _L3_attn_all

    def _L3_ffn_setup():
        import math
        import jax, jax.numpy as jnp
        import numpy as np
        CAPACITY_FACTOR = 1.25
        key = jax.random.key(seed)
        ks = jax.random.split(key, 5)
        B, L, D, F, E = (8, 2048, 64, 256, 8)
        h = jax.random.normal(ks[0], (B, L, D), dtype=jnp.float32)
        gate_w = jax.random.normal(ks[1], (D, E), dtype=jnp.float32) * 0.02
        gate_b = jnp.zeros((E,), dtype=jnp.float32)
        w1 = jax.random.normal(ks[2], (E, D, F), dtype=jnp.float32) * (1.0 / math.sqrt(D))
        b1 = jnp.zeros((E, F), dtype=jnp.float32)
        w2 = jax.random.normal(ks[3], (E, F, D), dtype=jnp.float32) * (1.0 / math.sqrt(F))
        b2 = jnp.zeros((E, D), dtype=jnp.float32)
        return {'h': h, 'gate_w': gate_w, 'gate_b': gate_b, 'w1': w1, 'b1': b1, 'w2': w2, 'b2': b2}
    _L3_ffn_all = _L3_ffn_setup()
    _L3_ffn_in = {k: v for k, v in _L3_ffn_all.items() if k in ('gate_w', 'gate_b', 'w1', 'b1', 'w2', 'b2')}
    del _L3_ffn_all
    return {'x': x, 'L0_attn_Wq': _L0_attn_in['Wq'], 'L0_attn_bq': _L0_attn_in['bq'], 'L0_attn_Wk': _L0_attn_in['Wk'], 'L0_attn_bk': _L0_attn_in['bk'], 'L0_attn_Wv': _L0_attn_in['Wv'], 'L0_attn_bv': _L0_attn_in['bv'], 'L0_attn_Wo': _L0_attn_in['Wo'], 'L0_attn_bo': _L0_attn_in['bo'], 'L0_ffn_Wr': _L0_ffn_in['Wr'], 'L0_ffn_br': _L0_ffn_in['br'], 'L0_ffn_W1': _L0_ffn_in['W1'], 'L0_ffn_b1': _L0_ffn_in['b1'], 'L0_ffn_W2': _L0_ffn_in['W2'], 'L0_ffn_b2': _L0_ffn_in['b2'], 'L0_ffn_gamma': _L0_ffn_in['gamma'], 'L0_ffn_beta': _L0_ffn_in['beta'], 'L1_attn_W_Q': _L1_attn_in['W_Q'], 'L1_attn_W_K': _L1_attn_in['W_K'], 'L1_attn_W_V': _L1_attn_in['W_V'], 'L1_ffn_ln1_w': _L1_ffn_in['ln1_w'], 'L1_ffn_ln2_w': _L1_ffn_in['ln2_w'], 'L1_ffn_wq': _L1_ffn_in['wq'], 'L1_ffn_wk': _L1_ffn_in['wk'], 'L1_ffn_wv': _L1_ffn_in['wv'], 'L1_ffn_wo': _L1_ffn_in['wo'], 'L1_ffn_router_w': _L1_ffn_in['router_w'], 'L1_ffn_w1': _L1_ffn_in['w1'], 'L1_ffn_w2': _L1_ffn_in['w2'], 'L1_ffn_w3': _L1_ffn_in['w3'], 'L2_attn_W_embed': _L2_attn_in['W_embed'], 'L2_attn_b_embed': _L2_attn_in['b_embed'], 'L2_attn_W_out': _L2_attn_in['W_out'], 'L2_attn_b_out': _L2_attn_in['b_out'], 'L2_ffn_attention_mask': _L2_ffn_in['attention_mask'], 'L2_ffn_wr': _L2_ffn_in['wr'], 'L2_ffn_br': _L2_ffn_in['br'], 'L2_ffn_w1': _L2_ffn_in['w1'], 'L2_ffn_b1': _L2_ffn_in['b1'], 'L2_ffn_w2': _L2_ffn_in['w2'], 'L2_ffn_b2': _L2_ffn_in['b2'], 'L3_attn_Wqkv': _L3_attn_in['Wqkv'], 'L3_attn_Wout': _L3_attn_in['Wout'], 'L3_attn_bout': _L3_attn_in['bout'], 'L3_ffn_gate_w': _L3_ffn_in['gate_w'], 'L3_ffn_gate_b': _L3_ffn_in['gate_b'], 'L3_ffn_w1': _L3_ffn_in['w1'], 'L3_ffn_b1': _L3_ffn_in['b1'], 'L3_ffn_w2': _L3_ffn_in['w2'], 'L3_ffn_b2': _L3_ffn_in['b2']}

def reference(x, L0_attn_Wq, L0_attn_bq, L0_attn_Wk, L0_attn_bk, L0_attn_Wv, L0_attn_bv, L0_attn_Wo, L0_attn_bo, L0_ffn_Wr, L0_ffn_br, L0_ffn_W1, L0_ffn_b1, L0_ffn_W2, L0_ffn_b2, L0_ffn_gamma, L0_ffn_beta, L1_attn_W_Q, L1_attn_W_K, L1_attn_W_V, L1_ffn_ln1_w, L1_ffn_ln2_w, L1_ffn_wq, L1_ffn_wk, L1_ffn_wv, L1_ffn_wo, L1_ffn_router_w, L1_ffn_w1, L1_ffn_w2, L1_ffn_w3, L2_attn_W_embed, L2_attn_b_embed, L2_attn_W_out, L2_attn_b_out, L2_ffn_attention_mask, L2_ffn_wr, L2_ffn_br, L2_ffn_w1, L2_ffn_b1, L2_ffn_w2, L2_ffn_b2, L3_attn_Wqkv, L3_attn_Wout, L3_attn_bout, L3_ffn_gate_w, L3_ffn_gate_b, L3_ffn_w1, L3_ffn_b1, L3_ffn_w2, L3_ffn_b2):
    import jax
    import jax.numpy as jnp

    def _L0_tok_ref(signal):
        import jax, jax.numpy as jnp
        import numpy as np
        B, L = (64, 4096)
        INTERP_FACTOR = 0.25
        WINDOW, STEP = (64, 64)
        ALPHA, BETA, TEMP = (0.12, 0.9, 1.0)
        A = -0.75

        def _cubic_w(t):
            at = jnp.abs(t)
            w_near = ((A + 2.0) * at - (A + 3.0)) * at * at + 1.0
            w_far = ((A * at - 5.0 * A) * at + 8.0 * A) * at - 4.0 * A
            return jnp.where(at <= 1.0, w_near, jnp.where(at < 2.0, w_far, 0.0))

        def cubic_interpolate_1d(signal, interp_factor):
            b, n = signal.shape
            num_points = int((n - 1) / interp_factor) + 1
            x = jnp.linspace(0.0, 1.0, num_points) * (n - 1)
            i0 = jnp.floor(x).astype(jnp.int32)
            frac = x - i0.astype(x.dtype)
            offs = jnp.arange(-1, 3)
            idx = jnp.clip(i0[:, None] + offs[None, :], 0, n - 1)
            w = _cubic_w(frac[:, None] - offs[None, :].astype(x.dtype))
            taps = signal[:, idx]
            return jnp.einsum('bpk,pk->bp', taps, w)

        def _apply_kernels(x):
            poly = (x + 1.3) ** 2
            gauss = jnp.exp(-0.5 * ((x - 0.7) / 1.0) ** 2)
            return 0.5 * poly + 0.5 * gauss

        def soft_minimum(a, b, temperature):
            b = jnp.broadcast_to(b, a.shape)
            stacked = jnp.stack([-a * temperature, -b * temperature], axis=0)
            return -jax.nn.logsumexp(stacked, axis=0) / temperature

        def _forward(signal):
            interp = cubic_interpolate_1d(signal, INTERP_FACTOR)
            n = interp.shape[1]
            n_windows = (n - WINDOW) // STEP + 1
            starts = jnp.arange(n_windows) * STEP
            idx = starts[:, None] + jnp.arange(WINDOW)[None, :]
            windows = interp[:, idx]
            kw = _apply_kernels(windows)
            M = jnp.abs(jnp.fft.fft(kw, axis=-1))
            Mmax = jnp.max(M, axis=-1, keepdims=True)
            thr = ALPHA * Mmax
            mask = jax.nn.sigmoid((M - thr) * TEMP)
            Mt = M * mask
            return soft_minimum(Mt, BETA * Mmax, TEMP)
        return _forward(signal)

    def _L0_attn_ref(x, Wq, bq, Wk, bk, Wv, bv, Wo, bo):
        import jax, jax.numpy as jnp
        import numpy as np
        DIM = 64
        HEADS = 4
        HEAD_DIM = DIM // HEADS
        SCALE = HEAD_DIM ** (-0.5)
        B, N, C = x.shape
        x = jnp.clip(x, -10000.0, 10000.0)

        def heads(t):
            return t.reshape(B, N, HEADS, HEAD_DIM).transpose(0, 2, 1, 3)
        q = heads((x @ Wq.T + bq).astype(jnp.float32))
        k = heads((x @ Wk.T + bk).astype(jnp.float32))
        v = heads((x @ Wv.T + bv).astype(jnp.float32))
        attn = jnp.einsum('bhnd,bhmd->bhnm', q, k) * SCALE
        attn = jax.nn.softmax(attn, axis=-1)
        out = jnp.einsum('bhnm,bhmd->bhnd', attn, v)
        out = out.transpose(0, 2, 1, 3).reshape(B, N, C)
        out = out.astype(jnp.bfloat16).astype(jnp.float32)
        return out @ Wo.T + bo

    def _L0_ffn_ref(x, Wr, br, W1, b1, W2, b2, gamma, beta):
        import math
        import jax, jax.numpy as jnp
        import numpy as np
        CAPACITY_FACTOR = 1.25
        TOP_K = 2
        LN_EPS = 1e-05

        def _layer_norm(x, gamma, beta):
            mu = jnp.mean(x, axis=-1, keepdims=True)
            var = jnp.var(x, axis=-1, keepdims=True)
            return (x - mu) * jax.lax.rsqrt(var + LN_EPS) * gamma + beta
        B, S, D = x.shape
        E = Wr.shape[1]
        N = B * S
        K = TOP_K
        logits = jnp.mean(x, axis=1) @ Wr + br
        routing_weights = jax.nn.softmax(logits, axis=-1)
        capacity = float(math.ceil(N * CAPACITY_FACTOR / E))
        expected_loads = routing_weights.sum(axis=0) * (N / B)
        scale = jnp.where(expected_loads > capacity, capacity / expected_loads, 1.0)
        routing_weights = jax.nn.softmax(routing_weights * scale, axis=-1)
        rw_tok = jnp.broadcast_to(routing_weights[:, None, :], (B, S, E)).reshape(N, E)
        top_w, top_i = jax.lax.top_k(rw_tok, K)
        top_w = jax.nn.softmax(top_w, axis=-1)
        xf = x.reshape(N, D)
        h = jax.nn.gelu(jnp.einsum('nd,edf->enf', xf, W1) + b1[:, None, :], approximate=False)
        y = jnp.einsum('enf,efd->end', h, W2) + b2[:, None, :]
        w_dense = jnp.zeros((N, E), x.dtype).at[jnp.arange(N)[:, None], top_i].add(top_w)
        out = jnp.einsum('ne,end->nd', w_dense, y).reshape(B, S, D)
        out = _layer_norm(out + x, gamma, beta)
        return out

    def _L1_attn_ref(X, W_Q, W_K, W_V):
        import jax, jax.numpy as jnp
        import numpy as np
        GAMMA = 0.96875
        ROPE_THETA = 10000.0

        def _rope(x):
            B, S, d = x.shape
            inv_freq = 1.0 / ROPE_THETA ** (jnp.arange(0, d, 2, dtype=jnp.float32) / d)
            angles = jnp.arange(S, dtype=jnp.float32)[:, None] * inv_freq[None, :]
            cos = jnp.cos(angles).astype(x.dtype)
            sin = jnp.sin(angles).astype(x.dtype)
            xs = x.reshape(B, S, d // 2, 2)
            x0, x1 = (xs[..., 0], xs[..., 1])
            out = jnp.stack([x0 * cos - x1 * sin, x1 * cos + x0 * sin], axis=-1)
            return out.reshape(B, S, d)

        def _decay_mask(S, dtype):
            n = jnp.arange(S)[:, None]
            m = jnp.arange(S)[None, :]
            diff = n - m
            D = jnp.exp(jnp.maximum(diff, 0).astype(jnp.float32) * np.log(GAMMA))
            return jnp.where(diff >= 0, D, 0.0).astype(dtype)
        B, S, _ = X.shape
        D = _decay_mask(S, X.dtype)
        Q = _rope(X @ W_Q)
        K = _rope(X @ W_K)
        V = X @ W_V
        ret = jnp.einsum('bqd,bkd->bqk', Q, K) * D[None]
        return ret @ V

    def _L1_ffn_ref(x, ln1_w, ln2_w, wq, wk, wv, wo, router_w, w1, w2, w3):
        import jax, jax.numpy as jnp
        import numpy as np
        B, T, C = (64, 96, 64)
        NH, NKV = (4, 2)
        HD = C // NH
        NREP = NH // NKV
        NE, TOPK = (8, 2)
        HID = int(8 / 3 * C)
        EPS_RMS = 1e-06

        def _rope_tables(t_len):
            inv_freq = 1.0 / 10000.0 ** (np.arange(0, HD, 2, dtype=np.float32) / HD)
            t = np.arange(t_len, dtype=np.float32)
            freqs = np.outer(t, inv_freq)
            emb = np.concatenate([freqs, freqs], axis=-1)
            return (jnp.asarray(np.cos(emb)), jnp.asarray(np.sin(emb)))

        def _rotate_half(x):
            h = x.shape[-1] // 2
            return jnp.concatenate([-x[..., h:], x[..., :h]], axis=-1)

        def _rmsnorm(v, w):
            return v * jax.lax.rsqrt(jnp.mean(v * v, axis=-1, keepdims=True) + EPS_RMS) * w
        Bx, Tx, Cx = x.shape
        h = _rmsnorm(x, ln1_w)
        q = (h @ wq.T).reshape(Bx, Tx, NH, HD).transpose(0, 2, 1, 3)
        k = (h @ wk.T).reshape(Bx, Tx, NKV, HD).transpose(0, 2, 1, 3)
        v = (h @ wv.T).reshape(Bx, Tx, NKV, HD).transpose(0, 2, 1, 3)
        cos, sin = _rope_tables(Tx)
        cos, sin = (cos[None, None], sin[None, None])
        q = q * cos + _rotate_half(q) * sin
        k = k * cos + _rotate_half(k) * sin
        k = jnp.repeat(k, NREP, axis=1)
        v = jnp.repeat(v, NREP, axis=1)
        scores = jnp.einsum('bhtd,bhsd->bhts', q, k) / jnp.sqrt(jnp.float32(HD))
        causal = jnp.tril(jnp.ones((Tx, Tx), dtype=bool))
        scores = jnp.where(causal[None, None], scores, jnp.float32(-1e+30))
        att = jax.nn.softmax(scores, axis=-1)
        y = jnp.einsum('bhts,bhsd->bhtd', att, v).transpose(0, 2, 1, 3).reshape(Bx, Tx, Cx)
        x = x + y @ wo.T
        flat = _rmsnorm(x, ln2_w).reshape(-1, Cx)
        probs = jax.nn.softmax(flat @ router_w.T, axis=-1)
        tp, ti = jax.lax.top_k(probs, TOPK)
        tp = tp / (jnp.sum(tp, axis=-1, keepdims=True) + 1e-09)
        weights = jnp.sum(tp[..., None] * jax.nn.one_hot(ti, NE, dtype=flat.dtype), axis=1)
        out = jnp.zeros_like(flat)
        for e in range(NE):
            hh = jax.nn.silu(flat @ w1[e].T) * (flat @ w3[e].T)
            out = out + weights[:, e:e + 1] * (hh @ w2[e].T)
        return x + out.reshape(Bx, Tx, Cx)

    def _L2_attn_ref(x, W_embed, b_embed, W_out, b_out):
        import jax, jax.numpy as jnp
        import numpy as np
        IN_CHANNELS = 64
        SCALE = IN_CHANNELS ** (-0.5)

        def head(W, b):
            e = jnp.einsum('bmc,hc->bmh', x, W) + b
            q, k, v = jnp.split(e, 3, axis=1)
            attn = jax.nn.softmax(jnp.einsum('bmd,bnd->bmn', q, k) * SCALE, axis=-1)
            return jnp.einsum('bmn,bnd->bmd', attn, v)
        outs = jax.vmap(head)(W_embed, b_embed)
        qkv = jnp.concatenate([outs[i] for i in range(outs.shape[0])], axis=1)
        out = jnp.einsum('bmd,cd->bmc', qkv, W_out) + b_out
        return out + x

    def _L2_ffn_ref(x, attention_mask, wr, br, w1, b1, w2, b2):
        import jax, jax.numpy as jnp
        import numpy as np
        B, S, D = (8, 1024, 64)
        H = 4 * D
        CAPACITY = 0.5
        b, s, d = x.shape
        weights = (jnp.einsum('bsd,do->bso', x, wr) + br)[..., 0]
        k = max(1, int(CAPACITY * s))
        kk = k - 1 if k > 1 else 1
        _, idx = jax.lax.top_k(weights, k)
        sel_idx = idx[:, :kk]
        sel = jnp.take_along_axis(x, sel_idx[:, :, None], axis=1)
        h = jax.nn.gelu(jnp.einsum('bkd,dh->bkh', sel, w1) + b1)
        y = jnp.einsum('bkh,hd->bkd', h, w2) + b2
        w_sel = jnp.take_along_axis(weights, sel_idx, axis=1)
        y = y * w_sel[..., None]
        batch_idx = jnp.arange(b)[:, None]
        processed = jnp.zeros_like(x).at[batch_idx, sel_idx].set(y)
        return processed + x

    def _L3_attn_ref(x, Wqkv, Wout, bout):
        import jax, jax.numpy as jnp
        import numpy as np
        HEADS = 8
        DIM_HEAD = 64
        KNN = 32
        SCALE = DIM_HEAD ** (-0.5)

        def _knn_adjacency(x, k):
            B, N, _ = x.shape
            x2 = jnp.sum(x * x, axis=-1)
            d2 = x2[:, :, None] + x2[:, None, :] - 2.0 * jnp.einsum('bnc,bmc->bnm', x, x)
            big = jnp.finfo(d2.dtype).max
            d2 = d2 + big * jnp.eye(N, dtype=d2.dtype)
            _, idx = jax.lax.top_k(-d2, k)
            rows = jnp.arange(N)[:, None]

            def scatter_one(idx_b):
                return jnp.zeros((N, N), dtype=bool).at[rows, idx_b].set(True)
            return jax.vmap(scatter_one)(idx)
        B, N, C = x.shape
        adj = _knn_adjacency(x, KNN)
        qkv = x @ Wqkv
        q, k, v = jnp.split(qkv, 3, axis=-1)
        split_heads = lambda t: t.reshape(B, N, HEADS, DIM_HEAD).transpose(0, 2, 1, 3)
        q, k, v = (split_heads(q), split_heads(k), split_heads(v))
        dots = jnp.einsum('bhnd,bhmd->bhnm', q, k) * SCALE
        dots = jnp.where(adj[:, None, :, :], dots, -jnp.inf)
        attn = jax.nn.softmax(dots, axis=-1)
        out = jnp.einsum('bhnm,bhmd->bhnd', attn, v)
        out = out.transpose(0, 2, 1, 3).reshape(B, N, HEADS * DIM_HEAD)
        return out @ Wout + bout

    def _L3_ffn_ref(h, gate_w, gate_b, w1, b1, w2, b2):
        import math
        import jax, jax.numpy as jnp
        import numpy as np
        CAPACITY_FACTOR = 1.25
        B, L, D = h.shape
        E = gate_w.shape[1]
        T = B * L
        C = max(1, math.ceil(CAPACITY_FACTOR * T / E))
        x = h.reshape(T, D)
        logits = x @ gate_w + gate_b
        probs = jax.nn.softmax(logits, axis=-1)
        idx = jnp.argmax(probs, axis=-1)
        prb = jnp.take_along_axis(probs, idx[:, None], axis=1)[:, 0]
        one_hot = jax.nn.one_hot(idx, E, dtype=jnp.float32)
        pos = (jnp.cumsum(one_hot, axis=0) * one_hot).sum(-1).astype(jnp.int32) - 1
        kept = pos < C
        pos_safe = jnp.where(kept, pos, C)
        buf = jnp.zeros((E, C, D), dtype=h.dtype).at[idx, pos_safe].set(x, mode='drop')
        hmid = jax.nn.relu(jnp.einsum('ecd,edf->ecf', buf, w1) + b1[:, None, :])
        ybuf = jnp.einsum('ecf,efd->ecd', hmid, w2) + b2[:, None, :]
        pos_g = jnp.minimum(pos, C - 1)
        y_tok = ybuf[idx, pos_g] * (prb * kept)[:, None]
        y = y_tok.reshape(B, L, D)
        y = jnp.nan_to_num(y, nan=0.0, posinf=10000.0, neginf=-10000.0)
        return y
    h = _L0_tok_ref(x)
    h = h + _L0_attn_ref(_layernorm(h, axis=-1), L0_attn_Wq, L0_attn_bq, L0_attn_Wk, L0_attn_bk, L0_attn_Wv, L0_attn_bv, L0_attn_Wo, L0_attn_bo)
    h = h + _L0_ffn_ref(_layernorm(h, axis=-1), L0_ffn_Wr, L0_ffn_br, L0_ffn_W1, L0_ffn_b1, L0_ffn_W2, L0_ffn_b2, L0_ffn_gamma, L0_ffn_beta)
    h = h + _L1_attn_ref(_layernorm(h, axis=-1), L1_attn_W_Q, L1_attn_W_K, L1_attn_W_V)
    h = h + _L1_ffn_ref(_layernorm(h, axis=-1), L1_ffn_ln1_w, L1_ffn_ln2_w, L1_ffn_wq, L1_ffn_wk, L1_ffn_wv, L1_ffn_wo, L1_ffn_router_w, L1_ffn_w1, L1_ffn_w2, L1_ffn_w3)
    h = h + _L2_attn_ref(_layernorm(h, axis=-1), L2_attn_W_embed, L2_attn_b_embed, L2_attn_W_out, L2_attn_b_out)
    h = h + _L2_ffn_ref(_layernorm(h, axis=-1), L2_ffn_attention_mask, L2_ffn_wr, L2_ffn_br, L2_ffn_w1, L2_ffn_b1, L2_ffn_w2, L2_ffn_b2)
    h = h + _L3_attn_ref(_layernorm(h, axis=-1), L3_attn_Wqkv, L3_attn_Wout, L3_attn_bout)
    h = h + _L3_ffn_ref(_layernorm(h, axis=-1), L3_ffn_gate_w, L3_ffn_gate_b, L3_ffn_w1, L3_ffn_b1, L3_ffn_w2, L3_ffn_b2)
    return h

_drawn_inputs = setup_inputs


def setup_inputs(seed=0):
    import zlib

    import numpy as np

    out = dict(_drawn_inputs(seed))
    spreads = {'L0_attn_bq': (0.0, 0.8),
     'L0_attn_bk': (0.0, 0.8),
     'L0_attn_bv': (0.0, 0.8),
     'L0_attn_bo': (0.0, 0.8),
     'L0_ffn_br': (0.0, 0.364),
     'L0_ffn_b1': (0.0, 0.8),
     'L0_ffn_b2': (0.0, 0.8),
     'L0_ffn_gamma': (1.0, 0.6),
     'L0_ffn_beta': (0.0, 0.8),
     'L1_ffn_ln1_w': (1.0, 0.6),
     'L1_ffn_ln2_w': (1.0, 0.6),
     'L2_attn_b_embed': (0.0, 0.8),
     'L2_attn_b_out': (0.0, 0.8),
     'L2_ffn_b1': (0.0, 0.8),
     'L2_ffn_b2': (0.0, 0.8),
     'L3_attn_bout': (0.0, 0.8),
     'L3_ffn_gate_b': (0.0, 0.8),
     'L3_ffn_b1': (0.0, 0.8),
     'L3_ffn_b2': (0.0, 0.8)}
    factors = {'L0_attn_Wq': 8.0,
     'L0_attn_Wk': 8.0,
     'L1_attn_W_Q': 5.592,
     'L1_attn_W_K': 3.769,
     'L1_attn_W_V': 5.486,
     'L1_ffn_wq': 8.0,
     'L1_ffn_wk': 8.0,
     'L1_ffn_wv': 8.0,
     'L1_ffn_wo': 8.0,
     'L1_ffn_router_w': 8.0,
     'L1_ffn_w1': 8.0,
     'L1_ffn_w2': 8.0,
     'L1_ffn_w3': 8.0,
     'L2_attn_W_embed': 8.0,
     'L2_attn_W_out': 8.0,
     'L2_ffn_wr': 8.0,
     'L2_ffn_w1': 8.0,
     'L2_ffn_w2': 8.0,
     'L3_ffn_gate_w': 8.0,
     'L3_ffn_w1': 8.0,
     'L3_ffn_w2': 8.0}
    for name, (base, spread) in spreads.items():
        noise = np.random.default_rng([zlib.crc32(name.encode()), seed]).standard_normal(out[name].shape)
        drawn = base * np.exp(spread * noise) if base else spread * noise
        out[name] = jnp.asarray(drawn.astype(out[name].dtype))
    for name, factor in factors.items():
        out[name] = (out[name] * factor).astype(out[name].dtype)
    return out
```

```python
import math
from contextlib import ExitStack

import numpy as np
import concourse.bass as bass
from concourse import mybir

F32 = mybir.dt.float32
BF16 = mybir.dt.bfloat16
ALU = mybir.AluOpType
ACT = mybir.ActivationFunctionType
AX = mybir.AxisListType

BATCH, SAMPLES = 64, 4000
C = 64
POINTS = 4 * (SAMPLES - 1) + 1
T = (POINTS - 64) // 64 + 1
PT = 125
OFF = T - PT
ROWS = (OFF, PT)
PAIRS = BATCH // 2
EXPERTS = 8
NEG = -1.0e30
PHASES = 11
TRANSPOSED = ("L0_attn_Wq", "L0_attn_Wk", "L0_attn_Wv", "L0_attn_Wo", "L1_ffn_wq", "L1_ffn_wk", "L1_ffn_wv",
              "L1_ffn_wo", "L1_ffn_router_w", "L2_attn_W_out")

PER = {
    "att0.const_loaded": 9,
    "att0.exp_ready": 8,
    "att0.loaded": 2,
    "att0.max_ready": 8,
    "att0.norm_centered": 2,
    "att0.norm_powered": 2,
    "att0.norm_squared": 2,
    "att0.norm_variance": 2,
    "att0.s_done": 8,
    "att0.st_done": 8,
    "att0.stored": 3,
    "att0.vec": 8,
    "att1.const_loaded": 16,
    "att1.exp_ready": 8,
    "att1.loaded": 2,
    "att1.masked": 8,
    "att1.max_ready": 8,
    "att1.norm_centered": 3,
    "att1.norm_powered": 3,
    "att1.norm_squared": 3,
    "att1.norm_variance": 3,
    "att1.r_done": 4,
    "att1.s_done": 8,
    "att1.st_done": 8,
    "att1.stored": 5,
    "att1.vec": 31,
    "att1.xT_done": 2,
    "att1.xT_ready": 2,
    "att2.const_loaded": 5,
    "att2.exp_ready": 6,
    "att2.loaded": 3,
    "att2.max_ready": 3,
    "att2.oT_ready": 3,
    "att2.o_done": 3,
    "att2.pt_done": 3,
    "att2.pt_ready": 3,
    "att2.qk_done": 3,
    "att2.qk_ready": 3,
    "att2.s_done": 3,
    "att2.stored": 3,
    "att2.v_done": 3,
    "att2.v_ready": 3,
    "att2.vec": 10,
    "att2.y_done": 3,
    "att3.const_loaded": 5,
    "att3.d_done": 2,
    "att3.exp_ready": 32,
    "att3.loaded": 2,
    "att3.max_ready": 16,
    "att3.oT_done": 4,
    "att3.oT_ready": 4,
    "att3.o_done": 2,
    "att3.o_ready": 2,
    "att3.pt_done": 16,
    "att3.pt_ready": 16,
    "att3.qk_done": 8,
    "att3.qk_ready": 8,
    "att3.s_done": 16,
    "att3.sq_ready": 2,
    "att3.stored": 2,
    "att3.v_done": 4,
    "att3.v_ready": 4,
    "att3.vec": 51,
    "ffn0.const_loaded": 7,
    "ffn0.hid_done": 8,
    "ffn0.hid_ready": 8,
    "ffn0.loaded": 3,
    "ffn0.norm_centered": 2,
    "ffn0.norm_powered": 2,
    "ffn0.norm_squared": 2,
    "ffn0.norm_variance": 2,
    "ffn0.stored": 2,
    "ffn0.vec": 14,
    "ffn0.y_done": 4,
    "ffn0.y_used": 4,
    "mod2.const_loaded": 8,
    "mod2.hid_done": 2,
    "mod2.hid_ready": 2,
    "mod2.loaded": 2,
    "mod2.stored": 2,
    "mod2.vec": 20,
    "moe1.const_loaded": 3,
    "moe1.gate_done": 16,
    "moe1.hid_ready": 16,
    "moe1.loaded": 4,
    "moe1.silu_ready": 16,
    "moe1.stored": 2,
    "moe1.vec": 4,
    "moe1.y_done": 4,
    "moe1.y_used": 4,
    "ret1.const_loaded": 8,
    "ret1.loaded": 2,
    "ret1.p_ready": 2,
    "ret1.qk_ready": 2,
    "ret1.r_done": 4,
    "ret1.s_done": 2,
    "ret1.stored": 2,
    "ret1.vec": 5,
    "route.const_loaded": 4,
    "route.expd": 3,
    "route.shifted": 3,
    "route.vec": 20,
    "sw3.const_loaded": 9,
    "sw3.hid_done": 16,
    "sw3.hid_ready": 16,
    "sw3.loaded": 2,
    "sw3.stored": 2,
    "sw3.vec": 25,
    "sw3.y_done": 4,
    "sw3.y_used": 4,
    "tok.act": 3,
    "tok.const_loaded": 2,
    "tok.loaded": 2,
    "tok.stored": 2,
    "tok.vec": 7,
}
MISCOUNTED = {}


class Event:

    def __init__(self, nc, stage, name, unit=1):
        self.key = f"{stage}.{name}"
        self.sem = nc.alloc_semaphore(name=f"{stage}_{name}")
        self.unit = unit
        self.per = PER.get(self.key, 1)
        self.fired = 0

    def one(self):
        self.fired += 1
        return self.sem, self.unit

    def after(self, i, k=None):
        k = self.per - 1 if k is None else k
        return self.sem, (i * self.per + k + 2) * self.unit

    def before(self, i):
        return self.sem, (i * self.per + 1) * self.unit

    def latest(self, i):
        return self.after(i, (self.fired - 1) % self.per)


class Stage:

    def __init__(self, nc, name):
        self.nc, self.name, self.events, self.ctx = nc, name, {}, ExitStack()
        self.gates = {}

    def __enter__(self):
        self.ctx.__enter__()
        return self

    def __exit__(self, *e):
        if e[0] is None:
            self.ctx.__exit__(None, None, None)
        for s in self.events.values():
            if s.fired != s.per and not (s.fired and s.fired % s.per == 0 and s.loops == s.fired // s.per):
                MISCOUNTED[s.key] = s.fired // s.loops
        sems = [s.sem for s in self.events.values()] + list(self.gates.values())
        self.nc.clear_and_free_semaphores(sems)
        self.nc.all_engine_barrier()

    def event(self, name, dma=False, bodies=1):
        s = self.events[name] = Event(self.nc, self.name, name, 16 if dma else 1)
        s.loops = bodies
        return s

    def sb(self, name, shape, dt=F32):
        return self.ctx.enter_context(self.nc.sbuf_tensor(f"{self.name}_{name}", shape, dt))

    def held(self, engine):
        gate = self.gates.get(engine.engine)
        if gate is None:
            gate = self.gates[engine.engine] = self.nc.alloc_semaphore(
                name=f"{self.name}_held_{len(self.gates)}")
        engine.sem_inc(gate, 1)

    def psum(self, name, shape, dt=F32):
        return self.ctx.enter_context(self.nc.psum_tensor(f"{self.name}_{name}", shape, dt))

    def block(self):
        for s in self.events.values():
            self.nc.sync.sem_inc(s.sem, s.unit)
        self.nc.all_engine_barrier()
        return self.nc.Block()


def bc(ap, n):
    return bass.AP(ap.tensor, ap.offset, [list(x) for x in ap.ap] + [[0, n]])


def bcm(ap, at, n):
    a = [list(x) for x in ap.ap]
    return bass.AP(ap.tensor, ap.offset, a[:at] + [[0, n]] + a[at:])


def load_pair(sp, tile, dram, i, width=C):
    src = dram[bass.ds(i * 2, 2)]
    return [sp.dma_start(tile[:, t, :, :], bass.AP(src.tensor, src.offset + t * OFF * width,
                                                   [[width, PT], [T * width, 2], [1, width]]))
            for t in range(2)]


def store_pair(sp, dram, tile, i, width=C):
    dst = dram[bass.ds(i * 2, 2)]
    return [sp.dma_start(bass.AP(dst.tensor, dst.offset + t * OFF * width,
                                 [[width, ROWS[t]], [T * width, 2], [1, width]]), tile[0:ROWS[t], t, :, :])
            for t in range(2)]


class Norm:

    def __init__(self, st, rows, groups):
        self.rows, self.g = rows, groups
        self.sum = st.sb("norm_sum", [rows, groups])
        self.xc = st.sb("norm_centered", [rows, groups, C])
        self.sq = st.sb("norm_squares", [rows, groups, C])
        self.var = st.sb("norm_var", [rows, groups])
        self.rstd = st.sb("norm_rstd", [rows, groups])
        self.expo = st.sb("norm_exponent", [rows, groups])
        self.centered = st.event("norm_centered")
        self.squared = st.event("norm_squared")
        self.variance = st.event("norm_variance")
        self.powered = st.event("norm_powered")

    def center(self, v, i, x, chain):
        v.reduce_sum(self.sum[:, :], x, AX.X).then_inc(*chain.one())
        v.wait_ge(*chain.latest(i))
        v.tensor_scalar(self.sum[:, :], self.sum[:, :], -1.0 / C, None, ALU.mult).then_inc(*chain.one())
        v.wait_ge(*chain.latest(i))
        v.tensor_tensor(self.xc[:, :, :], x, bc(self.sum[:, :], C), ALU.add).then_inc(*self.centered.one())

    def scale(self, v, i, k, x, out, eps, chain):
        v.wait_ge(*self.squared.after(i, k))
        v.reduce_sum(self.var[:, :], self.sq[:, :, :], AX.X).then_inc(*chain.one())
        v.wait_ge(*chain.latest(i))
        v.tensor_scalar(self.var[:, :], self.var[:, :], 1.0 / C, eps, ALU.mult, ALU.add).then_inc(
            *self.variance.one())
        v.wait_ge(*self.powered.after(i, k))
        return v.tensor_tensor(out, x, bc(self.rstd[:, :], C), ALU.mult)

    def square(self, a, i, k, x):
        a.wait_ge(*self.centered.after(i, k))
        a.activation(self.sq[:, :, :], x, ACT.Square).then_inc(*self.squared.one())

    def power(self, p, i, k):
        p.wait_ge(*self.variance.after(i, k))
        p.tensor_tensor(self.rstd[:, :], self.var[:, :], self.expo[:, :], ALU.pow).then_inc(*self.powered.one())


def g4(ap):
    return ap.rearrange("p t b c -> p (t b) c")


def stage_tokenizer(nc, A, h):
    WG = 8
    GROUPS = T // WG
    TAPS = 20
    NF = 33
    SPAN = 16 * (WG - 1) + TAPS
    r5 = math.sqrt(0.5)
    with Stage(nc, "tok") as st:
        xs = st.sb("samples", [BATCH, SPAN])
        wt = st.sb("taps", [TAPS, WG, 64])
        ident = st.sb("ident", [128, 128])
        dft = st.sb("dft", [64, 2 * NF])
        sT = st.sb("samplesT", [TAPS, WG, BATCH])
        poly = st.sb("poly", [64, WG * BATCH])
        gauss = st.sb("gauss", [64, WG * BATCH])
        kw = st.sb("kernelled", [64, WG * BATCH])
        sq = st.sb("squares", [128, 4, 2 * NF])
        m2 = st.sb("power", [128, 4, NF])
        mag = st.sb("magnitude", [128, 4, NF])
        half = st.sb("half", [128, 4, NF])
        top = st.sb("top", [128, 4])
        thr = st.sb("thr", [128, 2, 4])
        d = st.sb("d", [128, 4, NF])
        e = st.sb("e", [128, 4, NF])
        mt = st.sb("mt", [128, 4, NF])
        df = st.sb("df", [128, 4, NF])
        lg = st.sb("lg", [128, 4, NF])
        out = st.sb("out", [128, 4, C])
        bias = st.sb("bias", [128, 4])
        pT = st.psum("pT", [TAPS, WG, BATCH])
        pI = st.psum("pI", [64, WG * BATCH])
        pM = st.psum("pM", [128, 4, 128])

        const_loaded = st.event("const_loaded", dma=True)
        loaded = st.event("loaded", dma=True, bodies=2)
        memset_done = st.event("memset_done")
        transposed = st.event("transposed", bodies=2)
        samples_ready = st.event("samples_ready", bodies=2)
        interpolated = st.event("interpolated", bodies=2)
        kernels_done = st.event("kernels_done", bodies=2)
        act = st.event("act", bodies=2)
        windows_ready = st.event("windows_ready", bodies=2)
        spectrum = st.event("spectrum", bodies=2)
        vec = st.event("vec", bodies=2)
        squares_ready = st.event("squares_ready", bodies=2)
        power_ready = st.event("power_ready", bodies=2)
        magnitude_ready = st.event("magnitude_ready", bodies=2)
        excess_ready = st.event("excess_ready", bodies=2)
        excess_exp = st.event("excess_exp", bodies=2)
        gap_ready = st.event("gap_ready", bodies=2)
        gap_log = st.event("gap_log", bodies=2)
        out_ready = st.event("out_ready", bodies=2)
        stored = st.event("stored", dma=True, bodies=2)

        with st.block() as block:
            @block.sync
            def _(sp):
                sp.dma_start(ident[:, :], A["const_ident"][:, :]).then_inc(*const_loaded.one())
                sp.dma_start(dft[:, :], A["const_dft"][:, :]).then_inc(*const_loaded.one())

                def body(i, nw):
                    span = 16 * (nw - 1) + TAPS
                    sp.wait_ge(*transposed.before(i))
                    sp.dma_start(xs[:, 0:span], A["x_edge"][:, bass.ds(i * (16 * WG), span)]).then_inc(
                        *loaded.one())
                    sp.wait_ge(*interpolated.before(i))
                    sp.dma_start(wt[:, 0:nw, :], A["const_taps"][bass.ds(i * WG, nw)].rearrange(
                        "w k f -> k w f")).then_inc(*loaded.one())
                    sp.wait_ge(*out_ready.after(i))
                    q, r = max(1, nw // 2), min(nw, 2)
                    for w2 in range(2):
                        if w2 < r:
                            dst = h[:, bass.ds(i * WG + w2, 1), :]
                            dst = bass.AP(dst.tensor, dst.offset, [[T * C, 64], [2 * C, q], [1, C]])
                            sp.dma_start(dst, out[w2 * 64:w2 * 64 + 64, 0:q, :]).then_inc(*stored.one())
                with sp.Fori(0, GROUPS) as i:
                    body(i, WG)
                body(GROUPS, T - GROUPS * WG)
                stored.fired += 1
                sp.wait_ge(stored.sem, (2 * GROUPS + 2) * 16)

            @block.tensor
            def _(pe):
                pe.wait_ge(*const_loaded.after(0))

                def body(i, nw):
                    pe.wait_ge(*loaded.after(i))
                    pe.wait_ge(*samples_ready.before(i))
                    st.held(pe)
                    for w in range(nw):
                        ins = pe.transpose(pT[:, w, :], xs[:, 16 * w:16 * w + TAPS], ident[0:64, 0:64])
                    ins.then_inc(*transposed.one())
                    pe.wait_ge(*samples_ready.after(i))
                    pe.wait_ge(*kernels_done.before(i))
                    st.held(pe)
                    for w in range(nw):
                        ins = pe.matmul(pI[:, w * 64:w * 64 + 64], wt[:, w, :], sT[:, w, :], start=True,
                                        stop=True)
                    ins.then_inc(*interpolated.one())
                    pe.wait_ge(*windows_ready.after(i))
                    pe.wait_ge(*squares_ready.before(i))
                    rows = min(128, 64 * nw)
                    for q in range(64 * nw // rows):
                        ins = pe.matmul(pM[0:rows, q, 0:2 * NF], kw[:, q * rows:q * rows + rows], dft[:, :],
                                        start=True, stop=True)
                    ins.then_inc(*spectrum.one())
                with pe.Fori(0, GROUPS) as i:
                    body(i, WG)
                body(GROUPS, T - GROUPS * WG)

            @block.scalar
            def _(a):
                a.wait_ge(*memset_done.after(0))

                def body(i, nw):
                    n, rows = 64 * nw, min(128, 64 * nw)
                    Q = n // rows
                    a.wait_ge(*interpolated.after(i))
                    a.wait_ge(*windows_ready.before(i))
                    a.activation(poly[:, 0:n], pI[:, 0:n], ACT.Square, bias=bias[0:64, 0:1], scale=r5)
                    a.activation(gauss[:, 0:n], pI[:, 0:n], ACT.Square, bias=bias[0:64, 1:2]).then_inc(
                        *act.one())
                    a.wait_ge(*act.latest(i))
                    a.activation(gauss[:, 0:n], gauss[:, 0:n], ACT.Exp, bias=bias[0:64, 2:3],
                                 scale=-0.5).then_inc(*kernels_done.one())
                    a.wait_ge(*spectrum.after(i))
                    a.activation(sq[0:rows, 0:Q, :], pM[0:rows, 0:Q, 0:2 * NF], ACT.Square).then_inc(
                        *squares_ready.one())
                    a.wait_ge(*excess_ready.after(i))
                    a.activation(e[0:rows, 0:Q, :], d[0:rows, 0:Q, :], ACT.Exp, scale=-1.0).then_inc(
                        *excess_exp.one())
                    a.wait_ge(*gap_ready.after(i))
                    a.activation(lg[0:rows, 0:Q, :], df[0:rows, 0:Q, :], ACT.Abs).then_inc(*act.one())
                    a.wait_ge(*act.latest(i))
                    a.activation(lg[0:rows, 0:Q, :], lg[0:rows, 0:Q, :], ACT.Exp, scale=-1.0).then_inc(
                        *act.one())
                    a.wait_ge(*act.latest(i))
                    a.activation(lg[0:rows, 0:Q, :], lg[0:rows, 0:Q, :], ACT.Ln,
                                 bias=bias[0:rows, 3:4]).then_inc(*gap_log.one())
                with a.Fori(0, GROUPS) as i:
                    body(i, WG)
                body(GROUPS, T - GROUPS * WG)

            @block.gpsimd
            def _(p):
                p.memset(half[:, :, :], 0.5)
                p.memset(bias[:, 0:1], 1.3 * r5)
                p.memset(bias[:, 1:2], -0.7)
                p.memset(bias[:, 2:3], math.log(0.5))
                p.memset(bias[:, 3:4], 1.0).then_inc(*memset_done.one())
                p.wait_ge(*memset_done.after(0))

                def body(i, nw):
                    n, rows = 64 * nw, min(128, 64 * nw)
                    Q = n // rows
                    p.wait_ge(*power_ready.after(i))
                    p.tensor_tensor(mag[0:rows, 0:Q, :], m2[0:rows, 0:Q, :], half[0:rows, 0:Q, :],
                                    ALU.pow).then_inc(*magnitude_ready.one())
                with p.Fori(0, GROUPS) as i:
                    body(i, WG)
                body(GROUPS, T - GROUPS * WG)

            @block.vector
            def _(v):
                def body(i, nw):
                    n, rows = 64 * nw, min(128, 64 * nw)
                    Q = n // rows
                    R = slice(0, rows)
                    v.wait_ge(*transposed.after(i))
                    v.tensor_copy(sT[:, 0:nw, :], pT[:, 0:nw, :]).then_inc(*samples_ready.one())
                    v.wait_ge(*kernels_done.after(i))
                    v.tensor_tensor(kw[:, 0:n], poly[:, 0:n], gauss[:, 0:n], ALU.add).then_inc(
                        *windows_ready.one())
                    v.wait_ge(*squares_ready.after(i))
                    v.tensor_tensor(m2[R, 0:Q, :], sq[R, 0:Q, 0:NF], sq[R, 0:Q, NF:2 * NF], ALU.add).then_inc(
                        *power_ready.one())
                    v.wait_ge(*magnitude_ready.after(i))
                    v.reduce_max(top[R, 0:Q], mag[R, 0:Q, :], AX.X).then_inc(*vec.one())
                    v.wait_ge(*vec.latest(i))
                    v.tensor_scalar(thr[R, 0, 0:Q], top[R, 0:Q], 0.12, None, ALU.mult)
                    v.tensor_scalar(thr[R, 1, 0:Q], top[R, 0:Q], 0.9, None, ALU.mult).then_inc(*vec.one())
                    v.wait_ge(*vec.latest(i))
                    v.tensor_tensor(d[R, 0:Q, :], mag[R, 0:Q, :], bc(thr[R, 0, 0:Q], NF),
                                    ALU.subtract).then_inc(*excess_ready.one())
                    v.wait_ge(*excess_exp.after(i))
                    v.tensor_scalar(e[R, 0:Q, :], e[R, 0:Q, :], 1.0, None, ALU.add).then_inc(*vec.one())
                    v.wait_ge(*vec.latest(i))
                    v.reciprocal(e[R, 0:Q, :], e[R, 0:Q, :]).then_inc(*vec.one())
                    v.wait_ge(*vec.latest(i))
                    v.tensor_tensor(mt[R, 0:Q, :], mag[R, 0:Q, :], e[R, 0:Q, :], ALU.mult).then_inc(*vec.one())
                    v.wait_ge(*vec.latest(i))
                    v.tensor_tensor(df[R, 0:Q, :], mt[R, 0:Q, :], bc(thr[R, 1, 0:Q], NF),
                                    ALU.subtract).then_inc(*gap_ready.one())
                    v.tensor_tensor(mt[R, 0:Q, :], mt[R, 0:Q, :], bc(thr[R, 1, 0:Q], NF), ALU.min).then_inc(
                        *vec.one())
                    v.wait_ge(*vec.latest(i))
                    v.wait_ge(*gap_log.after(i))
                    v.wait_ge(stored.sem, i * 32 + 16)
                    v.tensor_tensor(out[R, 0:Q, 0:NF], mt[R, 0:Q, :], lg[R, 0:Q, :], ALU.subtract).then_inc(
                        *vec.one())
                    v.wait_ge(*vec.latest(i))
                    lo = out[R, 0:Q, 0:NF]
                    mirror = bass.AP(lo.tensor, lo.offset + NF - 2, [list(lo.ap[0]), list(lo.ap[1]), [-1, NF - 2]])
                    v.tensor_copy(out[R, 0:Q, NF:C], mirror).then_inc(*out_ready.one())
                with v.Fori(0, GROUPS) as i:
                    body(i, WG)
                body(GROUPS, T - GROUPS * WG)


def stage_attention0(nc, A, h, mean_dram):
    H, D = 4, 16
    with Stage(nc, "att0") as st:
        ident = st.sb("ident", [128, 128])
        wq = st.sb("wq", [C + 1, H, 32])
        wk = st.sb("wk", [C + 1, H, 32])
        wv = st.sb("wv", [C + 1, H, D + 1])
        wo = st.sb("wo", [C + 1, C])
        ones = st.sb("ones", [128, 1])
        X = st.sb("X", [PT, 2, 2, C])
        xn = st.sb("xn", [PT, 2, 2, C])
        xT = st.sb("xT", [C + 1, 2, T])
        qT = st.sb("qT", [128, 2, T])
        kT = st.sb("kT", [128, 2, T])
        qmT = st.sb("qmT", [128, 2, T])
        V = st.sb("V", [PT, 2, 2, H, D + 1])
        M = st.sb("M", [PT, 2, 2, H, 32])
        E = st.sb("E", [PT, 2, 2, H, T])
        rden = st.sb("rden", [PT, 4, H])
        ob = st.sb("ob", [PT, 4, H, D], BF16)
        of = st.sb("of", [PT, 2, 2, C])
        oT = st.sb("oT", [C + 1, 2, T])
        H1 = st.sb("H1", [PT, 2, 2, C])
        mean = st.sb("mean", [C, 2])
        norm = Norm(st, PT, 4)

        pX = st.psum("pX", [C, 2, 256])
        pQ = st.psum("pQ", [128, 512])
        pK = st.psum("pK", [128, 512])
        pS = st.psum("pS", [PT, 4, 512])
        pO = st.psum("pO", [PT, 4, 128])

        const_loaded = st.event("const_loaded", dma=True)
        zeroed = st.event("zeroed")
        memset_done = st.event("memset_done")
        vec0 = st.event("vec0")
        loaded = st.event("loaded", dma=True)
        vec = st.event("vec")
        xn_ready = st.event("xn_ready")
        xT_done = st.event("xT_done")
        xT_ready = st.event("xT_ready")
        q_done = st.event("q_done")
        k_done = st.event("k_done")
        q_ready = st.event("q_ready")
        k_ready = st.event("k_ready")
        v_done = st.event("v_done")
        v_ready = st.event("v_ready")
        s_done = st.event("s_done")
        max_ready = st.event("max_ready")
        qm_done = st.event("qm_done")
        qm_ready = st.event("qm_ready")
        st_done = st.event("st_done")
        exp_ready = st.event("exp_ready")
        o_done = st.event("o_done")
        o_ready = st.event("o_ready")
        oT_done = st.event("oT_done")
        oT_ready = st.event("oT_ready")
        y_done = st.event("y_done")
        h_ready = st.event("h_ready")
        h2_ready = st.event("h2_ready")
        mean_done = st.event("mean_done")
        mean_ready = st.event("mean_ready")
        stored = st.event("stored", dma=True)

        qv, kv = pQ[:, 0:2 * T], pK[:, 0:2 * T]

        with st.block() as block:
            @block.sync
            def _(sp):
                sp.dma_start(ident[:, :], A["const_ident"][:, :]).then_inc(*const_loaded.one())
                sp.wait_ge(*zeroed.after(0))
                for w, n, width in ((wq, "q", D), (wk, "k", D), (wv, "v", D)):
                    sp.dma_start(w[0:C, :, 0:D], A[f"L0_attn_W{n}T"].rearrange("c (h d) -> c h d", h=H)).then_inc(
                        *const_loaded.one())
                    sp.dma_start(w[C:C + 1, :, 0:D], A[f"L0_attn_b{n}"].rearrange(
                        "(o h d) -> o h d", o=1, h=H)).then_inc(*const_loaded.one())
                sp.dma_start(wo[0:C, :], A["L0_attn_WoT"]).then_inc(*const_loaded.one())
                sp.dma_start(wo[C:C + 1, :], A["L0_attn_bo"].rearrange("(o d) -> o d", o=1)).then_inc(
                    *const_loaded.one())
                with sp.Fori(0, PAIRS) as i:
                    sp.wait_ge(*h_ready.before(i))
                    st.held(sp)
                    for ins in load_pair(sp, X, h, i):
                        ins.then_inc(*loaded.one())
                    sp.wait_ge(*h_ready.after(i))
                    st.held(sp)
                    for ins in store_pair(sp, h, H1, i):
                        ins.then_inc(*stored.one())
                    sp.wait_ge(*mean_ready.after(i))
                    st.held(sp)
                    sp.dma_start(mean_dram[:, bass.ds(i * 2, 2)], mean[:, :]).then_inc(*stored.one())
                sp.wait_ge(*stored.after(PAIRS - 1))

            @block.gpsimd
            def _(p):
                p.wait_ge(*memset_done.after(0))
                with p.Fori(0, PAIRS) as i:
                    norm.power(p, i, 0)
                    norm.power(p, i, 1)

            @block.tensor
            def _(pe):
                pe.wait_ge(*const_loaded.after(0))
                pe.wait_ge(*memset_done.after(0))
                with pe.Fori(0, PAIRS) as i:
                    pe.wait_ge(*xn_ready.after(i))
                    st.held(pe)
                    for b in range(2):
                        for t in range(2):
                            ins = pe.transpose(pX[:, b, t * OFF:t * OFF + ROWS[t]], xn[0:ROWS[t], t, b, :],
                                               ident[0:ROWS[t], 0:ROWS[t]])
                    ins.then_inc(*xT_done.one())
                    pe.wait_ge(*xT_ready.after(i))
                    pe.matmul(qv, wq[:, :, :], xT[:, :, :], start=True, stop=True).then_inc(*q_done.one())
                    pe.matmul(kv, wk[:, :, :], xT[:, :, :], start=True, stop=True).then_inc(*k_done.one())
                    pe.wait_ge(*o_ready.before(i))
                    for t in range(2):
                        for b in range(2):
                            ins = pe.matmul(pO[:, 2 * t + b, 0:H * (D + 1)], xT[:, b, t * OFF:t * OFF + PT],
                                            wv[:, :, :], start=True, stop=True)
                    ins.then_inc(*v_done.one())
                    pe.wait_ge(*q_ready.after(i))
                    pe.wait_ge(*k_ready.after(i))
                    for b in range(2):
                        for hd in range(H):
                            if b == 0:
                                pe.wait_ge(*exp_ready.before(i))
                            else:
                                pe.wait_ge(*max_ready.after(i, hd))
                            r = 32 * hd
                            for t in range(2):
                                ins = pe.matmul(pS[:, hd, t * T:t * T + T],
                                                qT[r:r + D, b, t * OFF:t * OFF + PT], kT[r:r + D, b, :],
                                                start=True, stop=True, tile_position=(r, 0))
                            ins.then_inc(*s_done.one())
                    pe.wait_ge(*max_ready.after(i))
                    for b in range(2):
                        for t in range(2):
                            ins = pe.matmul(pQ[:, b * T + t * OFF:b * T + t * OFF + ROWS[t]],
                                            M[0:ROWS[t], t, b, :, :], ident[0:ROWS[t], 0:ROWS[t]],
                                            start=False, stop=True, skip_group_check=True)
                    ins.then_inc(*qm_done.one())
                    pe.wait_ge(*qm_ready.after(i))
                    for b in range(2):
                        for hd in range(H):
                            n = b * H + hd
                            if n >= 4:
                                pe.wait_ge(*exp_ready.after(i, n - 4))
                            r = 32 * hd
                            for t in range(2):
                                ins = pe.matmul(pS[:, n % 4, t * T:t * T + T],
                                                kT[r:r + D + 1, b, t * OFF:t * OFF + PT], qmT[r:r + D + 1, b, :],
                                                start=True, stop=True, tile_position=(r, 0))
                            ins.then_inc(*st_done.one())
                    pe.wait_ge(*v_ready.after(i))
                    for b in range(2):
                        for hd in range(H):
                            pe.wait_ge(*exp_ready.after(i, b * H + hd))
                            for t in range(2):
                                for kt in range(2):
                                    ins = pe.matmul(pO[:, 2 * t + b, hd * (D + 1):(hd + 1) * (D + 1)],
                                                    E[0:ROWS[kt], kt, b, hd, t * OFF:t * OFF + PT],
                                                    V[0:ROWS[kt], kt, b, hd, :], start=(kt == 0),
                                                    stop=(kt == 1))
                    ins.then_inc(*o_done.one())
                    pe.wait_ge(*o_ready.after(i))
                    st.held(pe)
                    for b in range(2):
                        for t in range(2):
                            ins = pe.transpose(pX[:, b, t * OFF:t * OFF + ROWS[t]], of[0:ROWS[t], t, b, :],
                                               ident[0:ROWS[t], 0:ROWS[t]])
                    ins.then_inc(*oT_done.one())
                    pe.wait_ge(*oT_ready.after(i))
                    for t in range(2):
                        for b in range(2):
                            ins = pe.matmul(pK[0:PT, (2 * t + b) * C:(2 * t + b + 1) * C],
                                            oT[:, b, t * OFF:t * OFF + PT], wo[:, :], start=True, stop=True)
                    ins.then_inc(*y_done.one())
                    pe.wait_ge(*h2_ready.after(i))
                    for b in range(2):
                        for t in range(2):
                            ins = pe.matmul(pX[:, b, 0:1], xn[0:ROWS[t], t, b, :], ones[0:ROWS[t], :],
                                            start=(t == 0), stop=(t == 1))
                    ins.then_inc(*mean_done.one())

            @block.scalar
            def _(a):
                with a.Fori(0, PAIRS) as i:
                    norm.square(a, i, 0, norm.xc[:, :, :])
                    a.wait_ge(*q_done.after(i))
                    a.activation(qT[:, :, :].rearrange("p b t -> p (b t)"), qv, ACT.Copy).then_inc(*q_ready.one())
                    a.wait_ge(*v_done.after(i))
                    a.activation(V[:, :, :, :, :].rearrange("p t b h d -> p (t b) (h d)"),
                                 pO[:, :, 0:H * (D + 1)], ACT.Copy).then_inc(*v_ready.one())
                    a.wait_ge(*qm_done.after(i))
                    a.activation(qmT[:, :, :].rearrange("p b t -> p (b t)"), qv, ACT.Copy).then_inc(
                        *qm_ready.one())
                    for b in range(2):
                        for hd in range(H):
                            n = b * H + hd
                            a.wait_ge(*st_done.after(i, n))
                            a.activation(E[:, :, b, hd, :], pS[:, n % 4, 0:2 * T].rearrange(
                                "p (t n) -> p t n", t=2), ACT.Exp, scale=D ** -0.5).then_inc(*exp_ready.one())
                    norm.square(a, i, 1, norm.xc[:, :, :])
                    a.wait_ge(*mean_done.after(i))
                    a.wait_ge(*stored.before(i))
                    a.activation(mean[:, :], pX[:, :, 0], ACT.Copy, scale=1.0 / T).then_inc(*mean_ready.one())

            @block.vector
            def _(v):
                v.memset(wq[:, :, :], 0.0)
                v.memset(wk[:, :, :], 0.0)
                v.memset(wv[:, :, :], 0.0).then_inc(*vec0.one())
                v.wait_ge(*vec0.after(0))
                v.memset(wk[C:C + 1, :, D:D + 1], 1.0)
                v.memset(wv[C:C + 1, :, D:D + 1], 1.0).then_inc(*zeroed.one())
                v.memset(ones[:, :], 1.0)
                v.memset(xT[C:C + 1, :, :], 1.0)
                v.memset(oT[C:C + 1, :, :], 1.0)
                v.memset(M[:, :, :, :, :], 0.0)
                v.memset(norm.expo[:, :], -0.5).then_inc(*memset_done.one())
                v.wait_ge(*memset_done.after(0))
                with v.Fori(0, PAIRS) as i:
                    v.wait_ge(*loaded.after(i))
                    norm.center(v, i, g4(X[:, :, :, :]), vec)
                    v.wait_ge(*mean_done.before(i))
                    norm.scale(v, i, 0, norm.xc[:, :, :], g4(xn[:, :, :, :]), 1e-5, vec).then_inc(
                        *xn_ready.one())
                    v.wait_ge(*xT_done.after(i))
                    v.tensor_scalar(xT[0:C, :, :], pX[:, :, 0:T], -10000.0, 10000.0, ALU.max,
                                    ALU.min).then_inc(*xT_ready.one())
                    v.wait_ge(*k_done.after(i))
                    v.tensor_copy(kT[:, :, :].rearrange("p b t -> p (b t)"), kv).then_inc(*k_ready.one())
                    for b in range(2):
                        for hd in range(H):
                            v.wait_ge(*s_done.after(i, b * H + hd))
                            v.tensor_reduce(M[:, :, b, hd, D], pS[:, hd, 0:2 * T].rearrange(
                                "p (t n) -> p t n", t=2), AX.X, ALU.max, negate=True).then_inc(*max_ready.one())
                    v.wait_ge(*o_done.after(i))
                    o5 = pO[:, :, 0:H * (D + 1)].rearrange("p g (h d) -> p g h d", h=H)
                    v.reciprocal(rden[:, :, :], o5[:, :, :, D]).then_inc(*vec.one())
                    v.wait_ge(*vec.latest(i))
                    for g in range(4):
                        ins = v.tensor_tensor(ob[:, g, :, :], o5[:, g, :, 0:D], bc(rden[:, g, :], D), ALU.mult)
                    ins.then_inc(*vec.one())
                    v.wait_ge(*vec.latest(i))
                    v.tensor_copy(g4(of[:, :, :, :]), ob[:, :, :, :].rearrange(
                        "p g h d -> p g (h d)")).then_inc(*o_ready.one())
                    v.wait_ge(*oT_done.after(i))
                    v.tensor_copy(oT[0:C, :, :], pX[:, :, 0:T]).then_inc(*oT_ready.one())
                    v.wait_ge(*y_done.after(i))
                    v.wait_ge(*stored.before(i))
                    v.tensor_tensor(g4(H1[:, :, :, :]), g4(X[:, :, :, :]),
                                    pK[0:PT, 0:4 * C].rearrange("p (g c) -> p g c", g=4), ALU.add).then_inc(
                        *h_ready.one())
                    v.wait_ge(*h_ready.after(i))
                    norm.center(v, i, g4(H1[:, :, :, :]), vec)
                    norm.scale(v, i, 1, norm.xc[:, :, :], g4(xn[:, :, :, :]), 1e-5, vec).then_inc(
                        *h2_ready.one())


class Pair:

    def __init__(self, st, tiles=2, rows=PT, ones_row=True):
        self.st, self.tiles, self.rows = st, tiles, rows
        self.X = st.sb("X", [rows, tiles, 2, C])
        self.xn = st.sb("xn", [rows, tiles, 2, C])
        self.H1 = st.sb("H1", [rows, tiles, 2, C])
        self.xT = st.sb("xT", [C + 1, 2, T])
        self.ident = st.sb("ident", [128, 128])
        self.norm = Norm(st, rows, 2 * tiles)
        self.const_loaded = st.event("const_loaded", dma=True)
        self.loaded = st.event("loaded", dma=True)
        self.stored = st.event("stored", dma=True)
        self.memset_done = st.event("memset_done")
        self.vec = st.event("vec")
        self.xn_ready = st.event("xn_ready")
        self.xT_done = st.event("xT_done")
        self.xT_ready = st.event("xT_ready")
        self.h_ready = st.event("h_ready")

    def memsets(self, v):
        v.memset(self.xT[C:C + 1, :, :], 1.0)
        v.memset(self.norm.expo[:, :], -0.5).then_inc(*self.memset_done.one())

    def normalise(self, v, i):
        v.wait_ge(*self.loaded.after(i))
        self.norm.center(v, i, g4(self.X[:, :, :, :]), self.vec)
        self.norm.scale(v, i, 0, self.norm.xc[:, :, :], g4(self.xn[:, :, :, :]), 1e-5, self.vec).then_inc(
            *self.xn_ready.one())


def transpose_rows(pe, dst, src, ident):
    for b in range(2):
        for t in range(2):
            ins = pe.transpose(dst[:, b, t * OFF:t * OFF + ROWS[t]], src[0:ROWS[t], t, b, :],
                               ident[0:ROWS[t], 0:ROWS[t]])
    return ins


def const(sp, signal, dst, src):
    sp.dma_start(dst, src).then_inc(*signal.one())


def row(ap):
    return bass.AP(ap.tensor, ap.offset, [[0, 1]] + [list(x) for x in ap.ap])


def every_row(ap, rows):
    return bass.AP(ap.tensor, ap.offset, [[0, rows]] + [list(x) for x in ap.ap])


class Rank:

    def __init__(self, st, rows, groups, k):
        self.rows, self.g, self.k = rows, groups, k
        self.gt = st.sb("rank_gt", [rows, groups, EXPERTS, EXPERTS])
        self.eq = st.sb("rank_eq", [rows, groups, EXPERTS, EXPERTS])
        self.rank = st.sb("rank", [rows, groups, EXPERTS])
        self.earlier = st.sb("rank_earlier", [rows, EXPERTS * EXPERTS])

    def select(self, v, i, w, sel, chain):
        e = EXPERTS
        other, own = bcm(w, 2, e), bc(w, e)
        v.tensor_tensor(self.gt[:, :, :, :], other, own, ALU.is_gt)
        v.tensor_tensor(self.eq[:, :, :, :], other, own, ALU.is_equal).then_inc(*chain.one())
        v.wait_ge(*chain.latest(i))
        v.tensor_tensor(self.eq[:, :, :, :].rearrange("p g e f -> p g (e f)"),
                        self.eq[:, :, :, :].rearrange("p g e f -> p g (e f)"),
                        bcm(self.earlier[:, :], 1, self.g), ALU.mult).then_inc(*chain.one())
        v.wait_ge(*chain.latest(i))
        v.tensor_tensor(self.gt[:, :, :, :], self.gt[:, :, :, :], self.eq[:, :, :, :], ALU.add).then_inc(
            *chain.one())
        v.wait_ge(*chain.latest(i))
        v.reduce_sum(self.rank[:, :, :], self.gt[:, :, :, :], AX.X).then_inc(*chain.one())
        v.wait_ge(*chain.latest(i))
        return v.tensor_scalar(sel, self.rank[:, :, :], float(self.k), None, ALU.is_lt)


def stage_router0(nc, A, mean_dram, route_dram):
    capacity = float(math.ceil(BATCH * T * 1.25 / EXPERTS))
    E, B = EXPERTS, BATCH
    with Stage(nc, "route") as st:
        mT = st.sb("mean", [C + 1, B])
        wr = st.sb("wr", [C + 1, E])
        ones = st.sb("ones", [B, B])
        z = st.sb("z", [B, E])
        s1 = st.sb("s1", [B, 1])
        p = st.sb("p", [B, E])
        ld = st.sb("load", [B, E])
        w = st.sb("w", [B, E])
        sel = st.sb("sel", [B, E])
        e2 = st.sb("e2", [B, E])
        rank = Rank(st, B, 1, 2)
        pL = st.psum("pL", [B, 2, E])
        const_loaded = st.event("const_loaded", dma=True)
        memset_done = st.event("memset_done")
        logits = st.event("logits")
        probs = st.event("probs")
        loads = st.event("loads")
        vec = st.event("vec")
        shifted = st.event("shifted")
        expd = st.event("expd")
        ready = st.event("ready")
        stored = st.event("stored", dma=True)
        with st.block() as block:
            @block.sync
            def _(sp):
                const(sp, const_loaded, mT[0:C, :], mean_dram[:, :])
                const(sp, const_loaded, wr[0:C, :], A["L0_ffn_Wr"])
                const(sp, const_loaded, wr[C:C + 1, :], row(A["L0_ffn_br"]))
                const(sp, const_loaded, rank.earlier[:, :], every_row(A["const_earlier"], B))
                sp.wait_ge(*ready.after(0))
                sp.dma_start(route_dram[:, :], w[:, :]).then_inc(*stored.one())
                sp.wait_ge(*stored.after(0))

            @block.tensor
            def _(pe):
                pe.wait_ge(*const_loaded.after(0))
                pe.wait_ge(*memset_done.after(0))
                pe.matmul(pL[:, 0, :], mT[:, :], wr[:, :], start=True, stop=True).then_inc(*logits.one())
                pe.wait_ge(*probs.after(0))
                pe.matmul(pL[:, 1, :], ones[:, :], p[:, :], start=True, stop=True).then_inc(*loads.one())

            @block.scalar
            def _(a):
                for k in range(3):
                    a.wait_ge(*shifted.after(0, k))
                    a.activation(z[:, :], z[:, :], ACT.Exp).then_inc(*expd.one())

            @block.vector
            def _(v):
                def link(ins):
                    ins.then_inc(*vec.one())
                    v.wait_ge(*vec.latest(0))

                def softmax(k, src, dst, sig):
                    link(v.reduce_max(s1[:, :], src, AX.X))
                    v.tensor_scalar(z[:, :], src, s1[:, 0:1], None, ALU.subtract).then_inc(*shifted.one())
                    v.wait_ge(*expd.after(0, k))
                    if k == 2:
                        link(v.tensor_tensor(z[:, :], z[:, :], sel[:, :], ALU.mult))
                    link(v.reduce_sum(s1[:, :], z[:, :], AX.X))
                    link(v.reciprocal(s1[:, :], s1[:, :]))
                    v.tensor_scalar(dst, z[:, :], s1[:, 0:1], None, ALU.mult).then_inc(*sig.one())
                    v.wait_ge(*sig.latest(0))

                v.memset(ones[:, :], 1.0)
                v.memset(mT[C:C + 1, :], 1.0).then_inc(*memset_done.one())
                v.wait_ge(*logits.after(0))
                softmax(0, pL[:, 0, :], p[:, :], probs)
                v.wait_ge(*loads.after(0))
                link(v.tensor_scalar(ld[:, :], pL[:, 1, :], float(T), None, ALU.mult))
                link(v.reciprocal(ld[:, :], ld[:, :]))
                link(v.tensor_scalar(ld[:, :], ld[:, :], capacity, 1.0, ALU.mult, ALU.min))
                link(v.tensor_tensor(p[:, :], p[:, :], ld[:, :], ALU.mult))
                softmax(1, p[:, :], w[:, :], vec)
                v.wait_ge(*const_loaded.after(0))
                link(rank.select(v, 0, w[:, :].rearrange("p (g e) -> p g e", g=1),
                                 sel[:, :].rearrange("p (g e) -> p g e", g=1), vec))
                softmax(2, w[:, :], w[:, :], ready)


def combine(v, i, pY, coef, Z, acc, chain):
    v.tensor_tensor(Z[:, :, :], pY.rearrange("p (e c) -> p e c", e=EXPERTS), bc(coef, C), ALU.mult).then_inc(
        *chain.one())
    v.wait_ge(*chain.latest(i))
    return v.reduce_sum(acc, Z[:, :, :].rearrange("p e c -> p c e"), AX.X)


def stage_ffn0(nc, A, h, route_dram):
    E, F = EXPERTS, 128
    with Stage(nc, "ffn0") as st:
        p = Pair(st)
        X, xn, xT, norm, vec, H1 = p.X, p.xn, p.xT, p.norm, p.vec, p.H1
        w1 = st.sb("w1", [C + 1, E, F])
        w2 = st.sb("w2", [F, E, C])
        b2 = st.sb("b2", [1, E * C])
        ones = st.sb("ones", [1, PT])
        gamma = st.sb("gamma", [PT, C])
        beta = st.sb("beta", [PT, C])
        wB = st.sb("wB", [PT, 2, E])
        hT = st.sb("hT", [F, E, 2 * T])
        Z = st.sb("Z", [PT, E, C])
        acc = st.sb("acc", [PT, 2, 2, C])
        pX = st.psum("pX", [C, 2, 256])
        pH = st.psum("pH", [F, 3, 512])
        pY = st.psum("pY", [PT, 4, 512])
        hid_done = st.event("hid_done")
        hid_ready = st.event("hid_ready")
        y_done = st.event("y_done")
        y_used = st.event("y_used")
        with st.block() as block:
            @block.sync
            def _(sp):
                cl = p.const_loaded
                const(sp, cl, p.ident[:, :], A["const_ident"])
                const(sp, cl, w1[0:C, :, :], A["L0_ffn_W1"].rearrange("e d f -> d e f"))
                const(sp, cl, w1[C:C + 1, :, :], row(A["L0_ffn_b1"]))
                const(sp, cl, w2[:, :, :], A["L0_ffn_W2"].rearrange("e f d -> f e d"))
                const(sp, cl, b2[:, :], row(A["L0_ffn_b2"].rearrange("e d -> (e d)")))
                const(sp, cl, gamma[:, :], every_row(A["L0_ffn_gamma"], PT))
                const(sp, cl, beta[:, :], every_row(A["L0_ffn_beta"], PT))
                with sp.Fori(0, PAIRS) as i:
                    sp.wait_ge(*p.h_ready.before(i))
                    st.held(sp)
                    for ins in load_pair(sp, X, h, i):
                        ins.then_inc(*p.loaded.one())
                    sp.dma_start(wB[:, :, :], every_row(route_dram[bass.ds(i * 2, 2), :], PT)).then_inc(
                        *p.loaded.one())
                    sp.wait_ge(*p.h_ready.after(i))
                    st.held(sp)
                    for ins in store_pair(sp, h, H1, i):
                        ins.then_inc(*p.stored.one())
                sp.wait_ge(*p.stored.after(PAIRS - 1))

            @block.gpsimd
            def _(g):
                g.wait_ge(*p.memset_done.after(0))
                with g.Fori(0, PAIRS) as i:
                    norm.power(g, i, 0)
                    norm.power(g, i, 1)

            @block.tensor
            def _(pe):
                pe.wait_ge(*p.const_loaded.after(0))
                pe.wait_ge(*p.memset_done.after(0))
                with pe.Fori(0, PAIRS) as i:
                    pe.wait_ge(*p.xn_ready.after(i))
                    st.held(pe)
                    transpose_rows(pe, pX, xn, p.ident).then_inc(*p.xT_done.one())
                    pe.wait_ge(*p.xT_ready.after(i))
                    for e in range(E):
                        if e >= 3:
                            pe.wait_ge(*hid_ready.after(i, e - 3))
                        pe.matmul(pH[:, e % 3, 0:2 * T], w1[:, e, :], xT[:, :, :], start=True,
                                  stop=True).then_inc(*hid_done.one())
                    pe.wait_ge(*hid_ready.after(i))
                    pe.wait_ge(*y_used.before(i))
                    st.held(pe)
                    for t in range(2):
                        for b in range(2):
                            n = 2 * t + b
                            pe.matmul(pY[:, n, :], ones[:, :], b2[:, :], start=True, stop=False)
                            for e in range(E):
                                ins = pe.matmul(pY[:, n, e * C:(e + 1) * C],
                                                hT[:, e, b * T + t * OFF:b * T + t * OFF + PT], w2[:, e, :],
                                                start=False, stop=(e == E - 1))
                            ins.then_inc(*y_done.one())

            @block.scalar
            def _(a):
                with a.Fori(0, PAIRS) as i:
                    norm.square(a, i, 0, norm.xc[:, :, :])
                    for e in range(E):
                        a.wait_ge(*hid_done.after(i, e))
                        a.wait_ge(*y_done.before(i))
                        a.activation(hT[:, e, :], pH[:, e % 3, 0:2 * T], ACT.Gelu).then_inc(*hid_ready.one())
                    norm.square(a, i, 1, norm.xc[:, :, :])

            @block.vector
            def _(v):
                v.memset(ones[:, :], 1.0)
                p.memsets(v)
                v.wait_ge(*p.memset_done.after(0))
                v.wait_ge(*p.const_loaded.after(0))

                def link(ins):
                    ins.then_inc(*vec.one())
                    v.wait_ge(*vec.latest(i))
                with v.Fori(0, PAIRS) as i:
                    p.normalise(v, i)
                    v.wait_ge(*p.xT_done.after(i))
                    v.tensor_copy(xT[0:C, :, :], pX[:, :, 0:T]).then_inc(*p.xT_ready.one())
                    for t in range(2):
                        for b in range(2):
                            n = 2 * t + b
                            v.wait_ge(*y_done.after(i, n))
                            combine(v, i, pY[:, n, :], wB[:, b, :], Z, acc[:, t, b, :], vec).then_inc(
                                *y_used.one())
                            v.wait_ge(*y_used.latest(i))
                    link(v.tensor_tensor(g4(acc[:, :, :, :]), g4(acc[:, :, :, :]), g4(xn[:, :, :, :]), ALU.add))
                    norm.center(v, i, g4(acc[:, :, :, :]), vec)
                    link(norm.scale(v, i, 1, norm.xc[:, :, :], g4(acc[:, :, :, :]), 1e-5, vec))
                    link(v.tensor_tensor(g4(acc[:, :, :, :]), g4(acc[:, :, :, :]), bcm(gamma[:, :], 1, 4), ALU.mult))
                    link(v.tensor_tensor(g4(acc[:, :, :, :]), g4(acc[:, :, :, :]), bcm(beta[:, :], 1, 4), ALU.add))
                    v.wait_ge(*p.stored.before(i))
                    v.tensor_tensor(g4(H1[:, :, :, :]), g4(acc[:, :, :, :]), g4(X[:, :, :, :]), ALU.add).then_inc(
                        *p.h_ready.one())


LOW = T + PT


def stage_retention1(nc, A, h):
    with Stage(nc, "ret1") as st:
        p = Pair(st)
        X, xn, xT, norm, vec, H1 = p.X, p.xn, p.xT, p.norm, p.vec, p.H1
        W = st.sb("W", [C, 5, C])
        cs = st.sb("cos_sin", [C, 2, T])
        decay = st.sb("decay", [PT, LOW])
        t1 = st.sb("t1", [C, 2, 2, T])
        t2 = st.sb("t2", [C, 2, 2, T])
        qk = st.sb("qk", [C, 2, 2, T])
        V = st.sb("V", [PT, 4, C])
        P = st.sb("P", [PT, 2, LOW])
        pX = st.psum("pX", [C, 2, 256])
        pR = st.psum("pR", [C, 4, 512])
        pV = st.psum("pV", [PT, 2, 4, C])
        pS = st.psum("pS", [PT, 2, 512])
        r_done = st.event("r_done")
        v_done = st.event("v_done")
        v_ready = st.event("v_ready")
        qk_ready = st.event("qk_ready")
        s_done = st.event("s_done")
        p_ready = st.event("p_ready")
        o_done = st.event("o_done")
        with st.block() as block:
            @block.sync
            def _(sp):
                cl = p.const_loaded
                const(sp, cl, p.ident[:, :], A["const_ident"])
                for k, n in enumerate(("Q", "Qx", "K", "Kx", "V")):
                    const(sp, cl, W[:, k, :], A[f"L1_attn_W_{n}"])
                const(sp, cl, cs[:, :, :], A["const_rope64"].rearrange("s c t -> c s t"))
                const(sp, cl, decay[:, :], A["const_decay"])
                with sp.Fori(0, PAIRS) as i:
                    sp.wait_ge(*p.h_ready.before(i))
                    st.held(sp)
                    for ins in load_pair(sp, X, h, i):
                        ins.then_inc(*p.loaded.one())
                    sp.wait_ge(*p.h_ready.after(i))
                    st.held(sp)
                    for ins in store_pair(sp, h, H1, i):
                        ins.then_inc(*p.stored.one())
                sp.wait_ge(*p.stored.after(PAIRS - 1))

            @block.gpsimd
            def _(g):
                g.wait_ge(*p.memset_done.after(0))
                with g.Fori(0, PAIRS) as i:
                    norm.power(g, i, 0)

            @block.tensor
            def _(pe):
                pe.wait_ge(*p.const_loaded.after(0))
                pe.wait_ge(*p.memset_done.after(0))
                with pe.Fori(0, PAIRS) as i:
                    pe.wait_ge(*p.xn_ready.after(i))
                    st.held(pe)
                    transpose_rows(pe, pX, xn, p.ident).then_inc(*p.xT_done.one())
                    pe.wait_ge(*p.xT_ready.after(i))
                    st.held(pe)
                    for k in range(4):
                        pe.matmul(pR[:, k, 0:2 * T], W[:, k, :], xT[0:C, :, :], start=True,
                                  stop=True).then_inc(*r_done.one())
                    for t in range(2):
                        for b in range(2):
                            ins = pe.matmul(pV[:, 0, 2 * t + b, :], xT[0:C, b, t * OFF:t * OFF + PT], W[:, 4, :],
                                            start=True, stop=True)
                    ins.then_inc(*v_done.one())
                    pe.wait_ge(*qk_ready.after(i))
                    st.held(pe)
                    for b in range(2):
                        pe.matmul(pS[:, b, 0:T], qk[:, 1, b, 0:PT], qk[:, 0, b, :], start=True, stop=True)
                        pe.matmul(pS[:, b, T:LOW], qk[:, 1, b, OFF:T], qk[:, 0, b, OFF:T], start=True,
                                  stop=True).then_inc(*s_done.one())
                    pe.wait_ge(*v_ready.after(i))
                    st.held(pe)
                    for b in range(2):
                        pe.wait_ge(*p_ready.after(i, b))
                        st.held(pe)
                        pe.matmul(pV[:, 1, b, :], P[0:OFF, b, 0:PT], V[0:OFF, b, :], start=True, stop=True)
                        pe.matmul(pV[:, 1, 2 + b, :], P[0:OFF, b, OFF:T], V[0:OFF, b, :], start=True, stop=False)
                        ins = pe.matmul(pV[:, 1, 2 + b, :], P[:, b, T:LOW], V[:, 2 + b, :], start=False, stop=True)
                    ins.then_inc(*o_done.one())

            @block.scalar
            def _(a):
                with a.Fori(0, PAIRS) as i:
                    norm.square(a, i, 0, norm.xc[:, :, :])
                    a.wait_ge(*v_done.after(i))
                    a.activation(V[:, :, :], pV[:, 0, :, :], ACT.Copy).then_inc(*v_ready.one())

            @block.vector
            def _(v):
                p.memsets(v)
                v.wait_ge(*p.memset_done.after(0))
                v.wait_ge(*p.const_loaded.after(0))
                with v.Fori(0, PAIRS) as i:
                    p.normalise(v, i)
                    v.wait_ge(*p.xT_done.after(i))
                    v.tensor_copy(xT[0:C, :, :], pX[:, :, 0:T]).then_inc(*p.xT_ready.one())
                    for k in range(2):
                        v.wait_ge(*r_done.after(i, 2 * k))
                        v.tensor_tensor(t1[:, k, :, :], pR[:, 2 * k, 0:2 * T].rearrange("c (b t) -> c b t", b=2),
                                        bcm(cs[:, 0, :], 1, 2), ALU.mult)
                        v.wait_ge(*r_done.after(i, 2 * k + 1))
                        v.tensor_tensor(t2[:, k, :, :], pR[:, 2 * k + 1, 0:2 * T].rearrange(
                            "c (b t) -> c b t", b=2), bcm(cs[:, 1, :], 1, 2), ALU.mult).then_inc(*vec.one())
                        v.wait_ge(*vec.latest(i))
                        v.tensor_tensor(qk[:, k, :, :], t1[:, k, :, :], t2[:, k, :, :], ALU.add).then_inc(
                            *qk_ready.one())
                    for b in range(2):
                        v.wait_ge(*s_done.after(i, b))
                        v.tensor_tensor(P[:, b, :], pS[:, b, 0:LOW], decay[:, :], ALU.mult).then_inc(*p_ready.one())
                    v.wait_ge(*o_done.after(i))
                    v.wait_ge(*p.stored.before(i))
                    v.tensor_tensor(g4(H1[:, :, :, :]), pV[:, 1, :, :], g4(X[:, :, :, :]), ALU.add).then_inc(
                        *p.h_ready.one())


def stage_attention1(nc, A, h, hx_dram, flatT_dram, mix_dram):
    H, D, KV = 4, 16, 2
    E = EXPERTS
    with Stage(nc, "att1") as st:
        p = Pair(st)
        X, xn, xT, norm, vec, H1 = p.X, p.xn, p.xT, p.norm, p.vec, p.H1
        wqk = st.sb("wqk", [C + 1, 4, H, 32])
        wv = st.sb("wv", [C + 1, KV, D + 1])
        wo = st.sb("wo", [C, C])
        wr = st.sb("wr", [C, E])
        ln1 = st.sb("ln1", [PT, C])
        ln2 = st.sb("ln2", [PT, C])
        cs = st.sb("cos_sin", [128, 2, T])
        maskQ = st.sb("maskQ", [PT, LOW])
        maskK = st.sb("maskK", [PT, LOW])
        r1 = st.sb("r1", [PT, 4, C])
        t1 = st.sb("t1", [128, 2, T])
        t2 = st.sb("t2", [128, 2, T])
        qT = st.sb("qT", [128, 2, T])
        kT = st.sb("kT", [128, 2, T])
        qmT = st.sb("qmT", [128, 2, T])
        V = st.sb("V", [PT, 4, KV, D + 1])
        M = st.sb("M", [PT, 2, 2, H, 32])
        SM = st.sb("SM", [PT, 2, LOW])
        EX = st.sb("EX", [PT, 2, H, LOW])
        rden = st.sb("rden", [PT, 4, H])
        of = st.sb("of", [PT, 2, 2, C])
        oT = st.sb("oT", [C, 2, T])
        x2 = st.sb("x2", [PT, 4, C])
        fl = st.sb("fl", [PT, 2, 2, C])
        flT = st.sb("flT", [C, 2, T])
        lg = st.sb("lg", [PT, 4, E])
        lsum = st.sb("lsum", [PT, 4])
        sel = st.sb("sel", [PT, 4, E])
        mix = st.sb("mix", [PT, 2, 2, E])
        rank = Rank(st, PT, 4, 2)
        pX = st.psum("pX", [C, 2, 256])
        pR = st.psum("pR", [128, 2, 512])
        pS = st.psum("pS", [PT, 4, 512])
        pO = st.psum("pO", [PT, 4, 128])

        cleared = st.event("cleared")
        zeroed = st.event("zeroed")
        r_done = st.event("r_done")
        q_ready = st.event("q_ready")
        k_ready = st.event("k_ready")
        v_done = st.event("v_done")
        v_ready = st.event("v_ready")
        s_done = st.event("s_done")
        max_ready = st.event("max_ready")
        m_done = st.event("m_done")
        qm_ready = st.event("qm_ready")
        st_done = st.event("st_done")
        masked = st.event("masked")
        exp_ready = st.event("exp_ready")
        o_done = st.event("o_done")
        o_ready = st.event("o_ready")
        y_done = st.event("y_done")
        fl_ready = st.event("fl_ready")
        flT_done = st.event("flT_done")
        flT_ready = st.event("flT_ready")
        l_done = st.event("l_done")
        l_shifted = st.event("l_shifted")
        l_exp = st.event("l_exp")
        mix_ready = st.event("mix_ready")
        with st.block() as block:
            @block.sync
            def _(sp):
                cl = p.const_loaded
                const(sp, cl, p.ident[:, :], A["const_ident"])
                const(sp, cl, cs[:, :, :], A["const_rope16"].rearrange("s c t -> c s t"))
                const(sp, cl, maskQ[:, :], A["const_maskQ"])
                const(sp, cl, maskK[:, :], A["const_maskK"])
                const(sp, cl, wo[:, :], A["L1_ffn_woT"])
                const(sp, cl, wr[:, :], A["L1_ffn_router_wT"])
                const(sp, cl, ln1[:, :], every_row(A["L1_ffn_ln1_w"], PT))
                const(sp, cl, ln2[:, :], every_row(A["L1_ffn_ln2_w"], PT))
                const(sp, cl, rank.earlier[:, :], every_row(A["const_earlier"], PT))
                sp.wait_ge(*zeroed.after(0))
                for k, n in enumerate(("wq", "wqx")):
                    const(sp, cl, wqk[0:C, k, :, 0:D], A[f"L1_ffn_{n}T"].rearrange("c (h d) -> c h d", h=H))
                for k, n in enumerate(("wk", "wkx")):
                    for r in range(H // KV):
                        const(sp, cl, wqk[0:C, 2 + k, :, 0:D].rearrange("c (k r) d -> c r k d", k=KV)[:, r, :, :],
                              A[f"L1_ffn_{n}T"].rearrange("c (k d) -> c k d", k=KV))
                const(sp, cl, wv[0:C, :, 0:D], A["L1_ffn_wvT"].rearrange("c (k d) -> c k d", k=KV))
                with sp.Fori(0, PAIRS) as i:
                    sp.wait_ge(*p.h_ready.before(i))
                    st.held(sp)
                    for ins in load_pair(sp, X, h, i):
                        ins.then_inc(*p.loaded.one())
                    sp.wait_ge(*p.h_ready.after(i))
                    st.held(sp)
                    for ins in store_pair(sp, hx_dram, H1, i):
                        ins.then_inc(*p.stored.one())
                    sp.wait_ge(*flT_ready.after(i))
                    st.held(sp)
                    sp.dma_start(flatT_dram[bass.ds(i, 1), :, :].rearrange("o c t -> (o c) t"),
                                 flT[:, :, :].rearrange("c b t -> c (b t)")).then_inc(*p.stored.one())
                    sp.wait_ge(*mix_ready.after(i))
                    st.held(sp)
                    for ins in store_pair(sp, mix_dram, mix, i, E):
                        ins.then_inc(*p.stored.one())
                sp.wait_ge(*p.stored.after(PAIRS - 1))

            @block.gpsimd
            def _(g):
                g.wait_ge(*p.memset_done.after(0))
                with g.Fori(0, PAIRS) as i:
                    for k in range(3):
                        norm.power(g, i, k)

            @block.tensor
            def _(pe):
                pe.wait_ge(*p.const_loaded.after(0))
                pe.wait_ge(*p.memset_done.after(0))
                with pe.Fori(0, PAIRS) as i:
                    pe.wait_ge(*p.xn_ready.after(i))
                    st.held(pe)
                    transpose_rows(pe, pX, p.H1, p.ident).then_inc(*p.xT_done.one())
                    pe.wait_ge(*p.xT_ready.after(i, 0))
                    for k in range(4):
                        if k >= 2:
                            pe.wait_ge(*q_ready.after(i))
                        pe.matmul(pR[:, k % 2, 0:2 * T], wqk[:, k, :, :], xT[:, :, :], start=True,
                                  stop=True).then_inc(*r_done.one())
                    st.held(pe)
                    for t in range(2):
                        for b in range(2):
                            ins = pe.matmul(pO[:, 2 * t + b, 0:KV * (D + 1)], xT[:, b, t * OFF:t * OFF + PT],
                                            wv[:, :, :], start=True, stop=True)
                    ins.then_inc(*v_done.one())
                    pe.wait_ge(*k_ready.after(i))
                    for b in range(2):
                        for hd in range(H):
                            if b == 0:
                                pe.wait_ge(*exp_ready.before(i))
                            else:
                                pe.wait_ge(*max_ready.after(i, hd))
                            r = 32 * hd
                            pe.matmul(pS[:, hd, 0:PT], qT[r:r + D, b, 0:PT], kT[r:r + D, b, 0:PT], start=True,
                                      stop=True, tile_position=(r, 0))
                            pe.matmul(pS[:, hd, PT:LOW], qT[r:r + D, b, OFF:T], kT[r:r + D, b, :], start=True,
                                      stop=True, tile_position=(r, 0)).then_inc(*s_done.one())
                    pe.wait_ge(*max_ready.after(i))
                    for b in range(2):
                        for t in range(2):
                            ins = pe.matmul(pR[:, 0, b * T + t * OFF:b * T + t * OFF + ROWS[t]],
                                            M[0:ROWS[t], t, b, :, :], p.ident[0:ROWS[t], 0:ROWS[t]],
                                            start=True, stop=True)
                    ins.then_inc(*m_done.one())
                    pe.wait_ge(*qm_ready.after(i))
                    for b in range(2):
                        for hd in range(H):
                            if b == 1:
                                pe.wait_ge(*masked.after(i, hd))
                            r = 32 * hd
                            pe.matmul(pS[:, hd, 0:T], kT[r:r + D + 1, b, 0:PT], qmT[r:r + D + 1, b, :], start=True,
                                      stop=True, tile_position=(r, 0))
                            pe.matmul(pS[:, hd, T:LOW], kT[r:r + D + 1, b, OFF:T], qmT[r:r + D + 1, b, OFF:T],
                                      start=True, stop=True, tile_position=(r, 0)).then_inc(*st_done.one())
                    pe.wait_ge(*v_ready.after(i))
                    for b in range(2):
                        for hd in range(H):
                            pe.wait_ge(*exp_ready.after(i, b * H + hd))
                            kv, c0 = hd // (H // KV), hd * (D + 1)
                            pe.matmul(pO[:, b, c0:c0 + D + 1], EX[0:OFF, b, hd, 0:PT], V[0:OFF, b, kv, :],
                                      start=True, stop=True)
                            pe.matmul(pO[:, 2 + b, c0:c0 + D + 1], EX[0:OFF, b, hd, OFF:T], V[0:OFF, b, kv, :],
                                      start=True, stop=False)
                            ins = pe.matmul(pO[:, 2 + b, c0:c0 + D + 1], EX[:, b, hd, T:LOW], V[:, 2 + b, kv, :],
                                            start=False, stop=True)
                    ins.then_inc(*o_done.one())
                    pe.wait_ge(*o_ready.after(i))
                    st.held(pe)
                    transpose_rows(pe, pX, of, p.ident).then_inc(*p.xT_done.one())
                    pe.wait_ge(*p.xT_ready.after(i, 1))
                    st.held(pe)
                    for t in range(2):
                        for b in range(2):
                            n = 2 * t + b
                            ins = pe.matmul(pR[0:PT, 1, n * C:(n + 1) * C], oT[:, b, t * OFF:t * OFF + PT], wo[:, :],
                                            start=True, stop=True)
                    ins.then_inc(*y_done.one())
                    pe.wait_ge(*fl_ready.after(i))
                    st.held(pe)
                    transpose_rows(pe, pX, fl, p.ident).then_inc(*flT_done.one())
                    pe.wait_ge(*flT_ready.after(i))
                    st.held(pe)
                    for t in range(2):
                        for b in range(2):
                            n = 2 * t + b
                            ins = pe.matmul(pR[0:PT, 0, n * E:(n + 1) * E], flT[:, b, t * OFF:t * OFF + PT],
                                            wr[:, :], start=True, stop=True)
                    ins.then_inc(*l_done.one())

            @block.scalar
            def _(a):
                with a.Fori(0, PAIRS) as i:
                    norm.square(a, i, 0, norm.xc[:, :, :])
                    norm.square(a, i, 1, g4(xn[:, :, :, :]))
                    a.wait_ge(*v_done.after(i))
                    a.activation(V[:, :, :, :].rearrange("p g k d -> p g (k d)"), pO[:, :, 0:KV * (D + 1)],
                                 ACT.Copy).then_inc(*v_ready.one())
                    for b in range(2):
                        for hd in range(H):
                            n = b * H + hd
                            a.wait_ge(*masked.after(i, n))
                            a.activation(EX[:, b, hd, :], EX[:, b, hd, :], ACT.Exp, scale=D ** -0.5).then_inc(
                                *exp_ready.one())
                    norm.square(a, i, 2, x2[:, :, :])
                    a.wait_ge(*l_shifted.after(i))
                    a.activation(lg[:, :, :], lg[:, :, :], ACT.Exp).then_inc(*l_exp.one())

            @block.vector
            def _(v):
                v.memset(wqk[:, :, :, :], 0.0)
                v.memset(M[:, :, :, :, :], 0.0)
                v.memset(wv[:, :, :], 0.0).then_inc(*cleared.one())
                v.wait_ge(*cleared.after(0))
                v.memset(wqk[C:C + 1, 2, :, D:D + 1], -1.0)
                v.memset(wv[C:C + 1, :, D:D + 1], 1.0).then_inc(*zeroed.one())
                p.memsets(v)
                v.wait_ge(*p.memset_done.after(0))
                v.wait_ge(*p.const_loaded.after(0))

                def link(ins):
                    ins.then_inc(*vec.one())
                    v.wait_ge(*vec.latest(i))

                def rotate(k, dst, sig):
                    v.wait_ge(*r_done.after(i, 2 * k))
                    v.tensor_tensor(t1[:, :, :], pR[:, 0, 0:2 * T].rearrange("c (b t) -> c b t", b=2),
                                    bcm(cs[:, 0, :], 1, 2), ALU.mult)
                    v.wait_ge(*r_done.after(i, 2 * k + 1))
                    link(v.tensor_tensor(t2[:, :, :], pR[:, 1, 0:2 * T].rearrange("c (b t) -> c b t", b=2),
                                         bcm(cs[:, 1, :], 1, 2), ALU.mult))
                    v.tensor_tensor(dst, t1[:, :, :], t2[:, :, :], ALU.add).then_inc(*sig.one())

                with v.Fori(0, PAIRS) as i:
                    v.wait_ge(*p.loaded.after(i))
                    norm.center(v, i, g4(X[:, :, :, :]), vec)
                    norm.scale(v, i, 0, norm.xc[:, :, :], g4(xn[:, :, :, :]), 1e-5, vec).then_inc(
                        *norm.centered.one())
                    link(norm.scale(v, i, 1, g4(xn[:, :, :, :]), r1[:, :, :], 1e-6, vec))
                    v.wait_ge(*p.stored.before(i))
                    v.tensor_tensor(g4(p.H1[:, :, :, :]), r1[:, :, :], bcm(ln1[:, :], 1, 4), ALU.mult).then_inc(
                        *p.xn_ready.one())
                    v.wait_ge(*p.xT_done.after(i, 0))
                    v.tensor_copy(xT[0:C, :, :], pX[:, :, 0:T]).then_inc(*p.xT_ready.one())
                    rotate(0, qT[:, :, :], q_ready)
                    rotate(1, kT[:, :, :], k_ready)
                    for b in range(2):
                        for hd in range(H):
                            v.wait_ge(*s_done.after(i, b * H + hd))
                            v.tensor_tensor(SM[:, hd % 2, :], pS[:, hd, 0:LOW], maskQ[:, :], ALU.add).then_inc(
                                *vec.one())
                            v.wait_ge(*vec.latest(i))
                            v.reduce_max(M[:, 0, b, hd, D:D + 1], SM[:, hd % 2, 0:PT], AX.X)
                            v.reduce_max(M[:, 1, b, hd, D:D + 1], SM[:, hd % 2, PT:LOW], AX.X).then_inc(
                                *max_ready.one())
                    v.wait_ge(*m_done.after(i))
                    v.tensor_tensor(qmT[:, :, :], qT[:, :, :], pR[:, 0, 0:2 * T].rearrange(
                        "c (b t) -> c b t", b=2), ALU.add).then_inc(*qm_ready.one())
                    for b in range(2):
                        for hd in range(H):
                            v.wait_ge(*st_done.after(i, b * H + hd))
                            v.tensor_tensor(EX[:, b, hd, :], pS[:, hd, 0:LOW], maskK[:, :], ALU.add).then_inc(
                                *masked.one())
                    v.wait_ge(*o_done.after(i))
                    o5 = pO[:, :, 0:H * (D + 1)].rearrange("p g (h d) -> p g h d", h=H)
                    link(v.reciprocal(rden[:, :, :], o5[:, :, :, D]))
                    for t in range(2):
                        for b in range(2):
                            g = 2 * t + b
                            ins = v.tensor_tensor(of[:, t, b, :].rearrange("p (h d) -> p h d", h=H),
                                                  o5[:, g, :, 0:D], bc(rden[:, g, :], D), ALU.mult)
                    ins.then_inc(*o_ready.one())
                    v.wait_ge(*p.xT_done.after(i, 1))
                    v.tensor_copy(oT[:, :, :], pX[:, :, 0:T]).then_inc(*p.xT_ready.one())
                    v.wait_ge(*y_done.after(i))
                    v.tensor_tensor(x2[:, :, :], g4(xn[:, :, :, :]), pR[0:PT, 1, 0:4 * C].rearrange(
                        "p (g c) -> p g c", g=4), ALU.add).then_inc(*norm.centered.one())
                    v.wait_ge(*norm.centered.latest(i))
                    v.tensor_tensor(g4(H1[:, :, :, :]), g4(X[:, :, :, :]), x2[:, :, :], ALU.add).then_inc(
                        *p.h_ready.one())
                    link(norm.scale(v, i, 2, x2[:, :, :], g4(fl[:, :, :, :]), 1e-6, vec))
                    v.tensor_tensor(g4(fl[:, :, :, :]), g4(fl[:, :, :, :]), bcm(ln2[:, :], 1, 4),
                                    ALU.mult).then_inc(*fl_ready.one())
                    v.wait_ge(*flT_done.after(i))
                    v.tensor_copy(flT[:, :, :], pX[:, :, 0:T]).then_inc(*flT_ready.one())
                    v.wait_ge(*l_done.after(i))
                    pl = pR[0:PT, 0, 0:4 * E].rearrange("p (g e) -> p g e", g=4)
                    link(v.reduce_max(lsum[:, :], pl, AX.X))
                    v.tensor_tensor(lg[:, :, :], pl, bc(lsum[:, :], E), ALU.subtract).then_inc(*l_shifted.one())
                    v.wait_ge(*l_exp.after(i))
                    link(v.reduce_sum(lsum[:, :], lg[:, :, :], AX.X))
                    link(v.reciprocal(lsum[:, :], lsum[:, :]))
                    link(v.tensor_tensor(lg[:, :, :], lg[:, :, :], bc(lsum[:, :], E), ALU.mult))
                    link(rank.select(v, i, lg[:, :, :], sel[:, :, :], vec))
                    link(v.tensor_tensor(lg[:, :, :], lg[:, :, :], sel[:, :, :], ALU.mult))
                    link(v.reduce_sum(lsum[:, :], lg[:, :, :], AX.X))
                    link(v.tensor_scalar(lsum[:, :], lsum[:, :], 1e-9, None, ALU.add))
                    link(v.reciprocal(lsum[:, :], lsum[:, :]))
                    v.tensor_tensor(g4(mix[:, :, :, :]), lg[:, :, :], bc(lsum[:, :], E), ALU.mult).then_inc(
                        *mix_ready.one())


def stage_experts1(nc, A, h, hx_dram, flatT_dram, mix_dram):
    E, HID, HC = EXPERTS, 170, 85
    NCH = E * 2
    with Stage(nc, "moe1") as st:
        xT = st.sb("xT", [C, 2 * T])
        w1 = st.sb("w1", [C, E * HID])
        w3 = st.sb("w3", [C, E * HID])
        w2 = st.sb("w2", [HC, NCH, C])
        X = st.sb("X", [PT, 2, 2, C])
        H1 = st.sb("H1", [PT, 2, 2, C])
        mix = st.sb("mix", [PT, 2, 2, E])
        sl = st.sb("silu", [HC, 2, 2 * T])
        hT = st.sb("hT", [HC, NCH, 2 * T])
        Z = st.sb("Z", [PT, E, C])
        acc = st.sb("acc", [PT, 4, C])
        pA = st.psum("pA", [HC, 2, 512])
        pG = st.psum("pG", [HC, 2, 512])
        pY = st.psum("pY", [PT, 4, 512])
        const_loaded = st.event("const_loaded", dma=True)
        xT_loaded = st.event("xT_loaded", dma=True)
        loaded = st.event("loaded", dma=True)
        stored = st.event("stored", dma=True)
        gate_done = st.event("gate_done")
        silu_ready = st.event("silu_ready")
        hid_ready = st.event("hid_ready")
        y_done = st.event("y_done")
        y_used = st.event("y_used")
        vec = st.event("vec")
        h_ready = st.event("h_ready")
        with st.block() as block:
            @block.sync
            def _(sp):
                const(sp, const_loaded, w1[:, :], A["L1_ffn_w1T"])
                const(sp, const_loaded, w3[:, :], A["L1_ffn_w3T"])
                const(sp, const_loaded, w2[:, :, :], A["L1_ffn_w2T"].rearrange("(n p) c -> p n c", p=HC))
                with sp.Fori(0, PAIRS) as i:
                    sp.wait_ge(*hid_ready.before(i))
                    st.held(sp)
                    sp.dma_start(xT[:, :], flatT_dram[bass.ds(i, 1), :, :].rearrange(
                        "o c t -> (o c) t")).then_inc(*xT_loaded.one())
                    sp.wait_ge(*h_ready.before(i))
                    st.held(sp)
                    for ins in load_pair(sp, X, hx_dram, i) + load_pair(sp, mix, mix_dram, i, E):
                        ins.then_inc(*loaded.one())
                    sp.wait_ge(*h_ready.after(i))
                    st.held(sp)
                    for ins in store_pair(sp, h, H1, i):
                        ins.then_inc(*stored.one())
                sp.wait_ge(*stored.after(PAIRS - 1))

            @block.tensor
            def _(pe):
                pe.wait_ge(*const_loaded.after(0))
                with pe.Fori(0, PAIRS) as i:
                    pe.wait_ge(*xT_loaded.after(i))
                    st.held(pe)
                    for n in range(NCH):
                        if n >= 2:
                            pe.wait_ge(*hid_ready.after(i, n - 2))
                            st.held(pe)
                        cols = slice(n * HC, (n + 1) * HC)
                        pe.matmul(pA[:, n % 2, 0:2 * T], w1[:, cols], xT[:, :], start=True, stop=True)
                        pe.matmul(pG[:, n % 2, 0:2 * T], w3[:, cols], xT[:, :], start=True,
                                  stop=True).then_inc(*gate_done.one())
                    pe.wait_ge(*hid_ready.after(i))
                    for t in range(2):
                        for b in range(2):
                            g = 2 * t + b
                            pe.wait_ge(*y_used.before(i))
                            for n in range(NCH):
                                e = n // 2
                                ins = pe.matmul(pY[:, g, e * C:(e + 1) * C],
                                                hT[:, n, b * T + t * OFF:b * T + t * OFF + PT], w2[:, n, :],
                                                start=(n % 2 == 0), stop=(n % 2 == 1))
                            ins.then_inc(*y_done.one())

            @block.scalar
            def _(a):
                with a.Fori(0, PAIRS) as i:
                    for n in range(NCH):
                        a.wait_ge(*gate_done.after(i, n))
                        a.activation(sl[:, n % 2, :], pA[:, n % 2, 0:2 * T], ACT.Silu).then_inc(*silu_ready.one())

            @block.vector
            def _(v):
                v.wait_ge(*const_loaded.after(0))
                with v.Fori(0, PAIRS) as i:
                    for n in range(NCH):
                        v.wait_ge(*silu_ready.after(i, n))
                        v.tensor_tensor(hT[:, n, :], sl[:, n % 2, :], pG[:, n % 2, 0:2 * T], ALU.mult).then_inc(
                            *hid_ready.one())
                    v.wait_ge(*loaded.after(i))
                    for t in range(2):
                        for b in range(2):
                            g = 2 * t + b
                            v.wait_ge(*y_done.after(i, g))
                            combine(v, i, pY[:, g, :], mix[:, t, b, :], Z, acc[:, g, :], vec).then_inc(
                                *y_used.one())
                            v.wait_ge(*y_used.latest(i))
                    v.wait_ge(*stored.before(i))
                    v.tensor_tensor(g4(H1[:, :, :, :]), acc[:, :, :], g4(X[:, :, :, :]), ALU.add).then_inc(
                        *h_ready.one())


def stage_attention2(nc, A, h):
    TH, HEADS, W = T // 3, 3, 192
    WC = W // 2
    SCALE = C ** -0.5
    with Stage(nc, "att2") as st:
        p = Pair(st, tiles=3, rows=TH)
        X, xn, xT, norm, vec, H1 = p.X, p.xn, p.xT, p.norm, p.vec, p.H1
        we = st.sb("we", [C + 1, HEADS, W])
        wo = st.sb("wo", [WC, 2, C])
        bo = st.sb("bo", [TH, C])
        qk = st.sb("qk", [WC, 2, 2, 2 * TH])
        V = st.sb("V", [TH, 2, W])
        nb = st.sb("nb", [TH, 2])
        den = st.sb("den", [TH, HEADS, 2])
        P = st.sb("P", [TH, 2, TH])
        PTr = st.sb("PTr", [TH, 2, TH])
        oT = st.sb("oT", [WC, 2, 2, TH])
        res = st.sb("res", [TH, HEADS, 2, C])
        pX = st.psum("pX", [C, 2, 256])
        pQ = st.psum("pQ", [WC, 2, 512])
        pV = st.psum("pV", [TH, 2, W])
        pS = st.psum("pS", [TH, 2, TH])
        pP = st.psum("pP", [TH, 2, TH])
        pO = st.psum("pO", [WC, 2, 2, TH])
        pY = st.psum("pY", [TH, HEADS, 2, C])
        qk_done = st.event("qk_done")
        qk_ready = st.event("qk_ready")
        v_done = st.event("v_done")
        v_ready = st.event("v_ready")
        s_done = st.event("s_done")
        max_ready = st.event("max_ready")
        exp_ready = st.event("exp_ready")
        pt_done = st.event("pt_done")
        pt_ready = st.event("pt_ready")
        o_done = st.event("o_done")
        oT_ready = st.event("oT_ready")
        y_done = st.event("y_done")

        def thirds(dram, i):
            d = dram[bass.ds(i * 2, 2)]
            return [bass.AP(d.tensor, d.offset + j * TH * C, [[C, TH], [T * C, 2], [1, C]]) for j in range(3)]
        with st.block() as block:
            @block.sync
            def _(sp):
                cl = p.const_loaded
                const(sp, cl, p.ident[:, :], A["const_ident"])
                const(sp, cl, we[0:C, :, :], A["L2_attn_W_embedT"].rearrange("n c w -> c n w"))
                const(sp, cl, we[C:C + 1, :, :], row(A["L2_attn_b_embed"]))
                const(sp, cl, wo[:, :, :], A["L2_attn_W_outT"].rearrange("(k w) c -> w k c", k=2))
                const(sp, cl, bo[:, :], every_row(A["L2_attn_b_out"], TH))
                with sp.Fori(0, PAIRS) as i:
                    sp.wait_ge(*p.h_ready.before(i))
                    st.held(sp)
                    for j, src in enumerate(thirds(h, i)):
                        sp.dma_start(X[:, j, :, :], src).then_inc(*p.loaded.one())
                    sp.wait_ge(*p.h_ready.after(i))
                    st.held(sp)
                    for j, dst in enumerate(thirds(h, i)):
                        sp.dma_start(dst, H1[:, j, :, :]).then_inc(*p.stored.one())
                sp.wait_ge(*p.stored.after(PAIRS - 1))

            @block.gpsimd
            def _(g):
                g.wait_ge(*p.memset_done.after(0))
                with g.Fori(0, PAIRS) as i:
                    norm.power(g, i, 0)

            @block.tensor
            def _(pe):
                pe.wait_ge(*p.const_loaded.after(0))
                pe.wait_ge(*p.memset_done.after(0))
                with pe.Fori(0, PAIRS) as i:
                    pe.wait_ge(*p.xn_ready.after(i))
                    st.held(pe)
                    for j in range(3):
                        for b in range(2):
                            ins = pe.transpose(pX[:, b, j * TH:(j + 1) * TH], xn[:, j, b, :],
                                               p.ident[0:TH, 0:TH])
                    ins.then_inc(*p.xT_done.one())
                    pe.wait_ge(*p.xT_ready.after(i))
                    for n in range(HEADS):
                        if n:
                            pe.wait_ge(*qk_ready.after(i, n - 1))
                        st.held(pe)
                        for k in range(2):
                            ins = pe.matmul(pQ[:, k, 0:4 * TH], we[:, n, k * WC:(k + 1) * WC],
                                            xT[:, :, 0:2 * TH], start=True, stop=True)
                        ins.then_inc(*qk_done.one())
                        if n:
                            pe.wait_ge(*v_ready.after(i, n - 1))
                        st.held(pe)
                        for b in range(2):
                            ins = pe.matmul(pV[:, b, :], xT[:, b, 2 * TH:T], we[:, n, :], start=True, stop=True)
                        ins.then_inc(*v_done.one())
                        pe.wait_ge(*qk_ready.after(i, n))
                        st.held(pe)
                        for b in range(2):
                            for k in range(2):
                                ins = pe.matmul(pS[:, b, :], qk[:, k, b, 0:TH], qk[:, k, b, TH:2 * TH],
                                                start=(k == 0), stop=(k == 1))
                        ins.then_inc(*s_done.one())
                        pe.wait_ge(*exp_ready.after(i, 2 * n + 1))
                        st.held(pe)
                        for b in range(2):
                            ins = pe.transpose(pP[:, b, :], P[:, b, :], p.ident[0:TH, 0:TH])
                        ins.then_inc(*pt_done.one())
                        pe.wait_ge(*pt_ready.after(i, n))
                        pe.wait_ge(*v_ready.after(i, n))
                        st.held(pe)
                        for k in range(2):
                            for b in range(2):
                                ins = pe.matmul(pO[:, k, b, :], V[:, b, k * WC:(k + 1) * WC], PTr[:, b, :],
                                                start=True, stop=True)
                        ins.then_inc(*o_done.one())
                        pe.wait_ge(*oT_ready.after(i, n))
                        st.held(pe)
                        for b in range(2):
                            for k in range(2):
                                ins = pe.matmul(pY[:, n, b, :], oT[:, k, b, :], wo[:, k, :], start=(k == 0),
                                                stop=(k == 1))
                        ins.then_inc(*y_done.one())

            @block.scalar
            def _(a):
                with a.Fori(0, PAIRS) as i:
                    norm.square(a, i, 0, norm.xc[:, :, :])
                    for n in range(HEADS):
                        a.wait_ge(*v_done.after(i, n))
                        a.activation(V[:, :, :], pV[:, :, :], ACT.Copy).then_inc(*v_ready.one())
                        a.wait_ge(*max_ready.after(i, n))
                        for b in range(2):
                            a.activation(P[:, b, :], pS[:, b, :], ACT.Exp, bias=nb[:, b:b + 1], scale=SCALE,
                                         accum_out=den[:, n, b:b + 1]).then_inc(*exp_ready.one())
                        a.wait_ge(*o_done.after(i, n))
                        a.activation(oT[:, :, :, :], pO[:, :, :, :], ACT.Copy).then_inc(*oT_ready.one())

            @block.vector
            def _(v):
                p.memsets(v)
                v.wait_ge(*p.memset_done.after(0))
                v.wait_ge(*p.const_loaded.after(0))

                def link(ins):
                    ins.then_inc(*vec.one())
                    v.wait_ge(*vec.latest(i))
                with v.Fori(0, PAIRS) as i:
                    p.normalise(v, i)
                    v.wait_ge(*p.xT_done.after(i))
                    v.tensor_copy(xT[0:C, :, :], pX[:, :, 0:T]).then_inc(*p.xT_ready.one())
                    for n in range(HEADS):
                        v.wait_ge(*qk_done.after(i, n))
                        v.tensor_copy(qk[:, :, :, :].rearrange("p k b t -> p k (b t)"),
                                      pQ[:, :, 0:4 * TH]).then_inc(*qk_ready.one())
                        v.wait_ge(*s_done.after(i, n))
                        link(v.reduce_max(nb[:, :], pS[:, :, :], AX.X))
                        v.tensor_scalar(nb[:, :], nb[:, :], -SCALE, None, ALU.mult).then_inc(*max_ready.one())
                        v.wait_ge(*pt_done.after(i, n))
                        v.tensor_copy(PTr[:, :, :], pP[:, :, :]).then_inc(*pt_ready.one())
                    v.wait_ge(*y_done.after(i))
                    link(v.reciprocal(den[:, :, :], den[:, :, :]))
                    link(v.tensor_tensor(g4(res[:, :, :, :]), g4(pY[:, :, :, :]),
                                         bc(den[:, :, :].rearrange("p n b -> p (n b)"), C), ALU.mult))
                    link(v.tensor_tensor(g4(res[:, :, :, :]), g4(res[:, :, :, :]), g4(xn[:, :, :, :]), ALU.add))
                    link(v.tensor_tensor(g4(res[:, :, :, :]), g4(res[:, :, :, :]), bcm(bo[:, :], 1, 6), ALU.add))
                    v.wait_ge(*p.stored.before(i))
                    v.tensor_tensor(g4(H1[:, :, :, :]), g4(res[:, :, :, :]), g4(X[:, :, :, :]), ALU.add).then_inc(
                        *p.h_ready.one())


def stage_depths2(nc, A, h):
    F, KEEP = 256, int(0.5 * T) - 1
    with Stage(nc, "mod2") as st:
        p = Pair(st)
        X, xn, xT, norm, vec, H1 = p.X, p.xn, p.xT, p.norm, p.vec, p.H1
        w1 = st.sb("w1", [C + 1, F])
        w2 = st.sb("w2", [128, 2, C])
        b2 = st.sb("b2", [1, C])
        ones = st.sb("ones", [1, PT])
        wr = st.sb("wr", [C + 1, PT])
        earlier = st.sb("earlier", [PT, 2, T])
        hT = st.sb("hT", [128, 2, 2 * T])
        W = st.sb("W", [PT, 2, T])
        junk = st.sb("junk", [PT, T])
        wn = st.sb("wn", [PT, 4])
        gt = st.sb("gt", [PT, 4])
        eq = st.sb("eq", [PT, 4])
        res = st.sb("res", [PT, 4, C])
        pX = st.psum("pX", [C, 2, 256])
        pW = st.psum("pW", [PT, 512])
        pH = st.psum("pH", [128, 2, 512])
        pY = st.psum("pY", [PT, 4, C])
        w_done = st.event("w_done")
        w_ready = st.event("w_ready")
        hid_done = st.event("hid_done")
        hid_ready = st.event("hid_ready")
        y_done = st.event("y_done")
        with st.block() as block:
            @block.sync
            def _(sp):
                cl = p.const_loaded
                const(sp, cl, p.ident[:, :], A["const_ident"])
                const(sp, cl, w1[0:C, :], A["L2_ffn_w1"])
                const(sp, cl, w1[C:C + 1, :], row(A["L2_ffn_b1"]))
                const(sp, cl, w2[:, :, :], A["L2_ffn_w2"].rearrange("(k f) c -> f k c", k=2))
                const(sp, cl, b2[:, :], row(A["L2_ffn_b2"]))
                const(sp, cl, wr[0:C, :], A["wr_wide"])
                const(sp, cl, wr[C:C + 1, :], A["br_wide"])
                const(sp, cl, earlier[:, :, :], A["const_before"])
                with sp.Fori(0, PAIRS) as i:
                    sp.wait_ge(*p.h_ready.before(i))
                    st.held(sp)
                    for ins in load_pair(sp, X, h, i):
                        ins.then_inc(*p.loaded.one())
                    sp.wait_ge(*p.h_ready.after(i))
                    st.held(sp)
                    for ins in store_pair(sp, h, H1, i):
                        ins.then_inc(*p.stored.one())
                sp.wait_ge(*p.stored.after(PAIRS - 1))

            @block.gpsimd
            def _(g):
                g.wait_ge(*p.memset_done.after(0))
                with g.Fori(0, PAIRS) as i:
                    norm.power(g, i, 0)

            @block.tensor
            def _(pe):
                pe.wait_ge(*p.const_loaded.after(0))
                pe.wait_ge(*p.memset_done.after(0))
                with pe.Fori(0, PAIRS) as i:
                    pe.wait_ge(*p.xn_ready.after(i))
                    st.held(pe)
                    transpose_rows(pe, pX, xn, p.ident).then_inc(*p.xT_done.one())
                    pe.wait_ge(*p.xT_ready.after(i))
                    pe.matmul(pW[:, 0:2 * T], wr[:, :], xT[:, :, :], start=True, stop=True).then_inc(*w_done.one())
                    for k in range(2):
                        pe.matmul(pH[:, k, 0:2 * T], w1[:, k * 128:(k + 1) * 128], xT[:, :, :], start=True,
                                  stop=True).then_inc(*hid_done.one())
                    pe.wait_ge(*hid_ready.after(i))
                    st.held(pe)
                    for t in range(2):
                        for b in range(2):
                            g = 2 * t + b
                            pe.matmul(pY[:, g, :], ones[:, :], b2[:, :], start=True, stop=False)
                            for k in range(2):
                                ins = pe.matmul(pY[:, g, :], hT[:, k, b * T + t * OFF:b * T + t * OFF + PT],
                                                w2[:, k, :], start=False, stop=(k == 1))
                    ins.then_inc(*y_done.one())

            @block.scalar
            def _(a):
                with a.Fori(0, PAIRS) as i:
                    norm.square(a, i, 0, norm.xc[:, :, :])
                    a.wait_ge(*w_done.after(i))
                    a.activation(W[:, :, :].rearrange("p b t -> p (b t)"), pW[:, 0:2 * T], ACT.Copy).then_inc(
                        *w_ready.one())
                    for k in range(2):
                        a.wait_ge(*hid_done.after(i, k))
                        a.activation(hT[:, k, :], pH[:, k, 0:2 * T], ACT.Gelu_apprx_tanh).then_inc(
                            *hid_ready.one())

            @block.vector
            def _(v):
                v.memset(ones[:, :], 1.0)
                p.memsets(v)
                v.wait_ge(*p.memset_done.after(0))
                v.wait_ge(*p.const_loaded.after(0))

                def link(ins):
                    ins.then_inc(*vec.one())
                    v.wait_ge(*vec.latest(i))
                with v.Fori(0, PAIRS) as i:
                    p.normalise(v, i)
                    v.wait_ge(*p.xT_done.after(i))
                    v.tensor_copy(xT[0:C, :, :], pX[:, :, 0:T]).then_inc(*p.xT_ready.one())
                    v.wait_ge(*w_ready.after(i))
                    for t in range(2):
                        for b in range(2):
                            link(v.tensor_tensor_reduce(junk[:, 0:PT], W[:, b, t * OFF:t * OFF + PT],
                                                        p.ident[0:PT, 0:PT], 1.0, 0.0, ALU.mult, ALU.add,
                                                        wn[:, 2 * t + b:2 * t + b + 1]))
                    for t in range(2):
                        for b in range(2):
                            g = 2 * t + b
                            link(v.tensor_scalar(junk[:, :], W[:, b, :], wn[:, g:g + 1], 0.0, ALU.is_gt, ALU.add,
                                                 accum_out=gt[:, g:g + 1]))
                            link(v.scalar_tensor_tensor(out=junk[:, :], in0=W[:, b, :], scalar=wn[:, g:g + 1],
                                                        in1=earlier[:, t, :], op0=ALU.is_equal, op1=ALU.mult,
                                                        accum_out=eq[:, g:g + 1]))
                    link(v.tensor_tensor(gt[:, :], gt[:, :], eq[:, :], ALU.add))
                    link(v.tensor_scalar(gt[:, :], gt[:, :], float(KEEP), None, ALU.is_lt))
                    link(v.tensor_tensor(gt[:, :], gt[:, :], wn[:, :], ALU.mult))
                    v.wait_ge(*y_done.after(i))
                    link(v.tensor_tensor(res[:, :, :], pY[:, :, :], bc(gt[:, :], C), ALU.mult))
                    link(v.tensor_tensor(res[:, :, :], res[:, :, :], g4(xn[:, :, :, :]), ALU.add))
                    v.wait_ge(*p.stored.before(i))
                    v.tensor_tensor(g4(H1[:, :, :, :]), res[:, :, :], g4(X[:, :, :, :]), ALU.add).then_inc(
                        *p.h_ready.one())


def stage_attention3(nc, A, h):
    H, D, KNN = 8, 64, 32
    HP = H // 2
    SCALE = D ** -0.5
    SELF, TAKEN = -3.4028234663852886e38, -3.0e38
    with Stage(nc, "att3") as st:
        p = Pair(st)
        X, xn, xT, norm, vec, H1 = p.X, p.xn, p.xT, p.norm, p.vec, p.H1
        wqkv = st.sb("wqkv", [C, 3, H * D])
        wo = st.sb("wo", [128, HP, C])
        bo = st.sb("bo", [PT, C])
        minus = st.sb("minus", [C, PT])
        diag = st.sb("diag", [PT, 2, T])
        xT2 = st.sb("xT2", [C, 2, T])
        xsq = st.sb("xsq", [C, 2, T])
        x2 = st.sb("x2", [PT, 4])
        sq = st.sb("sq", [PT, 4, C])
        near = st.sb("near", [PT, 4, T])
        top8 = st.sb("top8", [PT, 4, 8])
        mask = st.sb("mask", [PT, 4, T])
        qT = st.sb("qT", [128, HP, 2, T])
        kT = st.sb("kT", [128, HP, 2, T])
        V = st.sb("V", [PT, 4, H * D])
        SM = st.sb("SM", [PT, 2, 2, T])
        nb = st.sb("nb", [PT, 2, 2])
        P = st.sb("P", [PT, 2, 2, T])
        den = st.sb("den", [PT, 2, 2, H])
        PTr = st.sb("PTr", [PT, 2, 2, T])
        of = st.sb("of", [PT, 4, H * D])
        oT = st.sb("oT", [128, HP, 2, T])
        res = st.sb("res", [PT, 4, C])
        pX = st.psum("pX", [C, 2, 256])
        pQ = st.psum("pQ", [128, 1, 512])
        pS = st.psum("pS", [PT, 2, 512])
        pP = st.psum("pP", [PT, 2, 512])
        pO = st.psum("pO", [PT, 2, 512])
        d_done = st.event("d_done")
        sq_ready = st.event("sq_ready")
        near_ready = st.event("near_ready")
        qk_done = st.event("qk_done")
        qk_ready = st.event("qk_ready")
        v_done = st.event("v_done")
        v_ready = st.event("v_ready")
        s_done = st.event("s_done")
        max_ready = st.event("max_ready")
        exp_ready = st.event("exp_ready")
        pt_done = st.event("pt_done")
        pt_ready = st.event("pt_ready")
        o_done = st.event("o_done")
        o_ready = st.event("o_ready")
        oT_done = st.event("oT_done")
        oT_ready = st.event("oT_ready")
        y_done = st.event("y_done")
        with st.block() as block:
            @block.sync
            def _(sp):
                cl = p.const_loaded
                const(sp, cl, p.ident[:, :], A["const_ident"])
                const(sp, cl, wqkv[:, :, :], A["L3_attn_Wqkv"].rearrange("c (k n) -> c k n", k=3))
                const(sp, cl, wo[:, :, :], A["L3_attn_Wout"].rearrange("(k n) c -> n k c", k=HP))
                const(sp, cl, bo[:, :], every_row(A["L3_attn_bout"], PT))
                const(sp, cl, diag[:, :, :], A["const_self"])
                with sp.Fori(0, PAIRS) as i:
                    sp.wait_ge(*p.h_ready.before(i))
                    st.held(sp)
                    for ins in load_pair(sp, X, h, i):
                        ins.then_inc(*p.loaded.one())
                    sp.wait_ge(*p.h_ready.after(i))
                    st.held(sp)
                    for ins in store_pair(sp, h, H1, i):
                        ins.then_inc(*p.stored.one())
                sp.wait_ge(*p.stored.after(PAIRS - 1))

            @block.gpsimd
            def _(g):
                g.wait_ge(*p.memset_done.after(0))
                with g.Fori(0, PAIRS) as i:
                    norm.power(g, i, 0)

            @block.tensor
            def _(pe):
                pe.wait_ge(*p.const_loaded.after(0))
                pe.wait_ge(*p.memset_done.after(0))
                with pe.Fori(0, PAIRS) as i:
                    pe.wait_ge(*p.xn_ready.after(i))
                    st.held(pe)
                    transpose_rows(pe, pX, xn, p.ident).then_inc(*p.xT_done.one())
                    pe.wait_ge(*p.xT_ready.after(i))
                    pe.wait_ge(*sq_ready.after(i))
                    for b in range(2):
                        st.held(pe)
                        for t in range(2):
                            pe.matmul(pS[:, b, t * T:t * T + T], xT2[:, b, t * OFF:t * OFF + PT], xT[0:C, b, :],
                                      start=True, stop=False)
                            ins = pe.matmul(pS[:, b, t * T:t * T + T], minus[:, :], xsq[:, b, :],
                                            start=False, stop=True)
                        ins.then_inc(*d_done.one())
                    for n in range(2 * HP):
                        if n:
                            pe.wait_ge(*qk_ready.after(i, n - 1))
                            st.held(pe)
                        k, hp = n // HP, n % HP
                        pe.matmul(pQ[:, 0, 0:2 * T], wqkv[:, k, hp * 128:(hp + 1) * 128], xT[0:C, :, :],
                                  start=True, stop=True).then_inc(*qk_done.one())
                    for g in range(4):
                        t, b = g // 2, g % 2
                        if g >= 2:
                            pe.wait_ge(*v_ready.after(i, g - 2))
                            st.held(pe)
                        pe.matmul(pO[:, g % 2, :], xT[0:C, b, t * OFF:t * OFF + PT], wqkv[:, 2, :], start=True,
                                  stop=True).then_inc(*v_done.one())
                    pe.wait_ge(*qk_ready.after(i))
                    pe.wait_ge(*near_ready.after(i))
                    pe.wait_ge(*v_ready.after(i))
                    for b in range(2):
                        if b:
                            pe.wait_ge(*o_ready.after(i, b - 1))
                        for step in range(H + 1):
                            if step < H:
                                s = b * H + step
                                r, hp = 64 * (step % 2), step // 2
                                if s >= 2:
                                    pe.wait_ge(*max_ready.after(i, s - 2))
                                st.held(pe)
                                for t in range(2):
                                    ins = pe.matmul(pS[:, s % 2, t * T:t * T + T],
                                                    qT[r:r + D, hp, b, t * OFF:t * OFF + PT],
                                                    kT[r:r + D, hp, b, :], start=True, stop=True,
                                                    tile_position=(r, 0))
                                ins.then_inc(*s_done.one())
                            if step >= 1:
                                s, hd = b * H + step - 1, step - 1
                                pe.wait_ge(*exp_ready.after(i, 2 * s + 1))
                                if s >= 2:
                                    pe.wait_ge(*pt_ready.after(i, s - 2))
                                st.held(pe)
                                for t in range(2):
                                    for kt in range(2):
                                        ins = pe.transpose(
                                            pP[:, s % 2, kt * T + t * OFF:kt * T + t * OFF + ROWS[t]],
                                            P[0:ROWS[t], s % 2, t, kt * OFF:kt * OFF + PT],
                                            p.ident[0:ROWS[t], 0:ROWS[t]])
                                ins.then_inc(*pt_done.one())
                                pe.wait_ge(*pt_ready.after(i, s))
                                st.held(pe)
                                for t in range(2):
                                    for kt in range(2):
                                        ins = pe.matmul(pO[:, t, hd * D:(hd + 1) * D],
                                                        PTr[0:ROWS[kt], s % 2, kt, t * OFF:t * OFF + PT],
                                                        V[0:ROWS[kt], 2 * kt + b, hd * D:(hd + 1) * D],
                                                        start=(kt == 0), stop=(kt == 1))
                                if hd == H - 1:
                                    ins.then_inc(*o_done.one())
                    pe.wait_ge(*o_ready.after(i))
                    for hp in range(HP):
                        if hp:
                            pe.wait_ge(*oT_ready.after(i, hp - 1))
                        st.held(pe)
                        for b in range(2):
                            for t in range(2):
                                ins = pe.transpose(pQ[:, 0, b * T + t * OFF:b * T + t * OFF + ROWS[t]],
                                                   of[0:ROWS[t], 2 * t + b, hp * 128:(hp + 1) * 128],
                                                   p.ident[0:ROWS[t], 0:ROWS[t]])
                        ins.then_inc(*oT_done.one())
                    pe.wait_ge(*oT_ready.after(i))
                    st.held(pe)
                    for g in range(4):
                        t, b = g // 2, g % 2
                        for hp in range(HP):
                            ins = pe.matmul(pO[:, 0, g * C:(g + 1) * C], oT[:, hp, b, t * OFF:t * OFF + PT],
                                            wo[:, hp, :], start=(hp == 0), stop=(hp == HP - 1))
                    ins.then_inc(*y_done.one())

            @block.scalar
            def _(a):
                with a.Fori(0, PAIRS) as i:
                    norm.square(a, i, 0, norm.xc[:, :, :])
                    a.wait_ge(*p.xT_ready.after(i))
                    a.activation(xT2[:, :, :], xT[0:C, :, :], ACT.Copy, scale=2.0)
                    a.activation(xsq[:, :, :], xT[0:C, :, :], ACT.Square).then_inc(*sq_ready.one())
                    a.wait_ge(*p.xn_ready.after(i))
                    a.activation(sq[:, :, :], g4(xn[:, :, :, :]), ACT.Square).then_inc(*sq_ready.one())
                    for n in range(2 * HP):
                        k, hp = n // HP, n % HP
                        a.wait_ge(*qk_done.after(i, n))
                        a.activation((kT if k else qT)[:, hp, :, :].rearrange("c b t -> c (b t)"),
                                     pQ[:, 0, 0:2 * T], ACT.Copy).then_inc(*qk_ready.one())
                    for g in range(4):
                        a.wait_ge(*v_done.after(i, g))
                        a.activation(V[:, g, :], pO[:, g % 2, :], ACT.Copy).then_inc(*v_ready.one())
                    for s in range(2 * H):
                        b, hd = s // H, s % H
                        a.wait_ge(*max_ready.after(i, s))
                        if s >= 2:
                            a.wait_ge(*pt_done.after(i, s - 2))
                        for t in range(2):
                            a.activation(P[:, s % 2, t, :], SM[:, s % 2, t, :], ACT.Exp,
                                         bias=nb[:, s % 2, t:t + 1], scale=SCALE,
                                         accum_out=den[:, b, t, hd:hd + 1]).then_inc(*exp_ready.one())
                        a.wait_ge(*pt_done.after(i, s))
                        a.activation(PTr[:, s % 2, :, :].rearrange("p k t -> p (k t)"), pP[:, s % 2, 0:2 * T],
                                     ACT.Copy).then_inc(*pt_ready.one())
                    for hp in range(HP):
                        a.wait_ge(*oT_done.after(i, hp))
                        a.activation(oT[:, hp, :, :].rearrange("c b t -> c (b t)"), pQ[:, 0, 0:2 * T],
                                     ACT.Copy).then_inc(*oT_ready.one())

            @block.vector
            def _(v):
                v.memset(minus[:, :], -1.0)
                p.memsets(v)
                v.wait_ge(*p.memset_done.after(0))
                v.wait_ge(*p.const_loaded.after(0))

                def link(ins):
                    ins.then_inc(*vec.one())
                    v.wait_ge(*vec.latest(i))
                with v.Fori(0, PAIRS) as i:
                    p.normalise(v, i)
                    v.wait_ge(*p.xT_done.after(i))
                    v.tensor_copy(xT[0:C, :, :], pX[:, :, 0:T]).then_inc(*p.xT_ready.one())
                    v.wait_ge(*sq_ready.after(i))
                    link(v.reduce_sum(x2[:, :], sq[:, :, :], AX.X))
                    for b in range(2):
                        for t in range(2):
                            g = 2 * t + b
                            v.wait_ge(*d_done.after(i, b))
                            v.scalar_tensor_tensor(out=near[:, g, :], in0=pS[:, b, t * T:t * T + T],
                                                   scalar=x2[:, g:g + 1], in1=diag[:, t, :], op0=ALU.subtract,
                                                   op1=ALU.add).then_inc(*vec.one())
                            v.wait_ge(*vec.latest(i))
                    for turn in range(KNN // 8):
                        st.held(v)
                        for g in range(4):
                            ins = v.max(top8[:, g, :], near[:, g, :])
                        link(ins)
                        st.held(v)
                        for g in range(4):
                            ins = v.match_replace(near[:, g, :], top8[:, g, :], near[:, g, :], TAKEN)
                        link(ins)
                    v.tensor_scalar(mask[:, :, :], near[:, :, :], TAKEN, NEG, ALU.not_equal,
                                    ALU.mult).then_inc(*near_ready.one())
                    v.wait_ge(*near_ready.after(i))
                    for s in range(2 * H):
                        b = s // H
                        v.wait_ge(*s_done.after(i, s))
                        if s >= 2:
                            v.wait_ge(*exp_ready.after(i, 2 * (s - 2) + 1))
                        link(v.tensor_tensor(SM[:, s % 2, :, :], pS[:, s % 2, 0:2 * T].rearrange(
                            "p (t n) -> p t n", t=2), mask[:, b:4:2, :], ALU.add))
                        link(v.reduce_max(nb[:, s % 2, :], SM[:, s % 2, :, :], AX.X))
                        v.tensor_scalar(nb[:, s % 2, :], nb[:, s % 2, :], -SCALE, None, ALU.mult).then_inc(
                            *max_ready.one())
                        if s % H == H - 1:
                            v.wait_ge(*o_done.after(i, b))
                            link(v.reciprocal(den[:, b, :, :], den[:, b, :, :]))
                            for t in range(2):
                                ins = v.tensor_tensor(of[:, 2 * t + b, :].rearrange("p (h d) -> p h d", h=H),
                                                      pO[:, t, :].rearrange("p (h d) -> p h d", h=H),
                                                      bc(den[:, b, t, :], D), ALU.mult)
                            ins.then_inc(*o_ready.one())
                    v.wait_ge(*y_done.after(i))
                    link(v.tensor_tensor(res[:, :, :], pO[:, 0, 0:4 * C].rearrange("p (g c) -> p g c", g=4),
                                         bcm(bo[:, :], 1, 4), ALU.add))
                    v.wait_ge(*p.stored.before(i))
                    v.tensor_tensor(g4(H1[:, :, :, :]), res[:, :, :], g4(X[:, :, :, :]), ALU.add).then_inc(
                        *p.h_ready.one())


def stage_switch3(nc, A, h, out):
    E, F = EXPERTS, 256
    NCH = E * 2
    ROOM = max(1, math.ceil(1.25 * BATCH * T / E))
    BIG = 3.4028234663852886e38
    with Stage(nc, "sw3") as st:
        p = Pair(st)
        X, xn, xT, norm, vec, H1 = p.X, p.xn, p.xT, p.norm, p.vec, p.H1
        w1 = st.sb("w1", [C + 1, E * F])
        w2 = st.sb("w2", [128, NCH, C])
        b2 = st.sb("b2", [1, E * C])
        wg = st.sb("wg", [C + 1, E])
        ones = st.sb("ones", [128, 128])
        upto = st.sb("upto", [PT, PT])
        lg = st.sb("lg", [PT, 4, E])
        s1 = st.sb("s1", [PT, 4])
        prb = st.sb("prb", [PT, 4])
        hot = st.sb("hot", [PT, 4, E])
        base = st.sb("base", [PT, E])
        coef = st.sb("coef", [PT, 4, E])
        hT = st.sb("hT", [128, NCH, 2 * T])
        Z = st.sb("Z", [PT, E, C])
        acc = st.sb("acc", [PT, 2, 2, C])
        ok = st.sb("ok", [PT, 2, 2, C])
        fixed = st.sb("fixed", [PT, 2, 2, C])
        rank = Rank(st, PT, 4, 1)
        pX = st.psum("pX", [C, 2, 256])
        pH = st.psum("pH", [128, 2, 512])
        pL = st.psum("pL", [PT, 4, E])
        pC = st.psum("pC", [PT, 5, E])
        pY = st.psum("pY", [PT, 3, 512])
        l_done = st.event("l_done")
        l_shifted = st.event("l_shifted")
        l_exp = st.event("l_exp")
        hot_ready = st.event("hot_ready")
        c_done = st.event("c_done")
        hid_done = st.event("hid_done")
        hid_ready = st.event("hid_ready")
        y_done = st.event("y_done")
        y_used = st.event("y_used")
        with st.block() as block:
            @block.sync
            def _(sp):
                cl = p.const_loaded
                const(sp, cl, p.ident[:, :], A["const_ident"])
                const(sp, cl, w1[0:C, :], A["L3_ffn_w1T"])
                const(sp, cl, w1[C:C + 1, :], row(A["L3_ffn_b1"].rearrange("e f -> (e f)")))
                const(sp, cl, w2[:, :, :], A["L3_ffn_w2"].rearrange("e (k f) c -> f (e k) c", k=2))
                const(sp, cl, b2[:, :], row(A["L3_ffn_b2"].rearrange("e c -> (e c)")))
                const(sp, cl, wg[0:C, :], A["L3_ffn_gate_w"])
                const(sp, cl, wg[C:C + 1, :], row(A["L3_ffn_gate_b"]))
                const(sp, cl, upto[:, :], A["const_upto"])
                const(sp, cl, rank.earlier[:, :], every_row(A["const_earlier"], PT))
                with sp.Fori(0, PAIRS) as i:
                    sp.wait_ge(*p.h_ready.before(i))
                    st.held(sp)
                    for ins in load_pair(sp, X, h, i):
                        ins.then_inc(*p.loaded.one())
                    sp.wait_ge(*p.h_ready.after(i))
                    st.held(sp)
                    for ins in store_pair(sp, out, H1, i):
                        ins.then_inc(*p.stored.one())
                sp.wait_ge(*p.stored.after(PAIRS - 1))

            @block.gpsimd
            def _(g):
                g.wait_ge(*p.memset_done.after(0))
                with g.Fori(0, PAIRS) as i:
                    norm.power(g, i, 0)

            @block.tensor
            def _(pe):
                pe.wait_ge(*p.const_loaded.after(0))
                pe.wait_ge(*p.memset_done.after(0))
                with pe.Fori(0, PAIRS) as i:
                    pe.wait_ge(*p.xn_ready.after(i))
                    st.held(pe)
                    transpose_rows(pe, pX, xn, p.ident).then_inc(*p.xT_done.one())
                    pe.wait_ge(*p.xT_ready.after(i))
                    st.held(pe)
                    for b in range(2):
                        for t in range(2):
                            ins = pe.matmul(pL[:, 2 * b + t, :], xT[:, b, t * OFF:t * OFF + PT], wg[:, :],
                                            start=True, stop=True)
                    ins.then_inc(*l_done.one())
                    for n in range(NCH):
                        if n >= 2:
                            pe.wait_ge(*hid_ready.after(i, n - 2))
                        pe.matmul(pH[:, n % 2, 0:2 * T], w1[:, n * 128:(n + 1) * 128], xT[:, :, :], start=True,
                                  stop=True).then_inc(*hid_done.one())
                    pe.wait_ge(*hot_ready.after(i))
                    st.held(pe)
                    for g in range(4):
                        for k in range(g):
                            pe.matmul(pC[:, g, :], ones[0:ROWS[k % 2], 0:PT], hot[0:ROWS[k % 2], k, :],
                                      start=(k == 0), stop=False)
                        pe.matmul(pC[:, g, :], upto[0:ROWS[g % 2], :], hot[0:ROWS[g % 2], g, :],
                                  start=(g == 0), stop=True)
                    for k in range(4):
                        ins = pe.matmul(pC[:, 4, :], ones[0:ROWS[k % 2], 0:PT], hot[0:ROWS[k % 2], k, :],
                                        start=(k == 0), stop=(k == 3))
                    ins.then_inc(*c_done.one())
                    pe.wait_ge(*hid_ready.after(i))
                    for g in range(4):
                        b, t = g // 2, g % 2
                        if g >= 3:
                            pe.wait_ge(*y_used.after(i, g - 3))
                        else:
                            pe.wait_ge(*y_used.before(i))
                        st.held(pe)
                        pe.matmul(pY[:, g % 3, :], ones[0:1, 0:PT], b2[:, :], start=True, stop=False)
                        for n in range(NCH):
                            e = n // 2
                            ins = pe.matmul(pY[:, g % 3, e * C:(e + 1) * C],
                                            hT[:, n, b * T + t * OFF:b * T + t * OFF + PT], w2[:, n, :],
                                            start=False, stop=(n == NCH - 1))
                        ins.then_inc(*y_done.one())

            @block.scalar
            def _(a):
                with a.Fori(0, PAIRS) as i:
                    norm.square(a, i, 0, norm.xc[:, :, :])
                    a.wait_ge(*l_shifted.after(i))
                    a.activation(lg[:, :, :], lg[:, :, :], ACT.Exp).then_inc(*l_exp.one())
                    for n in range(NCH):
                        a.wait_ge(*hid_done.after(i, n))
                        a.activation(hT[:, n, :], pH[:, n % 2, 0:2 * T], ACT.Relu).then_inc(*hid_ready.one())

            @block.vector
            def _(v):
                v.memset(ones[:, :], 1.0)
                v.memset(base[:, :], 0.0)
                p.memsets(v)
                v.wait_ge(*p.memset_done.after(0))
                v.wait_ge(*p.const_loaded.after(0))

                def link(ins):
                    ins.then_inc(*vec.one())
                    v.wait_ge(*vec.latest(i))
                with v.Fori(0, PAIRS) as i:
                    p.normalise(v, i)
                    v.wait_ge(*p.xT_done.after(i))
                    v.tensor_copy(xT[0:C, :, :], pX[:, :, 0:T]).then_inc(*p.xT_ready.one())
                    v.wait_ge(*l_done.after(i))
                    link(v.reduce_max(s1[:, :], pL[:, :, :], AX.X))
                    v.tensor_tensor(lg[:, :, :], pL[:, :, :], bc(s1[:, :], E), ALU.subtract).then_inc(
                        *l_shifted.one())
                    v.wait_ge(*l_exp.after(i))
                    link(v.reduce_sum(s1[:, :], lg[:, :, :], AX.X))
                    link(v.reciprocal(s1[:, :], s1[:, :]))
                    link(v.tensor_tensor(lg[:, :, :], lg[:, :, :], bc(s1[:, :], E), ALU.mult))
                    v.reduce_max(prb[:, :], lg[:, :, :], AX.X)
                    rank.select(v, i, lg[:, :, :], hot[:, :, :], vec).then_inc(*hot_ready.one())
                    v.wait_ge(*hot_ready.after(i))
                    v.wait_ge(*c_done.after(i))
                    link(v.tensor_tensor(coef[:, :, :], pC[:, 0:4, :], bcm(base[:, :], 1, 4), ALU.add))
                    link(v.tensor_scalar(coef[:, :, :], coef[:, :, :], float(ROOM), None, ALU.is_le))
                    link(v.tensor_tensor(coef[:, :, :], coef[:, :, :], hot[:, :, :], ALU.mult))
                    v.tensor_tensor(coef[:, :, :], coef[:, :, :], bc(prb[:, :], E), ALU.mult)
                    link(v.tensor_tensor(base[:, :], base[:, :], pC[:, 4, :], ALU.add))
                    for g in range(4):
                        b, t = g // 2, g % 2
                        v.wait_ge(*y_done.after(i, g))
                        combine(v, i, pY[:, g % 3, :], coef[:, g, :], Z, acc[:, t, b, :], vec).then_inc(
                            *y_used.one())
                        v.wait_ge(*y_used.latest(i))
                    y, o, f = (g4(x[:, :, :, :]) for x in (acc, ok, fixed))
                    v.memset(f, 10000.0)
                    link(v.tensor_scalar(o, y, BIG, None, ALU.is_gt))
                    st.held(v)
                    link(v.copy_predicated(y, g4(ok[:, :, :, :]).bitcast(mybir.dt.uint32), f))
                    v.memset(f, -10000.0)
                    link(v.tensor_scalar(o, y, -BIG, None, ALU.is_lt))
                    st.held(v)
                    link(v.copy_predicated(y, g4(ok[:, :, :, :]).bitcast(mybir.dt.uint32), f))
                    v.memset(f, 0.0)
                    link(v.tensor_tensor(o, y, y, ALU.not_equal))
                    st.held(v)
                    link(v.copy_predicated(y, g4(ok[:, :, :, :]).bitcast(mybir.dt.uint32), f))
                    v.wait_ge(*p.stored.before(i))
                    v.tensor_tensor(g4(H1[:, :, :, :]), y, g4(X[:, :, :, :]), ALU.add).then_inc(
                        *p.h_ready.one())


def build(nc, A, out):
    h = nc.dram_tensor("h_stream", [BATCH, T, C], F32, kind="Internal").ap()
    mean = nc.dram_tensor("token_mean", [C, BATCH], F32, kind="Internal").ap()
    route = nc.dram_tensor("routing0", [BATCH, EXPERTS], F32, kind="Internal").ap()
    last = h if PHASES > 1 else out
    stage_tokenizer(nc, A, last)
    if PHASES >= 2:
        stage_attention0(nc, A, h, mean)
    if PHASES >= 3:
        stage_router0(nc, A, mean, route)
    if PHASES >= 4:
        stage_ffn0(nc, A, h, route)
    if PHASES >= 5:
        stage_retention1(nc, A, h)
    hx = nc.dram_tensor("stream_attended1", [BATCH, T, C], F32, kind="Internal").ap()
    flatT = nc.dram_tensor("normed1", [PAIRS, C, 2 * T], F32, kind="Internal").ap()
    mix = nc.dram_tensor("mixing1", [BATCH, T, EXPERTS], F32, kind="Internal").ap()
    if PHASES >= 6:
        stage_attention1(nc, A, h, hx, flatT, mix)
    if PHASES >= 7:
        stage_experts1(nc, A, h, hx, flatT, mix)
    if PHASES >= 8:
        stage_attention2(nc, A, h)
    if PHASES >= 9:
        stage_depths2(nc, A, h)
    if PHASES >= 10:
        stage_attention3(nc, A, h)
    if PHASES >= 11:
        stage_switch3(nc, A, h, out)
    if last is h and PHASES < 11:
        copy_out(nc, h, out)
    if MISCOUNTED:
        raise ValueError(f"MISCOUNTED {MISCOUNTED}")


def copy_out(nc, h, out):
    with Stage(nc, "copy") as st:
        done = st.event("done", dma=True)
        with st.block() as block:
            @block.sync
            def _(sp):
                sp.dma_start(out[:, :, :], h[:, :, :]).then_inc(*done.one())
                sp.wait_ge(*done.after(0))


def interpolation_taps():
    f = np.float32
    pos = np.arange(POINTS, dtype=f) * f(1.0 / (POINTS - 1))
    pos[-1] = 1.0
    x = pos * f(SAMPLES - 1)
    i0 = np.floor(x)
    frac = x - i0
    a = -0.75
    w = np.zeros((T, 20, 64), f)
    p = np.arange(T * 64)
    for off in range(-1, 3):
        t = np.abs(frac[p] - f(off))
        near = ((f(a + 2.0) * t - f(a + 3.0)) * t) * t + f(1.0)
        far = ((f(a) * t - f(5.0 * a)) * t + f(8.0 * a)) * t - f(4.0 * a)
        val = np.where(t <= 1.0, near, np.where(t < 2.0, far, f(0.0)))
        idx = np.clip(i0[p].astype(np.int64) + off, -1, SAMPLES - 1)
        w[p // 64, idx - (16 * (p // 64) - 2), p % 64] += val
    return w


def constants():
    f = np.float32
    n, k = np.arange(64)[:, None], np.arange(33)[None, :]
    ang = 2 * np.pi * ((n * k) % 64) / 64
    e = np.arange(EXPERTS)
    key = np.arange(PT)[:, None]
    gap = np.concatenate([np.arange(T)[None, :] - key, np.arange(PT)[None, :] - key], 1)
    decay = np.exp((np.maximum(gap, 0).astype(f) * f(np.log(0.96875))).astype(np.float64)).astype(f)
    inv = f(1.0) / np.power(10000.0, np.arange(0, 64, 2) / 64.0).astype(f)
    ang64 = np.repeat((np.arange(T, dtype=f)[:, None] * inv[None, :]).T, 2, axis=0).astype(np.float64)
    sign = np.where(np.arange(64) % 2, 1.0, -1.0)[:, None]
    inv16 = f(1.0) / f(10000.0) ** (np.arange(0, 16, 2, dtype=f) / 16)
    ang16 = np.concatenate([np.outer(np.arange(T, dtype=f), inv16)] * 2, -1).T
    rope16 = np.zeros((2, 4, 32, T), f)
    rope16[0, :, 0:16] = np.cos(ang16)
    rope16[0, :, 16] = 1.0
    rope16[1, :, 0:16] = np.sin(ang16) * np.where(np.arange(16) < 8, -1, 1)[:, None].astype(f)
    qry = np.arange(PT)[:, None]
    late = np.concatenate([np.arange(PT)[None, :] - qry, np.arange(T)[None, :] - qry - OFF], 1)
    token = np.arange(PT)[:, None, None] + np.array([0, OFF])[None, :, None]
    col = np.arange(T)[None, None, :]
    return {
        "const_before": (col < token).astype(f),
        "const_self": np.where(col == token, f(-3.4028234663852886e38), f(0)),
        "const_upto": (np.arange(PT)[:, None] <= np.arange(PT)[None, :]).astype(f),
        "const_rope16": rope16.reshape(2, 128, T),
        "const_maskQ": np.where(late > 0, f(NEG), f(0)),
        "const_maskK": np.where(gap < 0, f(NEG), f(0)),
        "const_earlier": (e[None, :] < e[:, None]).astype(f).ravel(),
        "const_decay": np.where(gap >= 0, decay, f(0)),
        "const_rope64": np.stack([np.cos(ang64), np.sin(ang64) * sign]).astype(f),
        "const_ident": np.eye(128, dtype=f),
        "const_dft": np.concatenate([np.cos(ang), -np.sin(ang)], 1).astype(f),
        "const_taps": interpolation_taps(),
    }


def kernel(**inputs):
    import numpy as _np
    import concourse.bacc as _bacc
    from concourse import mybir as _mybir
    from concourse.bass_utils import run_bass_kernel_spmd as _run

    nc = _bacc.Bacc("TRN2", target_bir_lowering=False, num_devices=1)
    given = {k: _np.asarray(v) for k, v in inputs.items()}
    x = given.pop("x")
    arrays = dict(constants())
    arrays["x_edge"] = _np.concatenate([x[:, :1], x[:, :1], x], axis=1)
    for name, a in given.items():
        if name in TRANSPOSED:
            arrays[name + "T"] = a.T
        else:
            arrays[name] = a
        if name in ("L1_attn_W_Q", "L1_attn_W_K"):
            arrays[name + "x"] = a.reshape(64, 32, 2)[:, :, ::-1].reshape(64, 64)
        if name in ("L1_ffn_wq", "L1_ffn_wk"):
            arrays[name + "xT"] = a.reshape(-1, 2, 8, 64)[:, ::-1].reshape(-1, 64).T
        if name in ("L1_ffn_w1", "L1_ffn_w3"):
            arrays[name + "T"] = a.transpose(2, 0, 1).reshape(64, -1)
        if name == "L1_ffn_w2":
            arrays[name + "T"] = a.transpose(0, 2, 1).reshape(-1, 64)
        if name == "L3_ffn_w1":
            arrays[name + "T"] = a.transpose(1, 0, 2).reshape(64, -1)
        if name == "L2_ffn_wr":
            arrays["wr_wide"] = _np.broadcast_to(a, (64, PT))
        if name == "L2_ffn_br":
            arrays["br_wide"] = _np.broadcast_to(a[None, :], (1, PT))
        if name == "L2_attn_W_embed":
            arrays[name + "T"] = a.transpose(0, 2, 1)
    for name in ("L1_ffn_w1", "L1_ffn_w2", "L1_ffn_w3", "L2_attn_W_embed", "L2_ffn_attention_mask",
                 "L2_ffn_wr", "L2_ffn_br", "L3_ffn_w1"):
        del arrays[name]
    arrays = {f"in_{k}": _np.ascontiguousarray(a) for k, a in arrays.items()}
    A = {k[3:]: nc.dram_tensor(k, a.shape, _mybir.dt.from_np(a.dtype), kind="ExternalInput").ap()
         for k, a in arrays.items()}
    out = nc.dram_tensor("out", (BATCH, T, C), F32, kind="ExternalOutput").ap()
    build(nc, A, out)
    r = _run(nc, [arrays], core_ids=[0])
    return r.results[0]["out"]
```

```python
import math
from contextlib import ExitStack

import numpy as np
import concourse.bass as bass
from concourse import mybir

F32 = mybir.dt.float32
BF16 = mybir.dt.bfloat16
ALU = mybir.AluOpType
ACT = mybir.ActivationFunctionType
AX = mybir.AxisListType

BATCH, SAMPLES = 64, 4000
C = 64
POINTS = 4 * (SAMPLES - 1) + 1
T = (POINTS - 64) // 64 + 1
PT = 125
OFF = T - PT
ROWS = (OFF, PT)
PAIRS = BATCH // 2
EXPERTS = 8
NEG = -1.0e30
BODIES = 4
PHASES = 11
TRANSPOSED = ("L0_attn_Wq", "L0_attn_Wk", "L0_attn_Wv", "L0_attn_Wo", "L1_ffn_wq", "L1_ffn_wk", "L1_ffn_wv",
              "L1_ffn_wo", "L1_ffn_router_w", "L2_attn_W_out")

PER = {
    "att0.const_loaded": 9,
    "att0.exp_ready": 8,
    "att0.loaded": 2,
    "att0.max_ready": 8,
    "att0.norm_centered": 2,
    "att0.norm_powered": 2,
    "att0.norm_squared": 2,
    "att0.norm_variance": 2,
    "att0.s_done": 8,
    "att0.st_done": 8,
    "att0.stored": 3,
    "att0.vec": 8,
    "att1.const_loaded": 16,
    "att1.exp_ready": 8,
    "att1.loaded": 2,
    "att1.masked": 8,
    "att1.max_ready": 8,
    "att1.norm_centered": 3,
    "att1.norm_powered": 3,
    "att1.norm_squared": 3,
    "att1.norm_variance": 3,
    "att1.r_done": 4,
    "att1.s_done": 8,
    "att1.st_done": 8,
    "att1.stored": 5,
    "att1.vec": 31,
    "att1.xT_done": 2,
    "att1.xT_ready": 2,
    "att2.const_loaded": 5,
    "att2.exp_ready": 6,
    "att2.loaded": 3,
    "att2.max_ready": 3,
    "att2.oT_ready": 3,
    "att2.o_done": 3,
    "att2.pt_done": 3,
    "att2.pt_ready": 3,
    "att2.qk_done": 3,
    "att2.qk_ready": 3,
    "att2.s_done": 3,
    "att2.stored": 3,
    "att2.v_done": 3,
    "att2.v_ready": 3,
    "att2.vec": 10,
    "att2.y_done": 3,
    "att3.const_loaded": 6,
    "att3.w_split": 5,
    "att3.x3_split": 5,
    "att3.front_vec": 5,
    "att3.d_done": 2,
    "att3.d_used": 2,
    "att3.proj_done": 12,
    "att3.proj_ready": 12,
    "att3.s_done": 16,
    "att3.max_ready": 16,
    "att3.exp_ready": 32,
    "att3.pt_done": 16,
    "att3.pt_ready": 16,
    "att3.o_done": 2,
    "att3.o_ready": 2,
    "att3.oT_done": 4,
    "att3.oT_ready": 4,
    "att3.y_done": 2,
    "att3.y_used": 2,
    "att3.round": 8,
    "att3.vec": 18,
    "att3.stored": 2,
    "att3.loaded": 2,
    "ffn0.const_loaded": 4,
    "ffn0.front_vec": 3,
    "ffn0.hid_done": 2,
    "ffn0.hid_ready": 2,
    "ffn0.loaded": 3,
    "ffn0.stored": 2,
    "ffn0.vec": 8,
    "ffn0.weights": 12,
    "mod2.const_loaded": 8,
    "mod2.hid_done": 2,
    "mod2.hid_ready": 2,
    "mod2.loaded": 2,
    "mod2.stored": 2,
    "mod2.vec": 20,
    "moe1.gate_done": 16,
    "moe1.hid_ready": 16,
    "moe1.loaded": 4,
    "moe1.silu_ready": 16,
    "moe1.stored": 2,
    "moe1.vec": 4,
    "moe1.w1_loaded": 2,
    "moe1.w3_loaded": 2,
    "moe1.w_split": 10,
    "moe1.x3_split": 5,
    "moe1.xT_loaded": 2,
    "moe1.y_done": 4,
    "moe1.y_used": 4,
    "ret1.const_loaded": 8,
    "ret1.loaded": 2,
    "ret1.p_ready": 2,
    "ret1.qk_ready": 2,
    "ret1.r_done": 4,
    "ret1.s_done": 2,
    "ret1.stored": 2,
    "ret1.vec": 5,
    "route.const_loaded": 5,
    "route.expd": 3,
    "route.shifted": 3,
    "route.stored": 2,
    "route.vec": 26,
    "sw3.const_loaded": 10,
    "sw3.front_vec": 15,
    "sw3.hid_done": 16,
    "sw3.hid_ready": 16,
    "sw3.loaded": 2,
    "sw3.stored": 2,
    "sw3.vec": 10,
    "sw3.w_split": 10,
    "sw3.x3_split": 5,
    "sw3.y_done": 4,
    "sw3.y_used": 4,
    "tok.act": 2,
    "tok.const_loaded": 2,
    "tok.loaded": 2,
    "tok.stored": 2,
    "tok.vec": 7,
}
MISCOUNTED = {}


class Event:

    def __init__(self, nc, stage, name, unit=1):
        self.key = f"{stage}.{name}"
        self.sem = nc.alloc_semaphore(name=f"{stage}_{name}")
        self.unit = unit
        self.per = PER.get(self.key, 1)
        self.fired = 0

    def start(self):
        return (self.per + 1) * self.unit

    def one(self):
        self.fired += 1
        return self.sem, self.unit

    def after(self, i, k=None):
        k = self.per - 1 if k is None else k
        return self.sem, (i * self.per + (self.per + k + 2)) * self.unit

    def before(self, i):
        return self.sem, (i * self.per + (self.per + 1)) * self.unit

    def lagging(self, i):
        return self.sem, (i * self.per + 1) * self.unit

    def latest(self, i):
        return self.after(i, (self.fired - 1) % self.per)


class TransferEvents:

    def __init__(self, nc, stage, name, start=16):
        self.key, self.start = f"{stage}.{name}", start
        self.sems = [nc.alloc_semaphore(name=f"{stage}_{name}_{u}") for u in range(2)]
        self.per = PER.get(self.key, 1)
        self.fired = 0

    def one(self, u):
        self.fired += 1
        return self.sems[u], 16

    def after(self, n, u):
        return self.sems[u], (n - u) * (8 * self.per) + 16 * self.per + self.start

    def lagging(self, n, u):
        return self.sems[u], (n - u) * (8 * self.per) + 16


class Stage:

    def __init__(self, nc, name):
        self.nc, self.name, self.events, self.ctx = nc, name, {}, ExitStack()
        self.gates = {}

    def __enter__(self):
        self.ctx.__enter__()
        return self

    def __exit__(self, *e):
        if e[0] is None:
            self.ctx.__exit__(None, None, None)
        for s in self.events.values():
            if s.fired != s.per and not (s.fired and s.fired % s.per == 0 and s.loops == s.fired // s.per):
                MISCOUNTED[s.key] = s.fired // s.loops
        sems = [x for s in self.events.values() for x in (s.sems if isinstance(s, TransferEvents) else [s.sem])]
        sems += list(self.gates.values())
        self.nc.clear_and_free_semaphores(sems)
        self.nc.all_engine_barrier()

    def event(self, name, dma=False, bodies=1):
        s = self.events[name] = Event(self.nc, self.name, name, 16 if dma else 1)
        s.loops = bodies
        return s

    def transfers(self, name, bodies=BODIES, start=16):
        s = self.events[name] = TransferEvents(self.nc, self.name, name, start)
        s.loops = bodies
        return s

    def sb(self, name, shape, dt=F32):
        return self.ctx.enter_context(self.nc.sbuf_tensor(f"{self.name}_{name}", shape, dt))

    def held(self, engine):
        gate = self.gates.get(engine.engine)
        if gate is None:
            gate = self.gates[engine.engine] = self.nc.alloc_semaphore(
                name=f"{self.name}_held_{len(self.gates)}")
        engine.sem_inc(gate, 1)

    def psum(self, name, shape, dt=F32):
        return self.ctx.enter_context(self.nc.psum_tensor(f"{self.name}_{name}", shape, dt))

    def block(self):
        for s in self.events.values():
            if isinstance(s, TransferEvents):
                for sem in s.sems if s.start else ():
                    self.nc.sync.sem_inc(sem, 16)
            else:
                self.nc.sync.sem_inc(s.sem, s.start())
        self.nc.all_engine_barrier()
        return self.nc.Block()


def bc(ap, n):
    return bass.AP(ap.tensor, ap.offset, [list(x) for x in ap.ap] + [[0, n]])


def bcm(ap, at, n):
    a = [list(x) for x in ap.ap]
    return bass.AP(ap.tensor, ap.offset, a[:at] + [[0, n]] + a[at:])


def load_pair(sp, tile, dram, i, width=C):
    src = dram[bass.ds(i * 2, 2)]
    return [sp.dma_start(tile[:, t, :, :], bass.AP(src.tensor, src.offset + t * OFF * width,
                                                   [[width, PT], [T * width, 2], [1, width]]))
            for t in range(2)]


def store_pair(sp, dram, tile, i, width=C):
    dst = dram[bass.ds(i * 2, 2)]
    return [sp.dma_start(bass.AP(dst.tensor, dst.offset + t * OFF * width,
                                 [[width, ROWS[t]], [T * width, 2], [1, width]]), tile[0:ROWS[t], t, :, :])
            for t in range(2)]


class Norm:

    def __init__(self, st, rows, groups, bodies=1, name="norm"):
        self.rows, self.g = rows, groups
        self.sum = st.sb(name + "_sum", [rows, groups])
        self.xc = st.sb(name + "_centered", [rows, groups, C])
        self.sq = st.sb(name + "_squares", [rows, groups, C])
        self.var = st.sb(name + "_var", [rows, groups])
        self.rstd = st.sb(name + "_rstd", [rows, groups])
        self.expo = st.sb(name + "_exponent", [rows, groups])
        self.centered = st.event(name + "_centered", bodies=bodies)
        self.squared = st.event(name + "_squared", bodies=bodies)
        self.variance = st.event(name + "_variance", bodies=bodies)
        self.powered = st.event(name + "_powered", bodies=bodies)

    def center(self, v, i, x, chain):
        v.reduce_sum(self.sum[:, :], x, AX.X).then_inc(*chain.one())
        v.wait_ge(*chain.latest(i))
        v.tensor_scalar(self.sum[:, :], self.sum[:, :], -1.0 / C, None, ALU.mult).then_inc(*chain.one())
        v.wait_ge(*chain.latest(i))
        v.tensor_tensor(self.xc[:, :, :], x, bc(self.sum[:, :], C), ALU.add).then_inc(*self.centered.one())

    def scale(self, v, i, k, x, out, eps, chain):
        v.wait_ge(*self.squared.after(i, k))
        v.reduce_sum(self.var[:, :], self.sq[:, :, :], AX.X).then_inc(*chain.one())
        v.wait_ge(*chain.latest(i))
        v.tensor_scalar(self.var[:, :], self.var[:, :], 1.0 / C, eps, ALU.mult, ALU.add).then_inc(
            *self.variance.one())
        v.wait_ge(*self.powered.after(i, k))
        return v.tensor_tensor(out, x, bc(self.rstd[:, :], C), ALU.mult)

    def square(self, a, i, k, x):
        a.wait_ge(*self.centered.after(i, k))
        a.activation(self.sq[:, :, :], x, ACT.Square).then_inc(*self.squared.one())

    def power(self, p, i, k):
        p.wait_ge(*self.variance.after(i, k))
        p.tensor_tensor(self.rstd[:, :], self.var[:, :], self.expo[:, :], ALU.pow).then_inc(*self.powered.one())

    def square_pool(self, p, i, k, x):
        p.wait_ge(*self.centered.after(i, k))
        p.tensor_tensor(self.sq[:, :, :], x, x, ALU.mult).then_inc(*self.squared.one())


def g4(ap):
    return ap.rearrange("p t b c -> p (t b) c")


def stage_tokenizer(nc, A, h):
    WG = 8
    GROUPS = T // WG
    TAPS = 20
    NF = 33
    SPAN = 16 * (WG - 1) + TAPS
    Q = (T + 1) // 2
    r5 = math.sqrt(0.5)
    with Stage(nc, "tok") as st:
        xs = st.sb("samples", [BATCH, 2, SPAN])
        wt = st.sb("taps", [TAPS, 2, WG, 64])
        ident = st.sb("ident", [64, 64])
        dft = st.sb("dft", [64, 2 * NF])
        sT = st.sb("samplesT", [TAPS, WG, BATCH])
        poly = st.sb("poly", [64, WG * BATCH])
        gauss = st.sb("gauss", [64, WG * BATCH])
        kw = st.sb("kernelled", [64, WG * BATCH])
        sq = st.sb("squares", [128, 4, 2 * NF])
        mag = st.sb("magnitude", [128, Q, NF])
        d = st.sb("excess", [128, Q, NF])
        lg = st.sb("gap", [128, Q, NF])
        top = st.sb("top", [128, Q])
        thr = st.sb("thr", [128, 2, Q])
        out = st.sb("out", [128, Q, C])
        bias = st.sb("bias", [128, 4])
        pT = st.psum("pT", [TAPS, 2, WG, BATCH])
        pI = st.psum("pI", [64, 2, WG * BATCH])
        pM = st.psum("pM", [128, 2, 4, 128])

        const_loaded = st.event("const_loaded", dma=True)
        loaded = st.transfers("loaded")
        memset_done = st.event("memset_done")
        transposed = st.event("transposed", bodies=BODIES)
        samples_ready = st.event("samples_ready", bodies=BODIES)
        interpolated = st.event("interpolated", bodies=BODIES)
        squared = st.event("squared", bodies=BODIES)
        kernels_done = st.event("kernels_done", bodies=BODIES)
        windows_ready = st.event("windows_ready", bodies=BODIES)
        spectrum = st.event("spectrum", bodies=BODIES)
        squares_ready = st.event("squares_ready", bodies=BODIES)
        power_ready = st.event("power_ready", bodies=BODIES)
        vec = st.event("vec")
        excess_ready = st.event("excess_ready")
        magnitude_ready = st.event("magnitude_ready")
        excess_exp = st.event("excess_exp")
        gap_ready = st.event("gap_ready")
        act = st.event("act")
        gap_log = st.event("gap_log")
        out_ready = st.event("out_ready")
        stored = st.event("stored", dma=True)

        def groups(engine, body):
            with engine.Fori(0, GROUPS // 2) as j:
                body(j * 2, 0, WG)
                body(j * 2 + 1, 1, WG)
            for i in range(GROUPS - GROUPS % 2, GROUPS):
                body(i, i % 2, WG)
            body(GROUPS, GROUPS % 2, T - GROUPS * WG)

        with st.block() as block:
            @block.sync
            def _(sp):
                sp.dma_start(ident[:, :], A["const_ident"][0:64, 0:64]).then_inc(*const_loaded.one())
                sp.dma_start(dft[:, :], A["const_dft"][:, :]).then_inc(*const_loaded.one())

                def body(i, u, nw):
                    span = 16 * (nw - 1) + TAPS
                    sp.wait_ge(*interpolated.lagging(i))
                    st.held(sp)
                    sp.dma_start(xs[:, u, 0:span], A["x_edge"][:, bass.ds(i * (16 * WG), span)]).then_inc(
                        *loaded.one(u))
                    sp.dma_start(wt[:, u, 0:nw, :], A["const_taps"][bass.ds(i * WG, nw)].rearrange(
                        "w k f -> k w f")).then_inc(*loaded.one(u))
                groups(sp, body)
                sp.wait_ge(*out_ready.after(0))
                for w2 in range(2):
                    n = Q - w2
                    dst = h[:, w2:w2 + 1, :]
                    dst = bass.AP(dst.tensor, dst.offset, [[T * C, 64], [2 * C, n], [1, C]])
                    sp.dma_start(dst, out[w2 * 64:w2 * 64 + 64, 0:n, :]).then_inc(*stored.one())
                sp.wait_ge(*stored.after(0))

            @block.tensor
            def _(pe):
                pe.wait_ge(*const_loaded.after(0))

                def body(i, u, nw):
                    pe.wait_ge(*loaded.after(i, u))
                    pe.wait_ge(*samples_ready.before(i))
                    st.held(pe)
                    for w in range(nw):
                        ins = pe.transpose(pT[:, u, w, :], xs[:, u, 16 * w:16 * w + TAPS], ident[:, :])
                    ins.then_inc(*transposed.one())
                    pe.wait_ge(*samples_ready.after(i))
                    pe.wait_ge(*kernels_done.before(i))
                    st.held(pe)
                    for w in range(nw):
                        ins = pe.matmul(pI[:, u, w * 64:w * 64 + 64], wt[:, u, w, :], sT[:, w, :], start=True,
                                        stop=True)
                    ins.then_inc(*interpolated.one())
                    pe.wait_ge(*windows_ready.after(i))
                    pe.wait_ge(*squares_ready.before(i))
                    st.held(pe)
                    rows = min(128, 64 * nw)
                    for q in range(64 * nw // rows):
                        ins = pe.matmul(pM[0:rows, u, q, 0:2 * NF], kw[:, q * rows:q * rows + rows], dft[:, :],
                                        start=True, stop=True)
                    ins.then_inc(*spectrum.one())
                groups(pe, body)

            @block.scalar
            def _(a):
                a.wait_ge(*memset_done.after(0))

                def body(i, u, nw):
                    n, rows = 64 * nw, min(128, 64 * nw)
                    a.wait_ge(*interpolated.after(i))
                    a.wait_ge(*windows_ready.before(i))
                    a.activation(poly[:, 0:n], pI[:, u, 0:n], ACT.Square, bias=bias[0:64, 0:1], scale=r5)
                    a.activation(gauss[:, 0:n], pI[:, u, 0:n], ACT.Square, bias=bias[0:64, 1:2]).then_inc(
                        *squared.one())
                    a.wait_ge(*squared.after(i))
                    a.activation(gauss[:, 0:n], gauss[:, 0:n], ACT.Exp, bias=bias[0:64, 2:3],
                                 scale=-0.5).then_inc(*kernels_done.one())
                    a.wait_ge(*spectrum.after(i))
                    a.wait_ge(*power_ready.before(i))
                    a.activation(sq[0:rows, 0:n // rows, :], pM[0:rows, u, 0:n // rows, 0:2 * NF],
                                 ACT.Square).then_inc(*squares_ready.one())
                groups(a, body)
                a.wait_ge(*power_ready.before(GROUPS + 1))
                a.activation(mag[:, :, :], mag[:, :, :], ACT.Sqrt).then_inc(*magnitude_ready.one())
                a.wait_ge(*excess_ready.after(0))
                a.activation(d[:, :, :], d[:, :, :], ACT.Exp, scale=-1.0).then_inc(*excess_exp.one())
                a.wait_ge(*gap_ready.after(0))
                a.activation(lg[:, :, :], lg[:, :, :], ACT.Abs).then_inc(*act.one())
                a.wait_ge(*act.latest(0))
                a.activation(lg[:, :, :], lg[:, :, :], ACT.Exp, scale=-1.0).then_inc(*act.one())
                a.wait_ge(*act.latest(0))
                a.activation(lg[:, :, :], lg[:, :, :], ACT.Ln, bias=bias[:, 3:4]).then_inc(*gap_log.one())

            @block.vector
            def _(v):
                v.memset(bias[:, 0:1], 1.3 * r5)
                v.memset(bias[:, 1:2], -0.7)
                v.memset(bias[:, 2:3], math.log(0.5))
                v.memset(mag[:, Q - 1, :], 0.0)
                v.memset(bias[:, 3:4], 1.0).then_inc(*memset_done.one())
                v.wait_ge(*memset_done.after(0))

                def link(ins):
                    ins.then_inc(*vec.one())
                    v.wait_ge(*vec.latest(0))

                def body(i, u, nw):
                    n, rows = 64 * nw, min(128, 64 * nw)
                    R, q = slice(0, rows), n // rows
                    v.wait_ge(*transposed.after(i))
                    v.wait_ge(*interpolated.before(i))
                    v.tensor_copy(sT[:, 0:nw, :], pT[:, u, 0:nw, :]).then_inc(*samples_ready.one())
                    v.wait_ge(*kernels_done.after(i))
                    v.wait_ge(*spectrum.before(i))
                    v.tensor_tensor(kw[:, 0:n], poly[:, 0:n], gauss[:, 0:n], ALU.add).then_inc(
                        *windows_ready.one())
                    v.wait_ge(*squares_ready.after(i))
                    v.tensor_tensor(mag[R, bass.ds(i * 4, q), :], sq[R, 0:q, 0:NF], sq[R, 0:q, NF:2 * NF],
                                    ALU.add).then_inc(*power_ready.one())
                groups(v, body)
                v.wait_ge(*magnitude_ready.after(0))
                link(v.reduce_max(top[:, :], mag[:, :, :], AX.X))
                v.tensor_scalar(thr[:, 0, :], top[:, :], 0.12, None, ALU.mult)
                link(v.tensor_scalar(thr[:, 1, :], top[:, :], 0.9, None, ALU.mult))
                v.tensor_tensor(d[:, :, :], mag[:, :, :], bc(thr[:, 0, :], NF), ALU.subtract).then_inc(
                    *excess_ready.one())
                v.wait_ge(*excess_exp.after(0))
                link(v.tensor_scalar(d[:, :, :], d[:, :, :], 1.0, None, ALU.add))
                link(v.reciprocal(d[:, :, :], d[:, :, :]))
                link(v.tensor_tensor(mag[:, :, :], mag[:, :, :], d[:, :, :], ALU.mult))
                v.tensor_tensor(lg[:, :, :], mag[:, :, :], bc(thr[:, 1, :], NF), ALU.subtract).then_inc(
                    *gap_ready.one())
                link(v.tensor_tensor(mag[:, :, :], mag[:, :, :], bc(thr[:, 1, :], NF), ALU.min))
                v.wait_ge(*gap_log.after(0))
                link(v.tensor_tensor(out[:, :, 0:NF], mag[:, :, :], lg[:, :, :], ALU.subtract))
                lo = out[:, :, 0:NF]
                mirror = bass.AP(lo.tensor, lo.offset + NF - 2, [list(lo.ap[0]), list(lo.ap[1]), [-1, NF - 2]])
                v.tensor_copy(out[:, :, NF:C], mirror).then_inc(*out_ready.one())


def stage_attention0(nc, A, h, mean_dram):
    H, D = 4, 16
    with Stage(nc, "att0") as st:
        ident = st.sb("ident", [128, 128])
        wq = st.sb("wq", [C + 1, H, 32])
        wk = st.sb("wk", [C + 1, H, 32])
        wv = st.sb("wv", [C + 1, H, D + 1])
        wo = st.sb("wo", [C + 1, C])
        ones = st.sb("ones", [128, 1])
        X = st.sb("X", [PT, 2, 2, C])
        xn = st.sb("xn", [PT, 2, 2, C])
        xT = st.sb("xT", [C + 1, 2, T])
        qT = st.sb("qT", [128, 2, T])
        kT = st.sb("kT", [128, 2, T])
        qmT = st.sb("qmT", [128, 2, T])
        V = st.sb("V", [PT, 2, 2, H, D + 1])
        M = st.sb("M", [PT, 2, 2, H, 32])
        E = st.sb("E", [PT, 2, 2, H, T])
        rden = st.sb("rden", [PT, 4, H])
        ob = st.sb("ob", [PT, 4, H, D], BF16)
        of = st.sb("of", [PT, 2, 2, C])
        oT = st.sb("oT", [C + 1, 2, T])
        H1 = st.sb("H1", [PT, 2, 2, C])
        mean = st.sb("mean", [C, 2])
        norm = Norm(st, PT, 4)

        pX = st.psum("pX", [C, 2, 256])
        pQ = st.psum("pQ", [128, 512])
        pK = st.psum("pK", [128, 512])
        pS = st.psum("pS", [PT, 4, 512])
        pO = st.psum("pO", [PT, 4, 128])

        const_loaded = st.event("const_loaded", dma=True)
        zeroed = st.event("zeroed")
        memset_done = st.event("memset_done")
        vec0 = st.event("vec0")
        loaded = st.event("loaded", dma=True)
        vec = st.event("vec")
        xn_ready = st.event("xn_ready")
        xT_done = st.event("xT_done")
        xT_ready = st.event("xT_ready")
        q_done = st.event("q_done")
        k_done = st.event("k_done")
        q_ready = st.event("q_ready")
        k_ready = st.event("k_ready")
        v_done = st.event("v_done")
        v_ready = st.event("v_ready")
        s_done = st.event("s_done")
        max_ready = st.event("max_ready")
        qm_done = st.event("qm_done")
        qm_ready = st.event("qm_ready")
        st_done = st.event("st_done")
        exp_ready = st.event("exp_ready")
        o_done = st.event("o_done")
        o_ready = st.event("o_ready")
        oT_done = st.event("oT_done")
        oT_ready = st.event("oT_ready")
        y_done = st.event("y_done")
        h_ready = st.event("h_ready")
        h2_ready = st.event("h2_ready")
        mean_done = st.event("mean_done")
        mean_ready = st.event("mean_ready")
        stored = st.event("stored", dma=True)

        qv, kv = pQ[:, 0:2 * T], pK[:, 0:2 * T]

        with st.block() as block:
            @block.sync
            def _(sp):
                sp.dma_start(ident[:, :], A["const_ident"][:, :]).then_inc(*const_loaded.one())
                sp.wait_ge(*zeroed.after(0))
                for w, n, width in ((wq, "q", D), (wk, "k", D), (wv, "v", D)):
                    sp.dma_start(w[0:C, :, 0:D], A[f"L0_attn_W{n}T"].rearrange("c (h d) -> c h d", h=H)).then_inc(
                        *const_loaded.one())
                    sp.dma_start(w[C:C + 1, :, 0:D], A[f"L0_attn_b{n}"].rearrange(
                        "(o h d) -> o h d", o=1, h=H)).then_inc(*const_loaded.one())
                sp.dma_start(wo[0:C, :], A["L0_attn_WoT"]).then_inc(*const_loaded.one())
                sp.dma_start(wo[C:C + 1, :], A["L0_attn_bo"].rearrange("(o d) -> o d", o=1)).then_inc(
                    *const_loaded.one())
                with sp.Fori(0, PAIRS) as i:
                    sp.wait_ge(*h_ready.before(i))
                    st.held(sp)
                    for ins in load_pair(sp, X, h, i):
                        ins.then_inc(*loaded.one())
                    sp.wait_ge(*h_ready.after(i))
                    st.held(sp)
                    for ins in store_pair(sp, h, H1, i):
                        ins.then_inc(*stored.one())
                    sp.wait_ge(*mean_ready.after(i))
                    st.held(sp)
                    sp.dma_start(mean_dram[:, bass.ds(i * 2, 2)], mean[:, :]).then_inc(*stored.one())
                sp.wait_ge(*stored.after(PAIRS - 1))

            @block.gpsimd
            def _(p):
                p.wait_ge(*memset_done.after(0))
                with p.Fori(0, PAIRS) as i:
                    norm.power(p, i, 0)
                    norm.power(p, i, 1)

            @block.tensor
            def _(pe):
                pe.wait_ge(*const_loaded.after(0))
                pe.wait_ge(*memset_done.after(0))
                with pe.Fori(0, PAIRS) as i:
                    pe.wait_ge(*xn_ready.after(i))
                    st.held(pe)
                    for b in range(2):
                        for t in range(2):
                            ins = pe.transpose(pX[:, b, t * OFF:t * OFF + ROWS[t]], xn[0:ROWS[t], t, b, :],
                                               ident[0:ROWS[t], 0:ROWS[t]])
                    ins.then_inc(*xT_done.one())
                    pe.wait_ge(*xT_ready.after(i))
                    pe.matmul(qv, wq[:, :, :], xT[:, :, :], start=True, stop=True).then_inc(*q_done.one())
                    pe.matmul(kv, wk[:, :, :], xT[:, :, :], start=True, stop=True).then_inc(*k_done.one())
                    pe.wait_ge(*o_ready.before(i))
                    for t in range(2):
                        for b in range(2):
                            ins = pe.matmul(pO[:, 2 * t + b, 0:H * (D + 1)], xT[:, b, t * OFF:t * OFF + PT],
                                            wv[:, :, :], start=True, stop=True)
                    ins.then_inc(*v_done.one())
                    pe.wait_ge(*q_ready.after(i))
                    pe.wait_ge(*k_ready.after(i))
                    for b in range(2):
                        for hd in range(H):
                            if b == 0:
                                pe.wait_ge(*exp_ready.before(i))
                            else:
                                pe.wait_ge(*max_ready.after(i, hd))
                            r = 32 * hd
                            for t in range(2):
                                ins = pe.matmul(pS[:, hd, t * T:t * T + T],
                                                qT[r:r + D, b, t * OFF:t * OFF + PT], kT[r:r + D, b, :],
                                                start=True, stop=True, tile_position=(r, 0))
                            ins.then_inc(*s_done.one())
                    pe.wait_ge(*max_ready.after(i))
                    for b in range(2):
                        for t in range(2):
                            ins = pe.matmul(pQ[:, b * T + t * OFF:b * T + t * OFF + ROWS[t]],
                                            M[0:ROWS[t], t, b, :, :], ident[0:ROWS[t], 0:ROWS[t]],
                                            start=False, stop=True, skip_group_check=True)
                    ins.then_inc(*qm_done.one())
                    pe.wait_ge(*qm_ready.after(i))
                    for b in range(2):
                        for hd in range(H):
                            n = b * H + hd
                            if n >= 4:
                                pe.wait_ge(*exp_ready.after(i, n - 4))
                            r = 32 * hd
                            for t in range(2):
                                ins = pe.matmul(pS[:, n % 4, t * T:t * T + T],
                                                kT[r:r + D + 1, b, t * OFF:t * OFF + PT], qmT[r:r + D + 1, b, :],
                                                start=True, stop=True, tile_position=(r, 0))
                            ins.then_inc(*st_done.one())
                    pe.wait_ge(*v_ready.after(i))
                    for b in range(2):
                        for hd in range(H):
                            pe.wait_ge(*exp_ready.after(i, b * H + hd))
                            for t in range(2):
                                for kt in range(2):
                                    ins = pe.matmul(pO[:, 2 * t + b, hd * (D + 1):(hd + 1) * (D + 1)],
                                                    E[0:ROWS[kt], kt, b, hd, t * OFF:t * OFF + PT],
                                                    V[0:ROWS[kt], kt, b, hd, :], start=(kt == 0),
                                                    stop=(kt == 1))
                    ins.then_inc(*o_done.one())
                    pe.wait_ge(*o_ready.after(i))
                    st.held(pe)
                    for b in range(2):
                        for t in range(2):
                            ins = pe.transpose(pX[:, b, t * OFF:t * OFF + ROWS[t]], of[0:ROWS[t], t, b, :],
                                               ident[0:ROWS[t], 0:ROWS[t]])
                    ins.then_inc(*oT_done.one())
                    pe.wait_ge(*oT_ready.after(i))
                    for t in range(2):
                        for b in range(2):
                            ins = pe.matmul(pK[0:PT, (2 * t + b) * C:(2 * t + b + 1) * C],
                                            oT[:, b, t * OFF:t * OFF + PT], wo[:, :], start=True, stop=True)
                    ins.then_inc(*y_done.one())
                    pe.wait_ge(*h2_ready.after(i))
                    for b in range(2):
                        for t in range(2):
                            ins = pe.matmul(pX[:, b, 0:1], xn[0:ROWS[t], t, b, :], ones[0:ROWS[t], :],
                                            start=(t == 0), stop=(t == 1))
                    ins.then_inc(*mean_done.one())

            @block.scalar
            def _(a):
                with a.Fori(0, PAIRS) as i:
                    norm.square(a, i, 0, norm.xc[:, :, :])
                    a.wait_ge(*q_done.after(i))
                    a.activation(qT[:, :, :].rearrange("p b t -> p (b t)"), qv, ACT.Copy).then_inc(*q_ready.one())
                    a.wait_ge(*v_done.after(i))
                    a.activation(V[:, :, :, :, :].rearrange("p t b h d -> p (t b) (h d)"),
                                 pO[:, :, 0:H * (D + 1)], ACT.Copy).then_inc(*v_ready.one())
                    a.wait_ge(*qm_done.after(i))
                    a.activation(qmT[:, :, :].rearrange("p b t -> p (b t)"), qv, ACT.Copy).then_inc(
                        *qm_ready.one())
                    for b in range(2):
                        for hd in range(H):
                            n = b * H + hd
                            a.wait_ge(*st_done.after(i, n))
                            a.activation(E[:, :, b, hd, :], pS[:, n % 4, 0:2 * T].rearrange(
                                "p (t n) -> p t n", t=2), ACT.Exp, scale=D ** -0.5).then_inc(*exp_ready.one())
                    norm.square(a, i, 1, norm.xc[:, :, :])
                    a.wait_ge(*mean_done.after(i))
                    a.wait_ge(*stored.before(i))
                    a.activation(mean[:, :], pX[:, :, 0], ACT.Copy, scale=1.0 / T).then_inc(*mean_ready.one())

            @block.vector
            def _(v):
                v.memset(wq[:, :, :], 0.0)
                v.memset(wk[:, :, :], 0.0)
                v.memset(wv[:, :, :], 0.0).then_inc(*vec0.one())
                v.wait_ge(*vec0.after(0))
                v.memset(wk[C:C + 1, :, D:D + 1], 1.0)
                v.memset(wv[C:C + 1, :, D:D + 1], 1.0).then_inc(*zeroed.one())
                v.memset(ones[:, :], 1.0)
                v.memset(xT[C:C + 1, :, :], 1.0)
                v.memset(oT[C:C + 1, :, :], 1.0)
                v.memset(M[:, :, :, :, :], 0.0)
                v.memset(norm.expo[:, :], -0.5).then_inc(*memset_done.one())
                v.wait_ge(*memset_done.after(0))
                with v.Fori(0, PAIRS) as i:
                    v.wait_ge(*loaded.after(i))
                    norm.center(v, i, g4(X[:, :, :, :]), vec)
                    v.wait_ge(*mean_done.before(i))
                    norm.scale(v, i, 0, norm.xc[:, :, :], g4(xn[:, :, :, :]), 1e-5, vec).then_inc(
                        *xn_ready.one())
                    v.wait_ge(*xT_done.after(i))
                    v.tensor_scalar(xT[0:C, :, :], pX[:, :, 0:T], -10000.0, 10000.0, ALU.max,
                                    ALU.min).then_inc(*xT_ready.one())
                    v.wait_ge(*k_done.after(i))
                    v.tensor_copy(kT[:, :, :].rearrange("p b t -> p (b t)"), kv).then_inc(*k_ready.one())
                    for b in range(2):
                        for hd in range(H):
                            v.wait_ge(*s_done.after(i, b * H + hd))
                            v.tensor_reduce(M[:, :, b, hd, D], pS[:, hd, 0:2 * T].rearrange(
                                "p (t n) -> p t n", t=2), AX.X, ALU.max, negate=True).then_inc(*max_ready.one())
                    v.wait_ge(*o_done.after(i))
                    o5 = pO[:, :, 0:H * (D + 1)].rearrange("p g (h d) -> p g h d", h=H)
                    v.reciprocal(rden[:, :, :], o5[:, :, :, D]).then_inc(*vec.one())
                    v.wait_ge(*vec.latest(i))
                    for g in range(4):
                        ins = v.tensor_tensor(ob[:, g, :, :], o5[:, g, :, 0:D], bc(rden[:, g, :], D), ALU.mult)
                    ins.then_inc(*vec.one())
                    v.wait_ge(*vec.latest(i))
                    v.tensor_copy(g4(of[:, :, :, :]), ob[:, :, :, :].rearrange(
                        "p g h d -> p g (h d)")).then_inc(*o_ready.one())
                    v.wait_ge(*oT_done.after(i))
                    v.tensor_copy(oT[0:C, :, :], pX[:, :, 0:T]).then_inc(*oT_ready.one())
                    v.wait_ge(*y_done.after(i))
                    v.wait_ge(*stored.before(i))
                    v.tensor_tensor(g4(H1[:, :, :, :]), g4(X[:, :, :, :]),
                                    pK[0:PT, 0:4 * C].rearrange("p (g c) -> p g c", g=4), ALU.add).then_inc(
                        *h_ready.one())
                    v.wait_ge(*h_ready.after(i))
                    norm.center(v, i, g4(H1[:, :, :, :]), vec)
                    norm.scale(v, i, 1, norm.xc[:, :, :], g4(xn[:, :, :, :]), 1e-5, vec).then_inc(
                        *h2_ready.one())


def pipelined(engine, front, main, steps=None):
    for step in [()] if steps is None else [(s,) for s in range(steps)]:
        front(0, 0, *step)
    with engine.Fori(0, PAIRS // 2 - 1) as j:
        for u in range(2):
            n = j * 2 + u
            main(n, u, lambda *step: front(n + 1, 1 - u, *step))
    main(PAIRS - 2, 0, lambda *step: front(PAIRS - 1, 1, *step))
    main(PAIRS - 1, 1, lambda *step: None)


class Front:

    def __init__(self, st, twice=False):
        self.st, self.twice = st, twice
        self.X = st.sb("X", [PT, 2, 2, 2, C])
        self.xn = st.sb("xn", [PT, 2, 2, 2, C * (1 + twice)])
        self.xT = st.sb("xT", [C + 1, 2, 2, T])
        self.H1 = st.sb("H1", [PT, 2, 2, 2, C])
        self.ident = st.sb("ident", [128, 128])
        self.norm = Norm(st, PT, 4, bodies=BODIES)
        self.pX = st.psum("pX", [C * (1 + twice), 2, 256])
        self.const_loaded = st.event("const_loaded", dma=True)
        self.memset_done = st.event("memset_done")
        self.loaded = st.transfers("loaded")
        self.front_vec = st.event("front_vec", bodies=BODIES)
        self.xn_ready = st.event("xn_ready", bodies=BODIES)
        self.xT_done = st.event("xT_done", bodies=BODIES)
        self.xT_ready = st.event("xT_ready", bodies=BODIES)
        self.h_ready = st.event("h_ready", bodies=BODIES)
        self.stored = st.transfers("stored")

    def memsets(self, v):
        v.memset(self.xT[C:C + 1, :, :, :], 1.0)
        v.memset(self.norm.expo[:, :], -0.5).then_inc(*self.memset_done.one())

    def load(self, sp, h, n, u):
        sp.wait_ge(*self.h_ready.lagging(n))
        self.st.held(sp)
        for ins in load_pair(sp, self.X[:, u, :, :, :], h, n):
            ins.then_inc(*self.loaded.one(u))

    def store(self, sp, h, n, u):
        sp.wait_ge(*self.h_ready.after(n))
        self.st.held(sp)
        for ins in store_pair(sp, h, self.H1[:, u, :, :, :], n):
            ins.then_inc(*self.stored.one(u))

    def all_stored(self, sp):
        for n in (PAIRS - 2, PAIRS - 1):
            sp.wait_ge(*self.stored.after(n, n % 2))

    def transpose(self, pe, n, u):
        pe.wait_ge(*self.xn_ready.after(n))
        pe.wait_ge(*self.xT_ready.before(n))
        self.st.held(pe)
        transpose_rows(pe, self.pX, self.xn[:, u, :, :, :], self.ident).then_inc(*self.xT_done.one())

    def square(self, a, n, u):
        self.norm.square(a, n, 0, self.norm.xc[:, :, :])

    def normalise(self, v, n, u):
        v.wait_ge(*self.loaded.after(n, u))
        self.norm.center(v, n, g4(self.X[:, u, :, :, :]), self.front_vec)
        ins = self.norm.scale(v, n, 0, self.norm.xc[:, :, :], g4(self.xn[:, u, :, :, 0:C]), 1e-5, self.front_vec)
        if self.twice:
            ins = v.tensor_tensor(g4(self.xn[:, u, :, :, C:2 * C]), self.norm.xc[:, :, :],
                                  bc(self.norm.rstd[:, :], C), ALU.mult)
        ins.then_inc(*self.xn_ready.one())

    def channels(self, v, n, u):
        v.wait_ge(*self.xT_done.after(n))
        v.tensor_copy(self.xT[0:C, u, :, :], self.pX[0:C, :, 0:T]).then_inc(*self.xT_ready.one())


class Pair:

    def __init__(self, st, tiles=2, rows=PT, ones_row=True):
        self.st, self.tiles, self.rows = st, tiles, rows
        self.X = st.sb("X", [rows, tiles, 2, C])
        self.xn = st.sb("xn", [rows, tiles, 2, C])
        self.H1 = st.sb("H1", [rows, tiles, 2, C])
        self.xT = st.sb("xT", [C + 1, 2, T])
        self.ident = st.sb("ident", [128, 128])
        self.norm = Norm(st, rows, 2 * tiles)
        self.const_loaded = st.event("const_loaded", dma=True)
        self.loaded = st.event("loaded", dma=True)
        self.stored = st.event("stored", dma=True)
        self.memset_done = st.event("memset_done")
        self.vec = st.event("vec")
        self.xn_ready = st.event("xn_ready")
        self.xT_done = st.event("xT_done")
        self.xT_ready = st.event("xT_ready")
        self.h_ready = st.event("h_ready")

    def memsets(self, v):
        v.memset(self.xT[C:C + 1, :, :], 1.0)
        v.memset(self.norm.expo[:, :], -0.5).then_inc(*self.memset_done.one())

    def normalise(self, v, i):
        v.wait_ge(*self.loaded.after(i))
        self.norm.center(v, i, g4(self.X[:, :, :, :]), self.vec)
        self.norm.scale(v, i, 0, self.norm.xc[:, :, :], g4(self.xn[:, :, :, :]), 1e-5, self.vec).then_inc(
            *self.xn_ready.one())


def transpose_rows(pe, dst, src, ident):
    for b in range(2):
        for t in range(2):
            ins = pe.transpose(dst[:, b, t * OFF:t * OFF + ROWS[t]], src[0:ROWS[t], t, b, :],
                               ident[0:ROWS[t], 0:ROWS[t]])
    return ins


def const(sp, signal, dst, src):
    sp.dma_start(dst, src).then_inc(*signal.one())


def row(ap):
    return bass.AP(ap.tensor, ap.offset, [[0, 1]] + [list(x) for x in ap.ap])


def every_row(ap, rows):
    return bass.AP(ap.tensor, ap.offset, [[0, rows]] + [list(x) for x in ap.ap])


class Rank:

    def __init__(self, st, rows, groups, k):
        self.rows, self.g, self.k = rows, groups, k
        self.gt = st.sb("rank_gt", [rows, groups, EXPERTS, EXPERTS])
        self.eq = st.sb("rank_eq", [rows, groups, EXPERTS, EXPERTS])
        self.rank = st.sb("rank", [rows, groups, EXPERTS])
        self.earlier = st.sb("rank_earlier", [rows, EXPERTS * EXPERTS])

    def select(self, v, i, w, sel, chain):
        e = EXPERTS
        other, own = bcm(w, 2, e), bc(w, e)
        v.tensor_tensor(self.gt[:, :, :, :], other, own, ALU.is_gt)
        v.tensor_tensor(self.eq[:, :, :, :], other, own, ALU.is_equal).then_inc(*chain.one())
        v.wait_ge(*chain.latest(i))
        v.tensor_tensor(self.eq[:, :, :, :].rearrange("p g e f -> p g (e f)"),
                        self.eq[:, :, :, :].rearrange("p g e f -> p g (e f)"),
                        bcm(self.earlier[:, :], 1, self.g), ALU.mult).then_inc(*chain.one())
        v.wait_ge(*chain.latest(i))
        v.tensor_tensor(self.gt[:, :, :, :], self.gt[:, :, :, :], self.eq[:, :, :, :], ALU.add).then_inc(
            *chain.one())
        v.wait_ge(*chain.latest(i))
        v.reduce_sum(self.rank[:, :, :], self.gt[:, :, :, :], AX.X).then_inc(*chain.one())
        v.wait_ge(*chain.latest(i))
        return v.tensor_scalar(sel, self.rank[:, :, :], float(self.k), None, ALU.is_lt)


def stage_router0(nc, A, mean_dram, route_dram, chosen_dram):
    capacity = float(math.ceil(BATCH * T * 1.25 / EXPERTS))
    E, B = EXPERTS, BATCH
    with Stage(nc, "route") as st:
        mT = st.sb("mean", [C + 1, B])
        wr = st.sb("wr", [C + 1, E])
        ones = st.sb("ones", [B, B])
        z = st.sb("z", [B, E])
        s1 = st.sb("s1", [B, 1])
        p = st.sb("p", [B, E])
        ld = st.sb("load", [B, E])
        w = st.sb("w", [B, E])
        sel = st.sb("sel", [B, E])
        pick = st.sb("pick", [B, 4, E])
        number = st.sb("number", [B, E])
        got = st.sb("got", [B, 4])
        chosen = st.sb("chosen", [B, 2], mybir.dt.int32)
        rank = Rank(st, B, 1, 2)
        pL = st.psum("pL", [B, 2, E])
        const_loaded = st.event("const_loaded", dma=True)
        memset_done = st.event("memset_done")
        logits = st.event("logits")
        probs = st.event("probs")
        loads = st.event("loads")
        vec = st.event("vec")
        shifted = st.event("shifted")
        expd = st.event("expd")
        ready = st.event("ready")
        stored = st.event("stored", dma=True)
        with st.block() as block:
            @block.sync
            def _(sp):
                const(sp, const_loaded, mT[0:C, :], mean_dram[:, :])
                const(sp, const_loaded, wr[0:C, :], A["L0_ffn_Wr"])
                const(sp, const_loaded, wr[C:C + 1, :], row(A["L0_ffn_br"]))
                const(sp, const_loaded, rank.earlier[:, :], every_row(A["const_earlier"], B))
                const(sp, const_loaded, number[:, :], every_row(A["const_number"], B))
                sp.wait_ge(*ready.after(0))
                sp.dma_start(route_dram[:, :], got[:, 2:4]).then_inc(*stored.one())
                sp.dma_start(chosen_dram[:, :], chosen[:, :]).then_inc(*stored.one())
                sp.wait_ge(*stored.after(0))

            @block.tensor
            def _(pe):
                pe.wait_ge(*const_loaded.after(0))
                pe.wait_ge(*memset_done.after(0))
                pe.matmul(pL[:, 0, :], mT[:, :], wr[:, :], start=True, stop=True).then_inc(*logits.one())
                pe.wait_ge(*probs.after(0))
                pe.matmul(pL[:, 1, :], ones[:, :], p[:, :], start=True, stop=True).then_inc(*loads.one())

            @block.scalar
            def _(a):
                for k in range(3):
                    a.wait_ge(*shifted.after(0, k))
                    a.activation(z[:, :], z[:, :], ACT.Exp).then_inc(*expd.one())

            @block.vector
            def _(v):
                def link(ins):
                    ins.then_inc(*vec.one())
                    v.wait_ge(*vec.latest(0))

                def softmax(k, src, dst, sig):
                    link(v.reduce_max(s1[:, :], src, AX.X))
                    v.tensor_scalar(z[:, :], src, s1[:, 0:1], None, ALU.subtract).then_inc(*shifted.one())
                    v.wait_ge(*expd.after(0, k))
                    if k == 2:
                        link(v.tensor_tensor(z[:, :], z[:, :], sel[:, :], ALU.mult))
                    link(v.reduce_sum(s1[:, :], z[:, :], AX.X))
                    link(v.reciprocal(s1[:, :], s1[:, :]))
                    v.tensor_scalar(dst, z[:, :], s1[:, 0:1], None, ALU.mult).then_inc(*sig.one())
                    v.wait_ge(*sig.latest(0))

                v.memset(ones[:, :], 1.0)
                v.memset(mT[C:C + 1, :], 1.0).then_inc(*memset_done.one())
                v.wait_ge(*logits.after(0))
                softmax(0, pL[:, 0, :], p[:, :], probs)
                v.wait_ge(*loads.after(0))
                link(v.tensor_scalar(ld[:, :], pL[:, 1, :], float(T), None, ALU.mult))
                link(v.reciprocal(ld[:, :], ld[:, :]))
                link(v.tensor_scalar(ld[:, :], ld[:, :], capacity, 1.0, ALU.mult, ALU.min))
                link(v.tensor_tensor(p[:, :], p[:, :], ld[:, :], ALU.mult))
                softmax(1, p[:, :], w[:, :], vec)
                v.wait_ge(*const_loaded.after(0))
                link(rank.select(v, 0, w[:, :].rearrange("p (g e) -> p g e", g=1),
                                 sel[:, :].rearrange("p (g e) -> p g e", g=1), vec))
                softmax(2, w[:, :], w[:, :], vec)
                for r in range(2):
                    link(v.tensor_scalar(sel[:, :], rank.rank[:, 0, :], float(r), None, ALU.is_equal))
                    v.tensor_tensor(pick[:, r, :], sel[:, :], number[:, :], ALU.mult)
                    link(v.tensor_tensor(pick[:, 2 + r, :], sel[:, :], w[:, :], ALU.mult))
                link(v.reduce_sum(got[:, :], pick[:, :, :], AX.X))
                v.tensor_copy(chosen[:, :], got[:, 0:2]).then_inc(*ready.one())


def combine(v, i, pY, coef, Z, acc, chain):
    v.tensor_tensor(Z[:, :, :], pY.rearrange("p (e c) -> p e c", e=EXPERTS), bc(coef, C), ALU.mult).then_inc(
        *chain.one())
    v.wait_ge(*chain.latest(i))
    return v.reduce_sum(acc, Z[:, :, :].rearrange("p e c -> p c e"), AX.X)


def stage_ffn0(nc, A, h, route_dram, chosen_dram):
    E, F = EXPERTS, 128
    with Stage(nc, "ffn0") as st:
        f = Front(st)
        tail = Norm(st, PT, 4, bodies=BODIES, name="tail")
        w1 = st.sb("w1", [C + 1, 2, 2, 2, F])
        w2 = st.sb("w2", [F, 2, 2, 2, C])
        b2 = st.sb("b2", [1, 2, 2, 2, C])
        wB = st.sb("wB", [PT, 2, 2, 2])
        number = st.sb("number", [1, BATCH * 2], mybir.dt.int32)
        ones = st.sb("ones", [1, PT])
        gamma = st.sb("gamma", [PT, C])
        beta = st.sb("beta", [PT, C])
        hT = st.sb("hT", [F, 2, 2, T])
        Z = st.sb("Z", [PT, 4, 2, C])
        acc = st.sb("acc", [PT, 4, C])
        pH = st.psum("pH", [F, 2, 512])
        pY = st.psum("pY", [PT, 2, 512])
        weights = st.transfers("weights")
        hid_done = st.event("hid_done", bodies=BODIES)
        hid_ready = st.event("hid_ready", bodies=BODIES)
        y_done = st.event("y_done", bodies=BODIES)
        y_used = st.event("y_used", bodies=BODIES)
        vec = st.event("vec", bodies=BODIES)
        with st.block() as block:
            @block.sync
            def _(sp):
                cl = f.const_loaded
                const(sp, cl, number[:, :], row(chosen_dram.rearrange("b k -> (b k)")))
                const(sp, cl, f.ident[:, :], A["const_ident"])
                const(sp, cl, gamma[:, :], every_row(A["L0_ffn_gamma"], PT))
                const(sp, cl, beta[:, :], every_row(A["L0_ffn_beta"], PT))
                sp.wait_ge(*cl.after(0))

                def front(n, u):
                    f.load(sp, h, n, u)
                    sp.dma_start(wB[:, u, :, :], every_row(route_dram[bass.ds(n * 2, 2), :], PT)).then_inc(
                        *f.loaded.one(u))
                    for b in range(2):
                        for k in range(2):
                            e = sp.value_load(number[0:1, bass.ds(n * 4 + (2 * b + k), 1)], min_val=0,
                                              max_val=E - 1)
                            sp.dma_start(w1[:, u, b, k, :], A["w1b1"][bass.ds(e, 1)].rearrange(
                                "o c f -> (o c) f")).then_inc(*weights.one(u))
                            sp.dma_start(w2[:, u, b, k, :], A["L0_ffn_W2"][bass.ds(e, 1)].rearrange(
                                "o f c -> (o f) c")).then_inc(*weights.one(u))
                            sp.dma_start(b2[:, u, b, k, :], A["L0_ffn_b2"][bass.ds(e, 1), :]).then_inc(
                                *weights.one(u))

                def main(n, u, ahead):
                    ahead()
                    f.store(sp, h, n, u)
                pipelined(sp, front, main)
                f.all_stored(sp)

            @block.gpsimd
            def _(g):
                g.wait_ge(*f.memset_done.after(0))

                def front(n, u):
                    f.norm.power(g, n, 0)

                def main(n, u, ahead):
                    ahead()
                    tail.square_pool(g, n, 0, tail.xc[:, :, :])
                    tail.power(g, n, 0)
                pipelined(g, front, main)

            @block.tensor
            def _(pe):
                pe.wait_ge(*f.const_loaded.after(0))
                pe.wait_ge(*f.memset_done.after(0))

                def front(n, u):
                    f.transpose(pe, n, u)

                def main(n, u, ahead):
                    pe.wait_ge(*f.xT_ready.after(n))
                    pe.wait_ge(*weights.after(n, u))
                    pe.wait_ge(*hid_ready.before(n))
                    st.held(pe)
                    for b in range(2):
                        for k in range(2):
                            ins = pe.matmul(pH[:, b, k * T:k * T + T], w1[:, u, b, k, :], f.xT[:, u, b, :],
                                            start=True, stop=True)
                        ins.then_inc(*hid_done.one())
                    ahead()
                    pe.wait_ge(*y_used.lagging(n))
                    st.held(pe)
                    for b in range(2):
                        pe.wait_ge(*hid_ready.after(n, b))
                        st.held(pe)
                        for t in range(2):
                            g0 = (2 * t + b) * 2 * C
                            pe.matmul(pY[:, u, g0:g0 + 2 * C], ones[:, :], b2[:, u, b, :, :], start=True,
                                      stop=False)
                            for k in range(2):
                                ins = pe.matmul(pY[:, u, g0 + k * C:g0 + k * C + C],
                                                hT[:, b, k, t * OFF:t * OFF + PT], w2[:, u, b, k, :], start=False,
                                                stop=(k == 1))
                    ins.then_inc(*y_done.one())
                pipelined(pe, front, main)

            @block.scalar
            def _(a):
                def front(n, u):
                    f.square(a, n, u)

                def main(n, u, ahead):
                    a.wait_ge(*y_done.before(n))
                    for b in range(2):
                        a.wait_ge(*hid_done.after(n, b))
                        a.activation(hT[:, b, :, :].rearrange("f k t -> f (k t)"), pH[:, b, 0:2 * T],
                                     ACT.Gelu).then_inc(*hid_ready.one())
                    ahead()
                pipelined(a, front, main)

            @block.vector
            def _(v):
                v.memset(ones[:, :], 1.0)
                v.memset(tail.expo[:, :], -0.5)
                f.memsets(v)
                v.wait_ge(*f.memset_done.after(0))
                v.wait_ge(*f.const_loaded.after(0))

                def front(n, u):
                    f.normalise(v, n, u)
                    f.channels(v, n, u)

                def main(n, u, ahead):
                    def link(ins):
                        ins.then_inc(*vec.one())
                        v.wait_ge(*vec.latest(n))
                    ahead()
                    v.wait_ge(*y_done.after(n))
                    for t in range(2):
                        ins = v.tensor_tensor(Z[:, 2 * t:2 * t + 2, :, :].rearrange("p b k c -> p (b k) c"),
                                              pY[:, u, t * 4 * C:(t + 1) * 4 * C].rearrange("p (g c) -> p g c", g=4),
                                              bc(wB[:, u, :, :].rearrange("p b k -> p (b k)"), C), ALU.mult)
                    ins.then_inc(*y_used.one())
                    v.wait_ge(*y_used.after(n))
                    link(v.tensor_tensor(acc[:, :, :], Z[:, :, 0, :], Z[:, :, 1, :], ALU.add))
                    link(v.tensor_tensor(acc[:, :, :], acc[:, :, :], g4(f.xn[:, u, :, :, :]), ALU.add))
                    tail.center(v, n, acc[:, :, :], vec)
                    link(tail.scale(v, n, 0, tail.xc[:, :, :], acc[:, :, :], 1e-5, vec))
                    link(v.tensor_tensor(acc[:, :, :], acc[:, :, :], bcm(gamma[:, :], 1, 4), ALU.mult))
                    link(v.tensor_tensor(acc[:, :, :], acc[:, :, :], bcm(beta[:, :], 1, 4), ALU.add))
                    v.wait_ge(*f.stored.lagging(n, u))
                    v.tensor_tensor(g4(f.H1[:, u, :, :, :]), acc[:, :, :], g4(f.X[:, u, :, :, :]),
                                    ALU.add).then_inc(*f.h_ready.one())
                pipelined(v, front, main)


LOW = T + PT


def stage_retention1(nc, A, h):
    with Stage(nc, "ret1") as st:
        p = Pair(st)
        X, xn, xT, norm, vec, H1 = p.X, p.xn, p.xT, p.norm, p.vec, p.H1
        W = st.sb("W", [C, 5, C])
        cs = st.sb("cos_sin", [C, 2, T])
        decay = st.sb("decay", [PT, LOW])
        t1 = st.sb("t1", [C, 2, 2, T])
        t2 = st.sb("t2", [C, 2, 2, T])
        qk = st.sb("qk", [C, 2, 2, T])
        V = st.sb("V", [PT, 4, C])
        P = st.sb("P", [PT, 2, LOW])
        pX = st.psum("pX", [C, 2, 256])
        pR = st.psum("pR", [C, 4, 512])
        pV = st.psum("pV", [PT, 2, 4, C])
        pS = st.psum("pS", [PT, 2, 512])
        r_done = st.event("r_done")
        v_done = st.event("v_done")
        v_ready = st.event("v_ready")
        qk_ready = st.event("qk_ready")
        s_done = st.event("s_done")
        p_ready = st.event("p_ready")
        o_done = st.event("o_done")
        with st.block() as block:
            @block.sync
            def _(sp):
                cl = p.const_loaded
                const(sp, cl, p.ident[:, :], A["const_ident"])
                for k, n in enumerate(("Q", "Qx", "K", "Kx", "V")):
                    const(sp, cl, W[:, k, :], A[f"L1_attn_W_{n}"])
                const(sp, cl, cs[:, :, :], A["const_rope64"].rearrange("s c t -> c s t"))
                const(sp, cl, decay[:, :], A["const_decay"])
                with sp.Fori(0, PAIRS) as i:
                    sp.wait_ge(*p.h_ready.before(i))
                    st.held(sp)
                    for ins in load_pair(sp, X, h, i):
                        ins.then_inc(*p.loaded.one())
                    sp.wait_ge(*p.h_ready.after(i))
                    st.held(sp)
                    for ins in store_pair(sp, h, H1, i):
                        ins.then_inc(*p.stored.one())
                sp.wait_ge(*p.stored.after(PAIRS - 1))

            @block.gpsimd
            def _(g):
                g.wait_ge(*p.memset_done.after(0))
                with g.Fori(0, PAIRS) as i:
                    norm.power(g, i, 0)

            @block.tensor
            def _(pe):
                pe.wait_ge(*p.const_loaded.after(0))
                pe.wait_ge(*p.memset_done.after(0))
                with pe.Fori(0, PAIRS) as i:
                    pe.wait_ge(*p.xn_ready.after(i))
                    st.held(pe)
                    transpose_rows(pe, pX, xn, p.ident).then_inc(*p.xT_done.one())
                    pe.wait_ge(*p.xT_ready.after(i))
                    st.held(pe)
                    for k in range(4):
                        pe.matmul(pR[:, k, 0:2 * T], W[:, k, :], xT[0:C, :, :], start=True,
                                  stop=True).then_inc(*r_done.one())
                    for t in range(2):
                        for b in range(2):
                            ins = pe.matmul(pV[:, 0, 2 * t + b, :], xT[0:C, b, t * OFF:t * OFF + PT], W[:, 4, :],
                                            start=True, stop=True)
                    ins.then_inc(*v_done.one())
                    pe.wait_ge(*qk_ready.after(i))
                    st.held(pe)
                    for b in range(2):
                        pe.matmul(pS[:, b, 0:T], qk[:, 1, b, 0:PT], qk[:, 0, b, :], start=True, stop=True)
                        pe.matmul(pS[:, b, T:LOW], qk[:, 1, b, OFF:T], qk[:, 0, b, OFF:T], start=True,
                                  stop=True).then_inc(*s_done.one())
                    pe.wait_ge(*v_ready.after(i))
                    st.held(pe)
                    for b in range(2):
                        pe.wait_ge(*p_ready.after(i, b))
                        st.held(pe)
                        pe.matmul(pV[:, 1, b, :], P[0:OFF, b, 0:PT], V[0:OFF, b, :], start=True, stop=True)
                        pe.matmul(pV[:, 1, 2 + b, :], P[0:OFF, b, OFF:T], V[0:OFF, b, :], start=True, stop=False)
                        ins = pe.matmul(pV[:, 1, 2 + b, :], P[:, b, T:LOW], V[:, 2 + b, :], start=False, stop=True)
                    ins.then_inc(*o_done.one())

            @block.scalar
            def _(a):
                with a.Fori(0, PAIRS) as i:
                    norm.square(a, i, 0, norm.xc[:, :, :])
                    a.wait_ge(*v_done.after(i))
                    a.activation(V[:, :, :], pV[:, 0, :, :], ACT.Copy).then_inc(*v_ready.one())

            @block.vector
            def _(v):
                p.memsets(v)
                v.wait_ge(*p.memset_done.after(0))
                v.wait_ge(*p.const_loaded.after(0))
                with v.Fori(0, PAIRS) as i:
                    p.normalise(v, i)
                    v.wait_ge(*p.xT_done.after(i))
                    v.tensor_copy(xT[0:C, :, :], pX[:, :, 0:T]).then_inc(*p.xT_ready.one())
                    for k in range(2):
                        v.wait_ge(*r_done.after(i, 2 * k))
                        v.tensor_tensor(t1[:, k, :, :], pR[:, 2 * k, 0:2 * T].rearrange("c (b t) -> c b t", b=2),
                                        bcm(cs[:, 0, :], 1, 2), ALU.mult)
                        v.wait_ge(*r_done.after(i, 2 * k + 1))
                        v.tensor_tensor(t2[:, k, :, :], pR[:, 2 * k + 1, 0:2 * T].rearrange(
                            "c (b t) -> c b t", b=2), bcm(cs[:, 1, :], 1, 2), ALU.mult).then_inc(*vec.one())
                        v.wait_ge(*vec.latest(i))
                        v.tensor_tensor(qk[:, k, :, :], t1[:, k, :, :], t2[:, k, :, :], ALU.add).then_inc(
                            *qk_ready.one())
                    for b in range(2):
                        v.wait_ge(*s_done.after(i, b))
                        v.tensor_tensor(P[:, b, :], pS[:, b, 0:LOW], decay[:, :], ALU.mult).then_inc(*p_ready.one())
                    v.wait_ge(*o_done.after(i))
                    v.wait_ge(*p.stored.before(i))
                    v.tensor_tensor(g4(H1[:, :, :, :]), pV[:, 1, :, :], g4(X[:, :, :, :]), ALU.add).then_inc(
                        *p.h_ready.one())


def stage_attention1(nc, A, h, hx_dram, flatT_dram, mix_dram):
    H, D, KV = 4, 16, 2
    E = EXPERTS
    with Stage(nc, "att1") as st:
        p = Pair(st)
        X, xn, xT, norm, vec, H1 = p.X, p.xn, p.xT, p.norm, p.vec, p.H1
        wqk = st.sb("wqk", [C + 1, 4, H, 32])
        wv = st.sb("wv", [C + 1, KV, D + 1])
        wo = st.sb("wo", [C, C])
        wr = st.sb("wr", [C, E])
        ln1 = st.sb("ln1", [PT, C])
        ln2 = st.sb("ln2", [PT, C])
        cs = st.sb("cos_sin", [128, 2, T])
        maskQ = st.sb("maskQ", [PT, LOW])
        maskK = st.sb("maskK", [PT, LOW])
        r1 = st.sb("r1", [PT, 4, C])
        t1 = st.sb("t1", [128, 2, T])
        t2 = st.sb("t2", [128, 2, T])
        qT = st.sb("qT", [128, 2, T])
        kT = st.sb("kT", [128, 2, T])
        qmT = st.sb("qmT", [128, 2, T])
        V = st.sb("V", [PT, 4, KV, D + 1])
        M = st.sb("M", [PT, 2, 2, H, 32])
        SM = st.sb("SM", [PT, 2, LOW])
        EX = st.sb("EX", [PT, 2, H, LOW])
        rden = st.sb("rden", [PT, 4, H])
        of = st.sb("of", [PT, 2, 2, C])
        oT = st.sb("oT", [C, 2, T])
        x2 = st.sb("x2", [PT, 4, C])
        fl = st.sb("fl", [PT, 2, 2, C])
        flT = st.sb("flT", [C, 2, T])
        lg = st.sb("lg", [PT, 4, E])
        lsum = st.sb("lsum", [PT, 4])
        sel = st.sb("sel", [PT, 4, E])
        mix = st.sb("mix", [PT, 2, 2, E])
        rank = Rank(st, PT, 4, 2)
        pX = st.psum("pX", [C, 2, 256])
        pR = st.psum("pR", [128, 2, 512])
        pS = st.psum("pS", [PT, 4, 512])
        pO = st.psum("pO", [PT, 4, 128])

        cleared = st.event("cleared")
        zeroed = st.event("zeroed")
        r_done = st.event("r_done")
        q_ready = st.event("q_ready")
        k_ready = st.event("k_ready")
        v_done = st.event("v_done")
        v_ready = st.event("v_ready")
        s_done = st.event("s_done")
        max_ready = st.event("max_ready")
        m_done = st.event("m_done")
        qm_ready = st.event("qm_ready")
        st_done = st.event("st_done")
        masked = st.event("masked")
        exp_ready = st.event("exp_ready")
        o_done = st.event("o_done")
        o_ready = st.event("o_ready")
        y_done = st.event("y_done")
        fl_ready = st.event("fl_ready")
        flT_done = st.event("flT_done")
        flT_ready = st.event("flT_ready")
        l_done = st.event("l_done")
        l_shifted = st.event("l_shifted")
        l_exp = st.event("l_exp")
        mix_ready = st.event("mix_ready")
        with st.block() as block:
            @block.sync
            def _(sp):
                cl = p.const_loaded
                const(sp, cl, p.ident[:, :], A["const_ident"])
                const(sp, cl, cs[:, :, :], A["const_rope16"].rearrange("s c t -> c s t"))
                const(sp, cl, maskQ[:, :], A["const_maskQ"])
                const(sp, cl, maskK[:, :], A["const_maskK"])
                const(sp, cl, wo[:, :], A["L1_ffn_woT"])
                const(sp, cl, wr[:, :], A["L1_ffn_router_wT"])
                const(sp, cl, ln1[:, :], every_row(A["L1_ffn_ln1_w"], PT))
                const(sp, cl, ln2[:, :], every_row(A["L1_ffn_ln2_w"], PT))
                const(sp, cl, rank.earlier[:, :], every_row(A["const_earlier"], PT))
                sp.wait_ge(*zeroed.after(0))
                for k, n in enumerate(("wq", "wqx")):
                    const(sp, cl, wqk[0:C, k, :, 0:D], A[f"L1_ffn_{n}T"].rearrange("c (h d) -> c h d", h=H))
                for k, n in enumerate(("wk", "wkx")):
                    for r in range(H // KV):
                        const(sp, cl, wqk[0:C, 2 + k, :, 0:D].rearrange("c (k r) d -> c r k d", k=KV)[:, r, :, :],
                              A[f"L1_ffn_{n}T"].rearrange("c (k d) -> c k d", k=KV))
                const(sp, cl, wv[0:C, :, 0:D], A["L1_ffn_wvT"].rearrange("c (k d) -> c k d", k=KV))
                with sp.Fori(0, PAIRS) as i:
                    sp.wait_ge(*p.h_ready.before(i))
                    st.held(sp)
                    for ins in load_pair(sp, X, h, i):
                        ins.then_inc(*p.loaded.one())
                    sp.wait_ge(*p.h_ready.after(i))
                    st.held(sp)
                    for ins in store_pair(sp, hx_dram, H1, i):
                        ins.then_inc(*p.stored.one())
                    sp.wait_ge(*flT_ready.after(i))
                    st.held(sp)
                    sp.dma_start(flatT_dram[bass.ds(i, 1), :, :].rearrange("o c t -> (o c) t"),
                                 flT[:, :, :].rearrange("c b t -> c (b t)")).then_inc(*p.stored.one())
                    sp.wait_ge(*mix_ready.after(i))
                    st.held(sp)
                    for ins in store_pair(sp, mix_dram, mix, i, E):
                        ins.then_inc(*p.stored.one())
                sp.wait_ge(*p.stored.after(PAIRS - 1))

            @block.gpsimd
            def _(g):
                g.wait_ge(*p.memset_done.after(0))
                with g.Fori(0, PAIRS) as i:
                    for k in range(3):
                        norm.power(g, i, k)

            @block.tensor
            def _(pe):
                pe.wait_ge(*p.const_loaded.after(0))
                pe.wait_ge(*p.memset_done.after(0))
                with pe.Fori(0, PAIRS) as i:
                    pe.wait_ge(*p.xn_ready.after(i))
                    st.held(pe)
                    transpose_rows(pe, pX, p.H1, p.ident).then_inc(*p.xT_done.one())
                    pe.wait_ge(*p.xT_ready.after(i, 0))
                    for k in range(4):
                        if k >= 2:
                            pe.wait_ge(*q_ready.after(i))
                        pe.matmul(pR[:, k % 2, 0:2 * T], wqk[:, k, :, :], xT[:, :, :], start=True,
                                  stop=True).then_inc(*r_done.one())
                    st.held(pe)
                    for t in range(2):
                        for b in range(2):
                            ins = pe.matmul(pO[:, 2 * t + b, 0:KV * (D + 1)], xT[:, b, t * OFF:t * OFF + PT],
                                            wv[:, :, :], start=True, stop=True)
                    ins.then_inc(*v_done.one())
                    pe.wait_ge(*k_ready.after(i))
                    for b in range(2):
                        for hd in range(H):
                            if b == 0:
                                pe.wait_ge(*exp_ready.before(i))
                            else:
                                pe.wait_ge(*max_ready.after(i, hd))
                            r = 32 * hd
                            pe.matmul(pS[:, hd, 0:PT], qT[r:r + D, b, 0:PT], kT[r:r + D, b, 0:PT], start=True,
                                      stop=True, tile_position=(r, 0))
                            pe.matmul(pS[:, hd, PT:LOW], qT[r:r + D, b, OFF:T], kT[r:r + D, b, :], start=True,
                                      stop=True, tile_position=(r, 0)).then_inc(*s_done.one())
                    pe.wait_ge(*max_ready.after(i))
                    for b in range(2):
                        for t in range(2):
                            ins = pe.matmul(pR[:, 0, b * T + t * OFF:b * T + t * OFF + ROWS[t]],
                                            M[0:ROWS[t], t, b, :, :], p.ident[0:ROWS[t], 0:ROWS[t]],
                                            start=True, stop=True)
                    ins.then_inc(*m_done.one())
                    pe.wait_ge(*qm_ready.after(i))
                    for b in range(2):
                        for hd in range(H):
                            if b == 1:
                                pe.wait_ge(*masked.after(i, hd))
                            r = 32 * hd
                            pe.matmul(pS[:, hd, 0:T], kT[r:r + D + 1, b, 0:PT], qmT[r:r + D + 1, b, :], start=True,
                                      stop=True, tile_position=(r, 0))
                            pe.matmul(pS[:, hd, T:LOW], kT[r:r + D + 1, b, OFF:T], qmT[r:r + D + 1, b, OFF:T],
                                      start=True, stop=True, tile_position=(r, 0)).then_inc(*st_done.one())
                    pe.wait_ge(*v_ready.after(i))
                    for b in range(2):
                        for hd in range(H):
                            pe.wait_ge(*exp_ready.after(i, b * H + hd))
                            kv, c0 = hd // (H // KV), hd * (D + 1)
                            pe.matmul(pO[:, b, c0:c0 + D + 1], EX[0:OFF, b, hd, 0:PT], V[0:OFF, b, kv, :],
                                      start=True, stop=True)
                            pe.matmul(pO[:, 2 + b, c0:c0 + D + 1], EX[0:OFF, b, hd, OFF:T], V[0:OFF, b, kv, :],
                                      start=True, stop=False)
                            ins = pe.matmul(pO[:, 2 + b, c0:c0 + D + 1], EX[:, b, hd, T:LOW], V[:, 2 + b, kv, :],
                                            start=False, stop=True)
                    ins.then_inc(*o_done.one())
                    pe.wait_ge(*o_ready.after(i))
                    st.held(pe)
                    transpose_rows(pe, pX, of, p.ident).then_inc(*p.xT_done.one())
                    pe.wait_ge(*p.xT_ready.after(i, 1))
                    st.held(pe)
                    for t in range(2):
                        for b in range(2):
                            n = 2 * t + b
                            ins = pe.matmul(pR[0:PT, 1, n * C:(n + 1) * C], oT[:, b, t * OFF:t * OFF + PT], wo[:, :],
                                            start=True, stop=True)
                    ins.then_inc(*y_done.one())
                    pe.wait_ge(*fl_ready.after(i))
                    st.held(pe)
                    transpose_rows(pe, pX, fl, p.ident).then_inc(*flT_done.one())
                    pe.wait_ge(*flT_ready.after(i))
                    st.held(pe)
                    for t in range(2):
                        for b in range(2):
                            n = 2 * t + b
                            ins = pe.matmul(pR[0:PT, 0, n * E:(n + 1) * E], flT[:, b, t * OFF:t * OFF + PT],
                                            wr[:, :], start=True, stop=True)
                    ins.then_inc(*l_done.one())

            @block.scalar
            def _(a):
                with a.Fori(0, PAIRS) as i:
                    norm.square(a, i, 0, norm.xc[:, :, :])
                    norm.square(a, i, 1, g4(xn[:, :, :, :]))
                    a.wait_ge(*v_done.after(i))
                    a.activation(V[:, :, :, :].rearrange("p g k d -> p g (k d)"), pO[:, :, 0:KV * (D + 1)],
                                 ACT.Copy).then_inc(*v_ready.one())
                    for b in range(2):
                        for hd in range(H):
                            n = b * H + hd
                            a.wait_ge(*masked.after(i, n))
                            a.activation(EX[:, b, hd, :], EX[:, b, hd, :], ACT.Exp, scale=D ** -0.5).then_inc(
                                *exp_ready.one())
                    norm.square(a, i, 2, x2[:, :, :])
                    a.wait_ge(*l_shifted.after(i))
                    a.activation(lg[:, :, :], lg[:, :, :], ACT.Exp).then_inc(*l_exp.one())

            @block.vector
            def _(v):
                v.memset(wqk[:, :, :, :], 0.0)
                v.memset(M[:, :, :, :, :], 0.0)
                v.memset(wv[:, :, :], 0.0).then_inc(*cleared.one())
                v.wait_ge(*cleared.after(0))
                v.memset(wqk[C:C + 1, 2, :, D:D + 1], -1.0)
                v.memset(wv[C:C + 1, :, D:D + 1], 1.0).then_inc(*zeroed.one())
                p.memsets(v)
                v.wait_ge(*p.memset_done.after(0))
                v.wait_ge(*p.const_loaded.after(0))

                def link(ins):
                    ins.then_inc(*vec.one())
                    v.wait_ge(*vec.latest(i))

                def rotate(k, dst, sig):
                    v.wait_ge(*r_done.after(i, 2 * k))
                    v.tensor_tensor(t1[:, :, :], pR[:, 0, 0:2 * T].rearrange("c (b t) -> c b t", b=2),
                                    bcm(cs[:, 0, :], 1, 2), ALU.mult)
                    v.wait_ge(*r_done.after(i, 2 * k + 1))
                    link(v.tensor_tensor(t2[:, :, :], pR[:, 1, 0:2 * T].rearrange("c (b t) -> c b t", b=2),
                                         bcm(cs[:, 1, :], 1, 2), ALU.mult))
                    v.tensor_tensor(dst, t1[:, :, :], t2[:, :, :], ALU.add).then_inc(*sig.one())

                with v.Fori(0, PAIRS) as i:
                    v.wait_ge(*p.loaded.after(i))
                    norm.center(v, i, g4(X[:, :, :, :]), vec)
                    norm.scale(v, i, 0, norm.xc[:, :, :], g4(xn[:, :, :, :]), 1e-5, vec).then_inc(
                        *norm.centered.one())
                    link(norm.scale(v, i, 1, g4(xn[:, :, :, :]), r1[:, :, :], 1e-6, vec))
                    v.wait_ge(*p.stored.before(i))
                    v.tensor_tensor(g4(p.H1[:, :, :, :]), r1[:, :, :], bcm(ln1[:, :], 1, 4), ALU.mult).then_inc(
                        *p.xn_ready.one())
                    v.wait_ge(*p.xT_done.after(i, 0))
                    v.tensor_copy(xT[0:C, :, :], pX[:, :, 0:T]).then_inc(*p.xT_ready.one())
                    rotate(0, qT[:, :, :], q_ready)
                    rotate(1, kT[:, :, :], k_ready)
                    for b in range(2):
                        for hd in range(H):
                            v.wait_ge(*s_done.after(i, b * H + hd))
                            v.tensor_tensor(SM[:, hd % 2, :], pS[:, hd, 0:LOW], maskQ[:, :], ALU.add).then_inc(
                                *vec.one())
                            v.wait_ge(*vec.latest(i))
                            v.reduce_max(M[:, 0, b, hd, D:D + 1], SM[:, hd % 2, 0:PT], AX.X)
                            v.reduce_max(M[:, 1, b, hd, D:D + 1], SM[:, hd % 2, PT:LOW], AX.X).then_inc(
                                *max_ready.one())
                    v.wait_ge(*m_done.after(i))
                    v.tensor_tensor(qmT[:, :, :], qT[:, :, :], pR[:, 0, 0:2 * T].rearrange(
                        "c (b t) -> c b t", b=2), ALU.add).then_inc(*qm_ready.one())
                    for b in range(2):
                        for hd in range(H):
                            v.wait_ge(*st_done.after(i, b * H + hd))
                            v.tensor_tensor(EX[:, b, hd, :], pS[:, hd, 0:LOW], maskK[:, :], ALU.add).then_inc(
                                *masked.one())
                    v.wait_ge(*o_done.after(i))
                    o5 = pO[:, :, 0:H * (D + 1)].rearrange("p g (h d) -> p g h d", h=H)
                    link(v.reciprocal(rden[:, :, :], o5[:, :, :, D]))
                    for t in range(2):
                        for b in range(2):
                            g = 2 * t + b
                            ins = v.tensor_tensor(of[:, t, b, :].rearrange("p (h d) -> p h d", h=H),
                                                  o5[:, g, :, 0:D], bc(rden[:, g, :], D), ALU.mult)
                    ins.then_inc(*o_ready.one())
                    v.wait_ge(*p.xT_done.after(i, 1))
                    v.tensor_copy(oT[:, :, :], pX[:, :, 0:T]).then_inc(*p.xT_ready.one())
                    v.wait_ge(*y_done.after(i))
                    v.tensor_tensor(x2[:, :, :], g4(xn[:, :, :, :]), pR[0:PT, 1, 0:4 * C].rearrange(
                        "p (g c) -> p g c", g=4), ALU.add).then_inc(*norm.centered.one())
                    v.wait_ge(*norm.centered.latest(i))
                    v.tensor_tensor(g4(H1[:, :, :, :]), g4(X[:, :, :, :]), x2[:, :, :], ALU.add).then_inc(
                        *p.h_ready.one())
                    link(norm.scale(v, i, 2, x2[:, :, :], g4(fl[:, :, :, :]), 1e-6, vec))
                    v.tensor_tensor(g4(fl[:, :, :, :]), g4(fl[:, :, :, :]), bcm(ln2[:, :], 1, 4),
                                    ALU.mult).then_inc(*fl_ready.one())
                    v.wait_ge(*flT_done.after(i))
                    v.tensor_copy(flT[:, :, :], pX[:, :, 0:T]).then_inc(*flT_ready.one())
                    v.wait_ge(*l_done.after(i))
                    pl = pR[0:PT, 0, 0:4 * E].rearrange("p (g e) -> p g e", g=4)
                    link(v.reduce_max(lsum[:, :], pl, AX.X))
                    v.tensor_tensor(lg[:, :, :], pl, bc(lsum[:, :], E), ALU.subtract).then_inc(*l_shifted.one())
                    v.wait_ge(*l_exp.after(i))
                    link(v.reduce_sum(lsum[:, :], lg[:, :, :], AX.X))
                    link(v.reciprocal(lsum[:, :], lsum[:, :]))
                    link(v.tensor_tensor(lg[:, :, :], lg[:, :, :], bc(lsum[:, :], E), ALU.mult))
                    link(rank.select(v, i, lg[:, :, :], sel[:, :, :], vec))
                    link(v.tensor_tensor(lg[:, :, :], lg[:, :, :], sel[:, :, :], ALU.mult))
                    link(v.reduce_sum(lsum[:, :], lg[:, :, :], AX.X))
                    link(v.tensor_scalar(lsum[:, :], lsum[:, :], 1e-9, None, ALU.add))
                    link(v.reciprocal(lsum[:, :], lsum[:, :]))
                    v.tensor_tensor(g4(mix[:, :, :, :]), lg[:, :, :], bc(lsum[:, :], E), ALU.mult).then_inc(
                        *mix_ready.one())


def split_weights(v, w, rest, hm, mh, lh, chain):
    top, low = slice(0, C), slice(C, 2 * C)

    def link(ins):
        ins.then_inc(*chain.one())
        v.wait_ge(*chain.latest(0))
    link(v.tensor_copy(lh[:, :], w[:, :]))
    link(v.tensor_tensor(rest[:, :], w[:, :], lh[:, :], ALU.subtract))
    link(v.tensor_copy(mh[:, :], rest[:, :]))
    v.tensor_tensor(rest[:, :], rest[:, :], mh[:, :], ALU.subtract)
    v.tensor_copy(hm[top, :], lh[top, :])
    link(v.tensor_copy(hm[low, :], mh[low, :]))
    v.tensor_copy(mh[low, :], lh[low, :])
    link(v.tensor_copy(lh[top, :], rest[top, :]))


class Thirds:

    def __init__(self, st, name, columns):
        self.st = st
        self.hm = st.sb(name + "_hm", [2 * C, 2, columns], BF16)
        self.hl = st.sb(name + "_hl", [2 * C, 2, columns], BF16)
        self.rest = st.sb(name + "_rest", [2 * C, columns])
        self.chain = st.event(name + "_split", bodies=BODIES)
        self.ready = st.event(name + "_ready", bodies=BODIES)

    def split(self, e, n, u, x):
        top, low = slice(0, C), slice(C, 2 * C)
        hm, hl, rest = (y.rearrange("c (b t) -> c b t", b=2) for y in (self.hm[:, u, :], self.hl[:, u, :],
                                                                       self.rest[:, :]))

        def link(ins):
            ins.then_inc(*self.chain.one())
            e.wait_ge(*self.chain.latest(n))
            self.st.held(e)
        e.wait_ge(*self.ready.before(n))
        self.st.held(e)
        link(e.tensor_copy(hl, x))
        link(e.tensor_tensor(rest, x, hl, ALU.subtract))
        link(e.tensor_copy(hm[top], hl[top]))
        link(e.tensor_copy(hm[low], rest[low]))
        link(e.tensor_tensor(rest[low], rest[low], hm[low], ALU.subtract))
        e.tensor_copy(hl[low], rest[low]).then_inc(*self.ready.one())

    def product(self, pe, out, u, hm, mh, lh):
        pe.matmul(out, hm, self.hm[:, u, :], start=True, stop=False)
        pe.matmul(out, mh, self.hm[:, u, :], start=False, stop=False)
        return pe.matmul(out, lh, self.hl[:, u, :], start=False, stop=True)


def stage_experts1(nc, A, h, hx_dram, flatT_dram, mix_dram):
    E, HID, HC = EXPERTS, 170, 85
    NCH = E * 2
    with Stage(nc, "moe1") as st:
        xT = st.sb("xT", [2 * C, 2, 2 * T])
        x3 = Thirds(st, "x3", 2 * T)
        w = st.sb("w", [2 * C, E * HID])
        rest = st.sb("rest", [2 * C, E * HID])
        stacks = [[st.sb(f"{x}_{y}", [2 * C, E * HID], BF16) for y in ("hm", "mh", "lh")] for x in ("w1", "w3")]
        w2 = st.sb("w2", [HC, NCH, C])
        X = st.sb("X", [PT, 2, 2, 2, C])
        H1 = st.sb("H1", [PT, 2, 2, 2, C])
        mix = st.sb("mix", [PT, 2, 2, 2, E])
        sl = st.sb("silu", [HC, 2, 2 * T])
        hT = st.sb("hT", [HC, 2, NCH, 2 * T])
        Z = st.sb("Z", [PT, E, C])
        acc = st.sb("acc", [PT, 4, C])
        pA = st.psum("pA", [HC, 2, 512])
        pG = st.psum("pG", [HC, 2, 512])
        pY = st.psum("pY", [PT, 4, 512])
        w1_loaded = st.event("w1_loaded", dma=True)
        w3_loaded = st.event("w3_loaded", dma=True)
        const_loaded = st.event("const_loaded", dma=True)
        w_split = st.event("w_split")
        w_used = st.event("w_used")
        weights_ready = st.event("weights_ready")
        xT_loaded = st.transfers("xT_loaded", start=0)
        loaded = st.transfers("loaded")
        stored = st.transfers("stored")
        gate_done = st.event("gate_done", bodies=BODIES)
        silu_ready = st.event("silu_ready", bodies=BODIES)
        hid_ready = st.event("hid_ready", bodies=BODIES)
        y_done = st.event("y_done", bodies=BODIES)
        y_used = st.event("y_used", bodies=BODIES)
        vec = st.event("vec", bodies=BODIES)
        h_ready = st.event("h_ready", bodies=BODIES)
        with st.block() as block:
            @block.sync
            def _(sp):
                for half in range(2):
                    const(sp, w1_loaded, w[half * C:(half + 1) * C, :], A["L1_ffn_w1T"])
                const(sp, const_loaded, w2[:, :, :], A["L1_ffn_w2T"].rearrange("(n p) c -> p n c", p=HC))
                sp.wait_ge(*w_used.after(0))
                for half in range(2):
                    const(sp, w3_loaded, w[half * C:(half + 1) * C, :], A["L1_ffn_w3T"])

                def front(n, u):
                    sp.wait_ge(*h_ready.lagging(n))
                    st.held(sp)
                    for ins in (load_pair(sp, X[:, u, :, :, :], hx_dram, n)
                                + load_pair(sp, mix[:, u, :, :, :], mix_dram, n, E)):
                        ins.then_inc(*loaded.one(u))

                def main(n, u, ahead):
                    ahead()
                    sp.wait_ge(*h_ready.after(n))
                    st.held(sp)
                    for ins in store_pair(sp, h, H1[:, u, :, :, :], n):
                        ins.then_inc(*stored.one(u))
                pipelined(sp, front, main)
                for n in (PAIRS - 2, PAIRS - 1):
                    sp.wait_ge(*stored.after(n, n % 2))

            @block.gpsimd
            def _(g):
                def front(n, u):
                    g.wait_ge(*x3.ready.before(n))
                    st.held(g)
                    for half in range(2):
                        g.dma_start(xT[half * C:(half + 1) * C, u, :], flatT_dram[bass.ds(n, 1), :, :].rearrange(
                            "o c t -> (o c) t")).then_inc(*xT_loaded.one(u))
                    g.wait_ge(*xT_loaded.after(n, u))
                    g.wait_ge(*gate_done.lagging(n))
                    st.held(g)
                    x3.split(g, n, u, xT[:, u, :].rearrange("c (b t) -> c b t", b=2))

                def main(n, u, ahead):
                    ahead()
                pipelined(g, front, main)

            @block.tensor
            def _(pe):
                pe.wait_ge(*const_loaded.after(0))
                pe.wait_ge(*weights_ready.after(0))

                def front(n, u, k):
                    if k == 0:
                        pe.wait_ge(*x3.ready.after(n))
                    pe.wait_ge(*hid_ready.after(n, k - 2))
                    st.held(pe)
                    cols = slice(k * HC, (k + 1) * HC)
                    x3.product(pe, pA[:, k % 2, 0:2 * T], u, *[x[:, cols] for x in stacks[0]])
                    x3.product(pe, pG[:, k % 2, 0:2 * T], u, *[x[:, cols] for x in stacks[1]]).then_inc(
                        *gate_done.one())

                def main(n, u, ahead):
                    for step in range(NCH):
                        ahead(step)
                        if step >= 12:
                            continue
                        g, part = step // 3, step % 3
                        t, b = g // 2, g % 2
                        if part == 0:
                            pe.wait_ge(*y_used.before(n))
                            pe.wait_ge(*hid_ready.after(n))
                            st.held(pe)
                        for k in range((0, 6, 12)[part], (6, 12, 16)[part]):
                            e = k // 2
                            ins = pe.matmul(pY[:, g, e * C:(e + 1) * C],
                                            hT[:, u, k, b * T + t * OFF:b * T + t * OFF + PT], w2[:, k, :],
                                            start=(k % 2 == 0), stop=(k % 2 == 1))
                        if part == 2:
                            ins.then_inc(*y_done.one())
                pipelined(pe, front, main, steps=NCH)

            @block.scalar
            def _(a):
                def front(n, u, k):
                    a.wait_ge(*gate_done.after(n, k))
                    a.activation(sl[:, k % 2, :], pA[:, k % 2, 0:2 * T], ACT.Silu).then_inc(*silu_ready.one())

                def main(n, u, ahead):
                    for step in range(NCH):
                        ahead(step)
                pipelined(a, front, main, steps=NCH)

            @block.vector
            def _(v):
                v.wait_ge(*w1_loaded.after(0))
                split_weights(v, w, rest, *stacks[0], w_split)
                v.sem_inc(*w_used.one())
                v.wait_ge(*w3_loaded.after(0))
                split_weights(v, w, rest, *stacks[1], w_split)
                v.sem_inc(*weights_ready.one())

                def front(n, u, k):
                    v.wait_ge(*silu_ready.after(n, k))
                    v.tensor_tensor(hT[:, u, k, :], sl[:, k % 2, :], pG[:, k % 2, 0:2 * T], ALU.mult).then_inc(
                        *hid_ready.one())

                def main(n, u, ahead):
                    v.wait_ge(*loaded.after(n, u))
                    for step in range(NCH):
                        ahead(step)
                        if step in (4, 7, 10, 13):
                            g = (step - 4) // 3
                            t, b = g // 2, g % 2
                            v.wait_ge(*y_done.after(n, g))
                            combine(v, n, pY[:, g, :], mix[:, u, t, b, :], Z, acc[:, g, :], vec).then_inc(
                                *y_used.one())
                            v.wait_ge(*y_used.latest(n))
                    v.wait_ge(*stored.lagging(n, u))
                    v.tensor_tensor(g4(H1[:, u, :, :, :]), acc[:, :, :], g4(X[:, u, :, :, :]), ALU.add).then_inc(
                        *h_ready.one())
                pipelined(v, front, main, steps=NCH)


def stage_attention2(nc, A, h):
    TH, HEADS, W = T // 3, 3, 192
    WC = W // 2
    SCALE = C ** -0.5
    with Stage(nc, "att2") as st:
        p = Pair(st, tiles=3, rows=TH)
        X, xn, xT, norm, vec, H1 = p.X, p.xn, p.xT, p.norm, p.vec, p.H1
        we = st.sb("we", [C + 1, HEADS, W])
        wo = st.sb("wo", [WC, 2, C])
        bo = st.sb("bo", [TH, C])
        qk = st.sb("qk", [WC, 2, 2, 2 * TH])
        V = st.sb("V", [TH, 2, W])
        nb = st.sb("nb", [TH, 2])
        den = st.sb("den", [TH, HEADS, 2])
        P = st.sb("P", [TH, 2, TH])
        PTr = st.sb("PTr", [TH, 2, TH])
        oT = st.sb("oT", [WC, 2, 2, TH])
        res = st.sb("res", [TH, HEADS, 2, C])
        pX = st.psum("pX", [C, 2, 256])
        pQ = st.psum("pQ", [WC, 2, 512])
        pV = st.psum("pV", [TH, 2, W])
        pS = st.psum("pS", [TH, 2, TH])
        pP = st.psum("pP", [TH, 2, TH])
        pO = st.psum("pO", [WC, 2, 2, TH])
        pY = st.psum("pY", [TH, HEADS, 2, C])
        qk_done = st.event("qk_done")
        qk_ready = st.event("qk_ready")
        v_done = st.event("v_done")
        v_ready = st.event("v_ready")
        s_done = st.event("s_done")
        max_ready = st.event("max_ready")
        exp_ready = st.event("exp_ready")
        pt_done = st.event("pt_done")
        pt_ready = st.event("pt_ready")
        o_done = st.event("o_done")
        oT_ready = st.event("oT_ready")
        y_done = st.event("y_done")

        def thirds(dram, i):
            d = dram[bass.ds(i * 2, 2)]
            return [bass.AP(d.tensor, d.offset + j * TH * C, [[C, TH], [T * C, 2], [1, C]]) for j in range(3)]
        with st.block() as block:
            @block.sync
            def _(sp):
                cl = p.const_loaded
                const(sp, cl, p.ident[:, :], A["const_ident"])
                const(sp, cl, we[0:C, :, :], A["L2_attn_W_embedT"].rearrange("n c w -> c n w"))
                const(sp, cl, we[C:C + 1, :, :], row(A["L2_attn_b_embed"]))
                const(sp, cl, wo[:, :, :], A["L2_attn_W_outT"].rearrange("(k w) c -> w k c", k=2))
                const(sp, cl, bo[:, :], every_row(A["L2_attn_b_out"], TH))
                with sp.Fori(0, PAIRS) as i:
                    sp.wait_ge(*p.h_ready.before(i))
                    st.held(sp)
                    for j, src in enumerate(thirds(h, i)):
                        sp.dma_start(X[:, j, :, :], src).then_inc(*p.loaded.one())
                    sp.wait_ge(*p.h_ready.after(i))
                    st.held(sp)
                    for j, dst in enumerate(thirds(h, i)):
                        sp.dma_start(dst, H1[:, j, :, :]).then_inc(*p.stored.one())
                sp.wait_ge(*p.stored.after(PAIRS - 1))

            @block.gpsimd
            def _(g):
                g.wait_ge(*p.memset_done.after(0))
                with g.Fori(0, PAIRS) as i:
                    norm.power(g, i, 0)

            @block.tensor
            def _(pe):
                pe.wait_ge(*p.const_loaded.after(0))
                pe.wait_ge(*p.memset_done.after(0))
                with pe.Fori(0, PAIRS) as i:
                    pe.wait_ge(*p.xn_ready.after(i))
                    st.held(pe)
                    for j in range(3):
                        for b in range(2):
                            ins = pe.transpose(pX[:, b, j * TH:(j + 1) * TH], xn[:, j, b, :],
                                               p.ident[0:TH, 0:TH])
                    ins.then_inc(*p.xT_done.one())
                    pe.wait_ge(*p.xT_ready.after(i))
                    for n in range(HEADS):
                        if n:
                            pe.wait_ge(*qk_ready.after(i, n - 1))
                        st.held(pe)
                        for k in range(2):
                            ins = pe.matmul(pQ[:, k, 0:4 * TH], we[:, n, k * WC:(k + 1) * WC],
                                            xT[:, :, 0:2 * TH], start=True, stop=True)
                        ins.then_inc(*qk_done.one())
                        if n:
                            pe.wait_ge(*v_ready.after(i, n - 1))
                        st.held(pe)
                        for b in range(2):
                            ins = pe.matmul(pV[:, b, :], xT[:, b, 2 * TH:T], we[:, n, :], start=True, stop=True)
                        ins.then_inc(*v_done.one())
                        pe.wait_ge(*qk_ready.after(i, n))
                        st.held(pe)
                        for b in range(2):
                            for k in range(2):
                                ins = pe.matmul(pS[:, b, :], qk[:, k, b, 0:TH], qk[:, k, b, TH:2 * TH],
                                                start=(k == 0), stop=(k == 1))
                        ins.then_inc(*s_done.one())
                        pe.wait_ge(*exp_ready.after(i, 2 * n + 1))
                        st.held(pe)
                        for b in range(2):
                            ins = pe.transpose(pP[:, b, :], P[:, b, :], p.ident[0:TH, 0:TH])
                        ins.then_inc(*pt_done.one())
                        pe.wait_ge(*pt_ready.after(i, n))
                        pe.wait_ge(*v_ready.after(i, n))
                        st.held(pe)
                        for k in range(2):
                            for b in range(2):
                                ins = pe.matmul(pO[:, k, b, :], V[:, b, k * WC:(k + 1) * WC], PTr[:, b, :],
                                                start=True, stop=True)
                        ins.then_inc(*o_done.one())
                        pe.wait_ge(*oT_ready.after(i, n))
                        st.held(pe)
                        for b in range(2):
                            for k in range(2):
                                ins = pe.matmul(pY[:, n, b, :], oT[:, k, b, :], wo[:, k, :], start=(k == 0),
                                                stop=(k == 1))
                        ins.then_inc(*y_done.one())

            @block.scalar
            def _(a):
                with a.Fori(0, PAIRS) as i:
                    norm.square(a, i, 0, norm.xc[:, :, :])
                    for n in range(HEADS):
                        a.wait_ge(*v_done.after(i, n))
                        a.activation(V[:, :, :], pV[:, :, :], ACT.Copy).then_inc(*v_ready.one())
                        a.wait_ge(*max_ready.after(i, n))
                        for b in range(2):
                            a.activation(P[:, b, :], pS[:, b, :], ACT.Exp, bias=nb[:, b:b + 1], scale=SCALE,
                                         accum_out=den[:, n, b:b + 1]).then_inc(*exp_ready.one())
                        a.wait_ge(*o_done.after(i, n))
                        a.activation(oT[:, :, :, :], pO[:, :, :, :], ACT.Copy).then_inc(*oT_ready.one())

            @block.vector
            def _(v):
                p.memsets(v)
                v.wait_ge(*p.memset_done.after(0))
                v.wait_ge(*p.const_loaded.after(0))

                def link(ins):
                    ins.then_inc(*vec.one())
                    v.wait_ge(*vec.latest(i))
                with v.Fori(0, PAIRS) as i:
                    p.normalise(v, i)
                    v.wait_ge(*p.xT_done.after(i))
                    v.tensor_copy(xT[0:C, :, :], pX[:, :, 0:T]).then_inc(*p.xT_ready.one())
                    for n in range(HEADS):
                        v.wait_ge(*qk_done.after(i, n))
                        v.tensor_copy(qk[:, :, :, :].rearrange("p k b t -> p k (b t)"),
                                      pQ[:, :, 0:4 * TH]).then_inc(*qk_ready.one())
                        v.wait_ge(*s_done.after(i, n))
                        link(v.reduce_max(nb[:, :], pS[:, :, :], AX.X))
                        v.tensor_scalar(nb[:, :], nb[:, :], -SCALE, None, ALU.mult).then_inc(*max_ready.one())
                        v.wait_ge(*pt_done.after(i, n))
                        v.tensor_copy(PTr[:, :, :], pP[:, :, :]).then_inc(*pt_ready.one())
                    v.wait_ge(*y_done.after(i))
                    link(v.reciprocal(den[:, :, :], den[:, :, :]))
                    link(v.tensor_tensor(g4(res[:, :, :, :]), g4(pY[:, :, :, :]),
                                         bc(den[:, :, :].rearrange("p n b -> p (n b)"), C), ALU.mult))
                    link(v.tensor_tensor(g4(res[:, :, :, :]), g4(res[:, :, :, :]), g4(xn[:, :, :, :]), ALU.add))
                    link(v.tensor_tensor(g4(res[:, :, :, :]), g4(res[:, :, :, :]), bcm(bo[:, :], 1, 6), ALU.add))
                    v.wait_ge(*p.stored.before(i))
                    v.tensor_tensor(g4(H1[:, :, :, :]), g4(res[:, :, :, :]), g4(X[:, :, :, :]), ALU.add).then_inc(
                        *p.h_ready.one())


def stage_depths2(nc, A, h):
    F, KEEP = 256, int(0.5 * T) - 1
    with Stage(nc, "mod2") as st:
        p = Pair(st)
        X, xn, xT, norm, vec, H1 = p.X, p.xn, p.xT, p.norm, p.vec, p.H1
        w1 = st.sb("w1", [C + 1, F])
        w2 = st.sb("w2", [128, 2, C])
        b2 = st.sb("b2", [1, C])
        ones = st.sb("ones", [1, PT])
        wr = st.sb("wr", [C + 1, PT])
        earlier = st.sb("earlier", [PT, 2, T])
        hT = st.sb("hT", [128, 2, 2 * T])
        W = st.sb("W", [PT, 2, T])
        junk = st.sb("junk", [PT, T])
        wn = st.sb("wn", [PT, 4])
        gt = st.sb("gt", [PT, 4])
        eq = st.sb("eq", [PT, 4])
        res = st.sb("res", [PT, 4, C])
        pX = st.psum("pX", [C, 2, 256])
        pW = st.psum("pW", [PT, 512])
        pH = st.psum("pH", [128, 2, 512])
        pY = st.psum("pY", [PT, 4, C])
        w_done = st.event("w_done")
        w_ready = st.event("w_ready")
        hid_done = st.event("hid_done")
        hid_ready = st.event("hid_ready")
        y_done = st.event("y_done")
        with st.block() as block:
            @block.sync
            def _(sp):
                cl = p.const_loaded
                const(sp, cl, p.ident[:, :], A["const_ident"])
                const(sp, cl, w1[0:C, :], A["L2_ffn_w1"])
                const(sp, cl, w1[C:C + 1, :], row(A["L2_ffn_b1"]))
                const(sp, cl, w2[:, :, :], A["L2_ffn_w2"].rearrange("(k f) c -> f k c", k=2))
                const(sp, cl, b2[:, :], row(A["L2_ffn_b2"]))
                const(sp, cl, wr[0:C, :], A["wr_wide"])
                const(sp, cl, wr[C:C + 1, :], A["br_wide"])
                const(sp, cl, earlier[:, :, :], A["const_before"])
                with sp.Fori(0, PAIRS) as i:
                    sp.wait_ge(*p.h_ready.before(i))
                    st.held(sp)
                    for ins in load_pair(sp, X, h, i):
                        ins.then_inc(*p.loaded.one())
                    sp.wait_ge(*p.h_ready.after(i))
                    st.held(sp)
                    for ins in store_pair(sp, h, H1, i):
                        ins.then_inc(*p.stored.one())
                sp.wait_ge(*p.stored.after(PAIRS - 1))

            @block.gpsimd
            def _(g):
                g.wait_ge(*p.memset_done.after(0))
                with g.Fori(0, PAIRS) as i:
                    norm.power(g, i, 0)

            @block.tensor
            def _(pe):
                pe.wait_ge(*p.const_loaded.after(0))
                pe.wait_ge(*p.memset_done.after(0))
                with pe.Fori(0, PAIRS) as i:
                    pe.wait_ge(*p.xn_ready.after(i))
                    st.held(pe)
                    transpose_rows(pe, pX, xn, p.ident).then_inc(*p.xT_done.one())
                    pe.wait_ge(*p.xT_ready.after(i))
                    pe.matmul(pW[:, 0:2 * T], wr[:, :], xT[:, :, :], start=True, stop=True).then_inc(*w_done.one())
                    for k in range(2):
                        pe.matmul(pH[:, k, 0:2 * T], w1[:, k * 128:(k + 1) * 128], xT[:, :, :], start=True,
                                  stop=True).then_inc(*hid_done.one())
                    pe.wait_ge(*hid_ready.after(i))
                    st.held(pe)
                    for t in range(2):
                        for b in range(2):
                            g = 2 * t + b
                            pe.matmul(pY[:, g, :], ones[:, :], b2[:, :], start=True, stop=False)
                            for k in range(2):
                                ins = pe.matmul(pY[:, g, :], hT[:, k, b * T + t * OFF:b * T + t * OFF + PT],
                                                w2[:, k, :], start=False, stop=(k == 1))
                    ins.then_inc(*y_done.one())

            @block.scalar
            def _(a):
                with a.Fori(0, PAIRS) as i:
                    norm.square(a, i, 0, norm.xc[:, :, :])
                    a.wait_ge(*w_done.after(i))
                    a.activation(W[:, :, :].rearrange("p b t -> p (b t)"), pW[:, 0:2 * T], ACT.Copy).then_inc(
                        *w_ready.one())
                    for k in range(2):
                        a.wait_ge(*hid_done.after(i, k))
                        a.activation(hT[:, k, :], pH[:, k, 0:2 * T], ACT.Gelu_apprx_tanh).then_inc(
                            *hid_ready.one())

            @block.vector
            def _(v):
                v.memset(ones[:, :], 1.0)
                p.memsets(v)
                v.wait_ge(*p.memset_done.after(0))
                v.wait_ge(*p.const_loaded.after(0))

                def link(ins):
                    ins.then_inc(*vec.one())
                    v.wait_ge(*vec.latest(i))
                with v.Fori(0, PAIRS) as i:
                    p.normalise(v, i)
                    v.wait_ge(*p.xT_done.after(i))
                    v.tensor_copy(xT[0:C, :, :], pX[:, :, 0:T]).then_inc(*p.xT_ready.one())
                    v.wait_ge(*w_ready.after(i))
                    for t in range(2):
                        for b in range(2):
                            link(v.tensor_tensor_reduce(junk[:, 0:PT], W[:, b, t * OFF:t * OFF + PT],
                                                        p.ident[0:PT, 0:PT], 1.0, 0.0, ALU.mult, ALU.add,
                                                        wn[:, 2 * t + b:2 * t + b + 1]))
                    for t in range(2):
                        for b in range(2):
                            g = 2 * t + b
                            link(v.tensor_scalar(junk[:, :], W[:, b, :], wn[:, g:g + 1], 0.0, ALU.is_gt, ALU.add,
                                                 accum_out=gt[:, g:g + 1]))
                            link(v.scalar_tensor_tensor(out=junk[:, :], in0=W[:, b, :], scalar=wn[:, g:g + 1],
                                                        in1=earlier[:, t, :], op0=ALU.is_equal, op1=ALU.mult,
                                                        accum_out=eq[:, g:g + 1]))
                    link(v.tensor_tensor(gt[:, :], gt[:, :], eq[:, :], ALU.add))
                    link(v.tensor_scalar(gt[:, :], gt[:, :], float(KEEP), None, ALU.is_lt))
                    link(v.tensor_tensor(gt[:, :], gt[:, :], wn[:, :], ALU.mult))
                    v.wait_ge(*y_done.after(i))
                    link(v.tensor_tensor(res[:, :, :], pY[:, :, :], bc(gt[:, :], C), ALU.mult))
                    link(v.tensor_tensor(res[:, :, :], res[:, :, :], g4(xn[:, :, :, :]), ALU.add))
                    v.wait_ge(*p.stored.before(i))
                    v.tensor_tensor(g4(H1[:, :, :, :]), res[:, :, :], g4(X[:, :, :, :]), ALU.add).then_inc(
                        *p.h_ready.one())


def stage_attention3(nc, A, h):
    H, D, KNN = 8, 64, 32
    HP = H // 2
    STEPS = 2 * H
    AHEAD = STEPS + 2
    D0, P0, R0, O0 = 6, 6, 8, 12
    SCALE = D ** -0.5
    SELF, TAKEN = -3.4028234663852886e38, -3.0e38
    with Stage(nc, "att3") as st:
        f = Front(st, twice=True)
        x3 = Thirds(st, "x3", 2 * T)
        w = st.sb("w", [2 * C, 3 * H * D])
        rest = st.sb("rest", [2 * C, 3 * H * D])
        stacks = [st.sb(f"wqkv_{y}", [2 * C, 3 * H * D], BF16) for y in ("hm", "mh", "lh")]
        wo = st.sb("wo", [128, HP, C])
        bo = st.sb("bo", [PT, C])
        diag = st.sb("diag", [PT, 2, T])
        xf = st.sb("xf", [2 * C, 2, 2, T])
        x1 = st.sb("x1", [2 * C, 2, T])
        x2 = st.sb("x2", [2 * C, 2, T])
        sq = st.sb("sq", [PT, 4, C])
        norm2 = st.sb("norm2", [PT, 4])
        near = st.sb("near", [PT, 4, T])
        top8 = st.sb("top8", [PT, 4, 8])
        mask = st.sb("mask", [PT, 2, 4, T])
        qT = st.sb("qT", [128, 2, HP, 2, T])
        kT = st.sb("kT", [128, 2, HP, 2, T])
        V = st.sb("V", [PT, 2, 4, H * D])
        SM = st.sb("SM", [PT, 2, 2, T])
        nb = st.sb("nb", [PT, 2, 2])
        P = st.sb("P", [PT, 2, 2, T])
        den = st.sb("den", [PT, 2, 2, H])
        PTr = st.sb("PTr", [PT, 2, 2, T])
        of = st.sb("of", [PT, 4, H * D])
        oT = st.sb("oT", [128, 2, HP, T])
        res = st.sb("res", [PT, 2, 2, C])
        pQ = st.psum("pQ", [128, 512])
        pS = st.psum("pS", [PT, 2, 512])
        pP = st.psum("pP", [128, 2, 512])
        pO = st.psum("pO", [PT, 2, 512])
        names = """sq_ready rows_squared d_done d_used proj_done proj_ready s_done max_ready exp_ready pt_done
            pt_ready o_done o_ready oT_done oT_ready y_done y_used vec round"""
        (sq_ready, rows_squared, d_done, d_used, proj_done, proj_ready, s_done, max_ready, exp_ready, pt_done,
         pt_ready, o_done, o_ready, oT_done, oT_ready, y_done, y_used, vec, rounds) = (
             st.event(x, bodies=BODIES) for x in names.split())
        w_split = st.event("w_split")
        w_ready = st.event("w_ready")
        pD = f.pX[:, :, :].rearrange("p a b -> p (a b)")

        with st.block() as block:
            @block.sync
            def _(sp):
                cl = f.const_loaded
                const(sp, cl, f.ident[:, :], A["const_ident"])
                for half in range(2):
                    const(sp, cl, w[half * C:(half + 1) * C, :], A["L3_attn_Wqkv"])
                const(sp, cl, wo[:, :, :], A["L3_attn_Wout"].rearrange("(k n) c -> n k c", k=HP))
                const(sp, cl, bo[:, :], every_row(A["L3_attn_bout"], PT))
                const(sp, cl, diag[:, :, :], A["const_self"])

                def front(n, u):
                    f.load(sp, h, n, u)

                def main(n, u, ahead):
                    ahead()
                    f.store(sp, h, n, u)
                pipelined(sp, front, main)
                f.all_stored(sp)

            @block.gpsimd
            def _(g):
                g.wait_ge(*f.memset_done.after(0))

                def front(n, u):
                    f.norm.power(g, n, 0)
                    g.wait_ge(*f.xT_ready.after(n))
                    g.wait_ge(*proj_done.lagging(n))
                    x3.split(g, n, u, xf[:, u, :, :])

                def main(n, u, ahead):
                    ahead()
                pipelined(g, front, main)

            @block.tensor
            def _(pe):
                pe.wait_ge(*f.const_loaded.after(0))
                pe.wait_ge(*f.memset_done.after(0))
                pe.wait_ge(*w_ready.after(0))

                def front(n, u, step):
                    if step == 2:
                        f.transpose(pe, n, u)
                    if step in (D0, D0 + 1):
                        b = step - D0
                        pe.wait_ge(*sq_ready.after(n))
                        if b:
                            pe.wait_ge(*d_used.after(n, b - 1))
                        st.held(pe)
                        for t in range(2):
                            ins = pe.matmul(pD[0:PT, t * T:t * T + T], x2[:, b, t * OFF:t * OFF + PT], x1[:, b, :],
                                            start=True, stop=True)
                        ins.then_inc(*d_done.one())
                    if step >= P0:
                        k = step - P0
                        if k == 0:
                            pe.wait_ge(*x3.ready.after(n))
                        pe.wait_ge(*proj_ready.after(n, k - 1))
                        st.held(pe)
                        if k < 2 * HP:
                            ins = x3.product(pe, pQ[:, 0:2 * T], u, *[x[:, k * 128:(k + 1) * 128] for x in stacks])
                        else:
                            t, b = (k - 2 * HP) // 2, k % 2
                            rows, cols = slice(b * T + t * OFF, b * T + t * OFF + PT), slice(2 * H * D, 3 * H * D)
                            pe.matmul(pQ[0:PT, :], x3.hm[:, u, rows], stacks[0][:, cols], start=True, stop=False)
                            pe.matmul(pQ[0:PT, :], x3.hm[:, u, rows], stacks[1][:, cols], start=False, stop=False)
                            ins = pe.matmul(pQ[0:PT, :], x3.hl[:, u, rows], stacks[2][:, cols], start=False,
                                            stop=True)
                        ins.then_inc(*proj_done.one())

                def outputs_turned(out, b, hps):
                    for k, hp in enumerate(hps):
                        for t in range(2):
                            ins = pe.transpose(out[:, k * T + t * OFF:k * T + t * OFF + ROWS[t]],
                                               of[0:ROWS[t], 2 * t + b, hp * 128:(hp + 1) * 128],
                                               f.ident[0:ROWS[t], 0:ROWS[t]])
                    ins.then_inc(*oT_done.one())

                def outputs_projected(out, b):
                    for t in range(2):
                        for hp in range(HP):
                            ins = pe.matmul(out[0:PT, t * C:(t + 1) * C], oT[:, b, hp, t * OFF:t * OFF + PT],
                                            wo[:, hp, :], start=(hp == 0), stop=(hp == HP - 1))
                    ins.then_inc(*y_done.one())

                def main(n, u, ahead):
                    pe.wait_ge(*proj_ready.after(n))
                    for step in range(AHEAD):
                        if step < STEPS:
                            s = step
                            r, hp, b = 64 * (s % 2), s % H // 2, s // H
                            pe.wait_ge(*max_ready.after(n, s - 2))
                            st.held(pe)
                            for t in range(2):
                                ins = pe.matmul(pS[:, s % 2, t * T:t * T + T],
                                                qT[r:r + D, u, hp, b, t * OFF:t * OFF + PT],
                                                kT[r:r + D, u, hp, b, :], start=True, stop=True,
                                                tile_position=(r, 0))
                            ins.then_inc(*s_done.one())
                        if 1 <= step <= STEPS:
                            s = step - 1
                            pe.wait_ge(*exp_ready.after(n, 2 * s + 1))
                            pe.wait_ge(*pt_ready.after(n, s - 2))
                            if s == 0:
                                pe.wait_ge(*y_used.before(n))
                            st.held(pe)
                            for t in range(2):
                                for kt in range(2):
                                    ins = pe.transpose(
                                        pP[0:PT, s % 2, kt * T + t * OFF:kt * T + t * OFF + ROWS[t]],
                                        P[0:ROWS[t], s % 2, t, kt * OFF:kt * OFF + PT],
                                        f.ident[0:ROWS[t], 0:ROWS[t]])
                            ins.then_inc(*pt_done.one())
                        ahead(step)
                        if step >= 2:
                            s = step - 2
                            b, hd = s // H, s % H
                            pe.wait_ge(*pt_ready.after(n, s))
                            if hd == 0:
                                pe.wait_ge(*o_ready.after(n, b - 1))
                            st.held(pe)
                            for t in range(2):
                                for kt in range(2):
                                    ins = pe.matmul(pO[:, t, hd * D:(hd + 1) * D],
                                                    PTr[0:ROWS[kt], s % 2, kt, t * OFF:t * OFF + PT],
                                                    V[0:ROWS[kt], u, 2 * kt + b, hd * D:(hd + 1) * D],
                                                    start=(kt == 0), stop=(kt == 1))
                            if hd == H - 1:
                                ins.then_inc(*o_done.one())
                        if step == O0:
                            pe.wait_ge(*o_ready.after(n, 0))
                            st.held(pe)
                            outputs_turned(pD, 0, (0, 1))
                        if step == O0 + 1:
                            pe.wait_ge(*oT_ready.after(n, 0))
                            st.held(pe)
                            outputs_turned(pD, 0, (2, 3))
                        if step == O0 + 2:
                            pe.wait_ge(*oT_ready.after(n, 1))
                            st.held(pe)
                            outputs_projected(pD, 0)
                    pe.wait_ge(*o_ready.after(n, 1))
                    st.held(pe)
                    outputs_turned(pP[:, 0, :], 1, (0, 1))
                    outputs_turned(pP[:, 1, :], 1, (2, 3))
                    pe.wait_ge(*oT_ready.after(n, 3))
                    st.held(pe)
                    outputs_projected(pP[:, 0, :], 1)
                pipelined(pe, front, main, steps=AHEAD)

            @block.scalar
            def _(a):
                def front(n, u, step):
                    if step == 0:
                        f.square(a, n, u)
                    if step == 2:
                        a.wait_ge(*f.xn_ready.after(n))
                        a.activation(sq[:, :, :], g4(f.xn[:, u, :, :, 0:C]), ACT.Square).then_inc(
                            *rows_squared.one())
                    if step == 4:
                        a.wait_ge(*f.xT_ready.after(n))
                        a.activation(x1[0:C, :, :], xf[0:C, u, :, :], ACT.Copy)
                        a.activation(x1[C:2 * C, :, :], xf[C:2 * C, u, :, :], ACT.Square)
                        a.activation(x2[0:C, :, :], xf[0:C, u, :, :], ACT.Copy, scale=2.0).then_inc(*sq_ready.one())
                    if step >= P0:
                        k = step - P0
                        a.wait_ge(*proj_done.after(n, k))
                        if k < 2 * HP:
                            a.activation((kT if k // HP else qT)[:, u, k % HP, :, :].rearrange("c b t -> c (b t)"),
                                         pQ[:, 0:2 * T], ACT.Copy, scale=1.0 if k // HP else SCALE).then_inc(
                                *proj_ready.one())
                        else:
                            a.activation(V[:, u, k - 2 * HP, :], pQ[0:PT, :], ACT.Copy).then_inc(*proj_ready.one())

                def main(n, u, ahead):
                    def turned(event, b, half, src):
                        a.wait_ge(*oT_done.after(n, event))
                        a.activation(oT[:, b, 2 * half:2 * half + 2, :].rearrange("c k t -> c (k t)"),
                                     src[:, 0:2 * T], ACT.Copy).then_inc(*oT_ready.one())
                    for step in range(AHEAD):
                        if 1 <= step <= STEPS:
                            s = step - 1
                            a.wait_ge(*pt_done.after(n, s))
                            a.activation(PTr[:, s % 2, :, :].rearrange("p k t -> p (k t)"), pP[0:PT, s % 2, 0:2 * T],
                                         ACT.Copy).then_inc(*pt_ready.one())
                        if step < STEPS:
                            s = step
                            b, hd = s // H, s % H
                            a.wait_ge(*max_ready.after(n, s))
                            for t in range(2):
                                a.activation(P[:, s % 2, t, :], SM[:, s % 2, t, :], ACT.Exp,
                                             bias=nb[:, s % 2, t:t + 1],
                                             accum_out=den[:, b, t, hd:hd + 1]).then_inc(*exp_ready.one())
                        ahead(step)
                        if step in (O0, O0 + 1):
                            turned(step - O0, 0, step - O0, pD)
                    for half in range(2):
                        turned(2 + half, 1, half, pP[:, half, :])
                pipelined(a, front, main, steps=AHEAD)

            @block.vector
            def _(v):
                v.memset(x2[C:2 * C, :, :], -1.0)
                f.memsets(v)
                v.wait_ge(*f.memset_done.after(0))
                v.wait_ge(*f.const_loaded.after(0))
                split_weights(v, w, rest, *stacks, w_split)
                v.sem_inc(*w_ready.one())

                def front(n, u, step):
                    def link(ins):
                        ins.then_inc(*f.front_vec.one())
                        v.wait_ge(*f.front_vec.latest(n))
                    if step == 0:
                        v.wait_ge(*f.loaded.after(n, u))
                        f.norm.center(v, n, g4(f.X[:, u, :, :, :]), f.front_vec)
                    if step == 1:
                        f.norm.scale(v, n, 0, f.norm.xc[:, :, :], g4(f.xn[:, u, :, :, 0:C]), 1e-5, f.front_vec)
                        v.tensor_tensor(g4(f.xn[:, u, :, :, C:2 * C]), f.norm.xc[:, :, :],
                                        bc(f.norm.rstd[:, :], C), ALU.mult).then_inc(*f.xn_ready.one())
                    if step == 3:
                        v.wait_ge(*f.xT_done.after(n))
                        v.tensor_copy(xf[:, u, :, :], f.pX[:, :, 0:T]).then_inc(*f.xT_ready.one())
                    if step in (D0, D0 + 1):
                        b = step - D0
                        if b == 0:
                            v.wait_ge(*rows_squared.after(n))
                            link(v.reduce_sum(norm2[:, :], sq[:, :, :], AX.X))
                        v.wait_ge(*d_done.after(n, b))
                        for t in range(2):
                            g = 2 * t + b
                            ins = v.scalar_tensor_tensor(out=near[:, g, :], in0=pD[0:PT, t * T:t * T + T],
                                                         scalar=norm2[:, g:g + 1], in1=diag[:, t, :],
                                                         op0=ALU.subtract, op1=ALU.add)
                        ins.then_inc(*d_used.one())
                        v.wait_ge(*d_used.after(n, b))
                    if R0 <= step < R0 + KNN // 4:
                        st.held(v)
                        for g in range(4):
                            if (step - R0) % 2 == 0:
                                ins = v.max(top8[:, g, :], near[:, g, :])
                            else:
                                ins = v.match_replace(near[:, g, :], top8[:, g, :], near[:, g, :], TAKEN)
                        ins.then_inc(*rounds.one())
                        v.wait_ge(*rounds.after(n, step - R0))
                        if step == R0 + KNN // 4 - 1:
                            link(v.tensor_scalar(mask[:, u, :, :], near[:, :, :], TAKEN, NEG, ALU.not_equal,
                                                 ALU.mult))

                def main(n, u, ahead):
                    def link(ins):
                        ins.then_inc(*vec.one())
                        v.wait_ge(*vec.latest(n))

                    def heads_done(b):
                        v.wait_ge(*o_done.after(n, b))
                        link(v.reciprocal(den[:, b, :, :], den[:, b, :, :]))
                        for t in range(2):
                            ins = v.tensor_tensor(of[:, 2 * t + b, :].rearrange("p (h d) -> p h d", h=H),
                                                  pO[:, t, :].rearrange("p (h d) -> p h d", h=H),
                                                  bc(den[:, b, t, :], D), ALU.mult)
                        ins.then_inc(*o_ready.one())

                    def residual(b, src):
                        v.wait_ge(*y_done.after(n, b))
                        v.tensor_tensor(res[:, b, :, :], src[0:PT, 0:2 * C].rearrange("p (t c) -> p t c", t=2),
                                        bcm(bo[:, :], 1, 2), ALU.add).then_inc(*y_used.one())
                        v.wait_ge(*y_used.after(n, b))
                        return v.tensor_tensor(f.H1[:, u, :, b, :], res[:, b, :, :], f.X[:, u, :, b, :], ALU.add)
                    for step in range(AHEAD):
                        if step < STEPS:
                            s = step
                            b = s // H
                            v.wait_ge(*s_done.after(n, s))
                            v.wait_ge(*exp_ready.after(n, 2 * (s - 2) + 1))
                            link(v.tensor_tensor(SM[:, s % 2, :, :], pS[:, s % 2, 0:2 * T].rearrange(
                                "p (t n) -> p t n", t=2), mask[:, u, b:4:2, :], ALU.add))
                            v.tensor_reduce(nb[:, s % 2, :], SM[:, s % 2, :, :], AX.X, ALU.max, negate=True).then_inc(
                                *max_ready.one())
                        if step == H + 1:
                            heads_done(0)
                        ahead(step)
                        if step == O0 + 3:
                            v.wait_ge(*f.stored.lagging(n, u))
                            residual(0, pD)
                    heads_done(1)
                    residual(1, pP[:, 0, :]).then_inc(*f.h_ready.one())
                pipelined(v, front, main, steps=AHEAD)


def stage_switch3(nc, A, h, out):
    E, F = EXPERTS, 256
    NCH = E * 2
    ROOM = max(1, math.ceil(1.25 * BATCH * T / E))
    BIG = 3.4028234663852886e38
    with Stage(nc, "sw3") as st:
        f = Front(st, twice=True)
        x3 = Thirds(st, "x3", 2 * T)
        w = st.sb("w", [2 * C, E * F])
        rest = st.sb("rest", [2 * C, E * F])
        stacks = [st.sb(f"w1_{y}", [2 * C, E * F], BF16) for y in ("hm", "mh", "lh")]
        b1 = st.sb("b1", [128, NCH])
        w2 = st.sb("w2", [128, NCH, C])
        b2 = st.sb("b2", [1, E * C])
        b2rest = st.sb("b2rest", [1, E * C])
        b2thirds = st.sb("b2thirds", [C + 1, E * C], BF16)
        ones16 = st.sb("ones16", [C + 1, PT], BF16)
        wg = st.sb("wg", [C + 1, E])
        ones = st.sb("ones", [128, 128])
        upto = st.sb("upto", [PT, PT])
        lg = st.sb("lg", [PT, 4, E])
        s1 = st.sb("s1", [PT, 4])
        prb = st.sb("prb", [PT, 4])
        hot = st.sb("hot", [PT, 4, E])
        base = st.sb("base", [PT, E])
        coef = st.sb("coef", [PT, 2, 4, E])
        hT = st.sb("hT", [128, NCH, 2 * T])
        Z = st.sb("Z", [PT, E, C])
        acc = st.sb("acc", [PT, 2, 2, C])
        ok = st.sb("ok", [PT, 2, 2, C])
        limits = st.sb("limits", [PT, 3, 4, C])
        rank = Rank(st, PT, 4, 1)
        pH = st.psum("pH", [128, 2, 512])
        pL = st.psum("pL", [PT, 4, E])
        pC = st.psum("pC", [PT, 5, E])
        pY = st.psum("pY", [PT, 3, 512])
        l_done = st.event("l_done", bodies=BODIES)
        l_shifted = st.event("l_shifted", bodies=BODIES)
        l_exp = st.event("l_exp", bodies=BODIES)
        hot_ready = st.event("hot_ready", bodies=BODIES)
        c_done = st.event("c_done", bodies=BODIES)
        hid_done = st.event("hid_done", bodies=BODIES)
        hid_ready = st.event("hid_ready", bodies=BODIES)
        y_done = st.event("y_done", bodies=BODIES)
        vec = st.event("vec", bodies=BODIES)
        w_split = st.event("w_split")
        w_ready = st.event("w_ready")
        y_used = st.event("y_used", bodies=BODIES)
        with st.block() as block:
            @block.sync
            def _(sp):
                cl = f.const_loaded
                const(sp, cl, f.ident[:, :], A["const_ident"])
                for half in range(2):
                    const(sp, cl, w[half * C:(half + 1) * C, :], A["L3_ffn_w1T"])
                const(sp, cl, b1[:, :], A["b1_columns"])
                const(sp, cl, w2[:, :, :], A["L3_ffn_w2"].rearrange("e (k f) c -> f (e k) c", k=2))
                const(sp, cl, b2[:, :], row(A["L3_ffn_b2"].rearrange("e c -> (e c)")))
                const(sp, cl, wg[0:C, :], A["L3_ffn_gate_w"])
                const(sp, cl, wg[C:C + 1, :], row(A["L3_ffn_gate_b"]))
                const(sp, cl, upto[:, :], A["const_upto"])
                const(sp, cl, rank.earlier[:, :], every_row(A["const_earlier"], PT))

                def front(n, u):
                    f.load(sp, h, n, u)

                def main(n, u, ahead):
                    ahead()
                    f.store(sp, out, n, u)
                pipelined(sp, front, main)
                f.all_stored(sp)

            @block.gpsimd
            def _(g):
                g.wait_ge(*f.memset_done.after(0))

                def front(n, u):
                    f.norm.power(g, n, 0)

                def main(n, u, ahead):
                    ahead()
                pipelined(g, front, main)

            @block.tensor
            def _(pe):
                pe.wait_ge(*f.const_loaded.after(0))
                pe.wait_ge(*f.memset_done.after(0))
                pe.wait_ge(*w_ready.after(0))

                def front(n, u, step):
                    if step == 0:
                        f.transpose(pe, n, u)
                    elif step == 1:
                        pe.wait_ge(*f.xT_ready.after(n))
                        st.held(pe)
                        for b in range(2):
                            for t in range(2):
                                ins = pe.matmul(pL[:, 2 * b + t, :], f.xT[:, u, b, t * OFF:t * OFF + PT], wg[:, :],
                                                start=True, stop=True)
                        ins.then_inc(*l_done.one())
                    else:
                        pe.wait_ge(*hot_ready.after(n))
                        st.held(pe)
                        for g in range(4):
                            for k in range(g):
                                pe.matmul(pC[:, g, :], ones[0:ROWS[k % 2], 0:PT], hot[0:ROWS[k % 2], k, :],
                                          start=(k == 0), stop=False)
                            pe.matmul(pC[:, g, :], upto[0:ROWS[g % 2], :], hot[0:ROWS[g % 2], g, :],
                                      start=(g == 0), stop=True)
                        for k in range(4):
                            ins = pe.matmul(pC[:, 4, :], ones[0:ROWS[k % 2], 0:PT], hot[0:ROWS[k % 2], k, :],
                                            start=(k == 0), stop=(k == 3))
                        ins.then_inc(*c_done.one())

                def main(n, u, ahead):
                    pe.wait_ge(*x3.ready.after(n))
                    for k in range(NCH):
                        pe.wait_ge(*hid_ready.after(n, k - 2))
                        st.held(pe)
                        x3.product(pe, pH[:, k % 2, 0:2 * T], u, *[x[:, k * 128:(k + 1) * 128] for x in stacks]
                                   ).then_inc(*hid_done.one())
                    ahead(0)
                    pe.wait_ge(*hid_ready.after(n))
                    for g in range(4):
                        b, t = g // 2, g % 2
                        if g >= 3:
                            pe.wait_ge(*y_used.after(n, g - 3))
                        else:
                            pe.wait_ge(*y_used.before(n))
                        st.held(pe)
                        pe.matmul(pY[:, g % 3, :], ones16[:, :], b2thirds[:, :], start=True, stop=False)
                        for k in range(NCH):
                            e = k // 2
                            ins = pe.matmul(pY[:, g % 3, e * C:(e + 1) * C],
                                            hT[:, k, b * T + t * OFF:b * T + t * OFF + PT], w2[:, k, :],
                                            start=False, stop=(k == NCH - 1))
                        ins.then_inc(*y_done.one())
                        if g in (1, 3):
                            ahead(1 + g // 2)
                pipelined(pe, front, main, steps=3)

            @block.scalar
            def _(a):
                a.wait_ge(*f.const_loaded.after(0))

                def front(n, u, step):
                    if step == 0:
                        f.square(a, n, u)
                    else:
                        a.wait_ge(*l_shifted.after(n))
                        a.activation(lg[:, :, :], lg[:, :, :], ACT.Exp).then_inc(*l_exp.one())

                def main(n, u, ahead):
                    for k in range(NCH):
                        a.wait_ge(*hid_done.after(n, k))
                        a.activation(hT[:, k, :], pH[:, k % 2, 0:2 * T], ACT.Relu, bias=b1[:, k:k + 1]).then_inc(
                            *hid_ready.one())
                        if k == 4:
                            ahead(0)
                    ahead(1)
                pipelined(a, front, main, steps=2)

            @block.vector
            def _(v):
                v.memset(ones[:, :], 1.0)
                v.memset(ones16[:, :], 1.0)
                v.memset(base[:, :], 0.0)
                v.memset(limits[:, 0, :, :], 10000.0)
                v.memset(limits[:, 1, :, :], -10000.0)
                v.memset(limits[:, 2, :, :], 0.0)
                v.memset(b2thirds[:, :], 0.0)
                f.memsets(v)
                v.wait_ge(*f.memset_done.after(0))
                v.wait_ge(*f.const_loaded.after(0))
                split_weights(v, w, rest, *stacks, w_split)
                for third in range(3):
                    r = b2 if third == 0 else b2rest
                    v.tensor_copy(b2thirds[32 * third:32 * third + 1, :], r[:, :]).then_inc(*w_split.one())
                    v.wait_ge(*w_split.latest(0))
                    if third < 2:
                        v.tensor_tensor(b2rest[:, :], r[:, :], b2thirds[32 * third:32 * third + 1, :],
                                        ALU.subtract).then_inc(*w_split.one())
                        v.wait_ge(*w_split.latest(0))
                v.sem_inc(*w_ready.one())

                def front(n, u, step):
                    def link(ins):
                        ins.then_inc(*f.front_vec.one())
                        v.wait_ge(*f.front_vec.latest(n))
                    if step == 0:
                        f.normalise(v, n, u)
                    elif step == 1:
                        v.wait_ge(*f.xT_done.after(n))
                        x3.split(v, n, u, f.pX[:, :, 0:T])
                        f.channels(v, n, u)
                    elif step == 2:
                        v.wait_ge(*l_done.after(n))
                        link(v.reduce_max(s1[:, :], pL[:, :, :], AX.X))
                        v.tensor_tensor(lg[:, :, :], pL[:, :, :], bc(s1[:, :], E), ALU.subtract).then_inc(
                            *l_shifted.one())
                        v.wait_ge(*l_exp.after(n))
                        link(v.reduce_sum(s1[:, :], lg[:, :, :], AX.X))
                        link(v.reciprocal(s1[:, :], s1[:, :]))
                        link(v.tensor_tensor(lg[:, :, :], lg[:, :, :], bc(s1[:, :], E), ALU.mult))
                        v.reduce_max(prb[:, :], lg[:, :, :], AX.X)
                        rank.select(v, n, lg[:, :, :], hot[:, :, :], f.front_vec).then_inc(*hot_ready.one())
                    else:
                        v.wait_ge(*hot_ready.after(n))
                        v.wait_ge(*c_done.after(n))
                        own = coef[:, u, :, :]
                        link(v.tensor_tensor(own, pC[:, 0:4, :], bcm(base[:, :], 1, 4), ALU.add))
                        link(v.tensor_scalar(own, own, float(ROOM), None, ALU.is_le))
                        link(v.tensor_tensor(own, own, hot[:, :, :], ALU.mult))
                        v.tensor_tensor(own, own, bc(prb[:, :], E), ALU.mult)
                        link(v.tensor_tensor(base[:, :], base[:, :], pC[:, 4, :], ALU.add))

                def main(n, u, ahead):
                    def link(ins):
                        ins.then_inc(*vec.one())
                        v.wait_ge(*vec.latest(n))
                    ahead(0)
                    ahead(1)
                    for g in range(4):
                        b, t = g // 2, g % 2
                        v.wait_ge(*y_done.after(n, g))
                        combine(v, n, pY[:, g % 3, :], coef[:, u, g, :], Z, acc[:, t, b, :], vec).then_inc(
                            *y_used.one())
                        v.wait_ge(*y_used.latest(n))
                        if g == 1:
                            ahead(2)
                    y, o = g4(acc[:, :, :, :]), g4(ok[:, :, :, :])
                    mask = o.bitcast(mybir.dt.uint32)
                    link(v.tensor_scalar(o, y, BIG, None, ALU.is_gt))
                    st.held(v)
                    link(v.copy_predicated(y, mask, limits[:, 0, :, :]))
                    link(v.tensor_scalar(o, y, -BIG, None, ALU.is_lt))
                    st.held(v)
                    link(v.copy_predicated(y, mask, limits[:, 1, :, :]))
                    link(v.tensor_tensor(o, y, y, ALU.not_equal))
                    st.held(v)
                    link(v.copy_predicated(y, mask, limits[:, 2, :, :]))
                    v.wait_ge(*f.stored.lagging(n, u))
                    v.tensor_tensor(g4(f.H1[:, u, :, :, :]), y, g4(f.X[:, u, :, :, :]), ALU.add).then_inc(
                        *f.h_ready.one())
                    ahead(3)
                pipelined(v, front, main, steps=4)


def build(nc, A, out):
    h = nc.dram_tensor("h_stream", [BATCH, T, C], F32, kind="Internal").ap()
    mean = nc.dram_tensor("token_mean", [C, BATCH], F32, kind="Internal").ap()
    route = nc.dram_tensor("routing0", [BATCH, 2], F32, kind="Internal").ap()
    chosen = nc.dram_tensor("chosen0", [BATCH, 2], mybir.dt.int32, kind="Internal").ap()
    last = h if PHASES > 1 else out
    stage_tokenizer(nc, A, last)
    if PHASES >= 2:
        stage_attention0(nc, A, h, mean)
    if PHASES >= 3:
        stage_router0(nc, A, mean, route, chosen)
    if PHASES >= 4:
        stage_ffn0(nc, A, h, route, chosen)
    if PHASES >= 5:
        stage_retention1(nc, A, h)
    hx = nc.dram_tensor("stream_attended1", [BATCH, T, C], F32, kind="Internal").ap()
    flatT = nc.dram_tensor("normed1", [PAIRS, C, 2 * T], F32, kind="Internal").ap()
    mix = nc.dram_tensor("mixing1", [BATCH, T, EXPERTS], F32, kind="Internal").ap()
    if PHASES >= 6:
        stage_attention1(nc, A, h, hx, flatT, mix)
    if PHASES >= 7:
        stage_experts1(nc, A, h, hx, flatT, mix)
    if PHASES >= 8:
        stage_attention2(nc, A, h)
    if PHASES >= 9:
        stage_depths2(nc, A, h)
    if PHASES >= 10:
        stage_attention3(nc, A, h)
    if PHASES >= 11:
        stage_switch3(nc, A, h, out)
    if last is h and PHASES < 11:
        copy_out(nc, h, out)
    if MISCOUNTED:
        raise ValueError(f"MISCOUNTED {MISCOUNTED}")


def copy_out(nc, h, out):
    with Stage(nc, "copy") as st:
        done = st.event("done", dma=True)
        with st.block() as block:
            @block.sync
            def _(sp):
                sp.dma_start(out[:, :, :], h[:, :, :]).then_inc(*done.one())
                sp.wait_ge(*done.after(0))


def interpolation_taps():
    f = np.float32
    pos = np.arange(POINTS, dtype=f) * f(1.0 / (POINTS - 1))
    pos[-1] = 1.0
    x = pos * f(SAMPLES - 1)
    i0 = np.floor(x)
    frac = x - i0
    a = -0.75
    w = np.zeros((T, 20, 64), f)
    p = np.arange(T * 64)
    for off in range(-1, 3):
        t = np.abs(frac[p] - f(off))
        near = ((f(a + 2.0) * t - f(a + 3.0)) * t) * t + f(1.0)
        far = ((f(a) * t - f(5.0 * a)) * t + f(8.0 * a)) * t - f(4.0 * a)
        val = np.where(t <= 1.0, near, np.where(t < 2.0, far, f(0.0)))
        idx = np.clip(i0[p].astype(np.int64) + off, -1, SAMPLES - 1)
        w[p // 64, idx - (16 * (p // 64) - 2), p % 64] += val
    return w


def constants():
    f = np.float32
    n, k = np.arange(64)[:, None], np.arange(33)[None, :]
    ang = 2 * np.pi * ((n * k) % 64) / 64
    e = np.arange(EXPERTS)
    key = np.arange(PT)[:, None]
    gap = np.concatenate([np.arange(T)[None, :] - key, np.arange(PT)[None, :] - key], 1)
    decay = np.exp((np.maximum(gap, 0).astype(f) * f(np.log(0.96875))).astype(np.float64)).astype(f)
    inv = f(1.0) / np.power(10000.0, np.arange(0, 64, 2) / 64.0).astype(f)
    ang64 = np.repeat((np.arange(T, dtype=f)[:, None] * inv[None, :]).T, 2, axis=0).astype(np.float64)
    sign = np.where(np.arange(64) % 2, 1.0, -1.0)[:, None]
    inv16 = f(1.0) / f(10000.0) ** (np.arange(0, 16, 2, dtype=f) / 16)
    ang16 = np.concatenate([np.outer(np.arange(T, dtype=f), inv16)] * 2, -1).T
    rope16 = np.zeros((2, 4, 32, T), f)
    rope16[0, :, 0:16] = np.cos(ang16)
    rope16[0, :, 16] = 1.0
    rope16[1, :, 0:16] = np.sin(ang16) * np.where(np.arange(16) < 8, -1, 1)[:, None].astype(f)
    qry = np.arange(PT)[:, None]
    late = np.concatenate([np.arange(PT)[None, :] - qry, np.arange(T)[None, :] - qry - OFF], 1)
    token = np.arange(PT)[:, None, None] + np.array([0, OFF])[None, :, None]
    col = np.arange(T)[None, None, :]
    return {
        "const_before": (col < token).astype(f),
        "const_self": np.where(col == token, f(-3.4028234663852886e38), f(0)),
        "const_upto": (np.arange(PT)[:, None] <= np.arange(PT)[None, :]).astype(f),
        "const_rope16": rope16.reshape(2, 128, T),
        "const_maskQ": np.where(late > 0, f(NEG), f(0)),
        "const_maskK": np.where(gap < 0, f(NEG), f(0)),
        "const_number": e.astype(f),
        "const_earlier": (e[None, :] < e[:, None]).astype(f).ravel(),
        "const_decay": np.where(gap >= 0, decay, f(0)),
        "const_rope64": np.stack([np.cos(ang64), np.sin(ang64) * sign]).astype(f),
        "const_ident": np.eye(128, dtype=f),
        "const_dft": np.concatenate([np.cos(ang), -np.sin(ang)], 1).astype(f),
        "const_taps": interpolation_taps(),
    }


def kernel(**inputs):
    import numpy as _np
    import concourse.bacc as _bacc
    from concourse import mybir as _mybir
    from concourse.bass_utils import run_bass_kernel_spmd as _run

    nc = _bacc.Bacc("TRN2", target_bir_lowering=False, num_devices=1)
    given = {k: _np.asarray(v) for k, v in inputs.items()}
    x = given.pop("x")
    arrays = dict(constants())
    arrays["x_edge"] = _np.concatenate([x[:, :1], x[:, :1], x], axis=1)
    for name, a in given.items():
        if name in TRANSPOSED:
            arrays[name + "T"] = a.T
        else:
            arrays[name] = a
        if name == "L0_ffn_W1":
            arrays["w1b1"] = _np.concatenate([a, given["L0_ffn_b1"][:, None, :]], axis=1)
        if name in ("L1_attn_W_Q", "L1_attn_W_K"):
            arrays[name + "x"] = a.reshape(64, 32, 2)[:, :, ::-1].reshape(64, 64)
        if name in ("L1_ffn_wq", "L1_ffn_wk"):
            arrays[name + "xT"] = a.reshape(-1, 2, 8, 64)[:, ::-1].reshape(-1, 64).T
        if name in ("L1_ffn_w1", "L1_ffn_w3"):
            arrays[name + "T"] = a.transpose(2, 0, 1).reshape(64, -1)
        if name == "L1_ffn_w2":
            arrays[name + "T"] = a.transpose(0, 2, 1).reshape(-1, 64)
        if name == "L3_ffn_w1":
            arrays[name + "T"] = a.transpose(1, 0, 2).reshape(64, -1)
        if name == "L3_ffn_b1":
            arrays["b1_columns"] = a.reshape(-1, 128).T
        if name == "L2_ffn_wr":
            arrays["wr_wide"] = _np.broadcast_to(a, (64, PT))
        if name == "L2_ffn_br":
            arrays["br_wide"] = _np.broadcast_to(a[None, :], (1, PT))
        if name == "L2_attn_W_embed":
            arrays[name + "T"] = a.transpose(0, 2, 1)
    for name in ("L0_ffn_W1", "L0_ffn_b1", "L1_ffn_w1", "L1_ffn_w2", "L1_ffn_w3", "L2_attn_W_embed", "L2_ffn_attention_mask",
                 "L2_ffn_wr", "L2_ffn_br", "L3_ffn_w1", "L3_ffn_b1"):
        del arrays[name]
    arrays = {f"in_{k}": _np.ascontiguousarray(a) for k, a in arrays.items()}
    A = {k[3:]: nc.dram_tensor(k, a.shape, _mybir.dt.from_np(a.dtype), kind="ExternalInput").ap()
         for k, a in arrays.items()}
    out = nc.dram_tensor("out", (BATCH, T, C), F32, kind="ExternalOutput").ap()
    build(nc, A, out)
    r = _run(nc, [arrays], core_ids=[0])
    return r.results[0]["out"]
```

```python
import math
from contextlib import ExitStack

import numpy as np
import concourse.bass as bass
from concourse import mybir

F32 = mybir.dt.float32
BF16 = mybir.dt.bfloat16
ALU = mybir.AluOpType
ACT = mybir.ActivationFunctionType
AX = mybir.AxisListType

BATCH, SAMPLES = 64, 4000
C = 64
POINTS = 4 * (SAMPLES - 1) + 1
T = (POINTS - 64) // 64 + 1
PT = 125
OFF = T - PT
ROWS = (OFF, PT)
PAIRS = BATCH // 2
EXPERTS = 8
NEG = -1.0e30
BODIES = 4
TRANSPOSED = ("L0_attn_Wq", "L0_attn_Wk", "L0_attn_Wv", "L0_attn_Wo", "L1_ffn_wq", "L1_ffn_wk", "L1_ffn_wv",
              "L1_ffn_wo", "L1_ffn_router_w", "L2_attn_W_out")

PER = {
    "att0.kept": 2,
    "att0.const_loaded": 9,
    "att0.exp_ready": 8,
    "att0.front_vec": 3,
    "att0.loaded": 2,
    "att0.max_ready": 8,
    "att0.s_done": 8,
    "att0.st_done": 8,
    "att0.stored": 2,
    "att0.vec": 5,
    "att1.kept": 2,
    "att1.const_loaded": 16,
    "att1.exp_ready": 8,
    "att1.front_vec": 15,
    "att1.handed_on": 3,
    "att1.loaded": 2,
    "att1.masked": 8,
    "att1.max_ready": 8,
    "att1.norm_centered": 2,
    "att1.norm_powered": 2,
    "att1.norm_squared": 2,
    "att1.norm_variance": 2,
    "att1.r_done": 4,
    "att1.s_done": 8,
    "att1.st_done": 8,
    "att1.stored": 2,
    "att1.vec": 16,
    "att2.kept": 3,
    "att2.const_loaded": 5,
    "att2.exp_ready": 6,
    "att2.front_vec": 3,
    "att2.loaded": 3,
    "att2.max_ready": 3,
    "att2.oT_ready": 3,
    "att2.o_done": 3,
    "att2.pt_done": 3,
    "att2.pt_ready": 3,
    "att2.qk_done": 3,
    "att2.qk_ready": 3,
    "att2.s_done": 3,
    "att2.stored": 3,
    "att2.v_done": 3,
    "att2.v_ready": 3,
    "att2.vec": 6,
    "att2.y_done": 3,
    "att3.kept": 2,
    "att3.const_loaded": 6,
    "att3.d_done": 2,
    "att3.d_used": 2,
    "att3.exp_ready": 32,
    "att3.front_vec": 5,
    "att3.loaded": 2,
    "att3.max_ready": 16,
    "att3.oT_done": 4,
    "att3.oT_ready": 4,
    "att3.o_done": 2,
    "att3.o_ready": 2,
    "att3.proj_done": 12,
    "att3.proj_ready": 12,
    "att3.pt_done": 16,
    "att3.pt_ready": 16,
    "att3.round": 8,
    "att3.s_done": 16,
    "att3.stored": 2,
    "att3.vec": 18,
    "att3.w_split": 5,
    "att3.x3_split": 5,
    "att3.y_done": 2,
    "att3.y_used": 2,
    "ffn0.kept": 2,
    "ffn0.const_loaded": 4,
    "ffn0.front_vec": 3,
    "ffn0.hid_done": 2,
    "ffn0.hid_ready": 2,
    "ffn0.loaded": 2,
    "ffn0.stored": 2,
    "ffn0.vec": 8,
    "ffn0.weights": 13,
    "mod2.kept": 2,
    "mod2.const_loaded": 8,
    "mod2.front_vec": 3,
    "mod2.hid_done": 2,
    "mod2.hid_ready": 2,
    "mod2.loaded": 2,
    "mod2.stored": 2,
    "mod2.vec": 16,
    "moe1.gate_done": 16,
    "moe1.hid_ready": 16,
    "moe1.loaded": 4,
    "moe1.silu_ready": 16,
    "moe1.stored": 2,
    "moe1.vec": 4,
    "moe1.w1_loaded": 2,
    "moe1.w3_loaded": 2,
    "moe1.w_split": 10,
    "moe1.x3_split": 5,
    "moe1.xT_loaded": 2,
    "moe1.y_done": 4,
    "moe1.y_used": 4,
    "ret1.kept": 2,
    "ret1.const_loaded": 8,
    "ret1.front_vec": 5,
    "ret1.loaded": 2,
    "ret1.p_ready": 2,
    "ret1.qk_ready": 2,
    "ret1.r_done": 4,
    "ret1.s_done": 2,
    "ret1.stored": 2,
    "route.const_loaded": 5,
    "route.expd": 3,
    "route.shifted": 3,
    "route.stored": 2,
    "route.vec": 26,
    "sw3.kept": 2,
    "sw3.const_loaded": 10,
    "sw3.front_vec": 15,
    "sw3.hid_done": 16,
    "sw3.hid_ready": 16,
    "sw3.loaded": 2,
    "sw3.stored": 2,
    "sw3.vec": 10,
    "sw3.w_split": 10,
    "sw3.x3_split": 5,
    "sw3.y_done": 4,
    "sw3.y_used": 4,
    "tok.act": 2,
    "tok.const_loaded": 2,
    "tok.loaded": 2,
    "tok.stored": 2,
    "tok.vec": 7,
}
MISCOUNTED = {}


class Event:

    def __init__(self, nc, stage, name, unit=1):
        self.key = f"{stage}.{name}"
        self.sem = nc.alloc_semaphore(name=f"{stage}_{name}")
        self.unit = unit
        self.per = PER.get(self.key, 1)
        self.fired = 0

    def start(self):
        return (self.per + 1) * self.unit

    def one(self):
        self.fired += 1
        return self.sem, self.unit

    def after(self, i, k=None):
        k = self.per - 1 if k is None else k
        return self.sem, (i * self.per + (self.per + k + 2)) * self.unit

    def before(self, i):
        return self.sem, (i * self.per + (self.per + 1)) * self.unit

    def lagging(self, i):
        return self.sem, (i * self.per + 1) * self.unit

    def latest(self, i):
        return self.after(i, (self.fired - 1) % self.per)


class TransferEvents:

    def __init__(self, nc, stage, name, start=16):
        self.key, self.start = f"{stage}.{name}", start
        self.sems = [nc.alloc_semaphore(name=f"{stage}_{name}_{u}") for u in range(2)]
        self.per = PER.get(self.key, 1)
        self.fired = 0

    def one(self, u):
        self.fired += 1
        return self.sems[u], 16

    def after(self, n, u):
        return self.sems[u], (n - u) * (8 * self.per) + 16 * self.per + self.start

    def lagging(self, n, u):
        return self.sems[u], (n - u) * (8 * self.per) + 16


class Stage:

    def __init__(self, nc, name):
        self.nc, self.name, self.events, self.ctx = nc, name, {}, ExitStack()
        self.gates = {}

    def __enter__(self):
        self.ctx.__enter__()
        return self

    def __exit__(self, *e):
        if e[0] is None:
            self.ctx.__exit__(None, None, None)
        for s in self.events.values():
            if s.fired != s.per and not (s.fired and s.fired % s.per == 0 and s.loops == s.fired // s.per):
                MISCOUNTED[s.key] = s.fired // s.loops
        sems = [x for s in self.events.values() for x in (s.sems if isinstance(s, TransferEvents) else [s.sem])]
        sems += list(self.gates.values())
        self.nc.clear_and_free_semaphores(sems)
        self.nc.all_engine_barrier()

    def event(self, name, dma=False, bodies=1):
        s = self.events[name] = Event(self.nc, self.name, name, 16 if dma else 1)
        s.loops = bodies
        return s

    def transfers(self, name, bodies=BODIES, start=16):
        s = self.events[name] = TransferEvents(self.nc, self.name, name, start)
        s.loops = bodies
        return s

    def sb(self, name, shape, dt=F32):
        return self.ctx.enter_context(self.nc.sbuf_tensor(f"{self.name}_{name}", shape, dt))

    def held(self, engine):
        gate = self.gates.get(engine.engine)
        if gate is None:
            gate = self.gates[engine.engine] = self.nc.alloc_semaphore(
                name=f"{self.name}_held_{len(self.gates)}")
        engine.sem_inc(gate, 1)

    def psum(self, name, shape, dt=F32):
        return self.ctx.enter_context(self.nc.psum_tensor(f"{self.name}_{name}", shape, dt))

    def block(self):
        for s in self.events.values():
            if isinstance(s, TransferEvents):
                for sem in s.sems if s.start else ():
                    self.nc.sync.sem_inc(sem, 16)
            else:
                self.nc.sync.sem_inc(s.sem, s.start())
        self.nc.all_engine_barrier()
        return self.nc.Block()


def bc(ap, n):
    return bass.AP(ap.tensor, ap.offset, [list(x) for x in ap.ap] + [[0, n]])


def bcm(ap, at, n):
    a = [list(x) for x in ap.ap]
    return bass.AP(ap.tensor, ap.offset, a[:at] + [[0, n]] + a[at:])


def load_pair(sp, tile, dram, i, width=C):
    src = dram[bass.ds(i * 2, 2)]
    return [sp.dma_start(tile[:, t, :, :], bass.AP(src.tensor, src.offset + t * OFF * width,
                                                   [[width, PT], [T * width, 2], [1, width]]))
            for t in range(2)]


def store_pair(sp, dram, tile, i, width=C):
    dst = dram[bass.ds(i * 2, 2)]
    return [sp.dma_start(bass.AP(dst.tensor, dst.offset + t * OFF * width,
                                 [[width, ROWS[t]], [T * width, 2], [1, width]]), tile[0:ROWS[t], t, :, :])
            for t in range(2)]


class Norm:

    def __init__(self, st, rows, groups, bodies=1, name="norm"):
        self.rows, self.g = rows, groups
        self.sum = st.sb(name + "_sum", [rows, groups])
        self.xc = st.sb(name + "_centered", [rows, groups, C])
        self.sq = st.sb(name + "_squares", [rows, groups, C])
        self.var = st.sb(name + "_var", [rows, groups])
        self.rstd = st.sb(name + "_rstd", [rows, groups])
        self.expo = st.sb(name + "_exponent", [rows, groups])
        self.centered = st.event(name + "_centered", bodies=bodies)
        self.squared = st.event(name + "_squared", bodies=bodies)
        self.variance = st.event(name + "_variance", bodies=bodies)
        self.powered = st.event(name + "_powered", bodies=bodies)

    def center(self, v, i, x, chain):
        v.reduce_sum(self.sum[:, :], x, AX.X).then_inc(*chain.one())
        v.wait_ge(*chain.latest(i))
        v.tensor_scalar(self.sum[:, :], self.sum[:, :], -1.0 / C, None, ALU.mult).then_inc(*chain.one())
        v.wait_ge(*chain.latest(i))
        v.tensor_tensor(self.xc[:, :, :], x, bc(self.sum[:, :], C), ALU.add).then_inc(*self.centered.one())

    def scale(self, v, i, k, x, out, eps, chain):
        v.wait_ge(*self.squared.after(i, k))
        v.reduce_sum(self.var[:, :], self.sq[:, :, :], AX.X).then_inc(*chain.one())
        v.wait_ge(*chain.latest(i))
        v.tensor_scalar(self.var[:, :], self.var[:, :], 1.0 / C, eps, ALU.mult, ALU.add).then_inc(
            *self.variance.one())
        v.wait_ge(*self.powered.after(i, k))
        return v.tensor_tensor(out, x, bc(self.rstd[:, :], C), ALU.mult)

    def square(self, a, i, k, x):
        a.wait_ge(*self.centered.after(i, k))
        a.activation(self.sq[:, :, :], x, ACT.Square).then_inc(*self.squared.one())

    def power(self, p, i, k):
        p.wait_ge(*self.variance.after(i, k))
        p.tensor_tensor(self.rstd[:, :], self.var[:, :], self.expo[:, :], ALU.pow).then_inc(*self.powered.one())

    def square_pool(self, p, i, k, x):
        p.wait_ge(*self.centered.after(i, k))
        p.tensor_tensor(self.sq[:, :, :], x, x, ALU.mult).then_inc(*self.squared.one())


def g4(ap):
    return ap.rearrange("p t b c -> p (t b) c")


def stage_tokenizer(nc, A, h):
    WG = 8
    GROUPS = T // WG
    TAPS = 20
    NF = 33
    SPAN = 16 * (WG - 1) + TAPS
    Q = (T + 1) // 2
    r5 = math.sqrt(0.5)
    with Stage(nc, "tok") as st:
        xs = st.sb("samples", [BATCH, 2, SPAN])
        wt = st.sb("taps", [TAPS, 2, WG, 64])
        ident = st.sb("ident", [64, 64])
        dft = st.sb("dft", [64, 2 * NF])
        sT = st.sb("samplesT", [TAPS, WG, BATCH])
        poly = st.sb("poly", [64, WG * BATCH])
        gauss = st.sb("gauss", [64, WG * BATCH])
        kw = st.sb("kernelled", [64, WG * BATCH])
        sq = st.sb("squares", [128, 4, 2 * NF])
        mag = st.sb("magnitude", [128, Q, NF])
        d = st.sb("excess", [128, Q, NF])
        lg = st.sb("gap", [128, Q, NF])
        top = st.sb("top", [128, Q])
        thr = st.sb("thr", [128, 2, Q])
        out = st.sb("out", [128, Q, C])
        bias = st.sb("bias", [128, 4])
        pT = st.psum("pT", [TAPS, 2, WG, BATCH])
        pI = st.psum("pI", [64, 2, WG * BATCH])
        pM = st.psum("pM", [128, 2, 4, 128])

        const_loaded = st.event("const_loaded", dma=True)
        loaded = st.transfers("loaded")
        memset_done = st.event("memset_done")
        transposed = st.event("transposed", bodies=BODIES)
        samples_ready = st.event("samples_ready", bodies=BODIES)
        interpolated = st.event("interpolated", bodies=BODIES)
        squared = st.event("squared", bodies=BODIES)
        kernels_done = st.event("kernels_done", bodies=BODIES)
        windows_ready = st.event("windows_ready", bodies=BODIES)
        spectrum = st.event("spectrum", bodies=BODIES)
        squares_ready = st.event("squares_ready", bodies=BODIES)
        power_ready = st.event("power_ready", bodies=BODIES)
        vec = st.event("vec")
        excess_ready = st.event("excess_ready")
        magnitude_ready = st.event("magnitude_ready")
        excess_exp = st.event("excess_exp")
        gap_ready = st.event("gap_ready")
        act = st.event("act")
        gap_log = st.event("gap_log")
        out_ready = st.event("out_ready")
        stored = st.event("stored", dma=True)

        def groups(engine, body):
            with engine.Fori(0, GROUPS // 2) as j:
                body(j * 2, 0, WG)
                body(j * 2 + 1, 1, WG)
            for i in range(GROUPS - GROUPS % 2, GROUPS):
                body(i, i % 2, WG)
            body(GROUPS, GROUPS % 2, T - GROUPS * WG)

        with st.block() as block:
            @block.sync
            def _(sp):
                sp.dma_start(ident[:, :], A["const_ident"][0:64, 0:64]).then_inc(*const_loaded.one())
                sp.dma_start(dft[:, :], A["const_dft"][:, :]).then_inc(*const_loaded.one())

                def body(i, u, nw):
                    span = 16 * (nw - 1) + TAPS
                    sp.wait_ge(*interpolated.lagging(i))
                    st.held(sp)
                    sp.dma_start(xs[:, u, 0:span], A["x_edge"][:, bass.ds(i * (16 * WG), span)]).then_inc(
                        *loaded.one(u))
                    sp.dma_start(wt[:, u, 0:nw, :], A["const_taps"][bass.ds(i * WG, nw)].rearrange(
                        "w k f -> k w f")).then_inc(*loaded.one(u))
                groups(sp, body)
                sp.wait_ge(*out_ready.after(0))
                for w2 in range(2):
                    n = Q - w2
                    dst = h[:, w2:w2 + 1, :]
                    dst = bass.AP(dst.tensor, dst.offset, [[T * C, 64], [2 * C, n], [1, C]])
                    sp.dma_start(dst, out[w2 * 64:w2 * 64 + 64, 0:n, :]).then_inc(*stored.one())
                sp.wait_ge(*stored.after(0))

            @block.tensor
            def _(pe):
                pe.wait_ge(*const_loaded.after(0))

                def body(i, u, nw):
                    pe.wait_ge(*loaded.after(i, u))
                    pe.wait_ge(*samples_ready.before(i))
                    st.held(pe)
                    for w in range(nw):
                        ins = pe.transpose(pT[:, u, w, :], xs[:, u, 16 * w:16 * w + TAPS], ident[:, :])
                    ins.then_inc(*transposed.one())
                    pe.wait_ge(*samples_ready.after(i))
                    pe.wait_ge(*kernels_done.before(i))
                    st.held(pe)
                    for w in range(nw):
                        ins = pe.matmul(pI[:, u, w * 64:w * 64 + 64], wt[:, u, w, :], sT[:, w, :], start=True,
                                        stop=True)
                    ins.then_inc(*interpolated.one())
                    pe.wait_ge(*windows_ready.after(i))
                    pe.wait_ge(*squares_ready.before(i))
                    st.held(pe)
                    rows = min(128, 64 * nw)
                    for q in range(64 * nw // rows):
                        ins = pe.matmul(pM[0:rows, u, q, 0:2 * NF], kw[:, q * rows:q * rows + rows], dft[:, :],
                                        start=True, stop=True)
                    ins.then_inc(*spectrum.one())
                groups(pe, body)

            @block.scalar
            def _(a):
                a.wait_ge(*memset_done.after(0))

                def body(i, u, nw):
                    n, rows = 64 * nw, min(128, 64 * nw)
                    a.wait_ge(*interpolated.after(i))
                    a.wait_ge(*windows_ready.before(i))
                    a.activation(poly[:, 0:n], pI[:, u, 0:n], ACT.Square, bias=bias[0:64, 0:1], scale=r5)
                    a.activation(gauss[:, 0:n], pI[:, u, 0:n], ACT.Square, bias=bias[0:64, 1:2]).then_inc(
                        *squared.one())
                    a.wait_ge(*squared.after(i))
                    a.activation(gauss[:, 0:n], gauss[:, 0:n], ACT.Exp, bias=bias[0:64, 2:3],
                                 scale=-0.5).then_inc(*kernels_done.one())
                    a.wait_ge(*spectrum.after(i))
                    a.wait_ge(*power_ready.before(i))
                    a.activation(sq[0:rows, 0:n // rows, :], pM[0:rows, u, 0:n // rows, 0:2 * NF],
                                 ACT.Square).then_inc(*squares_ready.one())
                groups(a, body)
                a.wait_ge(*power_ready.before(GROUPS + 1))
                a.activation(mag[:, :, :], mag[:, :, :], ACT.Sqrt).then_inc(*magnitude_ready.one())
                a.wait_ge(*excess_ready.after(0))
                a.activation(d[:, :, :], d[:, :, :], ACT.Exp, scale=-1.0).then_inc(*excess_exp.one())
                a.wait_ge(*gap_ready.after(0))
                a.activation(lg[:, :, :], lg[:, :, :], ACT.Abs).then_inc(*act.one())
                a.wait_ge(*act.latest(0))
                a.activation(lg[:, :, :], lg[:, :, :], ACT.Exp, scale=-1.0).then_inc(*act.one())
                a.wait_ge(*act.latest(0))
                a.activation(lg[:, :, :], lg[:, :, :], ACT.Ln, bias=bias[:, 3:4]).then_inc(*gap_log.one())

            @block.vector
            def _(v):
                v.memset(bias[:, 0:1], 1.3 * r5)
                v.memset(bias[:, 1:2], -0.7)
                v.memset(bias[:, 2:3], math.log(0.5))
                v.memset(mag[:, Q - 1, :], 0.0)
                v.memset(bias[:, 3:4], 1.0).then_inc(*memset_done.one())
                v.wait_ge(*memset_done.after(0))

                def link(ins):
                    ins.then_inc(*vec.one())
                    v.wait_ge(*vec.latest(0))

                def body(i, u, nw):
                    n, rows = 64 * nw, min(128, 64 * nw)
                    R, q = slice(0, rows), n // rows
                    v.wait_ge(*transposed.after(i))
                    v.wait_ge(*interpolated.before(i))
                    v.tensor_copy(sT[:, 0:nw, :], pT[:, u, 0:nw, :]).then_inc(*samples_ready.one())
                    v.wait_ge(*kernels_done.after(i))
                    v.wait_ge(*spectrum.before(i))
                    v.tensor_tensor(kw[:, 0:n], poly[:, 0:n], gauss[:, 0:n], ALU.add).then_inc(
                        *windows_ready.one())
                    v.wait_ge(*squares_ready.after(i))
                    v.tensor_tensor(mag[R, bass.ds(i * 4, q), :], sq[R, 0:q, 0:NF], sq[R, 0:q, NF:2 * NF],
                                    ALU.add).then_inc(*power_ready.one())
                groups(v, body)
                v.wait_ge(*magnitude_ready.after(0))
                link(v.reduce_max(top[:, :], mag[:, :, :], AX.X))
                v.tensor_scalar(thr[:, 0, :], top[:, :], 0.12, None, ALU.mult)
                link(v.tensor_scalar(thr[:, 1, :], top[:, :], 0.9, None, ALU.mult))
                v.tensor_tensor(d[:, :, :], mag[:, :, :], bc(thr[:, 0, :], NF), ALU.subtract).then_inc(
                    *excess_ready.one())
                v.wait_ge(*excess_exp.after(0))
                link(v.tensor_scalar(d[:, :, :], d[:, :, :], 1.0, None, ALU.add))
                link(v.reciprocal(d[:, :, :], d[:, :, :]))
                link(v.tensor_tensor(mag[:, :, :], mag[:, :, :], d[:, :, :], ALU.mult))
                v.tensor_tensor(lg[:, :, :], mag[:, :, :], bc(thr[:, 1, :], NF), ALU.subtract).then_inc(
                    *gap_ready.one())
                link(v.tensor_tensor(mag[:, :, :], mag[:, :, :], bc(thr[:, 1, :], NF), ALU.min))
                v.wait_ge(*gap_log.after(0))
                link(v.tensor_tensor(out[:, :, 0:NF], mag[:, :, :], lg[:, :, :], ALU.subtract))
                lo = out[:, :, 0:NF]
                mirror = bass.AP(lo.tensor, lo.offset + NF - 2, [list(lo.ap[0]), list(lo.ap[1]), [-1, NF - 2]])
                v.tensor_copy(out[:, :, NF:C], mirror).then_inc(*out_ready.one())


def pipelined(engine, front, main, steps=None):
    for step in [()] if steps is None else [(s,) for s in range(steps)]:
        front(0, 0, *step)
    with engine.Fori(0, PAIRS // 2 - 1) as j:
        for u in range(2):
            n = j * 2 + u
            main(n, u, lambda *step: front(n + 1, 1 - u, *step))
    main(PAIRS - 2, 0, lambda *step: front(PAIRS - 1, 1, *step))
    main(PAIRS - 1, 1, lambda *step: None)


class Front:

    def __init__(self, st, twice=False, tiles=2, rows=PT):
        self.st, self.twice = st, twice
        self.tiles = tiles
        self.F = st.sb("F", [rows, 2, tiles, 2, C])
        self.X = st.sb("X", [rows, 2, tiles, 2, C])
        self.xn = st.sb("xn", [rows, 2, tiles, 2, C * (1 + twice)])
        self.xT = st.sb("xT", [C + 1, 2, 2, T])
        self.H1 = st.sb("H1", [rows, 2, tiles, 2, C])
        self.ident = st.sb("ident", [128, 128])
        self.norm = Norm(st, rows, 2 * tiles, bodies=BODIES)
        self.pX = st.psum("pX", [C * (1 + twice), 2, 256])
        self.const_loaded = st.event("const_loaded", dma=True)
        self.memset_done = st.event("memset_done")
        self.loaded = st.transfers("loaded")
        self.kept = st.transfers("kept")
        self.front_vec = st.event("front_vec", bodies=BODIES)
        self.xn_ready = st.event("xn_ready", bodies=BODIES)
        self.xT_done = st.event("xT_done", bodies=BODIES)
        self.xT_ready = st.event("xT_ready", bodies=BODIES)
        self.h_ready = st.event("h_ready", bodies=BODIES)
        self.stored = st.transfers("stored")

    def memsets(self, v):
        v.memset(self.xT[C:C + 1, :, :, :], 1.0)
        v.memset(self.norm.expo[:, :], -0.5).then_inc(*self.memset_done.one())

    def stream(self, sp, src, dst, beside=None, after=None):
        def rows(dram, i):
            if self.tiles == 2:
                return None
            d = dram[bass.ds(i * 2, 2)]
            th = T // 3
            return [bass.AP(d.tensor, d.offset + j * th * C, [[C, th], [T * C, 2], [1, C]]) for j in range(3)]

        def load(tile, n):
            if self.tiles == 2:
                return load_pair(sp, tile, src, n)
            return [sp.dma_start(tile[:, j, :, :], x) for j, x in enumerate(rows(src, n))]

        def ahead(n, u):
            sp.wait_ge(*self.norm.centered.lagging(n))
            self.st.held(sp)
            for ins in load(self.F[:, u, :, :, :], n):
                ins.then_inc(*self.loaded.one(u))

        def keep(n, u):
            sp.wait_ge(*self.h_ready.lagging(n))
            self.st.held(sp)
            for ins in load(self.X[:, u, :, :, :], n):
                ins.then_inc(*self.kept.one(u))
            if beside:
                beside(n, u)

        def store(n, u):
            sp.wait_ge(*self.h_ready.after(n))
            self.st.held(sp)
            out = self.H1[:, u, :, :, :]
            if self.tiles == 2:
                ins = store_pair(sp, dst, out, n)
            else:
                ins = [sp.dma_start(x, out[:, j, :, :]) for j, x in enumerate(rows(dst, n))]
            for x in ins:
                x.then_inc(*self.stored.one(u))
            if after:
                after(n, u)
        for n in range(2):
            ahead(n, n)
            keep(n, n)
        with sp.Fori(0, PAIRS // 2 - 1) as j:
            for u in range(2):
                n = j * 2 + u
                ahead(n + 2, u)
                store(n, u)
                keep(n + 2, u)
        for n in (PAIRS - 2, PAIRS - 1):
            store(n, n % 2)
        for n in (PAIRS - 2, PAIRS - 1):
            sp.wait_ge(*self.stored.after(n, n % 2))

    def transpose(self, pe, n, u):
        pe.wait_ge(*self.xn_ready.after(n))
        pe.wait_ge(*self.xT_ready.before(n))
        self.st.held(pe)
        transpose_rows(pe, self.pX, self.xn[:, u, :, :, :], self.ident).then_inc(*self.xT_done.one())

    def square(self, a, n, u):
        self.norm.square(a, n, 0, self.norm.xc[:, :, :])

    def normalise(self, v, n, u):
        v.wait_ge(*self.loaded.after(n, u))
        self.norm.center(v, n, g4(self.F[:, u, :, :, :]), self.front_vec)
        ins = self.norm.scale(v, n, 0, self.norm.xc[:, :, :], g4(self.xn[:, u, :, :, 0:C]), 1e-5, self.front_vec)
        if self.twice:
            ins = v.tensor_tensor(g4(self.xn[:, u, :, :, C:2 * C]), self.norm.xc[:, :, :],
                                  bc(self.norm.rstd[:, :], C), ALU.mult)
        ins.then_inc(*self.xn_ready.one())

    def channels(self, v, n, u):
        v.wait_ge(*self.xT_done.after(n))
        v.tensor_copy(self.xT[0:C, u, :, :], self.pX[0:C, :, 0:T]).then_inc(*self.xT_ready.one())


def transpose_rows(pe, dst, src, ident):
    for b in range(2):
        for t in range(2):
            ins = pe.transpose(dst[:, b, t * OFF:t * OFF + ROWS[t]], src[0:ROWS[t], t, b, :],
                               ident[0:ROWS[t], 0:ROWS[t]])
    return ins


def const(sp, signal, dst, src):
    sp.dma_start(dst, src).then_inc(*signal.one())


def row(ap):
    return bass.AP(ap.tensor, ap.offset, [[0, 1]] + [list(x) for x in ap.ap])


def every_row(ap, rows):
    return bass.AP(ap.tensor, ap.offset, [[0, rows]] + [list(x) for x in ap.ap])


class Rank:

    def __init__(self, st, rows, groups, k):
        self.rows, self.g, self.k = rows, groups, k
        self.gt = st.sb("rank_gt", [rows, groups, EXPERTS, EXPERTS])
        self.eq = st.sb("rank_eq", [rows, groups, EXPERTS, EXPERTS])
        self.rank = st.sb("rank", [rows, groups, EXPERTS])
        self.earlier = st.sb("rank_earlier", [rows, EXPERTS * EXPERTS])

    def select(self, v, i, w, sel, chain):
        e = EXPERTS
        other, own = bcm(w, 2, e), bc(w, e)
        v.tensor_tensor(self.gt[:, :, :, :], other, own, ALU.is_gt)
        v.tensor_tensor(self.eq[:, :, :, :], other, own, ALU.is_equal).then_inc(*chain.one())
        v.wait_ge(*chain.latest(i))
        v.tensor_tensor(self.eq[:, :, :, :].rearrange("p g e f -> p g (e f)"),
                        self.eq[:, :, :, :].rearrange("p g e f -> p g (e f)"),
                        bcm(self.earlier[:, :], 1, self.g), ALU.mult).then_inc(*chain.one())
        v.wait_ge(*chain.latest(i))
        v.tensor_tensor(self.gt[:, :, :, :], self.gt[:, :, :, :], self.eq[:, :, :, :], ALU.add).then_inc(
            *chain.one())
        v.wait_ge(*chain.latest(i))
        v.reduce_sum(self.rank[:, :, :], self.gt[:, :, :, :], AX.X).then_inc(*chain.one())
        v.wait_ge(*chain.latest(i))
        return v.tensor_scalar(sel, self.rank[:, :, :], float(self.k), None, ALU.is_lt)


def stage_attention0(nc, A, h, mean_dram):
    H, D = 4, 16
    STEPS, AHEAD = 2 * H, 12
    S0 = 3
    with Stage(nc, "att0") as st:
        f = Front(st)
        tail = Norm(st, PT, 4, bodies=BODIES, name="tail")
        wq = st.sb("wq", [C + 1, H, 32])
        wk = st.sb("wk", [C + 1, H, 32])
        wv = st.sb("wv", [C + 1, H, D + 1])
        wo = st.sb("wo", [C + 1, C])
        ones = st.sb("ones", [128, 1])
        qT = st.sb("qT", [128, 2, T])
        kT = st.sb("kT", [128, 2, 2, T])
        qmT = st.sb("qmT", [128, 2, T])
        V = st.sb("V", [PT, 2, 2, 2, H, D + 1])
        M = st.sb("M", [PT, 2, 2, H, 32])
        E = st.sb("E", [PT, 2, 2, H, T])
        rden = st.sb("rden", [PT, 4, H])
        ob = st.sb("ob", [PT, 4, H, D], BF16)
        of = st.sb("of", [PT, 2, 2, C])
        oT = st.sb("oT", [C + 1, 2, T])
        h2 = st.sb("h2", [PT, 2, 2, C])
        mean = st.sb("mean", [C, 2 * (PAIRS + 1)])

        pX = f.pX
        pQ = st.psum("pQ", [128, 512])
        pK = st.psum("pK", [128, 512])
        pS = st.psum("pS", [PT, 4, 512])
        pO = st.psum("pO", [PT, 4, 128])
        zeroed = st.event("zeroed")
        vec0 = st.event("vec0")
        names = """vec q_done k_done q_ready k_ready v_done v_ready s_done max_ready qm_done qm_ready st_done
            exp_ready o_done o_ready oT_done oT_ready y_done h2_ready"""
        (vec, q_done, k_done, q_ready, k_ready, v_done, v_ready, s_done, max_ready, qm_done, qm_ready, st_done,
         exp_ready, o_done, o_ready, oT_done, oT_ready, y_done, h2_ready) = (
             st.event(x, bodies=BODIES) for x in names.split())
        mean_done = st.event("mean_done", bodies=BODIES + 1)
        mean_ready = st.event("mean_ready", bodies=BODIES + 1)
        mean_stored = st.event("mean_stored", dma=True)
        qv, kv = pQ[:, 0:2 * T], pK[:, 0:2 * T]
        vv = pK[0:PT, 0:4 * H * (D + 1)].rearrange("p (g e) -> p g e", g=4)

        with st.block() as block:
            @block.sync
            def _(sp):
                cl = f.const_loaded
                const(sp, cl, f.ident[:, :], A["const_ident"])
                sp.wait_ge(*zeroed.after(0))
                for w, n, width in ((wq, "q", D), (wk, "k", D), (wv, "v", D)):
                    const(sp, cl, w[0:C, :, 0:D], A[f"L0_attn_W{n}T"].rearrange("c (h d) -> c h d", h=H))
                    const(sp, cl, w[C:C + 1, :, 0:D], A[f"L0_attn_b{n}"].rearrange("(o h d) -> o h d", o=1, h=H))
                const(sp, cl, wo[0:C, :], A["L0_attn_WoT"])
                const(sp, cl, wo[C:C + 1, :], row(A["L0_attn_bo"]))
                f.stream(sp, h, h)
                sp.wait_ge(*mean_ready.after(PAIRS))
                sp.dma_start(mean_dram[:, :], mean[:, 2:]).then_inc(*mean_stored.one())
                sp.wait_ge(*mean_stored.after(0))

            @block.gpsimd
            def _(g):
                g.wait_ge(*f.memset_done.after(0))

                def front(n, u):
                    f.norm.power(g, n, 0)

                def main(n, u, ahead):
                    ahead()
                    tail.square_pool(g, n, 0, tail.xc[:, :, :])
                    tail.power(g, n, 0)
                pipelined(g, front, main)

            @block.tensor
            def _(pe):
                pe.wait_ge(*f.const_loaded.after(0))
                pe.wait_ge(*f.memset_done.after(0))

                def front(n, u, step):
                    if step == 1:
                        f.transpose(pe, n, u)
                    if step == 2:
                        pe.wait_ge(*f.xT_ready.after(n))
                        pe.wait_ge(*qm_ready.before(n))
                        st.held(pe)
                        pe.matmul(qv, wq[:, :, :], f.xT[:, u, :, :], start=True, stop=True).then_inc(*q_done.one())
                        pe.matmul(kv, wk[:, :, :], f.xT[:, u, :, :], start=True, stop=True).then_inc(*k_done.one())
                    if step == S0:
                        pe.wait_ge(*k_ready.after(n))
                        st.held(pe)
                        for t in range(2):
                            for b in range(2):
                                ins = pe.matmul(vv[:, 2 * t + b, :], f.xT[:, u, b, t * OFF:t * OFF + PT],
                                                wv[:, :, :], start=True, stop=True)
                        ins.then_inc(*v_done.one())
                        pe.wait_ge(*q_ready.after(n))
                    if S0 <= step < S0 + STEPS:
                        s = step - S0
                        b, hd = s // H, s % H
                        r = 32 * hd
                        pe.wait_ge(*max_ready.after(n, s - 2))
                        for t in range(2):
                            ins = pe.matmul(pS[:, 2 + s % 2, t * T:t * T + T],
                                            qT[r:r + D, b, t * OFF:t * OFF + PT], kT[r:r + D, u, b, :],
                                            start=True, stop=True, tile_position=(r, 0))
                        ins.then_inc(*s_done.one())
                    if step == S0 + STEPS:
                        pe.wait_ge(*max_ready.after(n))
                        for b in range(2):
                            for t in range(2):
                                ins = pe.matmul(pQ[:, b * T + t * OFF:b * T + t * OFF + ROWS[t]],
                                                M[0:ROWS[t], t, b, :, :], f.ident[0:ROWS[t], 0:ROWS[t]],
                                                start=False, stop=True, skip_group_check=True)
                        ins.then_inc(*qm_done.one())

                def token_sums(n):
                    pe.wait_ge(*h2_ready.before(n))
                    st.held(pe)
                    for b in range(2):
                        for t in range(2):
                            ins = pe.matmul(pX[:, b, 0:1], h2[0:ROWS[t], t, b, :], ones[0:ROWS[t], :],
                                            start=(t == 0), stop=(t == 1))
                    ins.then_inc(*mean_done.one())

                def main(n, u, ahead):
                    pe.wait_ge(*qm_ready.after(n))
                    for step in range(AHEAD):
                        if step < STEPS:
                            s = step
                            b, hd = s // H, s % H
                            r = 32 * hd
                            pe.wait_ge(*exp_ready.after(n, s - 2))
                            for t in range(2):
                                ins = pe.matmul(pS[:, s % 2, t * T:t * T + T],
                                                kT[r:r + D + 1, u, b, t * OFF:t * OFF + PT],
                                                qmT[r:r + D + 1, b, :], start=True, stop=True,
                                                tile_position=(r, 0))
                            ins.then_inc(*st_done.one())
                        ahead(step)
                        if 1 <= step <= STEPS:
                            s = step - 1
                            b, hd = s // H, s % H
                            pe.wait_ge(*exp_ready.after(n, s))
                            if s == 0:
                                pe.wait_ge(*v_ready.after(n))
                                pe.wait_ge(*o_ready.before(n))
                            for t in range(2):
                                for kt in range(2):
                                    ins = pe.matmul(pO[:, 2 * t + b, hd * (D + 1):(hd + 1) * (D + 1)],
                                                    E[0:ROWS[kt], kt, b, hd, t * OFF:t * OFF + PT],
                                                    V[0:ROWS[kt], u, kt, b, hd, :], start=(kt == 0),
                                                    stop=(kt == 1))
                            if s == STEPS - 1:
                                ins.then_inc(*o_done.one())
                        if step == 5:
                            token_sums(n)
                        if step == STEPS + 1:
                            pe.wait_ge(*o_ready.after(n))
                            pe.wait_ge(*mean_ready.after(n))
                            st.held(pe)
                            transpose_rows(pe, pX, of, f.ident).then_inc(*oT_done.one())
                        if step == STEPS + 2:
                            pe.wait_ge(*oT_ready.after(n))
                            st.held(pe)
                            for t in range(2):
                                for b in range(2):
                                    ins = pe.matmul(pK[0:PT, (2 * t + b) * C:(2 * t + b + 1) * C],
                                                    oT[:, b, t * OFF:t * OFF + PT], wo[:, :], start=True, stop=True)
                            ins.then_inc(*y_done.one())
                pipelined(pe, front, main, steps=AHEAD)
                token_sums(PAIRS)

            @block.scalar
            def _(a):
                def front(n, u, step):
                    if step == 0:
                        f.square(a, n, u)
                    if step == 2:
                        a.wait_ge(*q_done.after(n))
                        a.activation(qT[:, :, :].rearrange("p b t -> p (b t)"), qv, ACT.Copy).then_inc(
                            *q_ready.one())
                    if step == S0:
                        a.wait_ge(*v_done.after(n))
                        a.activation(V[:, u, :, :, :, :].rearrange("p t b h d -> p (t b) (h d)"), vv,
                                     ACT.Copy).then_inc(*v_ready.one())
                    if step == S0 + STEPS:
                        a.wait_ge(*qm_done.after(n))
                        a.activation(qmT[:, :, :].rearrange("p b t -> p (b t)"), qv, ACT.Copy).then_inc(
                            *qm_ready.one())

                def means(n):
                    a.wait_ge(*mean_done.after(n))
                    a.activation(mean[:, bass.ds(n * 2, 2)], pX[:, :, 0], ACT.Copy, scale=1.0 / T).then_inc(
                        *mean_ready.one())

                def main(n, u, ahead):
                    for step in range(AHEAD):
                        if step < STEPS:
                            a.wait_ge(*st_done.after(n, step))
                            a.activation(E[:, :, step // H, step % H, :], pS[:, step % 2, 0:2 * T].rearrange(
                                "p (t n) -> p t n", t=2), ACT.Exp, scale=D ** -0.5).then_inc(*exp_ready.one())
                        ahead(step)
                        if step == 5:
                            means(n)
                pipelined(a, front, main, steps=AHEAD)
                means(PAIRS)

            @block.vector
            def _(v):
                v.memset(wq[:, :, :], 0.0)
                v.memset(wk[:, :, :], 0.0)
                v.memset(wv[:, :, :], 0.0).then_inc(*vec0.one())
                v.wait_ge(*vec0.after(0))
                v.memset(wk[C:C + 1, :, D:D + 1], 1.0)
                v.memset(wv[C:C + 1, :, D:D + 1], 1.0).then_inc(*zeroed.one())
                v.memset(ones[:, :], 1.0)
                v.memset(oT[C:C + 1, :, :], 1.0)
                v.memset(M[:, :, :, :, :], 0.0)
                v.memset(h2[:, :, :, :], 0.0)
                v.memset(tail.expo[:, :], -0.5)
                f.memsets(v)
                v.wait_ge(*f.memset_done.after(0))

                def front(n, u, step):
                    if step == 0:
                        f.normalise(v, n, u)
                    if step == 1:
                        v.wait_ge(*f.xT_done.after(n))
                        v.tensor_scalar(f.xT[0:C, u, :, :], pX[:, :, 0:T], -10000.0, 10000.0, ALU.max,
                                        ALU.min).then_inc(*f.xT_ready.one())
                    if step == 2:
                        v.wait_ge(*k_done.after(n))
                        v.tensor_copy(kT[:, u, :, :].rearrange("p b t -> p (b t)"), kv).then_inc(*k_ready.one())
                    if S0 <= step < S0 + STEPS:
                        s = step - S0
                        b, hd = s // H, s % H
                        if s == 0:
                            v.wait_ge(*qm_done.before(n))
                        v.wait_ge(*s_done.after(n, s))
                        v.tensor_reduce(M[:, :, b, hd, D], pS[:, 2 + s % 2, 0:2 * T].rearrange(
                            "p (t n) -> p t n", t=2), AX.X, ALU.max, negate=True).then_inc(*max_ready.one())

                def main(n, u, ahead):
                    for step in range(AHEAD):
                        ahead(step)
                        if step == STEPS:
                            v.wait_ge(*o_done.after(n))
                            o5 = pO[:, :, 0:H * (D + 1)].rearrange("p g (h d) -> p g h d", h=H)
                            v.reciprocal(rden[:, :, :], o5[:, :, :, D]).then_inc(*vec.one())
                            v.wait_ge(*vec.latest(n))
                            for g in range(4):
                                ins = v.tensor_tensor(ob[:, g, :, :], o5[:, g, :, 0:D], bc(rden[:, g, :], D),
                                                      ALU.mult)
                            ins.then_inc(*vec.one())
                            v.wait_ge(*vec.latest(n))
                            v.tensor_copy(g4(of[:, :, :, :]), ob[:, :, :, :].rearrange(
                                "p g h d -> p g (h d)")).then_inc(*o_ready.one())
                        if step == STEPS + 1:
                            v.wait_ge(*oT_done.after(n))
                            v.tensor_copy(oT[0:C, :, :], pX[:, :, 0:T]).then_inc(*oT_ready.one())
                        if step == STEPS + 2:
                            v.wait_ge(*y_done.after(n))
                            v.wait_ge(*f.stored.lagging(n, u))
                            v.wait_ge(*f.kept.after(n, u))
                            own = g4(f.H1[:, u, :, :, :])
                            v.tensor_tensor(own, g4(f.X[:, u, :, :, :]),
                                            pK[0:PT, 0:4 * C].rearrange("p (g c) -> p g c", g=4), ALU.add).then_inc(
                                *f.h_ready.one())
                    v.wait_ge(*f.h_ready.after(n))
                    tail.center(v, n, own, vec)
                    v.wait_ge(*mean_done.after(n))
                    tail.scale(v, n, 0, tail.xc[:, :, :], g4(h2[:, :, :, :]), 1e-5, vec).then_inc(*h2_ready.one())
                pipelined(v, front, main, steps=AHEAD)


def stage_router0(nc, A, mean_dram, route_dram, chosen_dram):
    capacity = float(math.ceil(BATCH * T * 1.25 / EXPERTS))
    E, B = EXPERTS, BATCH
    with Stage(nc, "route") as st:
        mT = st.sb("mean", [C + 1, B])
        wr = st.sb("wr", [C + 1, E])
        ones = st.sb("ones", [B, B])
        z = st.sb("z", [B, E])
        s1 = st.sb("s1", [B, 1])
        p = st.sb("p", [B, E])
        ld = st.sb("load", [B, E])
        w = st.sb("w", [B, E])
        sel = st.sb("sel", [B, E])
        pick = st.sb("pick", [B, 4, E])
        number = st.sb("number", [B, E])
        got = st.sb("got", [B, 4])
        chosen = st.sb("chosen", [B, 2], mybir.dt.int32)
        rank = Rank(st, B, 1, 2)
        pL = st.psum("pL", [B, 2, E])
        const_loaded = st.event("const_loaded", dma=True)
        memset_done = st.event("memset_done")
        logits = st.event("logits")
        probs = st.event("probs")
        loads = st.event("loads")
        vec = st.event("vec")
        shifted = st.event("shifted")
        expd = st.event("expd")
        ready = st.event("ready")
        stored = st.event("stored", dma=True)
        with st.block() as block:
            @block.sync
            def _(sp):
                const(sp, const_loaded, mT[0:C, :], mean_dram[:, :])
                const(sp, const_loaded, wr[0:C, :], A["L0_ffn_Wr"])
                const(sp, const_loaded, wr[C:C + 1, :], row(A["L0_ffn_br"]))
                const(sp, const_loaded, rank.earlier[:, :], every_row(A["const_earlier"], B))
                const(sp, const_loaded, number[:, :], every_row(A["const_number"], B))
                sp.wait_ge(*ready.after(0))
                sp.dma_start(route_dram[:, :], got[:, 2:4]).then_inc(*stored.one())
                sp.dma_start(chosen_dram[:, :], chosen[:, :]).then_inc(*stored.one())
                sp.wait_ge(*stored.after(0))

            @block.tensor
            def _(pe):
                pe.wait_ge(*const_loaded.after(0))
                pe.wait_ge(*memset_done.after(0))
                pe.matmul(pL[:, 0, :], mT[:, :], wr[:, :], start=True, stop=True).then_inc(*logits.one())
                pe.wait_ge(*probs.after(0))
                pe.matmul(pL[:, 1, :], ones[:, :], p[:, :], start=True, stop=True).then_inc(*loads.one())

            @block.scalar
            def _(a):
                for k in range(3):
                    a.wait_ge(*shifted.after(0, k))
                    a.activation(z[:, :], z[:, :], ACT.Exp).then_inc(*expd.one())

            @block.vector
            def _(v):
                def link(ins):
                    ins.then_inc(*vec.one())
                    v.wait_ge(*vec.latest(0))

                def softmax(k, src, dst, sig):
                    link(v.reduce_max(s1[:, :], src, AX.X))
                    v.tensor_scalar(z[:, :], src, s1[:, 0:1], None, ALU.subtract).then_inc(*shifted.one())
                    v.wait_ge(*expd.after(0, k))
                    if k == 2:
                        link(v.tensor_tensor(z[:, :], z[:, :], sel[:, :], ALU.mult))
                    link(v.reduce_sum(s1[:, :], z[:, :], AX.X))
                    link(v.reciprocal(s1[:, :], s1[:, :]))
                    v.tensor_scalar(dst, z[:, :], s1[:, 0:1], None, ALU.mult).then_inc(*sig.one())
                    v.wait_ge(*sig.latest(0))

                v.memset(ones[:, :], 1.0)
                v.memset(mT[C:C + 1, :], 1.0).then_inc(*memset_done.one())
                v.wait_ge(*logits.after(0))
                softmax(0, pL[:, 0, :], p[:, :], probs)
                v.wait_ge(*loads.after(0))
                link(v.tensor_scalar(ld[:, :], pL[:, 1, :], float(T), None, ALU.mult))
                link(v.reciprocal(ld[:, :], ld[:, :]))
                link(v.tensor_scalar(ld[:, :], ld[:, :], capacity, 1.0, ALU.mult, ALU.min))
                link(v.tensor_tensor(p[:, :], p[:, :], ld[:, :], ALU.mult))
                softmax(1, p[:, :], w[:, :], vec)
                v.wait_ge(*const_loaded.after(0))
                link(rank.select(v, 0, w[:, :].rearrange("p (g e) -> p g e", g=1),
                                 sel[:, :].rearrange("p (g e) -> p g e", g=1), vec))
                softmax(2, w[:, :], w[:, :], vec)
                for r in range(2):
                    link(v.tensor_scalar(sel[:, :], rank.rank[:, 0, :], float(r), None, ALU.is_equal))
                    v.tensor_tensor(pick[:, r, :], sel[:, :], number[:, :], ALU.mult)
                    link(v.tensor_tensor(pick[:, 2 + r, :], sel[:, :], w[:, :], ALU.mult))
                link(v.reduce_sum(got[:, :], pick[:, :, :], AX.X))
                v.tensor_copy(chosen[:, :], got[:, 0:2]).then_inc(*ready.one())


def combine(v, i, pY, coef, Z, acc, chain):
    v.tensor_tensor(Z[:, :, :], pY.rearrange("p (e c) -> p e c", e=EXPERTS), bc(coef, C), ALU.mult).then_inc(
        *chain.one())
    v.wait_ge(*chain.latest(i))
    return v.reduce_sum(acc, Z[:, :, :].rearrange("p e c -> p c e"), AX.X)


def stage_ffn0(nc, A, h, route_dram, chosen_dram):
    E, F = EXPERTS, 128
    with Stage(nc, "ffn0") as st:
        f = Front(st)
        tail = Norm(st, PT, 4, bodies=BODIES, name="tail")
        w1 = st.sb("w1", [C + 1, 2, 2, 2, F])
        w2 = st.sb("w2", [F, 2, 2, 2, C])
        b2 = st.sb("b2", [1, 2, 2, 2, C])
        wB = st.sb("wB", [PT, 2, 2, 2])
        number = st.sb("number", [1, BATCH * 2], mybir.dt.int32)
        ones = st.sb("ones", [1, PT])
        gamma = st.sb("gamma", [PT, C])
        beta = st.sb("beta", [PT, C])
        hT = st.sb("hT", [F, 2, 2, T])
        Z = st.sb("Z", [PT, 4, 2, C])
        acc = st.sb("acc", [PT, 4, C])
        pH = st.psum("pH", [F, 2, 512])
        pY = st.psum("pY", [PT, 2, 512])
        weights = st.transfers("weights")
        hid_done = st.event("hid_done", bodies=BODIES)
        hid_ready = st.event("hid_ready", bodies=BODIES)
        y_done = st.event("y_done", bodies=BODIES)
        y_used = st.event("y_used", bodies=BODIES)
        vec = st.event("vec", bodies=BODIES)
        with st.block() as block:
            @block.sync
            def _(sp):
                cl = f.const_loaded
                const(sp, cl, number[:, :], row(chosen_dram.rearrange("b k -> (b k)")))
                const(sp, cl, f.ident[:, :], A["const_ident"])
                const(sp, cl, gamma[:, :], every_row(A["L0_ffn_gamma"], PT))
                const(sp, cl, beta[:, :], every_row(A["L0_ffn_beta"], PT))
                sp.wait_ge(*cl.after(0))

                def weights_of(n, u):
                    sp.dma_start(wB[:, u, :, :], every_row(route_dram[bass.ds(n * 2, 2), :], PT)).then_inc(
                        *weights.one(u))
                    for b in range(2):
                        for k in range(2):
                            e = sp.value_load(number[0:1, bass.ds(n * 4 + (2 * b + k), 1)], min_val=0,
                                              max_val=E - 1)
                            sp.dma_start(w1[:, u, b, k, :], A["w1b1"][bass.ds(e, 1)].rearrange(
                                "o c f -> (o c) f")).then_inc(*weights.one(u))
                            sp.dma_start(w2[:, u, b, k, :], A["L0_ffn_W2"][bass.ds(e, 1)].rearrange(
                                "o f c -> (o f) c")).then_inc(*weights.one(u))
                            sp.dma_start(b2[:, u, b, k, :], A["L0_ffn_b2"][bass.ds(e, 1), :]).then_inc(
                                *weights.one(u))
                f.stream(sp, h, h, beside=weights_of)

            @block.gpsimd
            def _(g):
                g.wait_ge(*f.memset_done.after(0))

                def front(n, u):
                    f.norm.power(g, n, 0)

                def main(n, u, ahead):
                    ahead()
                    tail.square_pool(g, n, 0, tail.xc[:, :, :])
                    tail.power(g, n, 0)
                pipelined(g, front, main)

            @block.tensor
            def _(pe):
                pe.wait_ge(*f.const_loaded.after(0))
                pe.wait_ge(*f.memset_done.after(0))

                def front(n, u):
                    f.transpose(pe, n, u)
                    pe.wait_ge(*f.xT_ready.after(n))
                    pe.wait_ge(*weights.after(n, u))
                    pe.wait_ge(*hid_ready.before(n))
                    st.held(pe)
                    for b in range(2):
                        for k in range(2):
                            ins = pe.matmul(pH[:, b, k * T:k * T + T], w1[:, u, b, k, :], f.xT[:, u, b, :],
                                            start=True, stop=True)
                        ins.then_inc(*hid_done.one())

                def main(n, u, ahead):
                    pe.wait_ge(*y_used.lagging(n))
                    st.held(pe)
                    for b in range(2):
                        pe.wait_ge(*hid_ready.after(n, b))
                        st.held(pe)
                        for t in range(2):
                            g0 = (2 * t + b) * 2 * C
                            pe.matmul(pY[:, u, g0:g0 + 2 * C], ones[:, :], b2[:, u, b, :, :], start=True,
                                      stop=False)
                            for k in range(2):
                                ins = pe.matmul(pY[:, u, g0 + k * C:g0 + k * C + C],
                                                hT[:, b, k, t * OFF:t * OFF + PT], w2[:, u, b, k, :], start=False,
                                                stop=(k == 1))
                    ins.then_inc(*y_done.one())
                    ahead()
                pipelined(pe, front, main)

            @block.scalar
            def _(a):
                def front(n, u):
                    f.square(a, n, u)
                    a.wait_ge(*y_done.before(n))
                    for b in range(2):
                        a.wait_ge(*hid_done.after(n, b))
                        a.activation(hT[:, b, :, :].rearrange("f k t -> f (k t)"), pH[:, b, 0:2 * T],
                                     ACT.Gelu).then_inc(*hid_ready.one())

                def main(n, u, ahead):
                    ahead()
                pipelined(a, front, main)

            @block.vector
            def _(v):
                v.memset(ones[:, :], 1.0)
                v.memset(tail.expo[:, :], -0.5)
                f.memsets(v)
                v.wait_ge(*f.memset_done.after(0))
                v.wait_ge(*f.const_loaded.after(0))

                def front(n, u, step):
                    if step == 0:
                        f.normalise(v, n, u)
                    else:
                        f.channels(v, n, u)

                def main(n, u, ahead):
                    def link(ins):
                        ins.then_inc(*vec.one())
                        v.wait_ge(*vec.latest(n))
                    ahead(0)
                    v.wait_ge(*weights.after(n, u))
                    v.wait_ge(*y_done.after(n))
                    for t in range(2):
                        ins = v.tensor_tensor(Z[:, 2 * t:2 * t + 2, :, :].rearrange("p b k c -> p (b k) c"),
                                              pY[:, u, t * 4 * C:(t + 1) * 4 * C].rearrange("p (g c) -> p g c", g=4),
                                              bc(wB[:, u, :, :].rearrange("p b k -> p (b k)"), C), ALU.mult)
                    ins.then_inc(*y_used.one())
                    v.wait_ge(*y_used.after(n))
                    ahead(1)
                    link(v.tensor_tensor(acc[:, :, :], Z[:, :, 0, :], Z[:, :, 1, :], ALU.add))
                    link(v.tensor_tensor(acc[:, :, :], acc[:, :, :], g4(f.xn[:, u, :, :, :]), ALU.add))
                    tail.center(v, n, acc[:, :, :], vec)
                    link(tail.scale(v, n, 0, tail.xc[:, :, :], acc[:, :, :], 1e-5, vec))
                    link(v.tensor_tensor(acc[:, :, :], acc[:, :, :], bcm(gamma[:, :], 1, 4), ALU.mult))
                    link(v.tensor_tensor(acc[:, :, :], acc[:, :, :], bcm(beta[:, :], 1, 4), ALU.add))
                    v.wait_ge(*f.stored.lagging(n, u))
                    v.wait_ge(*f.kept.after(n, u))
                    v.tensor_tensor(g4(f.H1[:, u, :, :, :]), acc[:, :, :], g4(f.X[:, u, :, :, :]),
                                    ALU.add).then_inc(*f.h_ready.one())
                pipelined(v, front, main, steps=2)


LOW = T + PT


def stage_retention1(nc, A, h):
    with Stage(nc, "ret1") as st:
        f = Front(st)
        W = st.sb("W", [C, 5, C])
        cs = st.sb("cos_sin", [C, 2, T])
        decay = st.sb("decay", [PT, LOW])
        t1 = st.sb("t1", [C, 2, 2, T])
        t2 = st.sb("t2", [C, 2, 2, T])
        qk = st.sb("qk", [C, 2, 2, T])
        V = st.sb("V", [PT, 4, C])
        P = st.sb("P", [PT, 2, LOW])
        pR = st.psum("pR", [C, 4, 512])
        pV = st.psum("pV", [PT, 2, 4, C])
        pS = st.psum("pS", [PT, 2, 512])
        r_done = st.event("r_done", bodies=BODIES)
        v_done = st.event("v_done", bodies=BODIES)
        v_ready = st.event("v_ready", bodies=BODIES)
        qk_ready = st.event("qk_ready", bodies=BODIES)
        s_done = st.event("s_done", bodies=BODIES)
        p_ready = st.event("p_ready", bodies=BODIES)
        o_done = st.event("o_done", bodies=BODIES)
        with st.block() as block:
            @block.sync
            def _(sp):
                cl = f.const_loaded
                const(sp, cl, f.ident[:, :], A["const_ident"])
                for k, n in enumerate(("Q", "Qx", "K", "Kx", "V")):
                    const(sp, cl, W[:, k, :], A[f"L1_attn_W_{n}"])
                const(sp, cl, cs[:, :, :], A["const_rope64"].rearrange("s c t -> c s t"))
                const(sp, cl, decay[:, :], A["const_decay"])
                f.stream(sp, h, h)

            @block.gpsimd
            def _(g):
                g.wait_ge(*f.memset_done.after(0))

                def front(n, u):
                    f.norm.power(g, n, 0)

                def main(n, u, ahead):
                    ahead()
                pipelined(g, front, main)

            @block.tensor
            def _(pe):
                pe.wait_ge(*f.const_loaded.after(0))
                pe.wait_ge(*f.memset_done.after(0))

                def front(n, u, step):
                    if step == 0:
                        f.transpose(pe, n, u)
                        return
                    pe.wait_ge(*f.xT_ready.after(n))
                    pe.wait_ge(*qk_ready.before(n))
                    st.held(pe)
                    for k in range(4):
                        pe.matmul(pR[:, k, 0:2 * T], W[:, k, :], f.xT[0:C, u, :, :], start=True,
                                  stop=True).then_inc(*r_done.one())
                    pe.wait_ge(*f.h_ready.before(n))
                    st.held(pe)
                    for t in range(2):
                        for b in range(2):
                            ins = pe.matmul(pV[:, 0, 2 * t + b, :], f.xT[0:C, u, b, t * OFF:t * OFF + PT], W[:, 4, :],
                                            start=True, stop=True)
                    ins.then_inc(*v_done.one())

                def main(n, u, ahead):
                    pe.wait_ge(*qk_ready.after(n))
                    pe.wait_ge(*p_ready.before(n))
                    st.held(pe)
                    for b in range(2):
                        pe.matmul(pS[:, b, 0:T], qk[:, 1, b, 0:PT], qk[:, 0, b, :], start=True, stop=True)
                        pe.matmul(pS[:, b, T:LOW], qk[:, 1, b, OFF:T], qk[:, 0, b, OFF:T], start=True,
                                  stop=True).then_inc(*s_done.one())
                    ahead(0)
                    pe.wait_ge(*v_ready.after(n))
                    st.held(pe)
                    for b in range(2):
                        pe.wait_ge(*p_ready.after(n, b))
                        st.held(pe)
                        pe.matmul(pV[:, 1, b, :], P[0:OFF, b, 0:PT], V[0:OFF, b, :], start=True, stop=True)
                        pe.matmul(pV[:, 1, 2 + b, :], P[0:OFF, b, OFF:T], V[0:OFF, b, :], start=True, stop=False)
                        ins = pe.matmul(pV[:, 1, 2 + b, :], P[:, b, T:LOW], V[:, 2 + b, :], start=False, stop=True)
                    ins.then_inc(*o_done.one())
                    ahead(1)
                pipelined(pe, front, main, steps=2)

            @block.scalar
            def _(a):
                def front(n, u):
                    f.square(a, n, u)
                    a.wait_ge(*v_done.after(n))
                    a.activation(V[:, :, :], pV[:, 0, :, :], ACT.Copy).then_inc(*v_ready.one())

                def main(n, u, ahead):
                    ahead()
                pipelined(a, front, main)

            @block.vector
            def _(v):
                f.memsets(v)
                v.wait_ge(*f.memset_done.after(0))
                v.wait_ge(*f.const_loaded.after(0))

                def front(n, u, step):
                    if step == 0:
                        f.normalise(v, n, u)
                    elif step == 1:
                        f.channels(v, n, u)
                    else:
                        for k in range(2):
                            v.wait_ge(*r_done.after(n, 2 * k))
                            v.tensor_tensor(t1[:, k, :, :], pR[:, 2 * k, 0:2 * T].rearrange("c (b t) -> c b t", b=2),
                                            bcm(cs[:, 0, :], 1, 2), ALU.mult)
                            v.wait_ge(*r_done.after(n, 2 * k + 1))
                            v.tensor_tensor(t2[:, k, :, :], pR[:, 2 * k + 1, 0:2 * T].rearrange(
                                "c (b t) -> c b t", b=2), bcm(cs[:, 1, :], 1, 2), ALU.mult).then_inc(
                                *f.front_vec.one())
                            v.wait_ge(*f.front_vec.latest(n))
                            v.tensor_tensor(qk[:, k, :, :], t1[:, k, :, :], t2[:, k, :, :], ALU.add).then_inc(
                                *qk_ready.one())

                def main(n, u, ahead):
                    ahead(0)
                    for b in range(2):
                        v.wait_ge(*s_done.after(n, b))
                        v.tensor_tensor(P[:, b, :], pS[:, b, 0:LOW], decay[:, :], ALU.mult).then_inc(*p_ready.one())
                    ahead(1)
                    v.wait_ge(*o_done.after(n))
                    v.wait_ge(*f.stored.lagging(n, u))
                    v.wait_ge(*f.kept.after(n, u))
                    v.tensor_tensor(g4(f.H1[:, u, :, :, :]), pV[:, 1, :, :], g4(f.X[:, u, :, :, :]), ALU.add).then_inc(
                        *f.h_ready.one())
                    ahead(2)
                pipelined(v, front, main, steps=3)


def stage_attention1(nc, A, h, hx_dram, flatT_dram, mix_dram):
    H, D, KV = 4, 16, 2
    E = EXPERTS
    with Stage(nc, "att1") as st:
        f = Front(st)
        norm = f.norm
        tail = Norm(st, PT, 4, bodies=BODIES, name="tail")
        wqk = st.sb("wqk", [C + 1, 4, H, 32])
        wv = st.sb("wv", [C + 1, KV, D + 1])
        wo = st.sb("wo", [C, C])
        wr = st.sb("wr", [C, E])
        ln1 = st.sb("ln1", [PT, C])
        ln2 = st.sb("ln2", [PT, C])
        cs = st.sb("cos_sin", [128, 2, T])
        maskQ = st.sb("maskQ", [PT, LOW])
        maskK = st.sb("maskK", [PT, LOW])
        r1 = st.sb("r1", [PT, 4, C])
        xg = st.sb("xg", [PT, 2, 2, C])
        t1 = st.sb("t1", [128, 2, T])
        t2 = st.sb("t2", [128, 2, T])
        qT = st.sb("qT", [128, 2, T])
        kT = st.sb("kT", [128, 2, 2, T])
        qmT = st.sb("qmT", [128, 2, T])
        V = st.sb("V", [PT, 2, 4, KV, D + 1])
        M = st.sb("M", [PT, 2, 2, H, 32])
        SM = st.sb("SM", [PT, 2, LOW])
        EX = st.sb("EX", [PT, 2, H, LOW])
        rden = st.sb("rden", [PT, 4, H])
        of = st.sb("of", [PT, 2, 2, C])
        oT = st.sb("oT", [C, 2, T])
        x2 = st.sb("x2", [PT, 4, C])
        fl = st.sb("fl", [PT, 2, 2, C])
        flT = st.sb("flT", [C, 2, 2, T])
        lg = st.sb("lg", [PT, 4, E])
        lsum = st.sb("lsum", [PT, 4])
        sel = st.sb("sel", [PT, 4, E])
        mix = st.sb("mix", [PT, 2, 2, 2, E])
        rank = Rank(st, PT, 4, 2)
        pX = f.pX
        pR = st.psum("pR", [128, 2, 512])
        pS = st.psum("pS", [PT, 4, 512])
        pO = st.psum("pO", [PT, 4, 128])

        cleared = st.event("cleared")
        zeroed = st.event("zeroed")
        names = """r_done q_ready k_ready v_done v_ready s_done max_ready m_done qm_ready st_done masked exp_ready
            o_done o_ready oT_done oT_ready y_done fl_ready flT_done flT_ready l_done l_shifted l_exp mix_ready
            vec"""
        (r_done, q_ready, k_ready, v_done, v_ready, s_done, max_ready, m_done, qm_ready, st_done, masked, exp_ready,
         o_done, o_ready, oT_done, oT_ready, y_done, fl_ready, flT_done, flT_ready, l_done, l_shifted, l_exp,
         mix_ready, vec) = (st.event(x, bodies=BODIES) for x in names.split())
        handed_on = st.transfers("handed_on")
        with st.block() as block:
            @block.sync
            def _(sp):
                cl = f.const_loaded
                const(sp, cl, f.ident[:, :], A["const_ident"])
                const(sp, cl, cs[:, :, :], A["const_rope16"].rearrange("s c t -> c s t"))
                const(sp, cl, maskQ[:, :], A["const_maskQ"])
                const(sp, cl, maskK[:, :], A["const_maskK"])
                const(sp, cl, wo[:, :], A["L1_ffn_woT"])
                const(sp, cl, wr[:, :], A["L1_ffn_router_wT"])
                const(sp, cl, ln1[:, :], every_row(A["L1_ffn_ln1_w"], PT))
                const(sp, cl, ln2[:, :], every_row(A["L1_ffn_ln2_w"], PT))
                const(sp, cl, rank.earlier[:, :], every_row(A["const_earlier"], PT))
                sp.wait_ge(*zeroed.after(0))
                for k, n in enumerate(("wq", "wqx")):
                    const(sp, cl, wqk[0:C, k, :, 0:D], A[f"L1_ffn_{n}T"].rearrange("c (h d) -> c h d", h=H))
                for k, n in enumerate(("wk", "wkx")):
                    for r in range(H // KV):
                        const(sp, cl, wqk[0:C, 2 + k, :, 0:D].rearrange("c (k r) d -> c r k d", k=KV)[:, r, :, :],
                              A[f"L1_ffn_{n}T"].rearrange("c (k d) -> c k d", k=KV))
                const(sp, cl, wv[0:C, :, 0:D], A["L1_ffn_wvT"].rearrange("c (k d) -> c k d", k=KV))

                def hand_on(n, u):
                    sp.wait_ge(*flT_ready.after(n))
                    st.held(sp)
                    sp.dma_start(flatT_dram[bass.ds(n, 1), :, :].rearrange("o c t -> (o c) t"),
                                 flT[:, u, :, :].rearrange("c b t -> c (b t)")).then_inc(*handed_on.one(u))
                    sp.wait_ge(*mix_ready.after(n))
                    st.held(sp)
                    for ins in store_pair(sp, mix_dram, mix[:, u, :, :, :], n, E):
                        ins.then_inc(*handed_on.one(u))
                f.stream(sp, h, hx_dram, after=hand_on)
                for n in (PAIRS - 2, PAIRS - 1):
                    sp.wait_ge(*handed_on.after(n, n % 2))

            @block.gpsimd
            def _(g):
                g.wait_ge(*f.memset_done.after(0))

                def front(n, u):
                    norm.power(g, n, 0)
                    norm.power(g, n, 1)

                def main(n, u, ahead):
                    ahead()
                    tail.power(g, n, 0)
                pipelined(g, front, main)

            @block.tensor
            def _(pe):
                pe.wait_ge(*f.const_loaded.after(0))
                pe.wait_ge(*f.memset_done.after(0))

                def front(n, u, step):
                    if step == 3:
                        pe.wait_ge(*f.xn_ready.after(n))
                        pe.wait_ge(*flT_ready.lagging(n))
                        st.held(pe)
                        transpose_rows(pe, pX, xg, f.ident).then_inc(*f.xT_done.one())
                    if step in (4, 5):
                        pe.wait_ge(*f.xT_ready.after(n))
                        if step == 5:
                            pe.wait_ge(*q_ready.after(n))
                        else:
                            pe.wait_ge(*qm_ready.before(n))
                        st.held(pe)
                        for k in (2 * (step - 4), 2 * (step - 4) + 1):
                            pe.matmul(pR[:, k % 2, 0:2 * T], wqk[:, k, :, :], f.xT[:, u, :, :], start=True,
                                      stop=True).then_inc(*r_done.one())
                    if step == 6:
                        pe.wait_ge(*k_ready.after(n))
                        st.held(pe)
                        for t in range(2):
                            for b in range(2):
                                g = 2 * t + b
                                ins = pe.matmul(pR[0:PT, 1, g * KV * (D + 1):(g + 1) * KV * (D + 1)],
                                                f.xT[:, u, b, t * OFF:t * OFF + PT], wv[:, :, :], start=True,
                                                stop=True)
                        ins.then_inc(*v_done.one())
                    if 8 <= step < 16:
                        s = step - 8
                        b, hd = s // H, s % H
                        r = 32 * hd
                        if s < H:
                            pe.wait_ge(*masked.after(n, s - H))
                        else:
                            pe.wait_ge(*max_ready.after(n, s - H))
                        pe.matmul(pS[:, hd, 0:PT], qT[r:r + D, b, 0:PT], kT[r:r + D, u, b, 0:PT], start=True,
                                  stop=True, tile_position=(r, 0))
                        pe.matmul(pS[:, hd, PT:LOW], qT[r:r + D, b, OFF:T], kT[r:r + D, u, b, :], start=True,
                                  stop=True, tile_position=(r, 0)).then_inc(*s_done.one())
                    if step == 16:
                        pe.wait_ge(*max_ready.after(n))
                        for b in range(2):
                            for t in range(2):
                                ins = pe.matmul(pR[:, 0, b * T + t * OFF:b * T + t * OFF + ROWS[t]],
                                                M[0:ROWS[t], t, b, :, :], f.ident[0:ROWS[t], 0:ROWS[t]],
                                                start=True, stop=True)
                        ins.then_inc(*m_done.one())

                def main(n, u, ahead):
                    def values(s):
                        b, hd = s // H, s % H
                        pe.wait_ge(*exp_ready.after(n, s))
                        kv, c0 = hd // (H // KV), hd * (D + 1)
                        pe.matmul(pO[:, b, c0:c0 + D + 1], EX[0:OFF, b, hd, 0:PT], V[0:OFF, u, b, kv, :],
                                  start=True, stop=True)
                        pe.matmul(pO[:, 2 + b, c0:c0 + D + 1], EX[0:OFF, b, hd, OFF:T], V[0:OFF, u, b, kv, :],
                                  start=True, stop=False)
                        return pe.matmul(pO[:, 2 + b, c0:c0 + D + 1], EX[:, b, hd, T:LOW], V[:, u, 2 + b, kv, :],
                                         start=False, stop=True)

                    def scores(s):
                        b, hd = s // H, s % H
                        r = 32 * hd
                        pe.wait_ge(*masked.after(n, s - H))
                        pe.matmul(pS[:, hd, 0:T], kT[r:r + D + 1, u, b, 0:PT], qmT[r:r + D + 1, b, :], start=True,
                                  stop=True, tile_position=(r, 0))
                        pe.matmul(pS[:, hd, T:LOW], kT[r:r + D + 1, u, b, OFF:T], qmT[r:r + D + 1, b, OFF:T],
                                  start=True, stop=True, tile_position=(r, 0)).then_inc(*st_done.one())
                    pe.wait_ge(*qm_ready.after(n))
                    scores(0)
                    scores(1)
                    for s in range(8):
                        if s < 6:
                            scores(s + 2)
                        ahead(s)
                        if s == 1:
                            pe.wait_ge(*v_ready.after(n))
                            pe.wait_ge(*o_ready.before(n))
                        if s:
                            values(s - 1)
                    ahead(8)
                    values(7).then_inc(*o_done.one())
                    ahead(9)
                    pe.wait_ge(*o_ready.after(n))
                    st.held(pe)
                    transpose_rows(pe, pX, of, f.ident).then_inc(*oT_done.one())
                    ahead(10)
                    pe.wait_ge(*oT_ready.after(n))
                    st.held(pe)
                    for t in range(2):
                        for b in range(2):
                            g = 2 * t + b
                            ins = pe.matmul(pR[0:PT, 1, g * C:(g + 1) * C], oT[:, b, t * OFF:t * OFF + PT], wo[:, :],
                                            start=True, stop=True)
                    ins.then_inc(*y_done.one())
                    ahead(11)
                    ahead(12)
                    pe.wait_ge(*fl_ready.after(n))
                    st.held(pe)
                    transpose_rows(pe, pX, fl, f.ident).then_inc(*flT_done.one())
                    ahead(13)
                    pe.wait_ge(*flT_ready.after(n))
                    st.held(pe)
                    for t in range(2):
                        for b in range(2):
                            g = 2 * t + b
                            ins = pe.matmul(pR[0:PT, 0, g * E:(g + 1) * E], flT[:, u, b, t * OFF:t * OFF + PT],
                                            wr[:, :], start=True, stop=True)
                    ins.then_inc(*l_done.one())
                    for step in (14, 15, 16):
                        ahead(step)
                pipelined(pe, front, main, steps=17)

            @block.scalar
            def _(a):
                def front(n, u, step):
                    if step == 0:
                        norm.square(a, n, 0, norm.xc[:, :, :])
                    if step == 1:
                        norm.square(a, n, 1, g4(f.xn[:, u, :, :, :]))
                    if step == 6:
                        a.wait_ge(*v_done.after(n))
                        a.activation(V[:, u, :, :, :].rearrange("p g k d -> p (g k d)"),
                                     pR[0:PT, 1, 0:4 * KV * (D + 1)], ACT.Copy).then_inc(*v_ready.one())

                def main(n, u, ahead):
                    for s in range(8):
                        b, hd = s // H, s % H
                        a.wait_ge(*masked.after(n, s))
                        a.activation(EX[:, b, hd, :], EX[:, b, hd, :], ACT.Exp, scale=D ** -0.5).then_inc(
                            *exp_ready.one())
                        ahead(s)
                    tail.square(a, n, 0, x2[:, :, :])
                    a.wait_ge(*l_shifted.after(n))
                    a.activation(lg[:, :, :], lg[:, :, :], ACT.Exp).then_inc(*l_exp.one())
                pipelined(a, front, main, steps=8)

            @block.vector
            def _(v):
                v.memset(wqk[:, :, :, :], 0.0)
                v.memset(M[:, :, :, :, :], 0.0)
                v.memset(wv[:, :, :], 0.0).then_inc(*cleared.one())
                v.wait_ge(*cleared.after(0))
                v.memset(wqk[C:C + 1, 2, :, D:D + 1], -1.0)
                v.memset(wv[C:C + 1, :, D:D + 1], 1.0).then_inc(*zeroed.one())
                v.memset(tail.expo[:, :], -0.5)
                f.memsets(v)
                v.wait_ge(*f.memset_done.after(0))
                v.wait_ge(*f.const_loaded.after(0))

                def front(n, u, step):
                    def link(ins):
                        ins.then_inc(*f.front_vec.one())
                        v.wait_ge(*f.front_vec.latest(n))

                    def rotate(k, dst, sig):
                        v.wait_ge(*r_done.after(n, 2 * k))
                        v.tensor_tensor(t1[:, :, :], pR[:, 0, 0:2 * T].rearrange("c (b t) -> c b t", b=2),
                                        bcm(cs[:, 0, :], 1, 2), ALU.mult)
                        v.wait_ge(*r_done.after(n, 2 * k + 1))
                        link(v.tensor_tensor(t2[:, :, :], pR[:, 1, 0:2 * T].rearrange("c (b t) -> c b t", b=2),
                                             bcm(cs[:, 1, :], 1, 2), ALU.mult))
                        v.tensor_tensor(dst, t1[:, :, :], t2[:, :, :], ALU.add).then_inc(*sig.one())
                    if step == 0:
                        v.wait_ge(*f.loaded.after(n, u))
                        norm.center(v, n, g4(f.F[:, u, :, :, :]), f.front_vec)
                    if step == 1:
                        norm.scale(v, n, 0, norm.xc[:, :, :], g4(f.xn[:, u, :, :, :]), 1e-5, f.front_vec).then_inc(
                            *norm.centered.one())
                    if step == 2:
                        link(norm.scale(v, n, 1, g4(f.xn[:, u, :, :, :]), r1[:, :, :], 1e-6, f.front_vec))
                        v.tensor_tensor(g4(xg[:, :, :, :]), r1[:, :, :], bcm(ln1[:, :], 1, 4), ALU.mult).then_inc(
                            *f.xn_ready.one())
                    if step == 3:
                        f.channels(v, n, u)
                    if step == 4:
                        rotate(0, qT[:, :, :], q_ready)
                    if step == 5:
                        rotate(1, kT[:, u, :, :], k_ready)
                    if 8 <= step < 16:
                        s = step - 8
                        b, hd = s // H, s % H
                        v.wait_ge(*s_done.after(n, s))
                        v.tensor_tensor(SM[:, s % 2, :], pS[:, hd, 0:LOW], maskQ[:, :], ALU.add).then_inc(
                            *f.front_vec.one())
                        v.wait_ge(*f.front_vec.latest(n))
                        v.reduce_max(M[:, 0, b, hd, D:D + 1], SM[:, s % 2, 0:PT], AX.X)
                        v.reduce_max(M[:, 1, b, hd, D:D + 1], SM[:, s % 2, PT:LOW], AX.X).then_inc(
                            *max_ready.one())
                    if step == 16:
                        v.wait_ge(*m_done.after(n))
                        v.tensor_tensor(qmT[:, :, :], qT[:, :, :], pR[:, 0, 0:2 * T].rearrange(
                            "c (b t) -> c b t", b=2), ALU.add).then_inc(*qm_ready.one())

                def main(n, u, ahead):
                    def link(ins):
                        ins.then_inc(*vec.one())
                        v.wait_ge(*vec.latest(n))
                    for s in range(8):
                        b, hd = s // H, s % H
                        v.wait_ge(*st_done.after(n, s))
                        v.tensor_tensor(EX[:, b, hd, :], pS[:, hd, 0:LOW], maskK[:, :], ALU.add).then_inc(
                            *masked.one())
                        ahead(s)
                    ahead(8)
                    v.wait_ge(*o_done.after(n))
                    o5 = pO[:, :, 0:H * (D + 1)].rearrange("p g (h d) -> p g h d", h=H)
                    link(v.reciprocal(rden[:, :, :], o5[:, :, :, D]))
                    for t in range(2):
                        for b in range(2):
                            g = 2 * t + b
                            ins = v.tensor_tensor(of[:, t, b, :].rearrange("p (h d) -> p h d", h=H),
                                                  o5[:, g, :, 0:D], bc(rden[:, g, :], D), ALU.mult)
                    ins.then_inc(*o_ready.one())
                    ahead(9)
                    v.wait_ge(*oT_done.after(n))
                    v.tensor_copy(oT[:, :, :], pX[:, :, 0:T]).then_inc(*oT_ready.one())
                    ahead(10)
                    v.wait_ge(*y_done.after(n))
                    v.tensor_tensor(x2[:, :, :], g4(f.xn[:, u, :, :, :]), pR[0:PT, 1, 0:4 * C].rearrange(
                        "p (g c) -> p g c", g=4), ALU.add).then_inc(*tail.centered.one())
                    v.wait_ge(*tail.centered.latest(n))
                    v.wait_ge(*f.stored.lagging(n, u))
                    v.wait_ge(*f.kept.after(n, u))
                    v.tensor_tensor(g4(f.H1[:, u, :, :, :]), g4(f.X[:, u, :, :, :]), x2[:, :, :], ALU.add).then_inc(
                        *f.h_ready.one())
                    ahead(11)
                    link(tail.scale(v, n, 0, x2[:, :, :], g4(fl[:, :, :, :]), 1e-6, vec))
                    v.tensor_tensor(g4(fl[:, :, :, :]), g4(fl[:, :, :, :]), bcm(ln2[:, :], 1, 4),
                                    ALU.mult).then_inc(*fl_ready.one())
                    ahead(12)
                    v.wait_ge(*flT_done.after(n))
                    v.wait_ge(*handed_on.lagging(n, u))
                    v.tensor_copy(flT[:, u, :, :], pX[:, :, 0:T]).then_inc(*flT_ready.one())
                    ahead(13)
                    v.wait_ge(*l_done.after(n))
                    pl = pR[0:PT, 0, 0:4 * E].rearrange("p (g e) -> p g e", g=4)
                    link(v.reduce_max(lsum[:, :], pl, AX.X))
                    v.tensor_tensor(lg[:, :, :], pl, bc(lsum[:, :], E), ALU.subtract).then_inc(*l_shifted.one())
                    for step in (14, 15, 16):
                        ahead(step)
                    v.wait_ge(*l_exp.after(n))
                    link(v.reduce_sum(lsum[:, :], lg[:, :, :], AX.X))
                    link(v.reciprocal(lsum[:, :], lsum[:, :]))
                    link(v.tensor_tensor(lg[:, :, :], lg[:, :, :], bc(lsum[:, :], E), ALU.mult))
                    link(rank.select(v, n, lg[:, :, :], sel[:, :, :], vec))
                    link(v.tensor_tensor(lg[:, :, :], lg[:, :, :], sel[:, :, :], ALU.mult))
                    link(v.reduce_sum(lsum[:, :], lg[:, :, :], AX.X))
                    link(v.tensor_scalar(lsum[:, :], lsum[:, :], 1e-9, None, ALU.add))
                    link(v.reciprocal(lsum[:, :], lsum[:, :]))
                    v.tensor_tensor(g4(mix[:, u, :, :, :]), lg[:, :, :], bc(lsum[:, :], E), ALU.mult).then_inc(
                        *mix_ready.one())
                pipelined(v, front, main, steps=17)


def split_weights(v, w, rest, hm, mh, lh, chain):
    top, low = slice(0, C), slice(C, 2 * C)

    def link(ins):
        ins.then_inc(*chain.one())
        v.wait_ge(*chain.latest(0))
    link(v.tensor_copy(lh[:, :], w[:, :]))
    link(v.tensor_tensor(rest[:, :], w[:, :], lh[:, :], ALU.subtract))
    link(v.tensor_copy(mh[:, :], rest[:, :]))
    v.tensor_tensor(rest[:, :], rest[:, :], mh[:, :], ALU.subtract)
    v.tensor_copy(hm[top, :], lh[top, :])
    link(v.tensor_copy(hm[low, :], mh[low, :]))
    v.tensor_copy(mh[low, :], lh[low, :])
    link(v.tensor_copy(lh[top, :], rest[top, :]))


class Thirds:

    def __init__(self, st, name, columns):
        self.st = st
        self.hm = st.sb(name + "_hm", [2 * C, 2, columns], BF16)
        self.hl = st.sb(name + "_hl", [2 * C, 2, columns], BF16)
        self.rest = st.sb(name + "_rest", [2 * C, columns])
        self.chain = st.event(name + "_split", bodies=BODIES)
        self.ready = st.event(name + "_ready", bodies=BODIES)

    def split(self, e, n, u, x):
        top, low = slice(0, C), slice(C, 2 * C)
        hm, hl, rest = (y.rearrange("c (b t) -> c b t", b=2) for y in (self.hm[:, u, :], self.hl[:, u, :],
                                                                       self.rest[:, :]))

        def link(ins):
            ins.then_inc(*self.chain.one())
            e.wait_ge(*self.chain.latest(n))
            self.st.held(e)
        e.wait_ge(*self.ready.before(n))
        self.st.held(e)
        link(e.tensor_copy(hl, x))
        link(e.tensor_tensor(rest, x, hl, ALU.subtract))
        link(e.tensor_copy(hm[top], hl[top]))
        link(e.tensor_copy(hm[low], rest[low]))
        link(e.tensor_tensor(rest[low], rest[low], hm[low], ALU.subtract))
        e.tensor_copy(hl[low], rest[low]).then_inc(*self.ready.one())

    def product(self, pe, out, u, hm, mh, lh):
        pe.matmul(out, hm, self.hm[:, u, :], start=True, stop=False)
        pe.matmul(out, mh, self.hm[:, u, :], start=False, stop=False)
        return pe.matmul(out, lh, self.hl[:, u, :], start=False, stop=True)


def stage_experts1(nc, A, h, hx_dram, flatT_dram, mix_dram):
    E, HID, HC = EXPERTS, 170, 85
    NCH = E * 2
    with Stage(nc, "moe1") as st:
        xT = st.sb("xT", [2 * C, 2, 2 * T])
        x3 = Thirds(st, "x3", 2 * T)
        w = st.sb("w", [2 * C, E * HID])
        rest = st.sb("rest", [2 * C, E * HID])
        stacks = [[st.sb(f"{x}_{y}", [2 * C, E * HID], BF16) for y in ("hm", "mh", "lh")] for x in ("w1", "w3")]
        w2 = st.sb("w2", [HC, NCH, C])
        X = st.sb("X", [PT, 2, 2, 2, C])
        H1 = st.sb("H1", [PT, 2, 2, 2, C])
        mix = st.sb("mix", [PT, 2, 2, 2, E])
        sl = st.sb("silu", [HC, 2, 2 * T])
        hT = st.sb("hT", [HC, 2, NCH, 2 * T])
        Z = st.sb("Z", [PT, E, C])
        acc = st.sb("acc", [PT, 4, C])
        pA = st.psum("pA", [HC, 2, 512])
        pG = st.psum("pG", [HC, 2, 512])
        pY = st.psum("pY", [PT, 4, 512])
        w1_loaded = st.event("w1_loaded", dma=True)
        w3_loaded = st.event("w3_loaded", dma=True)
        const_loaded = st.event("const_loaded", dma=True)
        w_split = st.event("w_split")
        w_used = st.event("w_used")
        weights_ready = st.event("weights_ready")
        xT_loaded = st.transfers("xT_loaded", start=0)
        loaded = st.transfers("loaded")
        stored = st.transfers("stored")
        gate_done = st.event("gate_done", bodies=BODIES)
        silu_ready = st.event("silu_ready", bodies=BODIES)
        hid_ready = st.event("hid_ready", bodies=BODIES)
        y_done = st.event("y_done", bodies=BODIES)
        y_used = st.event("y_used", bodies=BODIES)
        vec = st.event("vec", bodies=BODIES)
        h_ready = st.event("h_ready", bodies=BODIES)
        with st.block() as block:
            @block.sync
            def _(sp):
                for half in range(2):
                    const(sp, w1_loaded, w[half * C:(half + 1) * C, :], A["L1_ffn_w1T"])
                const(sp, const_loaded, w2[:, :, :], A["L1_ffn_w2T"].rearrange("(n p) c -> p n c", p=HC))
                sp.wait_ge(*w_used.after(0))
                for half in range(2):
                    const(sp, w3_loaded, w[half * C:(half + 1) * C, :], A["L1_ffn_w3T"])

                def front(n, u):
                    sp.wait_ge(*h_ready.lagging(n))
                    st.held(sp)
                    for ins in (load_pair(sp, X[:, u, :, :, :], hx_dram, n)
                                + load_pair(sp, mix[:, u, :, :, :], mix_dram, n, E)):
                        ins.then_inc(*loaded.one(u))

                def main(n, u, ahead):
                    ahead()
                    sp.wait_ge(*h_ready.after(n))
                    st.held(sp)
                    for ins in store_pair(sp, h, H1[:, u, :, :, :], n):
                        ins.then_inc(*stored.one(u))
                pipelined(sp, front, main)
                for n in (PAIRS - 2, PAIRS - 1):
                    sp.wait_ge(*stored.after(n, n % 2))

            @block.gpsimd
            def _(g):
                def front(n, u):
                    g.wait_ge(*x3.ready.before(n))
                    st.held(g)
                    for half in range(2):
                        g.dma_start(xT[half * C:(half + 1) * C, u, :], flatT_dram[bass.ds(n, 1), :, :].rearrange(
                            "o c t -> (o c) t")).then_inc(*xT_loaded.one(u))
                    g.wait_ge(*xT_loaded.after(n, u))
                    g.wait_ge(*gate_done.lagging(n))
                    st.held(g)
                    x3.split(g, n, u, xT[:, u, :].rearrange("c (b t) -> c b t", b=2))

                def main(n, u, ahead):
                    ahead()
                pipelined(g, front, main)

            @block.tensor
            def _(pe):
                pe.wait_ge(*const_loaded.after(0))
                pe.wait_ge(*weights_ready.after(0))

                def front(n, u, k):
                    if k == 0:
                        pe.wait_ge(*x3.ready.after(n))
                    pe.wait_ge(*hid_ready.after(n, k - 2))
                    st.held(pe)
                    cols = slice(k * HC, (k + 1) * HC)
                    x3.product(pe, pA[:, k % 2, 0:2 * T], u, *[x[:, cols] for x in stacks[0]])
                    x3.product(pe, pG[:, k % 2, 0:2 * T], u, *[x[:, cols] for x in stacks[1]]).then_inc(
                        *gate_done.one())

                def main(n, u, ahead):
                    for step in range(NCH):
                        ahead(step)
                        if step >= 12:
                            continue
                        g, part = step // 3, step % 3
                        t, b = g // 2, g % 2
                        if part == 0:
                            pe.wait_ge(*y_used.before(n))
                            pe.wait_ge(*hid_ready.after(n))
                            st.held(pe)
                        for k in range((0, 6, 12)[part], (6, 12, 16)[part]):
                            e = k // 2
                            ins = pe.matmul(pY[:, g, e * C:(e + 1) * C],
                                            hT[:, u, k, b * T + t * OFF:b * T + t * OFF + PT], w2[:, k, :],
                                            start=(k % 2 == 0), stop=(k % 2 == 1))
                        if part == 2:
                            ins.then_inc(*y_done.one())
                pipelined(pe, front, main, steps=NCH)

            @block.scalar
            def _(a):
                def front(n, u, k):
                    a.wait_ge(*gate_done.after(n, k))
                    a.activation(sl[:, k % 2, :], pA[:, k % 2, 0:2 * T], ACT.Silu).then_inc(*silu_ready.one())

                def main(n, u, ahead):
                    for step in range(NCH):
                        ahead(step)
                pipelined(a, front, main, steps=NCH)

            @block.vector
            def _(v):
                v.wait_ge(*w1_loaded.after(0))
                split_weights(v, w, rest, *stacks[0], w_split)
                v.sem_inc(*w_used.one())
                v.wait_ge(*w3_loaded.after(0))
                split_weights(v, w, rest, *stacks[1], w_split)
                v.sem_inc(*weights_ready.one())

                def front(n, u, k):
                    v.wait_ge(*silu_ready.after(n, k))
                    v.tensor_tensor(hT[:, u, k, :], sl[:, k % 2, :], pG[:, k % 2, 0:2 * T], ALU.mult).then_inc(
                        *hid_ready.one())

                def main(n, u, ahead):
                    v.wait_ge(*loaded.after(n, u))
                    for step in range(NCH):
                        ahead(step)
                        if step in (4, 7, 10, 13):
                            g = (step - 4) // 3
                            t, b = g // 2, g % 2
                            v.wait_ge(*y_done.after(n, g))
                            combine(v, n, pY[:, g, :], mix[:, u, t, b, :], Z, acc[:, g, :], vec).then_inc(
                                *y_used.one())
                            v.wait_ge(*y_used.latest(n))
                    v.wait_ge(*stored.lagging(n, u))
                    v.tensor_tensor(g4(H1[:, u, :, :, :]), acc[:, :, :], g4(X[:, u, :, :, :]), ALU.add).then_inc(
                        *h_ready.one())
                pipelined(v, front, main, steps=NCH)


def stage_attention2(nc, A, h):
    TH, HEADS, W = T // 3, 3, 192
    WC = W // 2
    SCALE = C ** -0.5
    with Stage(nc, "att2") as st:
        f = Front(st, tiles=3, rows=TH)
        we = st.sb("we", [C + 1, HEADS, W])
        wo = st.sb("wo", [WC, 2, C])
        bo = st.sb("bo", [TH, C])
        qk = st.sb("qk", [WC, 2, 2, 2 * TH])
        V = st.sb("V", [TH, 2, 2, W])
        nb = st.sb("nb", [TH, 2])
        den = st.sb("den", [TH, HEADS, 2])
        P = st.sb("P", [TH, 2, TH])
        PTr = st.sb("PTr", [TH, 2, TH])
        oT = st.sb("oT", [WC, 2, 2, TH])
        res = st.sb("res", [TH, HEADS, 2, C])
        pQ = st.psum("pQ", [WC, 2, 512])
        pV = st.psum("pV", [TH, 2, W])
        pS = st.psum("pS", [TH, 2, TH])
        pP = st.psum("pP", [TH, 2, TH])
        pO = st.psum("pO", [WC, 2, 2, TH])
        pY = st.psum("pY", [TH, HEADS, 2, C])
        names = """qk_done qk_ready v_done v_ready s_done max_ready exp_ready pt_done pt_ready o_done oT_ready
            y_done y_used vec"""
        (qk_done, qk_ready, v_done, v_ready, s_done, max_ready, exp_ready, pt_done, pt_ready, o_done, oT_ready,
         y_done, y_used, vec) = (st.event(x, bodies=BODIES) for x in names.split())

        with st.block() as block:
            @block.sync
            def _(sp):
                cl = f.const_loaded
                const(sp, cl, f.ident[:, :], A["const_ident"])
                const(sp, cl, we[0:C, :, :], A["L2_attn_W_embedT"].rearrange("n c w -> c n w"))
                const(sp, cl, we[C:C + 1, :, :], row(A["L2_attn_b_embed"]))
                const(sp, cl, wo[:, :, :], A["L2_attn_W_outT"].rearrange("(k w) c -> w k c", k=2))
                const(sp, cl, bo[:, :], every_row(A["L2_attn_b_out"], TH))

                f.stream(sp, h, h)

            @block.gpsimd
            def _(g):
                g.wait_ge(*f.memset_done.after(0))

                def front(n, u):
                    f.norm.power(g, n, 0)

                def main(n, u, ahead):
                    ahead()
                pipelined(g, front, main)

            @block.tensor
            def _(pe):
                pe.wait_ge(*f.const_loaded.after(0))
                pe.wait_ge(*f.memset_done.after(0))

                def embed(n, u, hd):
                    pe.wait_ge(*qk_ready.after(n, hd - 1))
                    st.held(pe)
                    for k in range(2):
                        ins = pe.matmul(pQ[:, k, 0:4 * TH], we[:, hd, k * WC:(k + 1) * WC],
                                        f.xT[:, u, :, 0:2 * TH], start=True, stop=True)
                    ins.then_inc(*qk_done.one())
                    pe.wait_ge(*v_ready.after(n, hd - 1))
                    st.held(pe)
                    for b in range(2):
                        ins = pe.matmul(pV[:, b, :], f.xT[:, u, b, 2 * TH:T], we[:, hd, :], start=True, stop=True)
                    ins.then_inc(*v_done.one())

                def front(n, u, step):
                    if step == 0:
                        pe.wait_ge(*f.xn_ready.after(n))
                        pe.wait_ge(*f.xT_ready.before(n))
                        st.held(pe)
                        for j in range(3):
                            for b in range(2):
                                ins = pe.transpose(f.pX[:, b, j * TH:(j + 1) * TH], f.xn[:, u, j, b, :],
                                                   f.ident[0:TH, 0:TH])
                        ins.then_inc(*f.xT_done.one())
                    else:
                        pe.wait_ge(*f.xT_ready.after(n))
                        embed(n, u, 0)

                def main(n, u, ahead):
                    def project(hd):
                        pe.wait_ge(*oT_ready.after(n, hd))
                        if hd == 0:
                            pe.wait_ge(*y_used.before(n))
                        st.held(pe)
                        for b in range(2):
                            for k in range(2):
                                ins = pe.matmul(pY[:, hd, b, :], oT[:, k, b, :], wo[:, k, :], start=(k == 0),
                                                stop=(k == 1))
                        ins.then_inc(*y_done.one())
                    for hd in range(HEADS):
                        pe.wait_ge(*qk_ready.after(n, hd))
                        pe.wait_ge(*exp_ready.after(n, 2 * hd - 1))
                        st.held(pe)
                        for b in range(2):
                            for k in range(2):
                                ins = pe.matmul(pS[:, b, :], qk[:, k, b, 0:TH], qk[:, k, b, TH:2 * TH],
                                                start=(k == 0), stop=(k == 1))
                        ins.then_inc(*s_done.one())
                        if hd < HEADS - 1:
                            embed(n, u, hd + 1)
                        else:
                            ahead(0)
                        if hd:
                            project(hd - 1)
                        pe.wait_ge(*exp_ready.after(n, 2 * hd + 1))
                        pe.wait_ge(*pt_ready.after(n, hd - 1))
                        st.held(pe)
                        for b in range(2):
                            ins = pe.transpose(pP[:, b, :], P[:, b, :], f.ident[0:TH, 0:TH])
                        ins.then_inc(*pt_done.one())
                        if hd == HEADS - 1:
                            ahead(1)
                        pe.wait_ge(*pt_ready.after(n, hd))
                        pe.wait_ge(*v_ready.after(n, hd))
                        pe.wait_ge(*oT_ready.after(n, hd - 1))
                        st.held(pe)
                        for k in range(2):
                            for b in range(2):
                                ins = pe.matmul(pO[:, k, b, :], V[:, hd % 2, b, k * WC:(k + 1) * WC], PTr[:, b, :],
                                                start=True, stop=True)
                        ins.then_inc(*o_done.one())
                    project(HEADS - 1)
                pipelined(pe, front, main, steps=2)

            @block.scalar
            def _(a):
                def values(n, hd):
                    a.wait_ge(*v_done.after(n, hd))
                    a.activation(V[:, hd % 2, :, :], pV[:, :, :], ACT.Copy).then_inc(*v_ready.one())

                def front(n, u, step):
                    if step == 0:
                        f.square(a, n, u)
                    else:
                        a.wait_ge(*o_done.before(n))
                        values(n, 0)

                def main(n, u, ahead):
                    for hd in range(HEADS):
                        a.wait_ge(*max_ready.after(n, hd))
                        for b in range(2):
                            a.activation(P[:, b, :], pS[:, b, :], ACT.Exp, bias=nb[:, b:b + 1], scale=SCALE,
                                         accum_out=den[:, hd, b:b + 1]).then_inc(*exp_ready.one())
                        if hd < HEADS - 1:
                            values(n, hd + 1)
                        a.wait_ge(*o_done.after(n, hd))
                        a.activation(oT[:, :, :, :], pO[:, :, :, :], ACT.Copy).then_inc(*oT_ready.one())
                        if hd == 0:
                            ahead(0)
                    ahead(1)
                pipelined(a, front, main, steps=2)

            @block.vector
            def _(v):
                f.memsets(v)
                v.wait_ge(*f.memset_done.after(0))
                v.wait_ge(*f.const_loaded.after(0))

                def queries_keys(n, hd):
                    v.wait_ge(*qk_done.after(n, hd))
                    v.tensor_copy(qk[:, :, :, :].rearrange("p k b t -> p k (b t)"), pQ[:, :, 0:4 * TH]).then_inc(
                        *qk_ready.one())

                def front(n, u, step):
                    if step == 0:
                        f.normalise(v, n, u)
                    elif step == 1:
                        f.channels(v, n, u)
                    else:
                        queries_keys(n, 0)

                def main(n, u, ahead):
                    def link(ins):
                        ins.then_inc(*vec.one())
                        v.wait_ge(*vec.latest(n))
                    for hd in range(HEADS):
                        v.wait_ge(*s_done.after(n, hd))
                        link(v.reduce_max(nb[:, :], pS[:, :, :], AX.X))
                        v.tensor_scalar(nb[:, :], nb[:, :], -SCALE, None, ALU.mult).then_inc(*max_ready.one())
                        if hd < HEADS - 1:
                            queries_keys(n, hd + 1)
                        else:
                            ahead(1)
                        v.wait_ge(*pt_done.after(n, hd))
                        v.tensor_copy(PTr[:, :, :], pP[:, :, :]).then_inc(*pt_ready.one())
                        if hd == 0:
                            ahead(0)
                    ahead(2)
                    v.wait_ge(*y_done.after(n))
                    link(v.reciprocal(den[:, :, :], den[:, :, :]))
                    r = g4(res[:, :, :, :])
                    v.tensor_tensor(r, g4(pY[:, :, :, :]), bc(den[:, :, :].rearrange("p n b -> p (n b)"), C),
                                    ALU.mult).then_inc(*y_used.one())
                    v.wait_ge(*y_used.after(n))
                    link(v.tensor_tensor(r, r, g4(f.xn[:, u, :, :, :]), ALU.add))
                    link(v.tensor_tensor(r, r, bcm(bo[:, :], 1, 6), ALU.add))
                    v.wait_ge(*f.stored.lagging(n, u))
                    v.wait_ge(*f.kept.after(n, u))
                    v.tensor_tensor(g4(f.H1[:, u, :, :, :]), r, g4(f.X[:, u, :, :, :]), ALU.add).then_inc(
                        *f.h_ready.one())
                pipelined(v, front, main, steps=3)


def stage_depths2(nc, A, h):
    F, KEEP = 256, int(0.5 * T) - 1
    with Stage(nc, "mod2") as st:
        f = Front(st)
        w1 = st.sb("w1", [C + 1, F])
        w2 = st.sb("w2", [128, 2, C])
        b2 = st.sb("b2", [1, C])
        ones = st.sb("ones", [1, PT])
        wr = st.sb("wr", [C + 1, PT])
        earlier = st.sb("earlier", [PT, 2, T])
        hT = st.sb("hT", [128, 2, 2, 2 * T])
        W = st.sb("W", [PT, 2, 2, T])
        junk = st.sb("junk", [PT, T])
        wn = st.sb("wn", [PT, 4])
        gt = st.sb("gt", [PT, 4])
        eq = st.sb("eq", [PT, 4])
        res = st.sb("res", [PT, 4, C])
        pW = st.psum("pW", [PT, 512])
        pH = st.psum("pH", [128, 2, 512])
        pY = st.psum("pY", [PT, 4, C])
        w_done = st.event("w_done", bodies=BODIES)
        w_ready = st.event("w_ready", bodies=BODIES)
        hid_done = st.event("hid_done", bodies=BODIES)
        hid_ready = st.event("hid_ready", bodies=BODIES)
        y_done = st.event("y_done", bodies=BODIES)
        y_used = st.event("y_used", bodies=BODIES)
        vec = st.event("vec", bodies=BODIES)
        with st.block() as block:
            @block.sync
            def _(sp):
                cl = f.const_loaded
                const(sp, cl, f.ident[:, :], A["const_ident"])
                const(sp, cl, w1[0:C, :], A["L2_ffn_w1"])
                const(sp, cl, w1[C:C + 1, :], row(A["L2_ffn_b1"]))
                const(sp, cl, w2[:, :, :], A["L2_ffn_w2"].rearrange("(k f) c -> f k c", k=2))
                const(sp, cl, b2[:, :], row(A["L2_ffn_b2"]))
                const(sp, cl, wr[0:C, :], A["wr_wide"])
                const(sp, cl, wr[C:C + 1, :], A["br_wide"])
                const(sp, cl, earlier[:, :, :], A["const_before"])
                f.stream(sp, h, h)

            @block.gpsimd
            def _(g):
                g.wait_ge(*f.memset_done.after(0))

                def front(n, u):
                    f.norm.power(g, n, 0)

                def main(n, u, ahead):
                    ahead()
                pipelined(g, front, main)

            @block.tensor
            def _(pe):
                pe.wait_ge(*f.const_loaded.after(0))
                pe.wait_ge(*f.memset_done.after(0))

                def front(n, u, step):
                    if step == 0:
                        f.transpose(pe, n, u)
                        return
                    pe.wait_ge(*f.xT_ready.after(n))
                    pe.wait_ge(*hid_ready.before(n))
                    pe.matmul(pW[:, 0:2 * T], wr[:, :], f.xT[:, u, :, :], start=True, stop=True).then_inc(
                        *w_done.one())
                    for k in range(2):
                        pe.matmul(pH[:, k, 0:2 * T], w1[:, k * 128:(k + 1) * 128], f.xT[:, u, :, :], start=True,
                                  stop=True).then_inc(*hid_done.one())

                def main(n, u, ahead):
                    pe.wait_ge(*hid_ready.after(n))
                    pe.wait_ge(*y_used.before(n))
                    st.held(pe)
                    for t in range(2):
                        for b in range(2):
                            g = 2 * t + b
                            pe.matmul(pY[:, g, :], ones[:, :], b2[:, :], start=True, stop=False)
                            for k in range(2):
                                ins = pe.matmul(pY[:, g, :], hT[:, u, k, b * T + t * OFF:b * T + t * OFF + PT],
                                                w2[:, k, :], start=False, stop=(k == 1))
                    ins.then_inc(*y_done.one())
                    ahead(0)
                    ahead(1)
                pipelined(pe, front, main, steps=2)

            @block.scalar
            def _(a):
                def front(n, u):
                    f.square(a, n, u)
                    a.wait_ge(*w_done.after(n))
                    a.activation(W[:, u, :, :].rearrange("p b t -> p (b t)"), pW[:, 0:2 * T], ACT.Copy).then_inc(
                        *w_ready.one())
                    for k in range(2):
                        a.wait_ge(*hid_done.after(n, k))
                        a.activation(hT[:, u, k, :], pH[:, k, 0:2 * T], ACT.Gelu_apprx_tanh).then_inc(
                            *hid_ready.one())

                def main(n, u, ahead):
                    ahead()
                pipelined(a, front, main)

            @block.vector
            def _(v):
                v.memset(ones[:, :], 1.0)
                f.memsets(v)
                v.wait_ge(*f.memset_done.after(0))
                v.wait_ge(*f.const_loaded.after(0))

                def front(n, u, step):
                    if step == 0:
                        f.normalise(v, n, u)
                    else:
                        f.channels(v, n, u)

                def main(n, u, ahead):
                    def link(ins):
                        ins.then_inc(*vec.one())
                        v.wait_ge(*vec.latest(n))
                    ahead(0)
                    v.wait_ge(*w_ready.after(n))
                    for t in range(2):
                        for b in range(2):
                            link(v.tensor_tensor_reduce(junk[:, 0:PT], W[:, u, b, t * OFF:t * OFF + PT],
                                                        f.ident[0:PT, 0:PT], 1.0, 0.0, ALU.mult, ALU.add,
                                                        wn[:, 2 * t + b:2 * t + b + 1]))
                    ahead(1)
                    for t in range(2):
                        for b in range(2):
                            g = 2 * t + b
                            link(v.tensor_scalar(junk[:, :], W[:, u, b, :], wn[:, g:g + 1], 0.0, ALU.is_gt, ALU.add,
                                                 accum_out=gt[:, g:g + 1]))
                            link(v.scalar_tensor_tensor(out=junk[:, :], in0=W[:, u, b, :], scalar=wn[:, g:g + 1],
                                                        in1=earlier[:, t, :], op0=ALU.is_equal, op1=ALU.mult,
                                                        accum_out=eq[:, g:g + 1]))
                    link(v.tensor_tensor(gt[:, :], gt[:, :], eq[:, :], ALU.add))
                    link(v.tensor_scalar(gt[:, :], gt[:, :], float(KEEP), None, ALU.is_lt))
                    link(v.tensor_tensor(gt[:, :], gt[:, :], wn[:, :], ALU.mult))
                    v.wait_ge(*y_done.after(n))
                    v.tensor_tensor(res[:, :, :], pY[:, :, :], bc(gt[:, :], C), ALU.mult).then_inc(*y_used.one())
                    v.wait_ge(*y_used.after(n))
                    link(v.tensor_tensor(res[:, :, :], res[:, :, :], g4(f.xn[:, u, :, :, :]), ALU.add))
                    v.wait_ge(*f.stored.lagging(n, u))
                    v.wait_ge(*f.kept.after(n, u))
                    v.tensor_tensor(g4(f.H1[:, u, :, :, :]), res[:, :, :], g4(f.X[:, u, :, :, :]), ALU.add).then_inc(
                        *f.h_ready.one())
                pipelined(v, front, main, steps=2)


def stage_attention3(nc, A, h):
    H, D, KNN = 8, 64, 32
    HP = H // 2
    STEPS = 2 * H
    AHEAD = STEPS + 2
    D0, P0, R0, O0 = 6, 6, 8, 12
    SCALE = D ** -0.5
    SELF, TAKEN = -3.4028234663852886e38, -3.0e38
    with Stage(nc, "att3") as st:
        f = Front(st, twice=True)
        x3 = Thirds(st, "x3", 2 * T)
        w = st.sb("w", [2 * C, 3 * H * D])
        rest = st.sb("rest", [2 * C, 3 * H * D])
        stacks = [st.sb(f"wqkv_{y}", [2 * C, 3 * H * D], BF16) for y in ("hm", "mh", "lh")]
        wo = st.sb("wo", [128, HP, C])
        bo = st.sb("bo", [PT, C])
        diag = st.sb("diag", [PT, 2, T])
        xf = st.sb("xf", [2 * C, 2, 2, T])
        x1 = st.sb("x1", [2 * C, 2, T])
        x2 = st.sb("x2", [2 * C, 2, T])
        sq = st.sb("sq", [PT, 4, C])
        norm2 = st.sb("norm2", [PT, 4])
        near = st.sb("near", [PT, 4, T])
        top8 = st.sb("top8", [PT, 4, 8])
        mask = st.sb("mask", [PT, 2, 4, T])
        qT = st.sb("qT", [128, 2, HP, 2, T])
        kT = st.sb("kT", [128, 2, HP, 2, T])
        V = st.sb("V", [PT, 2, 4, H * D])
        SM = st.sb("SM", [PT, 2, 2, T])
        nb = st.sb("nb", [PT, 2, 2])
        P = st.sb("P", [PT, 2, 2, T])
        den = st.sb("den", [PT, 2, 2, H])
        PTr = st.sb("PTr", [PT, 2, 2, T])
        of = st.sb("of", [PT, 4, H * D])
        oT = st.sb("oT", [128, 2, HP, T])
        res = st.sb("res", [PT, 2, 2, C])
        pQ = st.psum("pQ", [128, 512])
        pS = st.psum("pS", [PT, 2, 512])
        pP = st.psum("pP", [128, 2, 512])
        pO = st.psum("pO", [PT, 2, 512])
        names = """sq_ready rows_squared d_done d_used proj_done proj_ready s_done max_ready exp_ready pt_done
            pt_ready o_done o_ready oT_done oT_ready y_done y_used vec round"""
        (sq_ready, rows_squared, d_done, d_used, proj_done, proj_ready, s_done, max_ready, exp_ready, pt_done,
         pt_ready, o_done, o_ready, oT_done, oT_ready, y_done, y_used, vec, rounds) = (
             st.event(x, bodies=BODIES) for x in names.split())
        w_split = st.event("w_split")
        w_ready = st.event("w_ready")
        pD = f.pX[:, :, :].rearrange("p a b -> p (a b)")

        with st.block() as block:
            @block.sync
            def _(sp):
                cl = f.const_loaded
                const(sp, cl, f.ident[:, :], A["const_ident"])
                for half in range(2):
                    const(sp, cl, w[half * C:(half + 1) * C, :], A["L3_attn_Wqkv"])
                const(sp, cl, wo[:, :, :], A["L3_attn_Wout"].rearrange("(k n) c -> n k c", k=HP))
                const(sp, cl, bo[:, :], every_row(A["L3_attn_bout"], PT))
                const(sp, cl, diag[:, :, :], A["const_self"])
                f.stream(sp, h, h)

            @block.gpsimd
            def _(g):
                g.wait_ge(*f.memset_done.after(0))

                def front(n, u):
                    f.norm.power(g, n, 0)
                    g.wait_ge(*f.xT_ready.after(n))
                    g.wait_ge(*proj_done.lagging(n))
                    x3.split(g, n, u, xf[:, u, :, :])

                def main(n, u, ahead):
                    ahead()
                pipelined(g, front, main)

            @block.tensor
            def _(pe):
                pe.wait_ge(*f.const_loaded.after(0))
                pe.wait_ge(*f.memset_done.after(0))
                pe.wait_ge(*w_ready.after(0))

                def front(n, u, step):
                    if step == 2:
                        f.transpose(pe, n, u)
                    if step in (D0, D0 + 1):
                        b = step - D0
                        pe.wait_ge(*sq_ready.after(n))
                        if b:
                            pe.wait_ge(*d_used.after(n, b - 1))
                        st.held(pe)
                        for t in range(2):
                            ins = pe.matmul(pD[0:PT, t * T:t * T + T], x2[:, b, t * OFF:t * OFF + PT], x1[:, b, :],
                                            start=True, stop=True)
                        ins.then_inc(*d_done.one())
                    if step >= P0:
                        k = step - P0
                        if k == 0:
                            pe.wait_ge(*x3.ready.after(n))
                        pe.wait_ge(*proj_ready.after(n, k - 1))
                        st.held(pe)
                        if k < 2 * HP:
                            ins = x3.product(pe, pQ[:, 0:2 * T], u, *[x[:, k * 128:(k + 1) * 128] for x in stacks])
                        else:
                            t, b = (k - 2 * HP) // 2, k % 2
                            rows, cols = slice(b * T + t * OFF, b * T + t * OFF + PT), slice(2 * H * D, 3 * H * D)
                            pe.matmul(pQ[0:PT, :], x3.hm[:, u, rows], stacks[0][:, cols], start=True, stop=False)
                            pe.matmul(pQ[0:PT, :], x3.hm[:, u, rows], stacks[1][:, cols], start=False, stop=False)
                            ins = pe.matmul(pQ[0:PT, :], x3.hl[:, u, rows], stacks[2][:, cols], start=False,
                                            stop=True)
                        ins.then_inc(*proj_done.one())

                def outputs_turned(out, b, hps):
                    for k, hp in enumerate(hps):
                        for t in range(2):
                            ins = pe.transpose(out[:, k * T + t * OFF:k * T + t * OFF + ROWS[t]],
                                               of[0:ROWS[t], 2 * t + b, hp * 128:(hp + 1) * 128],
                                               f.ident[0:ROWS[t], 0:ROWS[t]])
                    ins.then_inc(*oT_done.one())

                def outputs_projected(out, b):
                    for t in range(2):
                        for hp in range(HP):
                            ins = pe.matmul(out[0:PT, t * C:(t + 1) * C], oT[:, b, hp, t * OFF:t * OFF + PT],
                                            wo[:, hp, :], start=(hp == 0), stop=(hp == HP - 1))
                    ins.then_inc(*y_done.one())

                def main(n, u, ahead):
                    pe.wait_ge(*proj_ready.after(n))
                    for step in range(AHEAD):
                        if step < STEPS:
                            s = step
                            r, hp, b = 64 * (s % 2), s % H // 2, s // H
                            pe.wait_ge(*max_ready.after(n, s - 2))
                            st.held(pe)
                            for t in range(2):
                                ins = pe.matmul(pS[:, s % 2, t * T:t * T + T],
                                                qT[r:r + D, u, hp, b, t * OFF:t * OFF + PT],
                                                kT[r:r + D, u, hp, b, :], start=True, stop=True,
                                                tile_position=(r, 0))
                            ins.then_inc(*s_done.one())
                        if 1 <= step <= STEPS:
                            s = step - 1
                            pe.wait_ge(*exp_ready.after(n, 2 * s + 1))
                            pe.wait_ge(*pt_ready.after(n, s - 2))
                            if s == 0:
                                pe.wait_ge(*y_used.before(n))
                            st.held(pe)
                            for t in range(2):
                                for kt in range(2):
                                    ins = pe.transpose(
                                        pP[0:PT, s % 2, kt * T + t * OFF:kt * T + t * OFF + ROWS[t]],
                                        P[0:ROWS[t], s % 2, t, kt * OFF:kt * OFF + PT],
                                        f.ident[0:ROWS[t], 0:ROWS[t]])
                            ins.then_inc(*pt_done.one())
                        ahead(step)
                        if step >= 2:
                            s = step - 2
                            b, hd = s // H, s % H
                            pe.wait_ge(*pt_ready.after(n, s))
                            if hd == 0:
                                pe.wait_ge(*o_ready.after(n, b - 1))
                            st.held(pe)
                            for t in range(2):
                                for kt in range(2):
                                    ins = pe.matmul(pO[:, t, hd * D:(hd + 1) * D],
                                                    PTr[0:ROWS[kt], s % 2, kt, t * OFF:t * OFF + PT],
                                                    V[0:ROWS[kt], u, 2 * kt + b, hd * D:(hd + 1) * D],
                                                    start=(kt == 0), stop=(kt == 1))
                            if hd == H - 1:
                                ins.then_inc(*o_done.one())
                        if step == O0:
                            pe.wait_ge(*o_ready.after(n, 0))
                            st.held(pe)
                            outputs_turned(pD, 0, (0, 1))
                        if step == O0 + 1:
                            pe.wait_ge(*oT_ready.after(n, 0))
                            st.held(pe)
                            outputs_turned(pD, 0, (2, 3))
                        if step == O0 + 2:
                            pe.wait_ge(*oT_ready.after(n, 1))
                            st.held(pe)
                            outputs_projected(pD, 0)
                    pe.wait_ge(*o_ready.after(n, 1))
                    st.held(pe)
                    outputs_turned(pP[:, 0, :], 1, (0, 1))
                    outputs_turned(pP[:, 1, :], 1, (2, 3))
                    pe.wait_ge(*oT_ready.after(n, 3))
                    st.held(pe)
                    outputs_projected(pP[:, 0, :], 1)
                pipelined(pe, front, main, steps=AHEAD)

            @block.scalar
            def _(a):
                def front(n, u, step):
                    if step == 0:
                        f.square(a, n, u)
                    if step == 2:
                        a.wait_ge(*f.xn_ready.after(n))
                        a.activation(sq[:, :, :], g4(f.xn[:, u, :, :, 0:C]), ACT.Square).then_inc(
                            *rows_squared.one())
                    if step == 4:
                        a.wait_ge(*f.xT_ready.after(n))
                        a.activation(x1[0:C, :, :], xf[0:C, u, :, :], ACT.Copy)
                        a.activation(x1[C:2 * C, :, :], xf[C:2 * C, u, :, :], ACT.Square)
                        a.activation(x2[0:C, :, :], xf[0:C, u, :, :], ACT.Copy, scale=2.0).then_inc(*sq_ready.one())
                    if step >= P0:
                        k = step - P0
                        a.wait_ge(*proj_done.after(n, k))
                        if k < 2 * HP:
                            a.activation((kT if k // HP else qT)[:, u, k % HP, :, :].rearrange("c b t -> c (b t)"),
                                         pQ[:, 0:2 * T], ACT.Copy, scale=1.0 if k // HP else SCALE).then_inc(
                                *proj_ready.one())
                        else:
                            a.activation(V[:, u, k - 2 * HP, :], pQ[0:PT, :], ACT.Copy).then_inc(*proj_ready.one())

                def main(n, u, ahead):
                    def turned(event, b, half, src):
                        a.wait_ge(*oT_done.after(n, event))
                        a.activation(oT[:, b, 2 * half:2 * half + 2, :].rearrange("c k t -> c (k t)"),
                                     src[:, 0:2 * T], ACT.Copy).then_inc(*oT_ready.one())
                    for step in range(AHEAD):
                        if 1 <= step <= STEPS:
                            s = step - 1
                            a.wait_ge(*pt_done.after(n, s))
                            a.activation(PTr[:, s % 2, :, :].rearrange("p k t -> p (k t)"), pP[0:PT, s % 2, 0:2 * T],
                                         ACT.Copy).then_inc(*pt_ready.one())
                        if step < STEPS:
                            s = step
                            b, hd = s // H, s % H
                            a.wait_ge(*max_ready.after(n, s))
                            for t in range(2):
                                a.activation(P[:, s % 2, t, :], SM[:, s % 2, t, :], ACT.Exp,
                                             bias=nb[:, s % 2, t:t + 1],
                                             accum_out=den[:, b, t, hd:hd + 1]).then_inc(*exp_ready.one())
                        ahead(step)
                        if step in (O0, O0 + 1):
                            turned(step - O0, 0, step - O0, pD)
                    for half in range(2):
                        turned(2 + half, 1, half, pP[:, half, :])
                pipelined(a, front, main, steps=AHEAD)

            @block.vector
            def _(v):
                v.memset(x2[C:2 * C, :, :], -1.0)
                f.memsets(v)
                v.wait_ge(*f.memset_done.after(0))
                v.wait_ge(*f.const_loaded.after(0))
                split_weights(v, w, rest, *stacks, w_split)
                v.sem_inc(*w_ready.one())

                def front(n, u, step):
                    def link(ins):
                        ins.then_inc(*f.front_vec.one())
                        v.wait_ge(*f.front_vec.latest(n))
                    if step == 0:
                        v.wait_ge(*f.loaded.after(n, u))
                        f.norm.center(v, n, g4(f.F[:, u, :, :, :]), f.front_vec)
                    if step == 1:
                        f.norm.scale(v, n, 0, f.norm.xc[:, :, :], g4(f.xn[:, u, :, :, 0:C]), 1e-5, f.front_vec)
                        v.tensor_tensor(g4(f.xn[:, u, :, :, C:2 * C]), f.norm.xc[:, :, :],
                                        bc(f.norm.rstd[:, :], C), ALU.mult).then_inc(*f.xn_ready.one())
                    if step == 3:
                        v.wait_ge(*f.xT_done.after(n))
                        v.tensor_copy(xf[:, u, :, :], f.pX[:, :, 0:T]).then_inc(*f.xT_ready.one())
                    if step in (D0, D0 + 1):
                        b = step - D0
                        if b == 0:
                            v.wait_ge(*rows_squared.after(n))
                            link(v.reduce_sum(norm2[:, :], sq[:, :, :], AX.X))
                        v.wait_ge(*d_done.after(n, b))
                        for t in range(2):
                            g = 2 * t + b
                            ins = v.scalar_tensor_tensor(out=near[:, g, :], in0=pD[0:PT, t * T:t * T + T],
                                                         scalar=norm2[:, g:g + 1], in1=diag[:, t, :],
                                                         op0=ALU.subtract, op1=ALU.add)
                        ins.then_inc(*d_used.one())
                        v.wait_ge(*d_used.after(n, b))
                    if R0 <= step < R0 + KNN // 4:
                        st.held(v)
                        for g in range(4):
                            if (step - R0) % 2 == 0:
                                ins = v.max(top8[:, g, :], near[:, g, :])
                            else:
                                ins = v.match_replace(near[:, g, :], top8[:, g, :], near[:, g, :], TAKEN)
                        ins.then_inc(*rounds.one())
                        v.wait_ge(*rounds.after(n, step - R0))
                        if step == R0 + KNN // 4 - 1:
                            link(v.tensor_scalar(mask[:, u, :, :], near[:, :, :], TAKEN, NEG, ALU.not_equal,
                                                 ALU.mult))

                def main(n, u, ahead):
                    def link(ins):
                        ins.then_inc(*vec.one())
                        v.wait_ge(*vec.latest(n))

                    def heads_done(b):
                        v.wait_ge(*o_done.after(n, b))
                        link(v.reciprocal(den[:, b, :, :], den[:, b, :, :]))
                        for t in range(2):
                            ins = v.tensor_tensor(of[:, 2 * t + b, :].rearrange("p (h d) -> p h d", h=H),
                                                  pO[:, t, :].rearrange("p (h d) -> p h d", h=H),
                                                  bc(den[:, b, t, :], D), ALU.mult)
                        ins.then_inc(*o_ready.one())

                    def residual(b, src):
                        v.wait_ge(*y_done.after(n, b))
                        v.tensor_tensor(res[:, b, :, :], src[0:PT, 0:2 * C].rearrange("p (t c) -> p t c", t=2),
                                        bcm(bo[:, :], 1, 2), ALU.add).then_inc(*y_used.one())
                        v.wait_ge(*y_used.after(n, b))
                        return v.tensor_tensor(f.H1[:, u, :, b, :], res[:, b, :, :], f.X[:, u, :, b, :], ALU.add)
                    for step in range(AHEAD):
                        if step < STEPS:
                            s = step
                            b = s // H
                            v.wait_ge(*s_done.after(n, s))
                            v.wait_ge(*exp_ready.after(n, 2 * (s - 2) + 1))
                            link(v.tensor_tensor(SM[:, s % 2, :, :], pS[:, s % 2, 0:2 * T].rearrange(
                                "p (t n) -> p t n", t=2), mask[:, u, b:4:2, :], ALU.add))
                            v.tensor_reduce(nb[:, s % 2, :], SM[:, s % 2, :, :], AX.X, ALU.max, negate=True).then_inc(
                                *max_ready.one())
                        if step == H + 1:
                            heads_done(0)
                        ahead(step)
                        if step == O0 + 3:
                            v.wait_ge(*f.stored.lagging(n, u))
                            v.wait_ge(*f.kept.after(n, u))
                            residual(0, pD)
                    heads_done(1)
                    residual(1, pP[:, 0, :]).then_inc(*f.h_ready.one())
                pipelined(v, front, main, steps=AHEAD)


def stage_switch3(nc, A, h, out):
    E, F = EXPERTS, 256
    NCH = E * 2
    ROOM = max(1, math.ceil(1.25 * BATCH * T / E))
    BIG = 3.4028234663852886e38
    with Stage(nc, "sw3") as st:
        f = Front(st, twice=True)
        x3 = Thirds(st, "x3", 2 * T)
        w = st.sb("w", [2 * C, E * F])
        rest = st.sb("rest", [2 * C, E * F])
        stacks = [st.sb(f"w1_{y}", [2 * C, E * F], BF16) for y in ("hm", "mh", "lh")]
        b1 = st.sb("b1", [128, NCH])
        w2 = st.sb("w2", [128, NCH, C])
        b2 = st.sb("b2", [1, E * C])
        b2rest = st.sb("b2rest", [1, E * C])
        b2thirds = st.sb("b2thirds", [C + 1, E * C], BF16)
        ones16 = st.sb("ones16", [PT, PT], BF16)
        upto16 = st.sb("upto16", [PT, PT], BF16)
        wg = st.sb("wg", [C + 1, E])
        upto = st.sb("upto", [PT, PT])
        lg = st.sb("lg", [PT, 4, E])
        s1 = st.sb("s1", [PT, 4])
        prb = st.sb("prb", [PT, 4])
        hot = st.sb("hot", [PT, 4, E], BF16)
        base = st.sb("base", [PT, E])
        coef = st.sb("coef", [PT, 2, 4, E])
        hT = st.sb("hT", [128, NCH, 2 * T])
        Z = st.sb("Z", [PT, E, C])
        acc = st.sb("acc", [PT, 2, 2, C])
        ok = st.sb("ok", [PT, 2, 2, C])
        limits = st.sb("limits", [PT, 3, 4, C])
        rank = Rank(st, PT, 4, 1)
        pH = st.psum("pH", [128, 2, 512])
        pL = st.psum("pL", [PT, 4, E])
        pC = st.psum("pC", [PT, 5, E])
        pY = st.psum("pY", [PT, 3, 512])
        l_done = st.event("l_done", bodies=BODIES)
        l_shifted = st.event("l_shifted", bodies=BODIES)
        l_exp = st.event("l_exp", bodies=BODIES)
        hot_ready = st.event("hot_ready", bodies=BODIES)
        c_done = st.event("c_done", bodies=BODIES)
        hid_done = st.event("hid_done", bodies=BODIES)
        hid_ready = st.event("hid_ready", bodies=BODIES)
        y_done = st.event("y_done", bodies=BODIES)
        vec = st.event("vec", bodies=BODIES)
        w_split = st.event("w_split")
        w_ready = st.event("w_ready")
        y_used = st.event("y_used", bodies=BODIES)
        with st.block() as block:
            @block.sync
            def _(sp):
                cl = f.const_loaded
                const(sp, cl, f.ident[:, :], A["const_ident"])
                for half in range(2):
                    const(sp, cl, w[half * C:(half + 1) * C, :], A["L3_ffn_w1T"])
                const(sp, cl, b1[:, :], A["b1_columns"])
                const(sp, cl, w2[:, :, :], A["L3_ffn_w2"].rearrange("e (k f) c -> f (e k) c", k=2))
                const(sp, cl, b2[:, :], row(A["L3_ffn_b2"].rearrange("e c -> (e c)")))
                const(sp, cl, wg[0:C, :], A["L3_ffn_gate_w"])
                const(sp, cl, wg[C:C + 1, :], row(A["L3_ffn_gate_b"]))
                const(sp, cl, upto[:, :], A["const_upto"])
                const(sp, cl, rank.earlier[:, :], every_row(A["const_earlier"], PT))
                f.stream(sp, h, out)

            @block.gpsimd
            def _(g):
                g.wait_ge(*f.memset_done.after(0))

                def front(n, u):
                    f.norm.power(g, n, 0)

                def main(n, u, ahead):
                    ahead()
                pipelined(g, front, main)

            @block.tensor
            def _(pe):
                pe.wait_ge(*f.const_loaded.after(0))
                pe.wait_ge(*f.memset_done.after(0))
                pe.wait_ge(*w_ready.after(0))

                def front(n, u, step):
                    if step == 0:
                        f.transpose(pe, n, u)
                    elif step == 1:
                        pe.wait_ge(*f.xT_ready.after(n))
                        st.held(pe)
                        for b in range(2):
                            for t in range(2):
                                ins = pe.matmul(pL[:, 2 * b + t, :], f.xT[:, u, b, t * OFF:t * OFF + PT], wg[:, :],
                                                start=True, stop=True)
                        ins.then_inc(*l_done.one())
                    else:
                        pe.wait_ge(*hot_ready.after(n))
                        st.held(pe)
                        for g in range(4):
                            for k in range(g):
                                pe.matmul(pC[:, g, :], ones16[0:ROWS[k % 2], :], hot[0:ROWS[k % 2], k, :],
                                          start=(k == 0), stop=False)
                            pe.matmul(pC[:, g, :], upto16[0:ROWS[g % 2], :], hot[0:ROWS[g % 2], g, :],
                                      start=(g == 0), stop=True)
                        for k in range(4):
                            ins = pe.matmul(pC[:, 4, :], ones16[0:ROWS[k % 2], :], hot[0:ROWS[k % 2], k, :],
                                            start=(k == 0), stop=(k == 3))
                        ins.then_inc(*c_done.one())

                def main(n, u, ahead):
                    pe.wait_ge(*x3.ready.after(n))
                    for k in range(NCH):
                        pe.wait_ge(*hid_ready.after(n, k - 2))
                        st.held(pe)
                        x3.product(pe, pH[:, k % 2, 0:2 * T], u, *[x[:, k * 128:(k + 1) * 128] for x in stacks]
                                   ).then_inc(*hid_done.one())
                    ahead(0)
                    pe.wait_ge(*hid_ready.after(n))
                    for g in range(4):
                        b, t = g // 2, g % 2
                        if g >= 3:
                            pe.wait_ge(*y_used.after(n, g - 3))
                        else:
                            pe.wait_ge(*y_used.before(n))
                        st.held(pe)
                        pe.matmul(pY[:, g % 3, :], ones16[0:C + 1, :], b2thirds[:, :], start=True, stop=False)
                        for k in range(NCH):
                            e = k // 2
                            ins = pe.matmul(pY[:, g % 3, e * C:(e + 1) * C],
                                            hT[:, k, b * T + t * OFF:b * T + t * OFF + PT], w2[:, k, :],
                                            start=False, stop=(k == NCH - 1))
                        ins.then_inc(*y_done.one())
                        if g in (1, 3):
                            ahead(1 + g // 2)
                pipelined(pe, front, main, steps=3)

            @block.scalar
            def _(a):
                a.wait_ge(*f.const_loaded.after(0))

                def front(n, u, step):
                    if step == 0:
                        f.square(a, n, u)
                    else:
                        a.wait_ge(*l_shifted.after(n))
                        a.activation(lg[:, :, :], lg[:, :, :], ACT.Exp).then_inc(*l_exp.one())

                def main(n, u, ahead):
                    for k in range(NCH):
                        a.wait_ge(*hid_done.after(n, k))
                        a.activation(hT[:, k, :], pH[:, k % 2, 0:2 * T], ACT.Relu, bias=b1[:, k:k + 1]).then_inc(
                            *hid_ready.one())
                        if k == 4:
                            ahead(0)
                    ahead(1)
                pipelined(a, front, main, steps=2)

            @block.vector
            def _(v):
                v.memset(ones16[:, :], 1.0)
                v.memset(base[:, :], 0.0)
                v.memset(limits[:, 0, :, :], 10000.0)
                v.memset(limits[:, 1, :, :], -10000.0)
                v.memset(limits[:, 2, :, :], 0.0)
                v.memset(b2thirds[:, :], 0.0)
                f.memsets(v)
                v.wait_ge(*f.memset_done.after(0))
                v.wait_ge(*f.const_loaded.after(0))
                split_weights(v, w, rest, *stacks, w_split)
                for third in range(3):
                    r = b2 if third == 0 else b2rest
                    v.tensor_copy(b2thirds[32 * third:32 * third + 1, :], r[:, :]).then_inc(*w_split.one())
                    v.wait_ge(*w_split.latest(0))
                    if third < 2:
                        v.tensor_tensor(b2rest[:, :], r[:, :], b2thirds[32 * third:32 * third + 1, :],
                                        ALU.subtract).then_inc(*w_split.one())
                        v.wait_ge(*w_split.latest(0))
                v.tensor_copy(upto16[:, :], upto[:, :]).then_inc(*w_ready.one())

                def front(n, u, step):
                    def link(ins):
                        ins.then_inc(*f.front_vec.one())
                        v.wait_ge(*f.front_vec.latest(n))
                    if step == 0:
                        f.normalise(v, n, u)
                    elif step == 1:
                        v.wait_ge(*f.xT_done.after(n))
                        x3.split(v, n, u, f.pX[:, :, 0:T])
                        f.channels(v, n, u)
                    elif step == 2:
                        v.wait_ge(*l_done.after(n))
                        link(v.reduce_max(s1[:, :], pL[:, :, :], AX.X))
                        v.tensor_tensor(lg[:, :, :], pL[:, :, :], bc(s1[:, :], E), ALU.subtract).then_inc(
                            *l_shifted.one())
                        v.wait_ge(*l_exp.after(n))
                        link(v.reduce_sum(s1[:, :], lg[:, :, :], AX.X))
                        link(v.reciprocal(s1[:, :], s1[:, :]))
                        link(v.tensor_tensor(lg[:, :, :], lg[:, :, :], bc(s1[:, :], E), ALU.mult))
                        v.reduce_max(prb[:, :], lg[:, :, :], AX.X)
                        rank.select(v, n, lg[:, :, :], hot[:, :, :], f.front_vec).then_inc(*hot_ready.one())
                    else:
                        v.wait_ge(*hot_ready.after(n))
                        v.wait_ge(*c_done.after(n))
                        own = coef[:, u, :, :]
                        link(v.tensor_tensor(own, pC[:, 0:4, :], bcm(base[:, :], 1, 4), ALU.add))
                        link(v.tensor_scalar(own, own, float(ROOM), None, ALU.is_le))
                        link(v.tensor_tensor(own, own, hot[:, :, :], ALU.mult))
                        v.tensor_tensor(own, own, bc(prb[:, :], E), ALU.mult)
                        link(v.tensor_tensor(base[:, :], base[:, :], pC[:, 4, :], ALU.add))

                def main(n, u, ahead):
                    def link(ins):
                        ins.then_inc(*vec.one())
                        v.wait_ge(*vec.latest(n))
                    ahead(0)
                    ahead(1)
                    for g in range(4):
                        b, t = g // 2, g % 2
                        v.wait_ge(*y_done.after(n, g))
                        combine(v, n, pY[:, g % 3, :], coef[:, u, g, :], Z, acc[:, t, b, :], vec).then_inc(
                            *y_used.one())
                        v.wait_ge(*y_used.latest(n))
                        if g == 1:
                            ahead(2)
                    y, o = g4(acc[:, :, :, :]), g4(ok[:, :, :, :])
                    mask = o.bitcast(mybir.dt.uint32)
                    link(v.tensor_scalar(o, y, BIG, None, ALU.is_gt))
                    st.held(v)
                    link(v.copy_predicated(y, mask, limits[:, 0, :, :]))
                    link(v.tensor_scalar(o, y, -BIG, None, ALU.is_lt))
                    st.held(v)
                    link(v.copy_predicated(y, mask, limits[:, 1, :, :]))
                    link(v.tensor_tensor(o, y, y, ALU.not_equal))
                    st.held(v)
                    link(v.copy_predicated(y, mask, limits[:, 2, :, :]))
                    v.wait_ge(*f.stored.lagging(n, u))
                    v.wait_ge(*f.kept.after(n, u))
                    v.tensor_tensor(g4(f.H1[:, u, :, :, :]), y, g4(f.X[:, u, :, :, :]), ALU.add).then_inc(
                        *f.h_ready.one())
                    ahead(3)
                pipelined(v, front, main, steps=4)


def build(nc, A, out):
    h = nc.dram_tensor("h_stream", [BATCH, T, C], F32, kind="Internal").ap()
    mean = nc.dram_tensor("token_mean", [C, BATCH], F32, kind="Internal").ap()
    route = nc.dram_tensor("routing0", [BATCH, 2], F32, kind="Internal").ap()
    chosen = nc.dram_tensor("chosen0", [BATCH, 2], mybir.dt.int32, kind="Internal").ap()
    hx = nc.dram_tensor("stream_attended1", [BATCH, T, C], F32, kind="Internal").ap()
    flatT = nc.dram_tensor("normed1", [PAIRS, C, 2 * T], F32, kind="Internal").ap()
    mix = nc.dram_tensor("mixing1", [BATCH, T, EXPERTS], F32, kind="Internal").ap()
    stage_tokenizer(nc, A, h)
    stage_attention0(nc, A, h, mean)
    stage_router0(nc, A, mean, route, chosen)
    stage_ffn0(nc, A, h, route, chosen)
    stage_retention1(nc, A, h)
    stage_attention1(nc, A, h, hx, flatT, mix)
    stage_experts1(nc, A, h, hx, flatT, mix)
    stage_attention2(nc, A, h)
    stage_depths2(nc, A, h)
    stage_attention3(nc, A, h)
    stage_switch3(nc, A, h, out)
    if MISCOUNTED:
        raise ValueError(f"events per iteration differ from PER: {MISCOUNTED}")


def interpolation_taps():
    f = np.float32
    pos = np.arange(POINTS, dtype=f) * f(1.0 / (POINTS - 1))
    pos[-1] = 1.0
    x = pos * f(SAMPLES - 1)
    i0 = np.floor(x)
    frac = x - i0
    a = -0.75
    w = np.zeros((T, 20, 64), f)
    p = np.arange(T * 64)
    for off in range(-1, 3):
        t = np.abs(frac[p] - f(off))
        near = ((f(a + 2.0) * t - f(a + 3.0)) * t) * t + f(1.0)
        far = ((f(a) * t - f(5.0 * a)) * t + f(8.0 * a)) * t - f(4.0 * a)
        val = np.where(t <= 1.0, near, np.where(t < 2.0, far, f(0.0)))
        idx = np.clip(i0[p].astype(np.int64) + off, -1, SAMPLES - 1)
        w[p // 64, idx - (16 * (p // 64) - 2), p % 64] += val
    return w


def constants():
    f = np.float32
    n, k = np.arange(64)[:, None], np.arange(33)[None, :]
    ang = 2 * np.pi * ((n * k) % 64) / 64
    e = np.arange(EXPERTS)
    key = np.arange(PT)[:, None]
    gap = np.concatenate([np.arange(T)[None, :] - key, np.arange(PT)[None, :] - key], 1)
    decay = np.exp((np.maximum(gap, 0).astype(f) * f(np.log(0.96875))).astype(np.float64)).astype(f)
    inv = f(1.0) / np.power(10000.0, np.arange(0, 64, 2) / 64.0).astype(f)
    ang64 = np.repeat((np.arange(T, dtype=f)[:, None] * inv[None, :]).T, 2, axis=0).astype(np.float64)
    sign = np.where(np.arange(64) % 2, 1.0, -1.0)[:, None]
    inv16 = f(1.0) / f(10000.0) ** (np.arange(0, 16, 2, dtype=f) / 16)
    ang16 = np.concatenate([np.outer(np.arange(T, dtype=f), inv16)] * 2, -1).T
    rope16 = np.zeros((2, 4, 32, T), f)
    rope16[0, :, 0:16] = np.cos(ang16)
    rope16[0, :, 16] = 1.0
    rope16[1, :, 0:16] = np.sin(ang16) * np.where(np.arange(16) < 8, -1, 1)[:, None].astype(f)
    qry = np.arange(PT)[:, None]
    late = np.concatenate([np.arange(PT)[None, :] - qry, np.arange(T)[None, :] - qry - OFF], 1)
    token = np.arange(PT)[:, None, None] + np.array([0, OFF])[None, :, None]
    col = np.arange(T)[None, None, :]
    return {
        "const_before": (col < token).astype(f),
        "const_self": np.where(col == token, f(-3.4028234663852886e38), f(0)),
        "const_upto": (np.arange(PT)[:, None] <= np.arange(PT)[None, :]).astype(f),
        "const_rope16": rope16.reshape(2, 128, T),
        "const_maskQ": np.where(late > 0, f(NEG), f(0)),
        "const_maskK": np.where(gap < 0, f(NEG), f(0)),
        "const_number": e.astype(f),
        "const_earlier": (e[None, :] < e[:, None]).astype(f).ravel(),
        "const_decay": np.where(gap >= 0, decay, f(0)),
        "const_rope64": np.stack([np.cos(ang64), np.sin(ang64) * sign]).astype(f),
        "const_ident": np.eye(128, dtype=f),
        "const_dft": np.concatenate([np.cos(ang), -np.sin(ang)], 1).astype(f),
        "const_taps": interpolation_taps(),
    }


def kernel(**inputs):
    import numpy as _np
    import concourse.bacc as _bacc
    from concourse import mybir as _mybir
    from concourse.bass_utils import run_bass_kernel_spmd as _run

    nc = _bacc.Bacc("TRN2", target_bir_lowering=False, num_devices=1)
    given = {k: _np.asarray(v) for k, v in inputs.items()}
    x = given.pop("x")
    arrays = dict(constants())
    arrays["x_edge"] = _np.concatenate([x[:, :1], x[:, :1], x], axis=1)
    for name, a in given.items():
        if name in TRANSPOSED:
            arrays[name + "T"] = a.T
        else:
            arrays[name] = a
        if name == "L0_ffn_W1":
            arrays["w1b1"] = _np.concatenate([a, given["L0_ffn_b1"][:, None, :]], axis=1)
        if name in ("L1_attn_W_Q", "L1_attn_W_K"):
            arrays[name + "x"] = a.reshape(64, 32, 2)[:, :, ::-1].reshape(64, 64)
        if name in ("L1_ffn_wq", "L1_ffn_wk"):
            arrays[name + "xT"] = a.reshape(-1, 2, 8, 64)[:, ::-1].reshape(-1, 64).T
        if name in ("L1_ffn_w1", "L1_ffn_w3"):
            arrays[name + "T"] = a.transpose(2, 0, 1).reshape(64, -1)
        if name == "L1_ffn_w2":
            arrays[name + "T"] = a.transpose(0, 2, 1).reshape(-1, 64)
        if name == "L3_ffn_w1":
            arrays[name + "T"] = a.transpose(1, 0, 2).reshape(64, -1)
        if name == "L3_ffn_b1":
            arrays["b1_columns"] = a.reshape(-1, 128).T
        if name == "L2_ffn_wr":
            arrays["wr_wide"] = _np.broadcast_to(a, (64, PT))
        if name == "L2_ffn_br":
            arrays["br_wide"] = _np.broadcast_to(a[None, :], (1, PT))
        if name == "L2_attn_W_embed":
            arrays[name + "T"] = a.transpose(0, 2, 1)
    for name in ("L0_ffn_W1", "L0_ffn_b1", "L1_ffn_w1", "L1_ffn_w2", "L1_ffn_w3", "L2_attn_W_embed", "L2_ffn_attention_mask",
                 "L2_ffn_wr", "L2_ffn_br", "L3_ffn_w1", "L3_ffn_b1"):
        del arrays[name]
    arrays = {f"in_{k}": _np.ascontiguousarray(a) for k, a in arrays.items()}
    A = {k[3:]: nc.dram_tensor(k, a.shape, _mybir.dt.from_np(a.dtype), kind="ExternalInput").ap()
         for k, a in arrays.items()}
    out = nc.dram_tensor("out", (BATCH, T, C), F32, kind="ExternalOutput").ap()
    build(nc, A, out)
    r = _run(nc, [arrays], core_ids=[0])
    return r.results[0]["out"]
```
